# Optimizing a Trainium2 kernel written in Bass

```python
import numpy as np
import jax
import jax.numpy as jnp

def _softmax(x, axis=-1):
    return jax.nn.softmax(x, axis=axis)

def _gelu(x):
    return jax.nn.gelu(x, approximate=True)

def _silu(x):
    return jax.nn.silu(x)

def _sigmoid(x):
    return jax.nn.sigmoid(x)

def _layernorm(x, axis=-1, eps=1e-05):
    m = jnp.mean(x, axis=axis, keepdims=True)
    v = jnp.var(x, axis=axis, keepdims=True)
    return (x - m) / jnp.sqrt(v + eps)

def _scatter_add(tgt, idx, src, axis=0):
    return tgt.at[idx].add(src)

def _segment_sum(src, seg, n):
    return jax.ops.segment_sum(src, seg, n)
kernel_name = 'mk_flamingo_gated_d4_seqx_r8_94ecb7'

def setup_inputs(seed: int=0):
    np.random.seed(seed)
    _w = jnp.asarray

    def _rec_inputs():
        import jax
        import jax.numpy as jnp
        _rk = jax.random.key(seed)
        x = -0.0002928 + 1 * jax.random.normal(jax.random.fold_in(_rk, 1), (64, 128, 128), jnp.float32)
        _lenS = 128 - jax.random.randint(jax.random.fold_in(_rk, 7), (64,), 0, max(1, 128 // 4) + 1, jnp.int32)
        _lenS2 = 77 - jax.random.randint(jax.random.fold_in(_rk, 8), (64,), 0, max(1, 77 // 4) + 1, jnp.int32)
        _ctx_512P = jax.random.normal(jax.random.fold_in(_rk, 11), (64, 16, 64), jnp.float32)
        _ctx_512c = jax.random.dirichlet(jax.random.fold_in(_rk, 511), 0.3 * jnp.ones((16,), jnp.float32), (64, 77))
        _ctx_512t = jnp.einsum('bsk,bkd->bsd', _ctx_512c, _ctx_512P)
        _ctx_512t = _ctx_512t * jax.lax.rsqrt(jnp.mean(jnp.square(_ctx_512t)) + 1e-12) * 0.953939
        ctx_512 = -0.000514642 + 1.00011 * (_ctx_512t + 0.3 * jax.random.normal(jax.random.fold_in(_rk, 611), (64, 77, 64), jnp.float32))
        _g = jax.random.normal(jax.random.fold_in(_rk, 9001), (2, 4), jnp.float32)
        _g = jnp.sign(_g) * jnp.maximum(jnp.abs(_g), 1.0) + (_g == 0) * 1.0
        g_xattn = _g[0]
        g_ffn = _g[1]
        return (x, ctx_512, g_xattn, g_ffn)
    x, ctx_512, g_xattn, g_ffn = _rec_inputs()

    def _L0_xattn_setup():
        import jax, jax.numpy as jnp
        import numpy as np
        DIM = 128
        LATENT_DIM = 64
        NUM_HEADS = 16
        HEAD_DIM = DIM // NUM_HEADS
        SCALE = HEAD_DIM ** (-0.5)
        key = jax.random.key(seed)
        k1, k2, k3, k4, k5 = jax.random.split(key, 5)
        B, xN, zN = (2, 256, 256)
        x = jax.random.normal(k1, (B, xN, DIM), dtype=jnp.float32)
        z = jax.random.normal(k2, (B, zN, LATENT_DIM), dtype=jnp.float32)
        Wq = jax.random.normal(k3, (DIM, DIM), dtype=jnp.float32) * DIM ** (-0.5)
        Wkv = jax.random.normal(k4, (2 * DIM, LATENT_DIM), dtype=jnp.float32) * LATENT_DIM ** (-0.5)
        Wo = jax.random.normal(k5, (DIM, DIM), dtype=jnp.float32) * DIM ** (-0.5)
        return {'x': x, 'z': z, 'Wq': Wq, 'Wkv': Wkv, 'Wo': Wo}
    _L0_xattn_all = _L0_xattn_setup()
    _L0_xattn_in = {k: v for k, v in _L0_xattn_all.items() if k in ('Wq', 'Wkv', 'Wo')}
    del _L0_xattn_all

    def _L0_ffn_setup():
        import jax, jax.numpy as jnp
        import numpy as np
        TOP_K = 2
        key = jax.random.key(seed)
        ks = jax.random.split(key, 7)
        B_, S, D, F, E, R = (2, 256, 128, 512, 4, 4)
        x = jax.random.normal(ks[0], (B_, S, D), dtype=jnp.float32)
        Wg = jax.random.normal(ks[1], (E, D), dtype=jnp.float32) * (1.0 / np.sqrt(D))
        bg = jnp.zeros((E,), dtype=jnp.float32)
        Wi = jax.random.normal(ks[2], (F, D), dtype=jnp.float32) * (1.0 / np.sqrt(D))
        Wo = jax.random.normal(ks[3], (D, F), dtype=jnp.float32) * (1.0 / np.sqrt(F))
        A = jax.random.normal(ks[4], (E, R, D), dtype=jnp.float32) * (1.0 / np.sqrt(D))
        Bm = jax.random.normal(ks[5], (E, F, R), dtype=jnp.float32) * 0.01
        return {'x': x, 'Wg': Wg, 'bg': bg, 'Wi': Wi, 'Wo': Wo, 'A': A, 'B': Bm}
    _L0_ffn_all = _L0_ffn_setup()
    _L0_ffn_in = {k: v for k, v in _L0_ffn_all.items() if k in ('Wg', 'bg', 'Wi', 'Wo', 'A', 'B')}
    del _L0_ffn_all

    def _L1_xattn_setup():
        import jax, jax.numpy as jnp
        import numpy as np
        NUM_HEADS = 16
        HEAD_DIM = 64
        Q_DIM = 128
        KV_DIM = 64
        INNER = NUM_HEADS * HEAD_DIM
        key = jax.random.key(seed)
        ks = jax.random.split(key, 7)
        B, N, M = (32, 128, 256)
        q = jax.random.normal(ks[0], (B, N, Q_DIM), dtype=jnp.float32)
        kv = jax.random.normal(ks[1], (B, M, KV_DIM), dtype=jnp.float32)
        Wq = jax.random.normal(ks[2], (Q_DIM, INNER), dtype=jnp.float32) / np.sqrt(Q_DIM)
        Wk = jax.random.normal(ks[3], (KV_DIM, INNER), dtype=jnp.float32) / np.sqrt(KV_DIM)
        Wv = jax.random.normal(ks[4], (KV_DIM, INNER), dtype=jnp.float32) / np.sqrt(KV_DIM)
        Wo = jax.random.normal(ks[5], (INNER, Q_DIM), dtype=jnp.float32) / np.sqrt(INNER)
        bo = jax.random.normal(ks[6], (Q_DIM,), dtype=jnp.float32) * 0.01
        return {'q': q, 'kv': kv, 'Wq': Wq, 'Wk': Wk, 'Wv': Wv, 'Wo': Wo, 'bo': bo}
    _L1_xattn_all = _L1_xattn_setup()
    _L1_xattn_in = {k: v for k, v in _L1_xattn_all.items() if k in ('Wq', 'Wk', 'Wv', 'Wo', 'bo')}
    del _L1_xattn_all

    def _L1_ffn_setup():
        import jax, jax.numpy as jnp
        import numpy as np
        B, T, D, F, E, TOP_K = (2, 256, 128, 512, 8, 2)
        INIT = 0.02
        key = jax.random.key(seed)
        k0, k1, k2, k3, k4 = jax.random.split(key, 5)
        x = jax.random.normal(k0, (B, T, D), dtype=jnp.float32)
        Wg = jax.random.normal(k1, (D, E), dtype=jnp.float32) * INIT
        W1 = jax.random.normal(k2, (E, D, F), dtype=jnp.float32) * INIT
        W3 = jax.random.normal(k3, (E, D, F), dtype=jnp.float32) * INIT
        W2 = jax.random.normal(k4, (E, F, D), dtype=jnp.float32) * INIT
        return {'x': x, 'Wg': Wg, 'W1': W1, 'W3': W3, 'W2': W2}
    _L1_ffn_all = _L1_ffn_setup()
    _L1_ffn_in = {k: v for k, v in _L1_ffn_all.items() if k in ('Wg', 'W1', 'W3', 'W2')}
    del _L1_ffn_all

    def _L2_xattn_setup():
        import jax, jax.numpy as jnp
        import numpy as np
        HEADS = 16
        D_MODEL = 128
        IMG_MODEL = 64
        D_K = D_MODEL // HEADS
        key = jax.random.key(seed)
        ks = jax.random.split(key, 12)
        B, LQ, LKV = (8, 256, 128)
        s_dm = 1.0 / np.sqrt(D_MODEL)
        s_im = 1.0 / np.sqrt(IMG_MODEL)
        return {'q': jax.random.normal(ks[0], (B, LQ, D_MODEL), jnp.float32), 'k': jax.random.normal(ks[1], (B, LKV, IMG_MODEL), jnp.float32), 'v': jax.random.normal(ks[2], (B, LKV, IMG_MODEL), jnp.float32), 'Wq': jax.random.normal(ks[3], (D_MODEL, D_MODEL), jnp.float32) * s_dm, 'bq': jnp.zeros((D_MODEL,), jnp.float32), 'Wk': jax.random.normal(ks[4], (IMG_MODEL, D_MODEL), jnp.float32) * s_im, 'bk': jnp.zeros((D_MODEL,), jnp.float32), 'Wv': jax.random.normal(ks[5], (IMG_MODEL, D_MODEL), jnp.float32) * s_im, 'bv': jnp.zeros((D_MODEL,), jnp.float32), 'Wo': jax.random.normal(ks[6], (D_MODEL, D_MODEL), jnp.float32) * s_dm, 'bo': jnp.zeros((D_MODEL,), jnp.float32)}
    _L2_xattn_all = _L2_xattn_setup()
    _L2_xattn_in = {k: v for k, v in _L2_xattn_all.items() if k in ('Wq', 'bq', 'Wk', 'bk', 'Wv', 'bv', 'Wo', 'bo')}
    del _L2_xattn_all

    def _L2_ffn_setup():
        import jax, jax.numpy as jnp
        import numpy as np
        H = 128
        M = 64
        E = 16
        TOP_K = 2
        SCALE = 2.5
        NORM_TOPK = True
        B, S = (1, 128)

        def _moe(x, gate_w, w_gate, w_up, w_down, ws_gate, ws_up, ws_down):
            T = x.shape[0]
            shared = jax.nn.silu(x @ ws_gate) * (x @ ws_up) @ ws_down
            scores = jax.nn.sigmoid(x.astype(jnp.float32) @ gate_w.T.astype(jnp.float32))
            topk_w, topk_idx = jax.lax.top_k(scores, TOP_K)
            if NORM_TOPK and TOP_K > 1:
                topk_w = topk_w / (topk_w.sum(-1, keepdims=True) + 1e-20)
            topk_w = topk_w * SCALE
            route = jnp.zeros((T, E), topk_w.dtype).at[jnp.arange(T)[:, None], topk_idx].set(topk_w)
            g = jnp.einsum('th,ehm->etm', x, w_gate)
            u = jnp.einsum('th,ehm->etm', x, w_up)
            eo = jnp.einsum('etm,emh->eth', jax.nn.silu(g) * u, w_down)
            routed = jnp.einsum('te,eth->th', route.astype(x.dtype), eo)
            return routed + shared
        key = jax.random.key(seed)
        ks = jax.random.split(key, 8)
        std = 0.02
        return {'hidden_states': jax.random.normal(ks[0], (B, S, H), jnp.float32), 'gate_w': jax.random.normal(ks[1], (E, H), jnp.float32) * std, 'w_gate': jax.random.normal(ks[2], (E, H, M), jnp.float32) * std, 'w_up': jax.random.normal(ks[3], (E, H, M), jnp.float32) * std, 'w_down': jax.random.normal(ks[4], (E, M, H), jnp.float32) * std, 'ws_gate': jax.random.normal(ks[5], (H, M), jnp.float32) * std, 'ws_up': jax.random.normal(ks[6], (H, M), jnp.float32) * std, 'ws_down': jax.random.normal(ks[7], (M, H), jnp.float32) * std}
    _L2_ffn_all = _L2_ffn_setup()
    _L2_ffn_in = {k: v for k, v in _L2_ffn_all.items() if k in ('gate_w', 'w_gate', 'w_up', 'w_down', 'ws_gate', 'ws_up', 'ws_down')}
    del _L2_ffn_all

    def _L3_xattn_setup():
        import jax, jax.numpy as jnp
        import numpy as np
        H, D, C1, C2, S, M, B, W = (16, 32, 128, 64, 256, 64, 2, 4)

        def _ln(x, g, b):
            m = jnp.mean(x, -1, keepdims=True)
            v = jnp.var(x, -1, keepdims=True)
            return (x - m) * jax.lax.rsqrt(v + 1e-05) * g + b

        def _mha(x, y, wq, wk, wv, li1_w, li1_b, lnx_g, lnx_b, lny_g, lny_b, ln3_g, ln3_b, li2_w, li2_b, li3_w, li3_b, causal):
            xn = _ln(x, lnx_g, lnx_b)
            yn = _ln(y, lny_g, lny_b)
            q = jnp.einsum('bsc,hcd->bhsd', xn, wq)
            k = jnp.einsum('btc,hcd->bhtd', yn, wk)
            v = jnp.einsum('btc,hcd->bhtd', yn, wv)
            a = jax.nn.softmax(jnp.einsum('bhsd,bhtd->bhst', q, k) * D ** (-0.5), axis=-1)
            if causal:
                s, t = (a.shape[-2], a.shape[-1])
                mask = (jnp.arange(t)[None, :] > jnp.arange(s)[:, None]).astype(a.dtype)
                a = a * mask
            o = jnp.einsum('bhst,bhtd->bhsd', a, v)
            o = o.transpose(0, 2, 1, 3).reshape(x.shape[0], x.shape[1], H * D)
            x_out = x + o @ li1_w + li1_b
            h = jax.nn.gelu(_ln(x_out, ln3_g, ln3_b) @ li2_w + li2_b, approximate=False)
            return x_out + h @ li3_w + li3_b
        key = jax.random.key(seed)
        ks = iter(jax.random.split(key, 64))

        def w(shape, scale=0.02):
            return jax.random.normal(next(ks), shape, jnp.float32) * scale
        inp = {'xx': jax.random.normal(next(ks), (B, S, C1), jnp.float32), 'ee': jax.random.normal(next(ks), (B, M, C2), jnp.float32), 'ln1_g': jnp.ones(C1, jnp.float32), 'ln1_b': jnp.zeros(C1, jnp.float32), 'ln2_g': jnp.ones(C1, jnp.float32), 'ln2_b': jnp.zeros(C1, jnp.float32)}
        for pfx, cy in (('a1', C1), ('a2', C2)):
            inp[pfx + '_wq'] = w((H, C1, D))
            inp[pfx + '_wk'] = w((H, cy, D))
            inp[pfx + '_wv'] = w((H, cy, D))
            inp[pfx + '_li1_w'] = w((H * D, C1))
            inp[pfx + '_li1_b'] = jnp.zeros(C1, jnp.float32)
            inp[pfx + '_lnx_g'] = jnp.ones(C1, jnp.float32)
            inp[pfx + '_lnx_b'] = jnp.zeros(C1, jnp.float32)
            inp[pfx + '_lny_g'] = jnp.ones(cy, jnp.float32)
            inp[pfx + '_lny_b'] = jnp.zeros(cy, jnp.float32)
            inp[pfx + '_ln3_g'] = jnp.ones(C1, jnp.float32)
            inp[pfx + '_ln3_b'] = jnp.zeros(C1, jnp.float32)
            inp[pfx + '_li2_w'] = w((C1, C1 * W))
            inp[pfx + '_li2_b'] = jnp.zeros(C1 * W, jnp.float32)
            inp[pfx + '_li3_w'] = w((C1 * W, C1))
            inp[pfx + '_li3_b'] = jnp.zeros(C1, jnp.float32)
        inp['training'] = 0
        return inp
    _L3_xattn_all = _L3_xattn_setup()
    _L3_xattn_in = {k: v for k, v in _L3_xattn_all.items() if k in ('ln1_g', 'ln1_b', 'ln2_g', 'ln2_b', 'a1_wq', 'a1_wk', 'a1_wv', 'a1_li1_w', 'a1_li1_b', 'a1_lnx_g', 'a1_lnx_b', 'a1_lny_g', 'a1_lny_b', 'a1_ln3_g', 'a1_ln3_b', 'a1_li2_w', 'a1_li2_b', 'a1_li3_w', 'a1_li3_b', 'a2_wq', 'a2_wk', 'a2_wv', 'a2_li1_w', 'a2_li1_b', 'a2_lnx_g', 'a2_lnx_b', 'a2_lny_g', 'a2_lny_b', 'a2_ln3_g', 'a2_ln3_b', 'a2_li2_w', 'a2_li2_b', 'a2_li3_w', 'a2_li3_b')}
    del _L3_xattn_all

    def _L3_ffn_setup():
        import jax, jax.numpy as jnp
        import numpy as np
        B, S, DIM = (4, 512, 128)
        BASE_COUPLING = 0.1
        NUM_CYCLES = 3

        def _gelu(x):
            return jax.nn.gelu(x, approximate=False)

        def _coupling_net(h, w1, b1, w2, b2, w3, b3, w4, b4):
            h = _gelu(h @ w1 + b1)
            h = _gelu(h @ w2 + b2)
            h = _gelu(h @ w3 + b3)
            return jax.nn.sigmoid(h @ w4 + b4)

        def _global_net(h, w1, b1, w2, b2, w3, b3):
            h = _gelu(h @ w1 + b1)
            h = _gelu(h @ w2 + b2)
            return jax.nn.sigmoid(h @ w3 + b3)

        def _twist(x):
            o_r, o_i, p_r, p_i = jnp.split(x, 4, axis=-1)
            return jnp.concatenate([p_r, -p_i, -o_r, o_i], axis=-1)
        key = jax.random.key(seed)
        ks = jax.random.split(key, 9)
        d = DIM

        def w(k, fan_in, fan_out):
            return jax.random.normal(k, (fan_in, fan_out), dtype=jnp.float32) / np.sqrt(fan_in).astype(np.float32)
        inp = {'x': jax.random.normal(ks[0], (B, S, d), dtype=jnp.float32)}
        cn_dims = [(d, d), (d, d // 2), (d // 2, d // 4), (d // 4, 1)]
        for i, (a, b) in enumerate(cn_dims):
            inp[f'cn_w{i + 1}'] = w(ks[1 + i], a, b)
            inp[f'cn_b{i + 1}'] = jnp.zeros((b,), dtype=jnp.float32)
        gc_dims = [(d, d // 2), (d // 2, d // 4), (d // 4, 1)]
        for i, (a, b) in enumerate(gc_dims):
            inp[f'gc_w{i + 1}'] = w(ks[5 + i], a, b)
            inp[f'gc_b{i + 1}'] = jnp.zeros((b,), dtype=jnp.float32)
        inp['adaptive_range'] = jnp.full((1,), 0.2, dtype=jnp.float32)
        return inp
    _L3_ffn_all = _L3_ffn_setup()
    _L3_ffn_in = {k: v for k, v in _L3_ffn_all.items() if k in ('cn_w1', 'cn_b1', 'cn_w2', 'cn_b2', 'cn_w3', 'cn_b3', 'cn_w4', 'cn_b4', 'gc_w1', 'gc_b1', 'gc_w2', 'gc_b2', 'gc_w3', 'gc_b3', 'adaptive_range')}
    del _L3_ffn_all
    return {'x': x, 'ctx_512': ctx_512, 'g_xattn': g_xattn, 'g_ffn': g_ffn, 'L0_xattn_Wq': _L0_xattn_in['Wq'], 'L0_xattn_Wkv': _L0_xattn_in['Wkv'], 'L0_xattn_Wo': _L0_xattn_in['Wo'], 'L0_ffn_Wg': _L0_ffn_in['Wg'], 'L0_ffn_bg': _L0_ffn_in['bg'], 'L0_ffn_Wi': _L0_ffn_in['Wi'], 'L0_ffn_Wo': _L0_ffn_in['Wo'], 'L0_ffn_A': _L0_ffn_in['A'], 'L0_ffn_B': _L0_ffn_in['B'], 'L1_xattn_Wq': _L1_xattn_in['Wq'], 'L1_xattn_Wk': _L1_xattn_in['Wk'], 'L1_xattn_Wv': _L1_xattn_in['Wv'], 'L1_xattn_Wo': _L1_xattn_in['Wo'], 'L1_xattn_bo': _L1_xattn_in['bo'], 'L1_ffn_Wg': _L1_ffn_in['Wg'], 'L1_ffn_W1': _L1_ffn_in['W1'], 'L1_ffn_W3': _L1_ffn_in['W3'], 'L1_ffn_W2': _L1_ffn_in['W2'], 'L2_xattn_Wq': _L2_xattn_in['Wq'], 'L2_xattn_bq': _L2_xattn_in['bq'], 'L2_xattn_Wk': _L2_xattn_in['Wk'], 'L2_xattn_bk': _L2_xattn_in['bk'], 'L2_xattn_Wv': _L2_xattn_in['Wv'], 'L2_xattn_bv': _L2_xattn_in['bv'], 'L2_xattn_Wo': _L2_xattn_in['Wo'], 'L2_xattn_bo': _L2_xattn_in['bo'], 'L2_ffn_gate_w': _L2_ffn_in['gate_w'], 'L2_ffn_w_gate': _L2_ffn_in['w_gate'], 'L2_ffn_w_up': _L2_ffn_in['w_up'], 'L2_ffn_w_down': _L2_ffn_in['w_down'], 'L2_ffn_ws_gate': _L2_ffn_in['ws_gate'], 'L2_ffn_ws_up': _L2_ffn_in['ws_up'], 'L2_ffn_ws_down': _L2_ffn_in['ws_down'], 'L3_xattn_ln1_g': _L3_xattn_in['ln1_g'], 'L3_xattn_ln1_b': _L3_xattn_in['ln1_b'], 'L3_xattn_ln2_g': _L3_xattn_in['ln2_g'], 'L3_xattn_ln2_b': _L3_xattn_in['ln2_b'], 'L3_xattn_a1_wq': _L3_xattn_in['a1_wq'], 'L3_xattn_a1_wk': _L3_xattn_in['a1_wk'], 'L3_xattn_a1_wv': _L3_xattn_in['a1_wv'], 'L3_xattn_a1_li1_w': _L3_xattn_in['a1_li1_w'], 'L3_xattn_a1_li1_b': _L3_xattn_in['a1_li1_b'], 'L3_xattn_a1_lnx_g': _L3_xattn_in['a1_lnx_g'], 'L3_xattn_a1_lnx_b': _L3_xattn_in['a1_lnx_b'], 'L3_xattn_a1_lny_g': _L3_xattn_in['a1_lny_g'], 'L3_xattn_a1_lny_b': _L3_xattn_in['a1_lny_b'], 'L3_xattn_a1_ln3_g': _L3_xattn_in['a1_ln3_g'], 'L3_xattn_a1_ln3_b': _L3_xattn_in['a1_ln3_b'], 'L3_xattn_a1_li2_w': _L3_xattn_in['a1_li2_w'], 'L3_xattn_a1_li2_b': _L3_xattn_in['a1_li2_b'], 'L3_xattn_a1_li3_w': _L3_xattn_in['a1_li3_w'], 'L3_xattn_a1_li3_b': _L3_xattn_in['a1_li3_b'], 'L3_xattn_a2_wq': _L3_xattn_in['a2_wq'], 'L3_xattn_a2_wk': _L3_xattn_in['a2_wk'], 'L3_xattn_a2_wv': _L3_xattn_in['a2_wv'], 'L3_xattn_a2_li1_w': _L3_xattn_in['a2_li1_w'], 'L3_xattn_a2_li1_b': _L3_xattn_in['a2_li1_b'], 'L3_xattn_a2_lnx_g': _L3_xattn_in['a2_lnx_g'], 'L3_xattn_a2_lnx_b': _L3_xattn_in['a2_lnx_b'], 'L3_xattn_a2_lny_g': _L3_xattn_in['a2_lny_g'], 'L3_xattn_a2_lny_b': _L3_xattn_in['a2_lny_b'], 'L3_xattn_a2_ln3_g': _L3_xattn_in['a2_ln3_g'], 'L3_xattn_a2_ln3_b': _L3_xattn_in['a2_ln3_b'], 'L3_xattn_a2_li2_w': _L3_xattn_in['a2_li2_w'], 'L3_xattn_a2_li2_b': _L3_xattn_in['a2_li2_b'], 'L3_xattn_a2_li3_w': _L3_xattn_in['a2_li3_w'], 'L3_xattn_a2_li3_b': _L3_xattn_in['a2_li3_b'], 'L3_ffn_cn_w1': _L3_ffn_in['cn_w1'], 'L3_ffn_cn_b1': _L3_ffn_in['cn_b1'], 'L3_ffn_cn_w2': _L3_ffn_in['cn_w2'], 'L3_ffn_cn_b2': _L3_ffn_in['cn_b2'], 'L3_ffn_cn_w3': _L3_ffn_in['cn_w3'], 'L3_ffn_cn_b3': _L3_ffn_in['cn_b3'], 'L3_ffn_cn_w4': _L3_ffn_in['cn_w4'], 'L3_ffn_cn_b4': _L3_ffn_in['cn_b4'], 'L3_ffn_gc_w1': _L3_ffn_in['gc_w1'], 'L3_ffn_gc_b1': _L3_ffn_in['gc_b1'], 'L3_ffn_gc_w2': _L3_ffn_in['gc_w2'], 'L3_ffn_gc_b2': _L3_ffn_in['gc_b2'], 'L3_ffn_gc_w3': _L3_ffn_in['gc_w3'], 'L3_ffn_gc_b3': _L3_ffn_in['gc_b3'], 'L3_ffn_adaptive_range': _L3_ffn_in['adaptive_range']}

def reference(x, ctx_512, g_xattn, g_ffn, L0_xattn_Wq, L0_xattn_Wkv, L0_xattn_Wo, L0_ffn_Wg, L0_ffn_bg, L0_ffn_Wi, L0_ffn_Wo, L0_ffn_A, L0_ffn_B, L1_xattn_Wq, L1_xattn_Wk, L1_xattn_Wv, L1_xattn_Wo, L1_xattn_bo, L1_ffn_Wg, L1_ffn_W1, L1_ffn_W3, L1_ffn_W2, L2_xattn_Wq, L2_xattn_bq, L2_xattn_Wk, L2_xattn_bk, L2_xattn_Wv, L2_xattn_bv, L2_xattn_Wo, L2_xattn_bo, L2_ffn_gate_w, L2_ffn_w_gate, L2_ffn_w_up, L2_ffn_w_down, L2_ffn_ws_gate, L2_ffn_ws_up, L2_ffn_ws_down, L3_xattn_ln1_g, L3_xattn_ln1_b, L3_xattn_ln2_g, L3_xattn_ln2_b, L3_xattn_a1_wq, L3_xattn_a1_wk, L3_xattn_a1_wv, L3_xattn_a1_li1_w, L3_xattn_a1_li1_b, L3_xattn_a1_lnx_g, L3_xattn_a1_lnx_b, L3_xattn_a1_lny_g, L3_xattn_a1_lny_b, L3_xattn_a1_ln3_g, L3_xattn_a1_ln3_b, L3_xattn_a1_li2_w, L3_xattn_a1_li2_b, L3_xattn_a1_li3_w, L3_xattn_a1_li3_b, L3_xattn_a2_wq, L3_xattn_a2_wk, L3_xattn_a2_wv, L3_xattn_a2_li1_w, L3_xattn_a2_li1_b, L3_xattn_a2_lnx_g, L3_xattn_a2_lnx_b, L3_xattn_a2_lny_g, L3_xattn_a2_lny_b, L3_xattn_a2_ln3_g, L3_xattn_a2_ln3_b, L3_xattn_a2_li2_w, L3_xattn_a2_li2_b, L3_xattn_a2_li3_w, L3_xattn_a2_li3_b, L3_ffn_cn_w1, L3_ffn_cn_b1, L3_ffn_cn_w2, L3_ffn_cn_b2, L3_ffn_cn_w3, L3_ffn_cn_b3, L3_ffn_cn_w4, L3_ffn_cn_b4, L3_ffn_gc_w1, L3_ffn_gc_b1, L3_ffn_gc_w2, L3_ffn_gc_b2, L3_ffn_gc_w3, L3_ffn_gc_b3, L3_ffn_adaptive_range):
    import jax
    import jax.numpy as jnp

    def _L0_xattn_ref(x, z, Wq, Wkv, Wo):
        import jax, jax.numpy as jnp
        import numpy as np
        DIM = 128
        LATENT_DIM = 64
        NUM_HEADS = 16
        HEAD_DIM = DIM // NUM_HEADS
        SCALE = HEAD_DIM ** (-0.5)
        B, xN, _ = x.shape
        _, zN, _ = z.shape
        Q = (x @ Wq.T).reshape(B, xN, NUM_HEADS, HEAD_DIM)
        KV = (z @ Wkv.T).reshape(B, zN, 2, NUM_HEADS, HEAD_DIM)
        K = KV[:, :, 0]
        V = KV[:, :, 1]
        attn = jnp.einsum('bqhd,bkhd->bhqk', Q, K) * SCALE
        attn = jax.nn.softmax(attn, axis=-1)
        O = jnp.einsum('bhqk,bkhd->bqhd', attn, V).reshape(B, xN, DIM)
        return O @ Wo.T

    def _L0_ffn_ref(x, Wg, bg, Wi, Wo, A, B):
        import jax, jax.numpy as jnp
        import numpy as np
        TOP_K = 2
        E = Wg.shape[0]
        logits = jnp.einsum('bsd,ed->bse', x, Wg) + bg
        scores = jax.nn.softmax(logits, axis=-1)
        topv, topi = jax.lax.top_k(scores, TOP_K)
        w = jnp.sum(jax.nn.one_hot(topi, E, dtype=x.dtype) * topv[..., None], axis=-2)
        base = jnp.einsum('bsd,fd->bsf', x, Wi)
        lora_low = jnp.einsum('bsd,erd->bser', x, A)
        lora = jnp.einsum('bser,efr->bsef', lora_low, B)
        h = jax.nn.relu(base[:, :, None, :] + lora)
        expert_out = jnp.einsum('bsef,df->bsed', h, Wo)
        out = jnp.einsum('bse,bsed->bsd', w, expert_out)
        return out

    def _L1_xattn_ref(q, kv, Wq, Wk, Wv, Wo, bo):
        import jax, jax.numpy as jnp
        import numpy as np
        NUM_HEADS = 16
        HEAD_DIM = 64
        Q_DIM = 128
        KV_DIM = 64
        INNER = NUM_HEADS * HEAD_DIM
        B, N, _ = q.shape
        M = kv.shape[1]
        scale = HEAD_DIM ** (-0.5)
        qh = (q @ Wq).reshape(B, N, NUM_HEADS, HEAD_DIM).transpose(0, 2, 1, 3)
        kh = (kv @ Wk).reshape(B, M, NUM_HEADS, HEAD_DIM).transpose(0, 2, 1, 3)
        vh = (kv @ Wv).reshape(B, M, NUM_HEADS, HEAD_DIM).transpose(0, 2, 1, 3)
        scores = jnp.einsum('bhnd,bhmd->bhnm', qh, kh) * scale
        attn = jax.nn.softmax(scores, axis=-1)
        out = jnp.einsum('bhnm,bhmd->bhnd', attn, vh)
        out = out.transpose(0, 2, 1, 3).reshape(B, N, INNER)
        return out @ Wo + bo

    def _L1_ffn_ref(x, Wg, W1, W3, W2):
        import jax, jax.numpy as jnp
        import numpy as np
        B, T, D, F, E, TOP_K = (2, 256, 128, 512, 8, 2)
        INIT = 0.02
        Bb, Tt, Dd = x.shape
        xf = x.reshape(-1, Dd)
        logits = xf @ Wg
        top_v, top_i = jax.lax.top_k(logits, TOP_K)
        top_w = jax.nn.softmax(top_v, axis=-1)
        h1 = jnp.einsum('nd,edf->enf', xf, W1)
        h3 = jnp.einsum('nd,edf->enf', xf, W3)
        y = jnp.einsum('enf,efd->end', jax.nn.silu(h1) * h3, W2)
        y = jnp.transpose(y, (1, 0, 2))
        sel = jnp.take_along_axis(y, top_i[:, :, None], axis=1)
        out = jnp.sum(sel * top_w[:, :, None], axis=1)
        return out.reshape(Bb, Tt, Dd)

    def _L2_xattn_ref(q, k, v, Wq, bq, Wk, bk, Wv, bv, Wo, bo):
        import jax, jax.numpy as jnp
        import numpy as np
        HEADS = 16
        D_MODEL = 128
        IMG_MODEL = 64
        D_K = D_MODEL // HEADS
        B, LQ, _ = q.shape
        LKV = k.shape[1]
        qh = (q @ Wq + bq).reshape(B, LQ, HEADS, D_K).transpose(0, 2, 1, 3)
        kh = (k @ Wk + bk).reshape(B, LKV, HEADS, D_K).transpose(0, 2, 1, 3)
        vh = (v @ Wv + bv).reshape(B, LKV, HEADS, D_K).transpose(0, 2, 1, 3)
        scale = 1.0 / np.sqrt(D_K)
        scores = jnp.einsum('bhqd,bhkd->bhqk', qh, kh) * scale
        attn = jax.nn.softmax(scores, axis=-1)
        out = jnp.einsum('bhqk,bhkd->bhqd', attn, vh)
        concat = out.transpose(0, 2, 1, 3).reshape(B, LQ, D_MODEL)
        return concat @ Wo + bo

    def _L2_ffn_ref(hidden_states, gate_w, w_gate, w_up, w_down, ws_gate, ws_up, ws_down):
        import jax, jax.numpy as jnp
        import numpy as np
        H = 128
        M = 64
        E = 16
        TOP_K = 2
        SCALE = 2.5
        NORM_TOPK = True
        B, S = (1, 128)

        def _moe(x, gate_w, w_gate, w_up, w_down, ws_gate, ws_up, ws_down):
            T = x.shape[0]
            shared = jax.nn.silu(x @ ws_gate) * (x @ ws_up) @ ws_down
            scores = jax.nn.sigmoid(x.astype(jnp.float32) @ gate_w.T.astype(jnp.float32))
            topk_w, topk_idx = jax.lax.top_k(scores, TOP_K)
            if NORM_TOPK and TOP_K > 1:
                topk_w = topk_w / (topk_w.sum(-1, keepdims=True) + 1e-20)
            topk_w = topk_w * SCALE
            route = jnp.zeros((T, E), topk_w.dtype).at[jnp.arange(T)[:, None], topk_idx].set(topk_w)
            g = jnp.einsum('th,ehm->etm', x, w_gate)
            u = jnp.einsum('th,ehm->etm', x, w_up)
            eo = jnp.einsum('etm,emh->eth', jax.nn.silu(g) * u, w_down)
            routed = jnp.einsum('te,eth->th', route.astype(x.dtype), eo)
            return routed + shared
        b, s, h = hidden_states.shape
        x = hidden_states.reshape(-1, h)
        out = _moe(x, gate_w, w_gate, w_up, w_down, ws_gate, ws_up, ws_down)
        return out.reshape(b, s, h)

    def _L3_xattn_ref(xx, ee, ln1_g, ln1_b, ln2_g, ln2_b, a1_wq, a1_wk, a1_wv, a1_li1_w, a1_li1_b, a1_lnx_g, a1_lnx_b, a1_lny_g, a1_lny_b, a1_ln3_g, a1_ln3_b, a1_li2_w, a1_li2_b, a1_li3_w, a1_li3_b, a2_wq, a2_wk, a2_wv, a2_li1_w, a2_li1_b, a2_lnx_g, a2_lnx_b, a2_lny_g, a2_lny_b, a2_ln3_g, a2_ln3_b, a2_li2_w, a2_li2_b, a2_li3_w, a2_li3_b, training):
        import jax, jax.numpy as jnp
        import numpy as np
        H, D, C1, C2, S, M, B, W = (16, 32, 128, 64, 256, 64, 2, 4)

        def _ln(x, g, b):
            m = jnp.mean(x, -1, keepdims=True)
            v = jnp.var(x, -1, keepdims=True)
            return (x - m) * jax.lax.rsqrt(v + 1e-05) * g + b

        def _mha(x, y, wq, wk, wv, li1_w, li1_b, lnx_g, lnx_b, lny_g, lny_b, ln3_g, ln3_b, li2_w, li2_b, li3_w, li3_b, causal):
            xn = _ln(x, lnx_g, lnx_b)
            yn = _ln(y, lny_g, lny_b)
            q = jnp.einsum('bsc,hcd->bhsd', xn, wq)
            k = jnp.einsum('btc,hcd->bhtd', yn, wk)
            v = jnp.einsum('btc,hcd->bhtd', yn, wv)
            a = jax.nn.softmax(jnp.einsum('bhsd,bhtd->bhst', q, k) * D ** (-0.5), axis=-1)
            if causal:
                s, t = (a.shape[-2], a.shape[-1])
                mask = (jnp.arange(t)[None, :] > jnp.arange(s)[:, None]).astype(a.dtype)
                a = a * mask
            o = jnp.einsum('bhst,bhtd->bhsd', a, v)
            o = o.transpose(0, 2, 1, 3).reshape(x.shape[0], x.shape[1], H * D)
            x_out = x + o @ li1_w + li1_b
            h = jax.nn.gelu(_ln(x_out, ln3_g, ln3_b) @ li2_w + li2_b, approximate=False)
            return x_out + h @ li3_w + li3_b
        x = _ln(xx, ln1_g, ln1_b)
        x = x + _mha(x, x, a1_wq, a1_wk, a1_wv, a1_li1_w, a1_li1_b, a1_lnx_g, a1_lnx_b, a1_lny_g, a1_lny_b, a1_ln3_g, a1_ln3_b, a1_li2_w, a1_li2_b, a1_li3_w, a1_li3_b, causal=True)
        x = _ln(x, ln2_g, ln2_b)
        return x + _mha(x, ee, a2_wq, a2_wk, a2_wv, a2_li1_w, a2_li1_b, a2_lnx_g, a2_lnx_b, a2_lny_g, a2_lny_b, a2_ln3_g, a2_ln3_b, a2_li2_w, a2_li2_b, a2_li3_w, a2_li3_b, causal=False)

    def _L3_ffn_ref(x, cn_w1, cn_b1, cn_w2, cn_b2, cn_w3, cn_b3, cn_w4, cn_b4, gc_w1, gc_b1, gc_w2, gc_b2, gc_w3, gc_b3, adaptive_range):
        import jax, jax.numpy as jnp
        import numpy as np
        B, S, DIM = (4, 512, 128)
        BASE_COUPLING = 0.1
        NUM_CYCLES = 3

        def _gelu(x):
            return jax.nn.gelu(x, approximate=False)

        def _coupling_net(h, w1, b1, w2, b2, w3, b3, w4, b4):
            h = _gelu(h @ w1 + b1)
            h = _gelu(h @ w2 + b2)
            h = _gelu(h @ w3 + b3)
            return jax.nn.sigmoid(h @ w4 + b4)

        def _global_net(h, w1, b1, w2, b2, w3, b3):
            h = _gelu(h @ w1 + b1)
            h = _gelu(h @ w2 + b2)
            return jax.nn.sigmoid(h @ w3 + b3)

        def _twist(x):
            o_r, o_i, p_r, p_i = jnp.split(x, 4, axis=-1)
            return jnp.concatenate([p_r, -p_i, -o_r, o_i], axis=-1)
        global_context = x.mean(axis=1, keepdims=True)
        gf = _global_net(global_context, gc_w1, gc_b1, gc_w2, gc_b2, gc_w3, gc_b3)
        out = x
        for _ in range(NUM_CYCLES):
            tf = _coupling_net(out, cn_w1, cn_b1, cn_w2, cn_b2, cn_w3, cn_b3, cn_w4, cn_b4)
            combined = 0.7 * gf + 0.3 * tf
            coupling = BASE_COUPLING + adaptive_range * (combined - 0.5) * 2.0
            out = out + coupling * _twist(out)
        return out
    x = x + jnp.tanh(g_xattn[0]) * _L0_xattn_ref(_layernorm(x, axis=-1), ctx_512, L0_xattn_Wq, L0_xattn_Wkv, L0_xattn_Wo)
    x = x + jnp.tanh(g_ffn[0]) * _L0_ffn_ref(_layernorm(x, axis=-1), L0_ffn_Wg, L0_ffn_bg, L0_ffn_Wi, L0_ffn_Wo, L0_ffn_A, L0_ffn_B)
    x = x + jnp.tanh(g_xattn[1]) * _L1_xattn_ref(_layernorm(x, axis=-1), ctx_512, L1_xattn_Wq, L1_xattn_Wk, L1_xattn_Wv, L1_xattn_Wo, L1_xattn_bo)
    x = x + jnp.tanh(g_ffn[1]) * _L1_ffn_ref(_layernorm(x, axis=-1), L1_ffn_Wg, L1_ffn_W1, L1_ffn_W3, L1_ffn_W2)
    x = x + jnp.tanh(g_xattn[2]) * _L2_xattn_ref(_layernorm(x, axis=-1), ctx_512, ctx_512, L2_xattn_Wq, L2_xattn_bq, L2_xattn_Wk, L2_xattn_bk, L2_xattn_Wv, L2_xattn_bv, L2_xattn_Wo, L2_xattn_bo)
    x = x + jnp.tanh(g_ffn[2]) * _L2_ffn_ref(_layernorm(x, axis=-1), L2_ffn_gate_w, L2_ffn_w_gate, L2_ffn_w_up, L2_ffn_w_down, L2_ffn_ws_gate, L2_ffn_ws_up, L2_ffn_ws_down)
    x = x + jnp.tanh(g_xattn[3]) * _L3_xattn_ref(_layernorm(x, axis=-1), ctx_512, L3_xattn_ln1_g, L3_xattn_ln1_b, L3_xattn_ln2_g, L3_xattn_ln2_b, L3_xattn_a1_wq, L3_xattn_a1_wk, L3_xattn_a1_wv, L3_xattn_a1_li1_w, L3_xattn_a1_li1_b, L3_xattn_a1_lnx_g, L3_xattn_a1_lnx_b, L3_xattn_a1_lny_g, L3_xattn_a1_lny_b, L3_xattn_a1_ln3_g, L3_xattn_a1_ln3_b, L3_xattn_a1_li2_w, L3_xattn_a1_li2_b, L3_xattn_a1_li3_w, L3_xattn_a1_li3_b, L3_xattn_a2_wq, L3_xattn_a2_wk, L3_xattn_a2_wv, L3_xattn_a2_li1_w, L3_xattn_a2_li1_b, L3_xattn_a2_lnx_g, L3_xattn_a2_lnx_b, L3_xattn_a2_lny_g, L3_xattn_a2_lny_b, L3_xattn_a2_ln3_g, L3_xattn_a2_ln3_b, L3_xattn_a2_li2_w, L3_xattn_a2_li2_b, L3_xattn_a2_li3_w, L3_xattn_a2_li3_b, 0)
    x = x + jnp.tanh(g_ffn[3]) * _L3_ffn_ref(_layernorm(x, axis=-1), L3_ffn_cn_w1, L3_ffn_cn_b1, L3_ffn_cn_w2, L3_ffn_cn_b2, L3_ffn_cn_w3, L3_ffn_cn_b3, L3_ffn_cn_w4, L3_ffn_cn_b4, L3_ffn_gc_w1, L3_ffn_gc_b1, L3_ffn_gc_w2, L3_ffn_gc_b2, L3_ffn_gc_w3, L3_ffn_gc_b3, L3_ffn_adaptive_range)
    return x

_drawn_inputs = setup_inputs


def setup_inputs(seed=0):
    import zlib

    import numpy as np

    out = dict(_drawn_inputs(seed))
    spreads = {'L0_ffn_bg': (0.0, 0.8),
     'L2_xattn_bq': (0.0, 0.626),
     'L2_xattn_bk': (0.0, 2.0),
     'L2_xattn_bv': (0.0, 0.1),
     'L2_xattn_bo': (0.0, 0.1),
     'L3_xattn_ln1_g': (1.0, 0.2),
     'L3_xattn_ln1_b': (0.0, 0.318),
     'L3_xattn_ln2_g': (1.0, 0.2),
     'L3_xattn_ln2_b': (0.0, 0.1),
     'L3_xattn_a1_li1_b': (0.0, 0.552),
     'L3_xattn_a1_lnx_g': (1.0, 0.6),
     'L3_xattn_a1_lnx_b': (0.0, 2.0),
     'L3_xattn_a1_lny_g': (1.0, 0.6),
     'L3_xattn_a1_lny_b': (0.0, 2.0),
     'L3_xattn_a1_ln3_g': (1.0, 0.6),
     'L3_xattn_a1_ln3_b': (0.0, 2.0),
     'L3_xattn_a1_li2_b': (0.0, 0.8),
     'L3_xattn_a1_li3_b': (0.0, 0.571),
     'L3_xattn_a2_li1_b': (0.0, 0.618),
     'L3_xattn_a2_lnx_g': (1.0, 0.6),
     'L3_xattn_a2_lnx_b': (0.0, 2.0),
     'L3_xattn_a2_lny_g': (1.0, 0.6),
     'L3_xattn_a2_lny_b': (0.0, 2.0),
     'L3_xattn_a2_ln3_g': (1.0, 0.6),
     'L3_xattn_a2_ln3_b': (0.0, 2.0),
     'L3_xattn_a2_li2_b': (0.0, 0.8),
     'L3_xattn_a2_li3_b': (0.0, 0.61),
     'L3_ffn_cn_b1': (0.0, 2.0),
     'L3_ffn_cn_b2': (0.0, 2.0),
     'L3_ffn_cn_b3': (0.0, 2.0),
     'L3_ffn_gc_b1': (0.0, 2.0),
     'L3_ffn_gc_b2': (0.0, 2.0)}
    factors = {'L0_ffn_A': 8.0,
     'L0_ffn_B': 8.0,
     'L1_xattn_bo': 8.0,
     'L1_ffn_Wg': 8.0,
     'L1_ffn_W1': 8.0,
     'L1_ffn_W3': 8.0,
     'L1_ffn_W2': 8.0,
     'L2_ffn_gate_w': 8.0,
     'L2_ffn_w_gate': 8.0,
     'L2_ffn_w_up': 8.0,
     'L2_ffn_w_down': 8.0,
     'L2_ffn_ws_gate': 8.0,
     'L2_ffn_ws_up': 8.0,
     'L2_ffn_ws_down': 8.0,
     'L3_xattn_a1_wq': 29.926,
     'L3_xattn_a1_wk': 30.438,
     'L3_xattn_a2_wq': 55.566,
     'L3_xattn_a2_wk': 55.123,
     'L3_ffn_cn_w1': 16.679,
     'L3_ffn_cn_w2': 76.503,
     'L3_ffn_cn_w3': 23.728,
     'L3_ffn_cn_w4': 51.701,
     'L3_xattn_a1_wv': 3.467,
     'L3_xattn_a1_li1_w': 3.475,
     'L3_xattn_a1_li2_w': 4.463,
     'L3_xattn_a1_li3_w': 4.19,
     'L3_xattn_a2_wv': 4.488,
     'L3_xattn_a2_li1_w': 4.52,
     'L3_xattn_a2_li2_w': 4.667,
     'L3_xattn_a2_li3_w': 4.383,
     'L3_ffn_gc_w1': 23.622,
     'L3_ffn_gc_w2': 28.202,
     'L3_ffn_gc_w3': 18.022}
    for name, (base, spread) in spreads.items():
        noise = np.random.default_rng([zlib.crc32(name.encode()), seed]).standard_normal(out[name].shape)
        drawn = base * np.exp(spread * noise) if base else spread * noise
        out[name] = jnp.asarray(drawn.astype(out[name].dtype))
    for name, factor in factors.items():
        out[name] = (out[name] * factor).astype(out[name].dtype)
    return out
```

```python
from contextlib import ExitStack

import numpy as np
import concourse.bass as bass
from concourse import mybir

F32 = mybir.dt.float32
ALU = mybir.AluOpType
ACT = mybir.ActivationFunctionType
AX = mybir.AxisListType.X

P = 128
HEADS = 16
KEYS = 77
CTX = 64
LN_EPS = 1e-5
BANK = 512
CHUNK = 4


class It:

    def __init__(self, b, half, par):
        self.b, self.half, self.par = b, half, par


def skewed(eng, n, steps, lead):
    lead = min(lead, n)
    last = max(lag for _, lag in steps)
    assert lead % 2 == 0 and n % 2 == 0 and (n == lead or lead >= last + 2)

    def peeled(ts):
        for t in ts:
            for step, lag in steps:
                if 0 <= t - lag < n:
                    step(It(t - lag, (t - lag) // 2, (t - lag) % 2))

    peeled(range(lead))
    if n > lead:
        with eng.Fori(lead // 2, n // 2) as pair:
            for u in range(2):
                for step, lag in steps:
                    step(It(pair * 2 + (u - lag), pair + (u - lag) // 2, (u - lag) % 2))
    peeled(range(n, n + last))


def seen(eng, sem, it, per=1, c=None, ago=0, back=0):
    value = it.b * per + ((per - 1 if c is None else c) + 1 - back - ago * per)
    if isinstance(value, int) and value <= 0:
        return
    eng.wait_ge(sem, value)


def loaded(eng, sems, it, per=1):
    eng.wait_ge(sems[it.par], (it.half + 1) * (16 * per))


class Stage:

    def __init__(self, nc, name):
        self.nc, self.name, self.sems, self.ctx = nc, name, [], ExitStack()

    def __enter__(self):
        return self

    def sb(self, name, shape):
        return self.ctx.enter_context(self.nc.sbuf_tensor(f"{self.name}_{name}", list(shape), F32))

    def sb2(self, name, shape):
        return [self.sb(f"{name}{i}", shape) for i in range(2)]

    def ps(self, name):
        return self.ctx.enter_context(self.nc.psum_tensor(f"{self.name}_{name}", [P, BANK], F32))

    def sem(self, name):
        s = self.ctx.enter_context(self.nc.semaphore(f"{self.name}_{name}"))
        self.sems.append(s)
        return s

    def sem2(self, name):
        return [self.sem(f"{name}{i}") for i in range(2)]

    def __exit__(self, *exc):
        if exc[0] is None:
            with self.nc.Block() as block:
                @block.gpsimd
                def _(pool):
                    for s in self.sems:
                        pool.sem_clear(s)
        self.ctx.__exit__(*exc)
        return False


class LnFront:

    def __init__(self, st, g, ps_xT):
        self.g, self.ps_xT = g, ps_xT
        self.stats, self.mv = st.sb2("stats", [P, 6]), st.sb2("mv", [P, 2])
        self.ve, self.rstd = st.sb2("ve", [P, 1]), st.sb2("rstd", [P, 1])
        self.xn, self.xT = st.sb2("xn", [P, P]), st.sb2("xT", [P, P])
        self.s_mv, self.s_ve = st.sem("s_mv"), st.sem("s_ve")
        self.s_rstd, self.s_xn = st.sem("s_rstd"), st.sem("s_xn")
        self.s_turned, self.s_xT = st.sem("s_turned"), st.sem("s_xT")

    def statistics(self, dve, it):
        p = it.par
        seen(dve, self.s_xn, it, ago=2)
        seen(dve, self.s_ve, it, ago=2)
        seen(dve, self.s_mv, it, ago=2)
        dve.bn_stats(self.stats[p][:, :], self.g.x[:, bass.ts(it.b, P)])
        dve.drain()
        dve.bn_aggr(self.mv[p][:, :], self.stats[p][:, :]).then_inc(self.s_mv, 1)

    def inverse_deviation(self, pool, it):
        p = it.par
        seen(pool, self.s_mv, it)
        seen(pool, self.s_rstd, it, ago=2)
        pool.tensor_tensor(self.ve[p][:, :], self.mv[p][:, 1:2], self.g.eps[:, 0:1], ALU.add).then_inc(self.s_ve, 1)
        seen(pool, self.s_ve, it)
        seen(pool, self.s_xn, it, ago=2)
        pool.tensor_tensor(self.rstd[p][:, :], self.ve[p][:, :], self.g.minus_half[:, 0:1],
                           ALU.pow).then_inc(self.s_rstd, 1)

    def normalize(self, dve, it):
        p = it.par
        seen(dve, self.s_mv, it)
        seen(dve, self.s_rstd, it)
        seen(dve, self.s_turned, it, ago=2)
        dve.tensor_scalar(self.xn[p][:, :], self.g.x[:, bass.ts(it.b, P)], self.mv[p][:, 0:1],
                          self.rstd[p][:, 0:1], ALU.subtract, ALU.mult).then_inc(self.s_xn, 1)

    def turn(self, pe, it):
        seen(pe, self.s_xn, it)
        seen(pe, self.s_xT, it, ago=1)
        pe.transpose(self.ps_xT, self.xn[it.par][:, :], self.g.ident[:, :]).then_inc(self.s_turned, 1)

    def fetch(self, act, it, used, per=1):
        seen(act, self.s_turned, it)
        seen(act, used, it, per=per, ago=2)
        act.copy(self.xT[it.par][:, :], self.ps_xT).then_inc(self.s_xT, 1)


class Softmax:

    def __init__(self, st, g, banks, heads_of_bank, keys, scale, ps_turn):
        self.g, self.banks, self.keys, self.scale = g, banks, keys, scale
        self.nb, self.first = len(heads_of_bank), [0]
        for n in heads_of_bank:
            self.first.append(self.first[-1] + n)
        self.ps_turn = ps_turn
        self.mx, self.probs = st.sb2("mx", [P, HEADS]), st.sb2("probs", [P, HEADS, keys])
        self.probsT = st.sb2("probsT", [keys, CHUNK * P])
        self.nc_ = HEADS // CHUNK
        self.s_scores, self.s_max, self.s_shift, self.s_exp = (
            st.sem("s_scores"), st.sem("s_max"), st.sem("s_shift"), st.sem("s_exp"))
        self.s_turn, self.s_fetch, self.s_values = st.sem("s_turnp"), st.sem("s_fetchp"), st.sem("s_values")

    def view(self, c):
        n = self.first[c + 1] - self.first[c]
        return self.banks[c][:, 0:n * self.keys].rearrange("p (h t) -> p h t", t=self.keys)

    def maximum(self, dve, it, c):
        a, b = self.first[c], self.first[c + 1]
        seen(dve, self.s_scores, it, self.nb, c)
        seen(dve, self.s_shift, it, self.nb, ago=2)
        dve.tensor_reduce(self.mx[it.par][:, a:b], self.view(c), AX, ALU.max).then_inc(self.s_max, 1)

    def shift(self, dve, it, c):
        a, b = self.first[c], self.first[c + 1]
        seen(dve, self.s_max, it, self.nb, c)
        seen(dve, self.s_turn, it, self.nc_, ago=2)
        dve.tensor_tensor(self.probs[it.par][:, a:b, :], self.view(c),
                          self.mx[it.par][:, a:b].unsqueeze(2).to_broadcast([P, b - a, self.keys]),
                          ALU.subtract).then_inc(self.s_shift, 1)

    def exponential(self, act, it, c):
        a, b = self.first[c], self.first[c + 1]
        seen(act, self.s_shift, it, self.nb, c)
        v = self.probs[it.par][:, a:b, :]
        act.activation(v, v, ACT.Exp, scale=self.scale).then_inc(self.s_exp, 1)

    def turn(self, pe, it, c, ready=None, ready_per=None):
        bank = max(k for k in range(self.nb) if self.first[k] < CHUNK * (c + 1))
        if ready is None:
            seen(pe, self.s_exp, it, self.nb, bank)
        else:
            seen(pe, ready, it, ready_per, c)
        seen(pe, self.s_fetch, it, self.nc_, c, back=2)
        for k in range(CHUNK):
            last = pe.transpose(self.ps_turn[c % 2][0:self.keys, k * P:(k + 1) * P],
                                self.probs[it.par][:, CHUNK * c + k, :], self.g.ident[:, :])
        last.then_inc(self.s_turn, 1)

    def fetch(self, act, it, c):
        seen(act, self.s_turn, it, self.nc_, c)
        seen(act, self.s_values, it, self.nc_, c, back=2)
        act.copy(self.probsT[c % 2][:, :], self.ps_turn[c % 2][0:self.keys, :]).then_inc(self.s_fetch, 1)

    def times_values(self, pe, it, c, out_of, values_of):
        seen(pe, self.s_fetch, it, self.nc_, c)
        for k in range(CHUNK):
            h = CHUNK * c + k
            last = pe.matmul(out_of(h), self.probsT[c % 2][:, k * P:(k + 1) * P], values_of(h), start=True, stop=True)
        last.then_inc(self.s_values, 1)


def small_head_attention(nc, g, name, wq, wk, wv, wo, bq=None, bk=None, bv=None, bo=None, gate=0):
    D = P // HEADS
    SPLIT = [6, 6, 4]
    scale = float(D) ** -0.5
    biased = bq is not None
    with Stage(nc, name) as st:
        wq_s, wk_s, wv_s, wo_s = (st.sb("wq", [P, P]), st.sb("wk", [CTX, P]), st.sb("wv", [CTX, P]),
                                  st.sb("wo", [P, P]))
        bqkv_s, bo_s, bvo_s = st.sb("bqkv", [P, 3]), st.sb("bo", [P, P]), st.sb("bvo", [P, P])
        s_bvo, s_bias = st.sem("s_bvo"), st.sem("s_bias")
        ctxT = st.sb2("ctxT", [CTX, KEYS])
        qT, kT = st.sb2("qT", [P, P]), st.sb2("kT", [P, KEYS])
        keys = st.sb2("keys", [P, HEADS, KEYS])
        vals = st.sb2("vals", [KEYS, HEADS, D + 1])
        recip, o_s, oT = st.sb2("recip", [P, HEADS]), st.sb2("o", [P, P]), st.sb2("oT", [P, P])
        scores = [st.ps(f"scores{i}") for i in range(3)]
        turned = [st.ps(f"turned{i}") for i in range(2)]
        pa, po, py = st.ps("pa"), st.ps("po"), st.ps("py")
        q_p, k_p, v_p = pa[:, P:2 * P], pa[:, 2 * P:2 * P + KEYS], pa[0:KEYS, 3 * P:4 * P]
        o_p = po[:, 0:HEADS * (D + 1)].rearrange("p (h e) -> p h e", e=D + 1)
        oT_p, y_p = py[:, 0:P], py[:, P:2 * P]
        ln = LnFront(st, g, pa[:, 0:P])
        sm = Softmax(st, g, scores, SPLIT, KEYS, scale, turned)
        s_w, s_ctx, s_ones = st.sem("s_w"), st.sem2("s_ctx"), st.sem("s_ones")
        s_kv, s_q, s_kT, s_vals, s_qT, s_keys = [st.sem(n) for n in ("s_kv", "s_q", "s_kT", "s_vals", "s_qT", "s_keys")]
        s_recip, s_o, s_oTp, s_oT, s_y, s_x, s_bo = [
            st.sem(n) for n in ("s_recip", "s_o", "s_oTp", "s_oT", "s_y", "s_x", "s_bo")]
        weights = [(wq_s[:, :], wq), (wk_s[:, :], wk), (wv_s[:, :], wv), (wo_s[:, :], wo)]
        if biased:
            weights += [(bqkv_s[:, 0:1], bq), (bqkv_s[:, 1:2], bk), (bqkv_s[:, 2:3], bv),
                        (bo_s[:, :], bo.partition_broadcast(P))]
        all_weights = 16 * len(weights)

        with nc.Block() as block:
            @block.sync
            def _(sp):
                for dst, src in weights:
                    sp.dma_start(dst, src).then_inc(s_w, 16)

                def context(it):
                    seen(sp, s_kv, it, ago=2)
                    sp.dma_start(ctxT[it.par][:, :], g.ctxT_d[:, bass.ds(it.b, 1), :].rearrange("c b t -> c (b t)")).then_inc(s_ctx[it.par], 16)

                skewed(sp, g.B, [(context, 0)], 2)

            @block.gpsimd
            def _(pool):
                for i in range(2):
                    pool.memset(vals[i][:, :, D:D + 1], 1.0).then_inc(s_ones, 1)

                def spread(it):
                    seen(pool, s_kT, it)
                    seen(pool, sm.s_scores, it, 3, ago=2)
                    pool.tensor_tensor(keys[it.par][:, :, :],
                                       kT[it.par][:, :].unsqueeze(1).to_broadcast([P, HEADS, KEYS]),
                                       g.head8[:, :].unsqueeze(2).to_broadcast([P, HEADS, KEYS]),
                                       ALU.mult).then_inc(s_keys, 1)

                skewed(pool, g.B, [(lambda it: ln.inverse_deviation(pool, it), 0), (spread, 1)], 4)

            @block.tensor
            def _(pe):
                pe.wait_ge(s_w, all_weights)
                if biased:
                    pe.matmul(y_p, bqkv_s[:, 2:3].to_broadcast([P, P]), wo_s[:, :], start=True, stop=True).then_inc(s_bvo, 1)
                    pe.wait_ge(s_bias, 1)

                def keys_values(it):
                    p = it.par
                    loaded(pe, s_ctx, it)
                    seen(pe, s_qT, it, ago=1)
                    ln.turn(pe, it)
                    pe.matmul(k_p, wk_s[:, :], ctxT[p][:, :], start=True, stop=True)
                    pe.matmul(v_p, ctxT[p][:, :], wv_s[:, :], start=True, stop=True).then_inc(s_kv, 1)

                def queries(it):
                    p = it.par
                    seen(pe, ln.s_xT, it)
                    seen(pe, s_kT, it)
                    seen(pe, s_vals, it)
                    pe.matmul(q_p, wq_s[:, :], ln.xT[p][:, :], start=True, stop=True).then_inc(s_q, 1)

                def score(it, c):
                    a, b = sm.first[c], sm.first[c + 1]
                    seen(pe, s_qT, it)
                    seen(pe, s_keys, it)
                    seen(pe, sm.s_shift, it, 3, c, back=3)
                    pe.matmul(scores[c][:, 0:(b - a) * KEYS], qT[it.par][:, :],
                              keys[it.par][:, a:b, :].rearrange("p h t -> p (h t)"),
                              start=True, stop=True).then_inc(sm.s_scores, 1)

                def weigh(it, c):
                    if c == 0:
                        seen(pe, s_vals, it)
                        seen(pe, s_o, it, ago=1)
                        pe.wait_ge(s_ones, 2)
                    sm.times_values(pe, it, c, lambda h: o_p[:, h, :], lambda h: vals[it.par][:, h, :])

                def turn_o(it):
                    seen(pe, s_o, it)
                    seen(pe, s_x, it, ago=1)
                    pe.transpose(oT_p, o_s[it.par][:, :], g.ident[:, :]).then_inc(s_oTp, 1)

                def output(it):
                    seen(pe, s_oT, it)
                    pe.matmul(y_p, oT[it.par][:, :], wo_s[:, :], start=True, stop=True).then_inc(s_y, 1)

                steps = [(turn_o, 4)] + [(lambda it, c=c: score(it, c), 2) for c in range(3)]
                steps += [(output, 4), (keys_values, 1)]
                steps += [(lambda it: sm.turn(pe, it, 0), 3), (lambda it: sm.turn(pe, it, 1), 3)]
                steps += [(lambda it: weigh(it, 0), 3), (lambda it: sm.turn(pe, it, 2), 3), (lambda it: weigh(it, 1), 3),
                          (lambda it: sm.turn(pe, it, 3), 3), (lambda it: weigh(it, 2), 3), (lambda it: weigh(it, 3), 3), (queries, 1)]
                skewed(pe, g.B, steps, 6)

            @block.scalar
            def _(act):
                act.wait_ge(s_w, all_weights)

                def project(it):
                    p = it.par
                    seen(act, s_kv, it)
                    ln.fetch(act, it, s_q)
                    seen(act, s_keys, it, ago=2)
                    if biased:
                        act.activation(kT[p][:, :], k_p, ACT.Identity, bias=bqkv_s[:, 1:2]).then_inc(s_kT, 1)
                    else:
                        act.copy(kT[p][:, :], k_p).then_inc(s_kT, 1)

                def fetch_values(it):
                    seen(act, sm.s_values, it, 4, ago=2)
                    act.copy(vals[it.par][:, :, 0:D], v_p.rearrange("p (h d) -> p h d", d=D)).then_inc(s_vals, 1)

                def fetch_q(it):
                    p = it.par
                    seen(act, s_q, it)
                    seen(act, sm.s_scores, it, 3, ago=2)
                    if biased:
                        act.activation(qT[p][:, :], q_p, ACT.Identity, bias=bqkv_s[:, 0:1]).then_inc(s_qT, 1)
                    else:
                        act.copy(qT[p][:, :], q_p).then_inc(s_qT, 1)

                def fetch_o(it):
                    seen(act, s_oTp, it)
                    seen(act, s_y, it, ago=2)
                    act.copy(oT[it.par][:, :], oT_p).then_inc(s_oT, 1)

                steps = [(fetch_o, 4), (project, 1), (lambda it: sm.fetch(act, it, 0), 3)]
                steps += [(lambda it, c=c: sm.fetch(act, it, c), 3) for c in range(1, 4)]
                steps += [(fetch_values, 1), (fetch_q, 1)]
                steps += [(lambda it, c=c: sm.exponential(act, it, c), 2) for c in range(3)]
                skewed(act, g.B, steps, 6)

            @block.vector
            def _(dve):
                if biased:
                    dve.wait_ge(s_w, all_weights)
                    dve.wait_ge(s_bvo, 1)
                    dve.tensor_tensor(bvo_s[:, :], y_p, bo_s[:, :], ALU.add).then_inc(s_bias, 1)

                def divide(it):
                    p = it.par
                    seen(dve, sm.s_values, it, 4)
                    seen(dve, s_o, it, ago=2)
                    dve.reciprocal(recip[p][:, :], o_p[:, :, D]).then_inc(s_recip, 1)
                    seen(dve, s_recip, it)
                    seen(dve, s_oTp, it, ago=2)
                    dve.tensor_tensor(o_s[p][:, :].rearrange("p (h d) -> p h d", d=D), o_p[:, :, 0:D],
                                      recip[p][:, :].unsqueeze(2).to_broadcast([P, HEADS, D]),
                                      ALU.mult).then_inc(s_o, 1)

                def add(it):
                    x = g.x[:, bass.ts(it.b, P)]
                    if biased:
                        seen(dve, s_xnormed, it)
                        dve.scalar_tensor_tensor(x, bvo_s[:, :], g.gates[:, gate:gate + 1], x, ALU.mult, ALU.add).then_inc(s_bo, 1)
                        seen(dve, s_bo, it)
                    seen(dve, s_y, it)
                    seen(dve, ln.s_xn, it)
                    dve.scalar_tensor_tensor(x, y_p, g.gates[:, gate:gate + 1], x, ALU.mult, ALU.add).then_inc(s_x, 1)

                s_xnormed = ln.s_xn
                steps = [(lambda it: ln.normalize(dve, it), 1), (lambda it: ln.statistics(dve, it), 0)]
                for c in range(3):
                    steps += [(lambda it, c=c: sm.maximum(dve, it, c), 2), (lambda it, c=c: sm.shift(dve, it, c), 2)]
                steps += [(add, 4), (divide, 3)]
                skewed(dve, g.B, steps, 6)


GROUP = 4


class GroupFront:

    def __init__(self, st, g, ps_xT):
        self.g, self.ps_xT = g, ps_xT
        self.stats, self.mv = st.sb("stats", [P, GROUP, 6]), st.sb2("mv", [P, GROUP, 2])
        self.ve, self.rstd = st.sb2("ve", [P, GROUP]), st.sb2("rstd", [P, GROUP])
        self.xn, self.xT = st.sb2("xn", [P, GROUP * P]), st.sb2("xT", [P, GROUP * P])
        self.s_mv, self.s_ve, self.s_rstd = st.sem("s_mv"), st.sem("s_ve"), st.sem("s_rstd")
        self.s_xn, self.s_turned, self.s_xT = st.sem("s_xn"), st.sem("s_turned"), st.sem("s_xT")

    def statistics(self, dve, it):
        seen(dve, self.s_xn, it, ago=2)
        seen(dve, self.s_ve, it, ago=2)
        for j in range(GROUP):
            dve.bn_stats(self.stats[:, j, :], self.g.x[:, bass.ts(it.b * GROUP + j, P)])
        dve.drain()
        for j in range(GROUP):
            last = dve.bn_aggr(self.mv[it.par][:, j, :], self.stats[:, j, :])
        last.then_inc(self.s_mv, 1)
        dve.drain()

    def inverse_deviation(self, pool, it):
        p = it.par
        seen(pool, self.s_mv, it)
        seen(pool, self.s_rstd, it, ago=2)
        pool.tensor_tensor(self.ve[p][:, :], self.mv[p][:, :, 1], self.g.eps[:, :], ALU.add).then_inc(self.s_ve, 1)
        seen(pool, self.s_ve, it)
        seen(pool, self.s_xn, it, ago=2)
        pool.tensor_tensor(self.rstd[p][:, :], self.ve[p][:, :], self.g.minus_half[:, :], ALU.pow).then_inc(self.s_rstd, 1)

    def normalize(self, dve, it, used=None):
        p = it.par
        seen(dve, self.s_rstd, it)
        seen(dve, self.s_turned, it, ago=2)
        for j in range(GROUP):
            last = dve.tensor_scalar(self.xn[p][:, j * P:(j + 1) * P], self.g.x[:, bass.ts(it.b * GROUP + j, P)],
                                     self.mv[p][:, j, 0:1], self.rstd[p][:, j:j + 1], ALU.subtract, ALU.mult)
        last.then_inc(self.s_xn, 1)

    def turn(self, pe, it):
        seen(pe, self.s_xn, it)
        seen(pe, self.s_xT, it, ago=1)
        for j in range(GROUP):
            last = pe.transpose(self.ps_xT[:, j * P:(j + 1) * P], self.xn[it.par][:, j * P:(j + 1) * P], self.g.ident[:, :])
        last.then_inc(self.s_turned, 1)

    def fetch(self, act, it, used, per=1):
        seen(act, self.s_turned, it)
        seen(act, used, it, per=per, ago=2)
        act.copy(self.xT[it.par][:, :], self.ps_xT[:, :]).then_inc(self.s_xT, 1)


class Router:

    def __init__(self, st, g, experts, front, ps, wg, bias=None):
        E = self.E = experts
        self.g, self.front, self.ps, self.wg, self.bias = g, front, ps, wg, bias
        self.logits, self.act_in = st.sb("logits", [P, GROUP, E]), st.sb("act_in", [P, GROUP, E])
        self.act_out, self.sel = st.sb("act_out", [P, GROUP, E]), st.sb("sel", [P, GROUP, E])
        self.same, self.above = st.sb("same", [P, GROUP, E, E]), st.sb("above", [P, GROUP, E, E])
        self.before = st.sb("before", [P, E, E])
        self.rank, self.one = st.sb("rank", [P, GROUP, E]), st.sb("one", [P, GROUP])
        self.w = st.sb2("route", [P, GROUP, E])
        self.s_before, self.s_logits, self.s_in, self.s_out, self.s_w = [
            st.sem(n) for n in ("s_before", "s_logits", "s_in", "s_out", "s_route")]

    def make_before(self, pool):
        pool.memset(self.before[:, :, :], 1.0).then_inc(self.s_before, 1)
        pool.wait_ge(self.s_before, 1)
        pool.affine_select(out=self.before[:, :, :], in_=self.before[:, :, :], compare_op=ALU.is_ge, fill=0.0,
                           base=-1, pattern=[[1, self.E], [-1, self.E]], channel_multiplier=0).then_inc(self.s_before, 1)

    def score(self, pe, it):
        seen(pe, self.front.s_xT, it)
        seen(pe, self.s_in, it, ago=1)
        for j in range(GROUP):
            last = pe.matmul(self.ps[:, j * self.E:(j + 1) * self.E], self.front.xT[it.par][:, j * P:(j + 1) * P],
                             self.wg[:, :], start=True, stop=True)
        last.then_inc(self.s_logits, 1)

    def wide(self, v):
        return v[:, :].unsqueeze(2).to_broadcast([P, GROUP, self.E])

    def fetch(self, dve, it, less_maximum):
        E = self.E
        seen(dve, self.s_logits, it)
        seen(dve, self.s_out, it, ago=1)
        src = self.ps[:, 0:GROUP * E].rearrange("p (j e) -> p j e", e=E)
        if self.bias is None:
            dve.tensor_copy(self.logits[:, :, :], src)
        else:
            dve.tensor_tensor(self.logits[:, :, :], src, self.bias[:, :].unsqueeze(1).to_broadcast([P, GROUP, E]), ALU.add)
        dve.drain()
        if less_maximum:
            dve.tensor_reduce(self.one[:, :], self.logits[:, :, :], AX, ALU.max)
            dve.drain()
            dve.tensor_tensor(self.act_in[:, :, :], self.logits[:, :, :], self.wide(self.one), ALU.subtract).then_inc(self.s_in, 1)
        else:
            dve.tensor_copy(self.act_in[:, :, :], self.logits[:, :, :]).then_inc(self.s_in, 1)

    def function(self, act, it, func):
        seen(act, self.s_in, it)
        seen(act, self.s_w, it, ago=1)
        act.activation(self.act_out[:, :, :], self.act_in[:, :, :], func).then_inc(self.s_out, 1)

    def normalized(self, dve, v, eps=None, times=None):
        dve.tensor_reduce(self.one[:, :], v[:, :, :], AX, ALU.add)
        dve.drain()
        if eps is not None:
            dve.tensor_scalar(self.one[:, :], self.one[:, :], eps, None, ALU.add)
            dve.drain()
        dve.reciprocal(self.one[:, :], self.one[:, :])
        dve.drain()
        if times is not None:
            dve.tensor_scalar(self.one[:, :], self.one[:, :], times, None, ALU.mult)
            dve.drain()

    def top_two(self, dve, v):
        E = self.E
        other = v[:, :, :].unsqueeze(2).to_broadcast([P, GROUP, E, E])
        own = v[:, :, :].unsqueeze(3).to_broadcast([P, GROUP, E, E])
        dve.tensor_tensor(self.same[:, :, :, :], other, own, ALU.is_equal)
        dve.tensor_tensor(self.above[:, :, :, :], other, own, ALU.is_gt)
        dve.drain()
        flat = self.same[:, :, :, :].rearrange("p j a b -> p j (a b)")
        dve.tensor_tensor(flat, flat, self.before[:, :, :].rearrange("p a b -> p (a b)").unsqueeze(1).to_broadcast(
            [P, GROUP, E * E]), ALU.mult)
        dve.drain()
        dve.tensor_tensor(self.same[:, :, :, :], self.same[:, :, :, :], self.above[:, :, :, :], ALU.add)
        dve.drain()
        dve.tensor_reduce(self.rank[:, :, :], self.same[:, :, :, :], AX, ALU.add)
        dve.drain()
        dve.tensor_scalar(self.sel[:, :, :], self.rank[:, :, :], 1.5, None, ALU.is_lt)
        dve.drain()


def l0_ffn(nc, g, a):
    E, R, F = 4, 4, 512
    FT = F // P
    n = g.B // GROUP
    with Stage(nc, "l0f") as st:
        wg, bg, wi = st.sb("wg", [P, E]), st.sb("bg", [P, E]), st.sb("wi", [P, F])
        la, lb, wo = st.sb("la", [R, E, P]), st.sb("lb", [R, E, F]), st.sb("wo", [P, FT, P])
        we = st.sb("we", [P, E, F])
        relu = [st.sb(f"relu{e}", [P, F]) for e in range(E)]
        hs, hT = st.sb2("hs", [P, F]), st.sb2("hT", [P, F])
        ps_xT, ps_lg, ps_hT, ps_y = st.ps("xT"), st.ps("lg"), st.ps("hT"), st.ps("y")
        ps_h = [st.ps(f"h{e}") for e in range(E)]
        fr = GroupFront(st, g, ps_xT)
        rt = Router(st, g, E, fr, ps_lg, wg, bg)
        s_w, s_low, s_we = st.sem("s_w"), st.sem("s_low"), st.sem("s_we")
        s_h, s_relu, s_pair, s_hs, s_hTp, s_hT, s_y, s_x = [
            st.sem(k) for k in ("s_h", "s_relu", "s_pair", "s_hs", "s_hTp", "s_hT", "s_y", "s_x")]
        weights = [(wg[:, :], a["L0_Wg"]), (bg[:, :], a["L0_bg"].partition_broadcast(P)), (wi[:, :], a["L0_Wi"]),
                   (la[:, :, :], a["L0_A"]), (lb[:, :, :], a["L0_B"]), (wo[:, :, :], a["L0_Wof"])]

        with nc.Block() as block:
            @block.sync
            def _(sp):
                for dst, src in weights:
                    sp.dma_start(dst, src).then_inc(s_w, 16)

            @block.gpsimd
            def _(pool):
                rt.make_before(pool)
                skewed(pool, n, [(lambda it: fr.inverse_deviation(pool, it), 0)], 2)

            @block.tensor
            def _(pe):
                pe.wait_ge(s_w, 16 * len(weights))
                for e in range(E):
                    pe.matmul(ps_h[e][:, :], la[:, e, :], lb[:, e, :], start=True, stop=True).then_inc(s_low, 1)

                def hidden(it, j, e):
                    if j == 0 and e == 0:
                        pe.wait_ge(s_we, E)
                    seen(pe, s_relu, it, 4 * GROUP, 4 * j + e, back=4)
                    pe.matmul(ps_h[e][:, :], fr.xT[it.par][:, j * P:(j + 1) * P], we[:, e, :],
                              start=True, stop=True).then_inc(s_h, 1)

                def turn(it, j):
                    seen(pe, s_hs, it, GROUP, j)
                    seen(pe, s_hT, it, GROUP, j, back=1)
                    for t in range(FT):
                        last = pe.transpose(ps_hT[:, t * P:(t + 1) * P], hs[j % 2][:, t * P:(t + 1) * P], g.ident[:, :])
                    last.then_inc(s_hTp, 1)

                def down(it, j):
                    seen(pe, s_hT, it, GROUP, j)
                    seen(pe, s_x, it, GROUP, j, back=1)
                    for t in range(FT):
                        last = pe.matmul(ps_y[:, 0:P], hT[j % 2][:, t * P:(t + 1) * P], wo[:, t, :],
                                         start=(t == 0), stop=(t == FT - 1))
                    last.then_inc(s_y, 1)

                def main(it):
                    for j in range(GROUP + 2):
                        for e in range(E):
                            if j < GROUP:
                                hidden(it, j, e)
                            if e == 1 and 1 <= j <= GROUP:
                                turn(it, j - 1)
                            if e == 2 and j >= 2:
                                down(it, j - 2)
                        if j == 0:
                            pass

                skewed(pe, n, [(main, 2), (lambda it: fr.turn(pe, it), 1), (lambda it: rt.score(pe, it), 1)], 4)

            @block.scalar
            def _(act):
                def main(it):
                    for j in range(GROUP + 1):
                        for e in range(E):
                            if j < GROUP:
                                seen(act, s_h, it, 4 * GROUP, 4 * j + e)
                                if j == 0 and e == 0:
                                    seen(act, rt.s_w, it)
                                seen(act, s_pair, it, 3 * GROUP, 3 * j + 2, back=3)
                                act.activation(relu[e][:, :], ps_h[e][:, :], ACT.Relu,
                                               scale=rt.w[it.par][:, j, e:e + 1]).then_inc(s_relu, 1)
                            if e == 1 and j >= 1:
                                seen(act, s_hTp, it, GROUP, j - 1)
                                seen(act, s_y, it, GROUP, j - 1, back=2)
                                act.copy(hT[(j - 1) % 2][:, :], ps_hT[:, :]).then_inc(s_hT, 1)

                skewed(act, n, [(main, 2), (lambda it: fr.fetch(act, it, s_h, 4 * GROUP), 1),
                                (lambda it: rt.function(act, it, ACT.Exp), 1)], 4)

            @block.vector
            def _(dve):
                dve.wait_ge(s_w, 16 * len(weights))
                for e in range(E):
                    dve.wait_ge(s_low, e + 1)
                    dve.tensor_tensor(we[:, e, :], ps_h[e][:, :], wi[:, :], ALU.add).then_inc(s_we, 1)
                dve.wait_ge(rt.s_before, 2)

                def route(it):
                    rt.fetch(dve, it, True)
                    seen(dve, rt.s_out, it)
                    rt.normalized(dve, rt.act_out)
                    dve.tensor_tensor(rt.act_in[:, :, :], rt.act_out[:, :, :], rt.wide(rt.one), ALU.mult)
                    dve.drain()
                    rt.top_two(dve, rt.act_in)
                    seen(dve, s_relu, it, 4 * GROUP, ago=2)
                    dve.tensor_tensor(rt.w[it.par][:, :, :], rt.act_in[:, :, :], rt.sel[:, :, :], ALU.mult).then_inc(rt.s_w, 1)

                def add(it, j):
                    x = g.x[:, bass.ts(it.b * GROUP + j, P)]
                    seen(dve, s_y, it, GROUP, j)
                    dve.scalar_tensor_tensor(x, ps_y[:, 0:P], g.gates[:, 4:5], x, ALU.mult, ALU.add).then_inc(s_x, 1)

                def main(it):
                    seen(dve, fr.s_xn, it)
                    for j in range(GROUP):
                        seen(dve, s_relu, it, 4 * GROUP, 4 * j + 1)
                        dve.tensor_tensor(relu[0][:, :], relu[0][:, :], relu[1][:, :], ALU.add).then_inc(s_pair, 1)
                        seen(dve, s_relu, it, 4 * GROUP, 4 * j + 3)
                        dve.tensor_tensor(relu[2][:, :], relu[2][:, :], relu[3][:, :], ALU.add).then_inc(s_pair, 1)
                        seen(dve, s_pair, it, 3 * GROUP, 3 * j + 1)
                        seen(dve, s_hTp, it, GROUP, j, back=2)
                        dve.tensor_tensor(hs[j % 2][:, :], relu[0][:, :], relu[2][:, :], ALU.add).then_inc(s_pair, 1)
                        seen(dve, s_pair, it, 3 * GROUP, 3 * j + 2)
                        dve.sem_inc(s_hs, 1)
                        if j >= 2:
                            add(it, j - 2)
                    add(it, 2)
                    add(it, 3)

                skewed(dve, n, [(lambda it: fr.normalize(dve, it), 1), (lambda it: fr.statistics(dve, it), 0),
                                (main, 2), (route, 1)], 4)


def l1_ffn(nc, g, a):
    E, F = 8, 512
    FT = F // P
    T = E * FT
    n = g.B // GROUP
    with Stage(nc, "l1f") as st:
        wg, w1, w3, w2 = st.sb("wg", [P, E]), st.sb("w1", [P, E, F]), st.sb("w3", [P, E, F]), st.sb("w2", [P, E, FT, P])
        silu = st.sb2("silu", [P, GROUP * P])
        gated = [[st.sb(f"gated{i}{t}", [P, GROUP * P]) for t in range(FT)] for i in range(2)]
        acc = st.sb("acc", [P, GROUP * P])
        ps_xT, ps_lg = st.ps("xT"), st.ps("lg")
        ps_1, ps_3, ps_y = [[st.ps(f"{k}{i}") for i in range(2)] for k in ("h1", "h3", "y")]
        fr = GroupFront(st, g, ps_xT)
        rt = Router(st, g, E, fr, ps_lg, wg)
        s_g, s_w13, s_w2 = st.sem("s_g"), [st.sem(f"s_w13{e}") for e in range(E)], st.sem("s_w2")
        s_up, s_silu, s_gated, s_y, s_acc, s_x = [st.sem(k) for k in ("s_up", "s_silu", "s_gated", "s_y", "s_acc", "s_x")]

        with nc.Block() as block:
            @block.sync
            def _(sp):
                sp.dma_start(wg[:, :], a["L1_Wg"]).then_inc(s_g, 16)
                for e in range(E):
                    sp.dma_start(w1[:, e, :], a["L1_W1"][:, e, :]).then_inc(s_w13[e], 16)
                    sp.dma_start(w3[:, e, :], a["L1_W3"][:, e, :]).then_inc(s_w13[e], 16)
                sp.dma_start(w2[:, :, :, :], a["L1_W2"]).then_inc(s_w2, 16)

            @block.gpsimd
            def _(pool):
                rt.make_before(pool)
                skewed(pool, n, [(lambda it: fr.inverse_deviation(pool, it), 0)], 2)

            @block.tensor
            def _(pe):
                pe.wait_ge(s_g, 16)

                def up(it, e, t):
                    c = e * FT + t
                    if t == 0:
                        pe.wait_ge(s_w13[e], 32)
                    seen(pe, s_silu, it, T, c, back=2)
                    seen(pe, s_gated, it, T, c, back=2)
                    pe.matmul(ps_1[t % 2][:, :], w1[:, e, t * P:(t + 1) * P], fr.xT[it.par][:, :], start=True, stop=True)
                    pe.matmul(ps_3[t % 2][:, :], w3[:, e, t * P:(t + 1) * P], fr.xT[it.par][:, :],
                              start=True, stop=True).then_inc(s_up, 1)

                def down(it, e):
                    seen(pe, s_gated, it, T, e * FT + FT - 1)
                    seen(pe, s_acc, it, E, e, back=2)
                    pe.wait_ge(s_w2, 16)
                    for j in range(GROUP):
                        for t in range(FT):
                            last = pe.matmul(ps_y[e % 2][:, j * P:(j + 1) * P], gated[e % 2][t][:, j * P:(j + 1) * P],
                                             w2[:, e, t, :], start=(t == 0), stop=(t == FT - 1))
                    last.then_inc(s_y, 1)

                def main(it):
                    for e in range(E):
                        for t in range(FT):
                            up(it, e, t)
                            if t == 1 and e > 0:
                                down(it, e - 1)

                skewed(pe, n, [(main, 2), (lambda it: fr.turn(pe, it), 1), (lambda it: rt.score(pe, it), 1),
                               (lambda it: down(it, E - 1), 2)], 4)

            @block.scalar
            def _(act):
                def main(it):
                    for c in range(T):
                        seen(act, s_up, it, T, c)
                        seen(act, s_gated, it, T, c, back=2)
                        act.activation(silu[c % 2][:, :], ps_1[c % 2][:, :], ACT.Silu).then_inc(s_silu, 1)

                skewed(act, n, [(main, 2), (lambda it: fr.fetch(act, it, s_up, T), 1),
                                (lambda it: rt.function(act, it, ACT.Exp), 1)], 4)

            @block.vector
            def _(dve):
                dve.wait_ge(rt.s_before, 2)

                def route(it):
                    rt.fetch(dve, it, True)
                    rt.top_two(dve, rt.logits)
                    seen(dve, rt.s_out, it)
                    dve.tensor_tensor(rt.act_in[:, :, :], rt.act_out[:, :, :], rt.sel[:, :, :], ALU.mult)
                    dve.drain()
                    rt.normalized(dve, rt.act_in)
                    seen(dve, s_acc, it, E, ago=2)
                    dve.tensor_tensor(rt.w[it.par][:, :, :], rt.act_in[:, :, :], rt.wide(rt.one), ALU.mult).then_inc(rt.s_w, 1)

                def gate(it, e, t):
                    c = e * FT + t
                    seen(dve, s_silu, it, T, c)
                    if t == 0:
                        seen(dve, s_y, it, E, e, back=2)
                    dve.tensor_tensor(gated[e % 2][t][:, :], ps_3[t % 2][:, :], silu[t % 2][:, :], ALU.mult).then_inc(s_gated, 1)

                def collect(it, e):
                    seen(dve, s_y, it, E, e)
                    if e > 0:
                        seen(dve, s_acc, it, E, e, back=1)
                    else:
                        seen(dve, s_x, it, ago=1)
                        seen(dve, rt.s_w, it)
                    for j in range(GROUP):
                        y, w, o = ps_y[e % 2][:, j * P:(j + 1) * P], rt.w[it.par][:, j, e:e + 1], acc[:, j * P:(j + 1) * P]
                        if e == 0:
                            last = dve.tensor_scalar(o, y, w, None, ALU.mult)
                        else:
                            last = dve.scalar_tensor_tensor(o, y, w, o, ALU.mult, ALU.add)
                    last.then_inc(s_acc, 1)

                def main(it):
                    for e in range(E):
                        for t in range(FT):
                            gate(it, e, t)
                            if t == 1 and e > 0:
                                collect(it, e - 1)

                def add(it):
                    collect(it, E - 1)
                    x = g.x[:, bass.ts(it.b, GROUP * P)]
                    seen(dve, s_acc, it, E)
                    seen(dve, fr.s_xn, it)
                    dve.scalar_tensor_tensor(x, acc[:, :], g.gates[:, 5:6], x, ALU.mult, ALU.add).then_inc(s_x, 1)

                skewed(dve, n, [(lambda it: fr.normalize(dve, it), 1), (lambda it: fr.statistics(dve, it), 0),
                                (main, 2), (route, 1), (add, 2)], 4)


def l2_ffn(nc, g, a):
    E, M = 16, 64
    SCALE = 2.5
    CH = 3
    n = g.B // GROUP
    K = CH * GROUP
    with Stage(nc, "l2f") as st:
        wg = st.sb("wg", [P, E])
        gate_w, up_w, down_w = st.sb("gate", [P, E * M]), st.sb("up", [P, E * M]), st.sb("down", [P, E * M // P, P])
        sg, su, sd = st.sb("sg", [P, M]), st.sb("su", [P, M]), st.sb("sd", [M, P])
        silu, prod, hid = st.sb2("silu", [P, BANK]), st.sb2("prod", [P, BANK]), st.sb2("hid", [P, BANK])
        hT = st.sb2("hT", [P, BANK])
        ps_xT, ps_lg, ps_hT, ps_y = st.ps("xT"), st.ps("lg"), st.ps("hT"), st.ps("y")
        ps_g, ps_u = [[st.ps(f"{k}{i}") for i in range(2)] for k in "gu"]
        fr = GroupFront(st, g, ps_xT)
        rt = Router(st, g, E, fr, ps_lg, wg)
        s_w, s_pass = st.sem("s_w"), st.sem("s_pass")
        s_up, s_silu, s_prod, s_hid, s_hTp, s_hT, s_down, s_x = [
            st.sem(k) for k in ("s_up", "s_silu", "s_prod", "s_hid", "s_hTp", "s_hT", "s_down", "s_x")]
        weights = [(wg[:, :], a["L2_gw"]), (gate_w[:, :], a["L2_wg"]), (up_w[:, :], a["L2_wu"]),
                   (down_w[:, :, :], a["L2_wd"]), (sg[:, :], a["L2_sg"]), (su[:, :], a["L2_su"]), (sd[:, :], a["L2_sd"])]

        def width(c):
            return M if c == 2 else BANK

        with nc.Block() as block:
            @block.sync
            def _(sp):
                for dst, src in weights:
                    sp.dma_start(dst, src).then_inc(s_w, 16)

            @block.gpsimd
            def _(pool):
                rt.make_before(pool)

                def weigh(it):
                    for j in range(GROUP):
                        for c in range(2):
                            k = CH * j + c
                            if k == 0:
                                seen(pool, rt.s_w, it)
                            seen(pool, s_prod, it, K, k)
                            seen(pool, s_hTp, it, K, k, back=2)
                            pool.tensor_tensor(hid[k % 2][:, :].rearrange("p (e m) -> p e m", m=M),
                                               prod[k % 2][:, :].rearrange("p (e m) -> p e m", m=M),
                                               rt.w[it.par][:, j, 8 * c:8 * c + 8].unsqueeze(2).to_broadcast([P, 8, M]),
                                               ALU.mult).then_inc(s_hid, 1)

                skewed(pool, n, [(lambda it: fr.inverse_deviation(pool, it), 0), (weigh, 2)], 4)

            @block.tensor
            def _(pe):
                pe.wait_ge(s_w, 16 * len(weights))

                def up(it, k):
                    j, c = k // CH, k % CH
                    x = fr.xT[it.par][:, j * P:(j + 1) * P]
                    wgt = sg[:, :] if c == 2 else gate_w[:, c * BANK:(c + 1) * BANK]
                    wup = su[:, :] if c == 2 else up_w[:, c * BANK:(c + 1) * BANK]
                    seen(pe, s_silu, it, K, k, back=2)
                    seen(pe, s_prod, it, K, k, back=2)
                    pe.matmul(ps_g[k % 2][:, 0:width(c)], x, wgt, start=True, stop=True)
                    pe.matmul(ps_u[k % 2][:, 0:width(c)], x, wup, start=True, stop=True).then_inc(s_up, 1)

                def turn(it, k):
                    j, c = k // CH, k % CH
                    if c == 2:
                        seen(pe, s_prod, it, K, k)
                    else:
                        seen(pe, s_hid, it, 2 * GROUP, 2 * j + c)
                    seen(pe, s_hT, it, K, k, back=1)
                    if c == 2:
                        pe.sem_inc(s_pass, 1)
                        last = pe.transpose(ps_hT[0:M, 0:P], prod[k % 2][:, 0:M], g.ident[:, :])
                    else:
                        for t in range(4):
                            last = pe.transpose(ps_hT[:, t * P:(t + 1) * P], hid[k % 2][:, t * P:(t + 1) * P], g.ident[:, :])
                    last.then_inc(s_hTp, 1)

                def down(it, k):
                    j, c = k // CH, k % CH
                    seen(pe, s_hT, it, K, k)
                    if c == 0:
                        seen(pe, s_x, it, GROUP, j, back=1)
                    if c == 2:
                        last = pe.matmul(ps_y[:, 0:P], hT[k % 2][0:M, 0:P], sd[:, :], start=False, stop=True)
                    else:
                        for t in range(4):
                            last = pe.matmul(ps_y[:, 0:P], hT[k % 2][:, t * P:(t + 1) * P], down_w[:, 4 * c + t, :],
                                             start=(c == 0 and t == 0), stop=False)
                    last.then_inc(s_down, 1)

                def main(it):
                    for k in range(K + 2):
                        if k < K:
                            up(it, k)
                        if 1 <= k <= K:
                            turn(it, k - 1)
                        if k >= 2:
                            down(it, k - 2)

                skewed(pe, n, [(main, 2), (lambda it: fr.turn(pe, it), 1), (lambda it: rt.score(pe, it), 1)], 4)

            @block.scalar
            def _(act):
                def main(it):
                    for k in range(K + 1):
                        if k < K:
                            w = width(k % CH)
                            seen(act, s_up, it, K, k)
                            seen(act, s_prod, it, K, k, back=2)
                            act.activation(silu[k % 2][:, 0:w], ps_g[k % 2][:, 0:w], ACT.Silu).then_inc(s_silu, 1)
                        if k >= 1:
                            q = k - 1
                            seen(act, s_hTp, it, K, q)
                            seen(act, s_down, it, K, q, back=2)
                            if q % CH == 2:
                                act.copy(hT[q % 2][0:M, 0:P], ps_hT[0:M, 0:P]).then_inc(s_hT, 1)
                            else:
                                act.copy(hT[q % 2][:, :], ps_hT[:, :]).then_inc(s_hT, 1)

                skewed(act, n, [(main, 2), (lambda it: fr.fetch(act, it, s_up, K), 1),
                                (lambda it: rt.function(act, it, ACT.Sigmoid), 1)], 4)

            @block.vector
            def _(dve):
                dve.wait_ge(rt.s_before, 2)

                def route(it):
                    rt.fetch(dve, it, False)
                    seen(dve, rt.s_out, it)
                    rt.top_two(dve, rt.act_out)
                    dve.tensor_tensor(rt.act_in[:, :, :], rt.act_out[:, :, :], rt.sel[:, :, :], ALU.mult)
                    dve.drain()
                    rt.normalized(dve, rt.act_in, eps=1e-20, times=SCALE)
                    seen(dve, s_hid, it, 2 * GROUP, ago=2)
                    dve.tensor_tensor(rt.w[it.par][:, :, :], rt.act_in[:, :, :], rt.wide(rt.one), ALU.mult).then_inc(rt.s_w, 1)

                def add(it, j):
                    x = g.x[:, bass.ts(it.b * GROUP + j, P)]
                    seen(dve, s_down, it, K, CH * j + 2)
                    dve.scalar_tensor_tensor(x, ps_y[:, 0:P], g.gates[:, 6:7], x, ALU.mult, ALU.add).then_inc(s_x, 1)

                def main(it):
                    seen(dve, fr.s_xn, it)
                    for k in range(K):
                        j, c = k // CH, k % CH
                        w = width(c)
                        seen(dve, s_silu, it, K, k)
                        if k >= 2 or True:
                            seen(dve, s_hTp, it, K, k, back=2)
                        dve.tensor_tensor(prod[k % 2][:, 0:w], ps_u[k % 2][:, 0:w], silu[k % 2][:, 0:w], ALU.mult).then_inc(s_prod, 1)
                        if c == 1 and j > 0:
                            add(it, j - 1)
                    add(it, GROUP - 1)

                skewed(dve, n, [(lambda it: fr.normalize(dve, it), 1), (lambda it: fr.statistics(dve, it), 0),
                                (main, 2), (route, 1)], 4)


def l1_xattn(nc, g, a):
    D = 64
    PAIRS = HEADS // 2
    SPLIT = [6, 6, 4]
    W = CTX + 1
    scale = float(D) ** -0.5
    with Stage(nc, "l1x") as st:
        wqT, wkT = st.sb("wqT", [D, HEADS, P]), st.sb("wkT", [D, HEADS, CTX])
        wvT, wo = st.sb("wvT", [D, HEADS, CTX]), st.sb("wo", [D, HEADS, P])
        qk, vo, bo = st.sb("qk", [P, HEADS * CTX]), st.sb("vo", [P, PAIRS, P]), st.sb("bo", [P, P])
        pair_ctx, ctx1 = st.sb2("pair_ctx", [P, 2 * KEYS]), st.sb2("ctx1", [KEYS, W])
        qT = st.sb2("qT", [P, PAIRS, P])
        recip, o_s, oT = st.sb2("recip", [P, HEADS]), st.sb2("o", [P, HEADS, CTX]), st.sb2("oT", [P, PAIRS, P])
        scores = [st.ps(f"scores{i}") for i in range(3)]
        turned = [st.ps(f"turned{i}") for i in range(2)]
        pa, po, py = st.ps("pa"), st.ps("po"), st.ps("py")
        o_p = po[:, 0:CHUNK * W].rearrange("p (h e) -> p h e", e=W)
        y_p = py[:, 0:P]
        ln = LnFront(st, g, pa[:, 0:P])
        sm = Softmax(st, g, scores, SPLIT, KEYS, scale, turned)
        s_w, s_ctx, s_set = st.sem("s_w"), st.sem2("s_ctx"), st.sem("s_set")
        s_pre, s_fused = st.sem("s_pre"), st.sem("s_fused")
        s_q, s_qT, s_recip, s_o, s_oTp, s_oT, s_y, s_x, s_bo = [
            st.sem(n) for n in ("s_q", "s_qT", "s_recip", "s_o", "s_oTp", "s_oT", "s_y", "s_x", "s_bo")]
        weights = [(wqT[:, :, :], a["L1_WqT"]), (wkT[:, :, :], a["L1_WkT"]), (wvT[:, :, :], a["L1_WvT"]),
                   (wo[:, :, :], a["L1_Woh"]), (bo[:, :], a["L1_bo"].partition_broadcast(P))]

        with nc.Block() as block:
            @block.sync
            def _(sp):
                for dst, src in weights:
                    sp.dma_start(dst, src).then_inc(s_w, 16)
                sp.wait_ge(s_set, 4)

                def context(it):
                    p = it.par
                    seen(sp, sm.s_scores, it, 3, ago=2)
                    seen(sp, sm.s_values, it, 4, ago=2)
                    one = g.ctxT_d[:, bass.ds(it.b, 1), :].rearrange("c b t -> c (b t)")
                    sp.dma_start(pair_ctx[p][0:CTX, 0:KEYS], one).then_inc(s_ctx[p], 16)
                    sp.dma_start(pair_ctx[p][CTX:P, KEYS:2 * KEYS], one).then_inc(s_ctx[p], 16)
                    sp.dma_start(ctx1[p][:, 0:CTX], g.ctx_d[:, bass.ds(it.b, 1), :].rearrange("t b c -> t (b c)")).then_inc(s_ctx[p], 16)

                skewed(sp, g.B, [(context, 0)], 2)

            @block.gpsimd
            def _(pool):
                for i in range(2):
                    pool.memset(pair_ctx[i][:, :], 0.0).then_inc(s_set, 1)
                    pool.memset(ctx1[i][:, CTX:W], 1.0).then_inc(s_set, 1)
                skewed(pool, g.B, [(lambda it: ln.inverse_deviation(pool, it), 0)], 4)

            @block.tensor
            def _(pe):
                pe.wait_ge(s_w, 16 * len(weights))
                banks = [scores[0], scores[1], turned[0], turned[1]]
                for h in range(HEADS):
                    last = pe.matmul(banks[h // 8][:, (h % 8) * CTX:(h % 8 + 1) * CTX], wqT[:, h, :], wkT[:, h, :],
                                     start=True, stop=True)
                    if h % 8 == 7:
                        last.then_inc(s_pre, 1)
                for h in range(HEADS):
                    r, i = CTX * (h % 2), h // 2
                    last = pe.matmul(banks[2 + i // 4][r:r + CTX, (i % 4) * P:(i % 4 + 1) * P], wvT[:, h, :], wo[:, h, :],
                                     start=True, stop=True)
                    if h % 8 == 7:
                        last.then_inc(s_pre, 1)
                pe.wait_ge(s_fused, 4)

                def turn(it):
                    seen(pe, s_qT, it, 2, ago=1)
                    ln.turn(pe, it)

                def queries(it, c):
                    if c == 0:
                        seen(pe, ln.s_xT, it)
                    else:
                        seen(pe, s_qT, it, 2, 0)
                    for k in range(4):
                        last = pe.matmul(pa[:, k * P:(k + 1) * P], qk[:, (4 * c + k) * P:(4 * c + k + 1) * P],
                                         ln.xT[it.par][:, :], start=True, stop=True)
                    last.then_inc(s_q, 1)

                def score(it, c):
                    loaded(pe, s_ctx, it, 3)
                    seen(pe, s_qT, it, 2)
                    seen(pe, sm.s_shift, it, 3, c, back=3)
                    for h in range(sm.first[c], sm.first[c + 1], 2):
                        r = (h - sm.first[c]) * KEYS
                        last = pe.matmul(scores[c][:, r:r + 2 * KEYS], qT[it.par][:, h // 2, :], pair_ctx[it.par][:, :],
                                         start=True, stop=True)
                    last.then_inc(sm.s_scores, 1)

                def weigh(it, c):
                    seen(pe, s_o, it, 4, c, back=1)
                    sm.times_values(pe, it, c, lambda h: o_p[:, h % CHUNK, :], lambda h: ctx1[it.par][:, :])

                def turn_o(it, c):
                    seen(pe, s_o, it, 4)
                    if c == 0:
                        seen(pe, s_x, it, ago=1)
                    else:
                        seen(pe, s_oT, it, 2, 0)
                    for k in range(4):
                        i = 4 * c + k
                        last = pe.transpose(py[:, k * P:(k + 1) * P],
                                            o_s[it.par][:, 2 * i:2 * i + 2, :].rearrange("p h e -> p (h e)"), g.ident[:, :])
                    last.then_inc(s_oTp, 1)

                def output(it):
                    seen(pe, s_oT, it, 2)
                    for i in range(PAIRS):
                        last = pe.matmul(y_p, oT[it.par][:, i, :], vo[:, i, :], start=(i == 0), stop=(i == PAIRS - 1))
                    last.then_inc(s_y, 1)

                steps = [(lambda it: turn_o(it, 0), 4), (lambda it: score(it, 0), 2), (turn, 1), (lambda it: score(it, 1), 2),
                         (lambda it: turn_o(it, 1), 4), (lambda it: sm.turn(pe, it, 0), 3), (lambda it: score(it, 2), 2),
                         (lambda it: queries(it, 0), 1), (lambda it: sm.turn(pe, it, 1), 3), (output, 4),
                         (lambda it: weigh(it, 0), 3), (lambda it: sm.turn(pe, it, 2), 3), (lambda it: queries(it, 1), 1),
                         (lambda it: weigh(it, 1), 3), (lambda it: sm.turn(pe, it, 3), 3),
                         (lambda it: weigh(it, 2), 3), (lambda it: weigh(it, 3), 3)]
                skewed(pe, g.B, steps, 6)

            @block.scalar
            def _(act):
                for i, (bank, dst) in enumerate([(scores[0], qk[:, 0:BANK]), (scores[1], qk[:, BANK:2 * BANK]),
                                                 (turned[0], vo[:, 0:4, :].rearrange("p i d -> p (i d)")),
                                                 (turned[1], vo[:, 4:8, :].rearrange("p i d -> p (i d)"))]):
                    act.wait_ge(s_pre, i + 1)
                    act.copy(dst, bank[:, :]).then_inc(s_fused, 1)

                def fetch_q(it, c):
                    seen(act, s_q, it, 2, c)
                    seen(act, sm.s_scores, it, 3, ago=2)
                    act.copy(qT[it.par][:, 4 * c:4 * c + 4, :].rearrange("p i t -> p (i t)"), pa[:, :]).then_inc(s_qT, 1)

                def fetch_o(it, c):
                    seen(act, s_oTp, it, 2, c)
                    seen(act, s_y, it, ago=2)
                    act.copy(oT[it.par][:, 4 * c:4 * c + 4, :].rearrange("p i t -> p (i t)"), py[:, :]).then_inc(s_oT, 1)

                steps = [(lambda it: fetch_o(it, 0), 4), (lambda it: ln.fetch(act, it, s_q, 2), 1), (lambda it: fetch_o(it, 1), 4),
                         (lambda it: sm.fetch(act, it, 0), 3), (lambda it: fetch_q(it, 0), 1), (lambda it: sm.fetch(act, it, 1), 3),
                         (lambda it: sm.exponential(act, it, 0), 2), (lambda it: sm.fetch(act, it, 2), 3),
                         (lambda it: fetch_q(it, 1), 1), (lambda it: sm.exponential(act, it, 1), 2),
                         (lambda it: sm.fetch(act, it, 3), 3), (lambda it: sm.exponential(act, it, 2), 2)]
                skewed(act, g.B, steps, 6)

            @block.vector
            def _(dve):
                dve.wait_ge(s_w, 16 * len(weights))

                def divide(it, c):
                    p = it.par
                    seen(dve, sm.s_values, it, 4, c)
                    seen(dve, s_o, it, 4, c, back=8)
                    dve.reciprocal(recip[p][:, 4 * c:4 * c + 4], o_p[:, :, CTX]).then_inc(s_recip, 1)
                    seen(dve, s_recip, it, 4, c)
                    seen(dve, s_oTp, it, 2, ago=2)
                    dve.tensor_tensor(o_s[p][:, 4 * c:4 * c + 4, :], o_p[:, :, 0:CTX],
                                      recip[p][:, 4 * c:4 * c + 4].unsqueeze(2).to_broadcast([P, CHUNK, CTX]),
                                      ALU.mult).then_inc(s_o, 1)

                def add(it):
                    x = g.x[:, bass.ts(it.b, P)]
                    seen(dve, ln.s_xn, it)
                    dve.scalar_tensor_tensor(x, bo[:, :], g.gates[:, 1:2], x, ALU.mult, ALU.add).then_inc(s_bo, 1)
                    seen(dve, s_bo, it)
                    seen(dve, s_y, it)
                    dve.scalar_tensor_tensor(x, y_p, g.gates[:, 1:2], x, ALU.mult, ALU.add).then_inc(s_x, 1)

                steps = [(lambda it: ln.normalize(dve, it), 1), (lambda it: ln.statistics(dve, it), 0)]
                for c in range(3):
                    steps += [(lambda it, c=c: sm.maximum(dve, it, c), 2), (lambda it, c=c: sm.shift(dve, it, c), 2)]
                steps.append((add, 4))
                steps += [(lambda it, c=c: divide(it, c), 3) for c in range(4)]
                skewed(dve, g.B, steps, 6)


class Norm:

    def __init__(self, st, g, name, rows, width):
        self.g, self.rows, self.width = g, rows, width
        self.stats, self.mv = st.sb(f"{name}_st", [rows, 6]), st.sb2(f"{name}_mv", [rows, 2])
        self.ve, self.rstd = st.sb2(f"{name}_ve", [rows, 1]), st.sb2(f"{name}_rs", [rows, 1])
        self.s_mv, self.s_ve, self.s_rstd, self.s_hat, self.s_pass = [
            st.sem(f"{name}_{k}") for k in ("s_mv", "s_ve", "s_rstd", "s_hat", "s_pass")]

    def statistics(self, dve, it, src):
        seen(dve, self.s_hat, it, ago=2)
        seen(dve, self.s_ve, it, ago=2)
        dve.sem_inc(self.s_pass, 1)
        dve.bn_stats(self.stats[:, :], src)
        dve.drain()
        dve.bn_aggr(self.mv[it.par][:, :], self.stats[:, :]).then_inc(self.s_mv, 1)
        dve.drain()

    def inverse_deviation(self, pool, it):
        p, r = it.par, self.rows
        seen(pool, self.s_mv, it)
        seen(pool, self.s_rstd, it, ago=2)
        pool.tensor_tensor(self.ve[p][:, :], self.mv[p][:, 1:2], self.g.eps[0:r, 0:1], ALU.add).then_inc(self.s_ve, 1)
        seen(pool, self.s_ve, it)
        seen(pool, self.s_hat, it, ago=2)
        pool.tensor_tensor(self.rstd[p][:, :], self.ve[p][:, :], self.g.minus_half[0:r, 0:1], ALU.pow).then_inc(self.s_rstd, 1)

    def hat(self, dve, it, src, dst):
        p = it.par
        seen(dve, self.s_rstd, it)
        dve.tensor_scalar(dst, src, self.mv[p][:, 0:1], self.rstd[p][:, 0:1], ALU.subtract, ALU.mult).then_inc(self.s_hat, 1)


def l3_attention(nc, g, a, name, pre, first):
    D = 32
    G4 = P // D
    J = HEADS // G4
    T = P if first else KEYS
    C = P if first else CTX
    scale = float(D) ** -0.5
    with Stage(nc, name) as st:
        wq, wk, wv = st.sb("wq", [P, HEADS * D]), st.sb("wk", [C, HEADS * D]), st.sb("wv", [C, HEADS * D])
        li1, bias, col = st.sb("li1", [P, J, P]), st.sb("bias", [P, P]), st.sb("col", [P, 4])
        ln1_g, ln1_b = st.sb("ln1_g", [P, P]), st.sb("ln1_b", [P, P])
        xa, xh = st.sb2("xa", [P, P]), st.sb2("xh", [P, P])
        ctx_in, yh = st.sb2("ctx_in", [KEYS, CTX]), st.sb2("yh", [KEYS, CTX])
        xT, yT = st.sb2("xT", [P, P]), st.sb2("yT", [C, T])
        qT, kT, vals = st.sb2("qT", [P, J, P]), st.sb2("kT", [P, J, T]), st.sb2("vals", [T, HEADS * D])
        keys = st.sb2("keys", [P, J, G4, T])
        total, recip = st.sb2("total", [P, HEADS]), st.sb2("recip", [P, HEADS])
        o_s, oT = st.sb2("o", [P, HEADS * D]), st.sb2("oT", [P, J, P])
        later = st.sb("later", [P, T])
        scores = [st.ps(f"scores{i}") for i in range(4)]
        turned = [st.ps(f"turned{i}") for i in range(2)]
        pa, po = st.ps("pa"), st.ps("po")
        sm = Softmax(st, g, scores, [4] * 4, T, scale, turned)
        n3 = Norm(st, g, "n3", P, P)
        if first:
            n1, n2 = Norm(st, g, "n1", P, P), Norm(st, g, "n2", P, P)
            s_aff = st.sem("s_aff")
        else:
            ny = Norm(st, g, "ny", KEYS, CTX)
        s_w, s_ctx, s_mask, s_x1 = st.sem("s_w"), st.sem2("s_ctx"), st.sem("s_later"), st.sem("s_x1")
        s_turn, s_xT, s_q, s_qT, s_k, s_kT, s_v, s_vals, s_keys = [
            st.sem(n) for n in ("s_turn", "s_xT", "s_q", "s_qT", "s_k", "s_kT", "s_v", "s_vals", "s_keys")]
        s_sum, s_masked, s_recip, s_o, s_oTp, s_oT, s_y, s_out, s_bias = [
            st.sem(n) for n in ("s_sum", "s_masked", "s_recip", "s_o", "s_oTp", "s_oT", "s_y", "s_out", "s_bias")]
        k_ = lambda n: a[f"{pre}_{n}"]
        weights = [(wq[:, :], k_("wq")), (wk[:, :], k_("wk")), (wv[:, :], k_("wv")), (li1[:, :, :], k_("li1_w")),
                   (bias[:, :], k_("li1_b").partition_broadcast(P)), (col[:, 0:1], k_("lnx_g")), (col[:, 1:2], k_("lnx_b")),
                   (col[0:C, 2:3], k_("lny_g")), (col[0:C, 3:4], k_("lny_b"))]
        if first:
            weights += [(ln1_g[:, :], a["ln1_g"].partition_broadcast(P)), (ln1_b[:, :], a["ln1_b"].partition_broadcast(P))]
        all_weights = 16 * len(weights)

        def z(it):
            return g.z[:, bass.ts(it.b, P)]

        with nc.Block() as block:
            @block.sync
            def _(sp):
                for dst, src in weights:
                    sp.dma_start(dst, src).then_inc(s_w, 16)
                if not first:
                    def context(it):
                        seen(sp, ny.s_hat, it, ago=2)
                        sp.dma_start(ctx_in[it.par][:, :], g.ctx_d[:, bass.ds(it.b, 1), :].rearrange("t b c -> t (b c)")).then_inc(s_ctx[it.par], 16)

                    skewed(sp, g.B, [(context, 0)], 2)

            @block.gpsimd
            def _(pool):
                if first:
                    pool.memset(later[:, :], 1.0).then_inc(s_mask, 1)
                    pool.wait_ge(s_mask, 1)
                    pool.affine_select(out=later[:, :], in_=later[:, :], compare_op=ALU.is_gt, fill=0.0,
                                       base=0, pattern=[[1, T]], channel_multiplier=-1).then_inc(s_mask, 1)
                    pool.wait_ge(s_mask, 2)

                def spread(it):
                    seen(pool, s_kT, it)
                    seen(pool, sm.s_scores, it, 4, ago=2)
                    pool.tensor_tensor(keys[it.par][:, :, :, :],
                                       kT[it.par][:, :, :].unsqueeze(2).to_broadcast([P, J, G4, T]),
                                       g.head32[:, :].unsqueeze(1).unsqueeze(3).to_broadcast([P, J, G4, T]),
                                       ALU.mult).then_inc(s_keys, 1)

                def drop_earlier(it, c):
                    v = sm.probs[it.par][:, 4 * c:4 * c + 4, :]
                    seen(pool, s_sum, it, 4, c)
                    pool.tensor_tensor(v, v, later[:, :].unsqueeze(1).to_broadcast([P, 4, T]), ALU.mult).then_inc(s_masked, 1)

                if first:
                    steps = [(lambda it: n1.inverse_deviation(pool, it), 0), (lambda it: n2.inverse_deviation(pool, it), 1),
                             (lambda it: n3.inverse_deviation(pool, it), 2), (spread, 3)]
                    steps += [(lambda it, c=c: drop_earlier(it, c), 4) for c in range(4)]
                else:
                    steps = [(lambda it: n3.inverse_deviation(pool, it), 2), (lambda it: ny.inverse_deviation(pool, it), 2),
                             (spread, 3)]
                skewed(pool, g.B, steps, 8)

            @block.tensor
            def _(pe):
                pe.wait_ge(s_w, all_weights)

                def turn(it):
                    seen(pe, n3.s_hat, it)
                    seen(pe, s_vals, it, ago=1)
                    if not first:
                        seen(pe, ny.s_hat, it)
                    last = pe.transpose(pa[:, 0:P], xh[it.par][:, :], g.ident[:, :])
                    if not first:
                        last = pe.transpose(pa[0:CTX, P:P + KEYS], yh[it.par][:, :], g.ident[0:KEYS, 0:KEYS])
                    last.then_inc(s_turn, 1)

                def queries(it):
                    seen(pe, s_xT, it)
                    for j in range(J):
                        last = pe.matmul(pa[:, j * P:(j + 1) * P], wq[:, j * P:(j + 1) * P], xT[it.par][:, :], start=True, stop=True)
                    last.then_inc(s_q, 1)

                def keys_of(it):
                    seen(pe, s_qT, it)
                    for j in range(J):
                        last = pe.matmul(pa[:, j * T:(j + 1) * T], wk[:, j * P:(j + 1) * P], yT[it.par][:, :], start=True, stop=True)
                    last.then_inc(s_k, 1)

                def values(it):
                    seen(pe, s_kT, it)
                    pe.matmul(pa[0:T, :], yT[it.par][:, :], wv[:, :], start=True, stop=True).then_inc(s_v, 1)

                def score(it, c):
                    seen(pe, s_keys, it)
                    seen(pe, s_qT, it)
                    seen(pe, sm.s_shift, it, 4, c, back=4)
                    pe.matmul(scores[c][:, 0:G4 * T], qT[it.par][:, c, :], keys[it.par][:, c, :, :].rearrange("p h t -> p (h t)"),
                              start=True, stop=True).then_inc(sm.s_scores, 1)

                def turn_p(it, c):
                    sm.turn(pe, it, c, s_masked if first else None, 4)

                def weigh(it, c):
                    if c == 0:
                        seen(pe, s_vals, it)
                        seen(pe, s_out, it, ago=1)
                    sm.times_values(pe, it, c, lambda h: po[:, h * D:(h + 1) * D], lambda h: vals[it.par][:, h * D:(h + 1) * D])

                def turn_o(it):
                    seen(pe, s_o, it)
                    for j in range(J):
                        last = pe.transpose(po[:, j * P:(j + 1) * P], o_s[it.par][:, j * P:(j + 1) * P], g.ident[:, :])
                    last.then_inc(s_oTp, 1)

                def output(it):
                    seen(pe, s_oT, it)
                    for j in range(J):
                        last = pe.matmul(po[:, 0:P], oT[it.par][:, j, :], li1[:, j, :], start=(j == 0), stop=(j == J - 1))
                    last.then_inc(s_y, 1)

                steps = [(turn_o, 6), (lambda it: score(it, 0), 4), (turn, 3), (lambda it: score(it, 1), 4), (output, 6),
                         (lambda it: score(it, 2), 4), (queries, 3), (lambda it: score(it, 3), 4),
                         (lambda it: turn_p(it, 0), 5), (lambda it: turn_p(it, 1), 5), (keys_of, 3), (lambda it: weigh(it, 0), 5),
                         (lambda it: turn_p(it, 2), 5), (lambda it: weigh(it, 1), 5), (values, 3),
                         (lambda it: turn_p(it, 3), 5), (lambda it: weigh(it, 2), 5), (lambda it: weigh(it, 3), 5)]
                skewed(pe, g.B, steps, 8)

            @block.scalar
            def _(act):
                act.wait_ge(s_w, all_weights)

                def fetch_x(it):
                    p = it.par
                    seen(act, s_turn, it)
                    seen(act, s_q, it, ago=2)
                    act.activation(xT[p][:, :], pa[:, 0:P], ACT.Identity, bias=col[:, 1:2], scale=col[:, 0:1])
                    seen(act, s_v, it, ago=2)
                    src = pa[:, 0:P] if first else pa[0:CTX, P:P + KEYS]
                    act.activation(yT[p][:, :], src, ACT.Identity, bias=col[0:C, 3:4], scale=col[0:C, 2:3]).then_inc(s_xT, 1)

                def fetch_q(it):
                    seen(act, s_q, it)
                    seen(act, sm.s_scores, it, 4, ago=2)
                    act.copy(qT[it.par][:, :, :].rearrange("p j t -> p (j t)"), pa[:, :]).then_inc(s_qT, 1)

                def fetch_k(it):
                    seen(act, s_k, it)
                    seen(act, s_keys, it, ago=2)
                    act.copy(kT[it.par][:, :, :].rearrange("p j t -> p (j t)"), pa[:, 0:J * T]).then_inc(s_kT, 1)

                def fetch_v(it):
                    seen(act, s_v, it)
                    seen(act, sm.s_values, it, 4, ago=2)
                    act.copy(vals[it.par][:, :], pa[0:T, :]).then_inc(s_vals, 1)

                def fetch_o(it):
                    seen(act, s_oTp, it)
                    seen(act, s_y, it, ago=2)
                    act.copy(oT[it.par][:, :, :].rearrange("p j t -> p (j t)"), po[:, :]).then_inc(s_oT, 1)

                steps = [(fetch_o, 6), (fetch_x, 3), (lambda it: sm.exponential(act, it, 0), 4), (fetch_q, 3),
                         (lambda it: sm.exponential(act, it, 1), 4),
                         (lambda it: sm.fetch(act, it, 0), 5), (lambda it: sm.fetch(act, it, 1), 5), (fetch_k, 3),
                         (lambda it: sm.exponential(act, it, 2), 4),
                         (lambda it: sm.fetch(act, it, 2), 5), (lambda it: sm.fetch(act, it, 3), 5),
                         (lambda it: sm.exponential(act, it, 3), 4), (fetch_v, 3)]
                skewed(act, g.B, steps, 8)

            @block.vector
            def _(dve):
                dve.wait_ge(s_w, all_weights)

                def stats1(it):
                    n1.statistics(dve, it, g.x[:, bass.ts(it.b, P)])

                def stats2(it):
                    seen(dve, s_x1, it, ago=2)
                    n1.hat(dve, it, g.x[:, bass.ts(it.b, P)], xa[it.par][:, :])
                    seen(dve, n1.s_hat, it)
                    n2.statistics(dve, it, xa[it.par][:, :])

                def stats3(it):
                    v = xa[it.par][:, :]
                    n2.hat(dve, it, v, v)
                    seen(dve, n2.s_hat, it)
                    dve.tensor_tensor(v, v, ln1_g[:, :], ALU.mult).then_inc(s_aff, 1)
                    seen(dve, s_aff, it)
                    dve.tensor_tensor(z(it), v, ln1_b[:, :], ALU.add).then_inc(s_x1, 1)
                    seen(dve, s_x1, it)
                    n3.statistics(dve, it, z(it))

                def stats_z(it):
                    n3.statistics(dve, it, z(it))
                    loaded(dve, s_ctx, it)
                    ny.statistics(dve, it, ctx_in[it.par][:, :])

                def hat(it):
                    seen(dve, s_turn, it, ago=2)
                    n3.hat(dve, it, z(it), xh[it.par][:, :])
                    if not first:
                        ny.hat(dve, it, ctx_in[it.par][:, :], yh[it.par][:, :])

                def row_sum(it, c):
                    seen(dve, sm.s_exp, it, 4, c)
                    seen(dve, s_recip, it, ago=2)
                    dve.tensor_reduce(total[it.par][:, 4 * c:4 * c + 4], sm.probs[it.par][:, 4 * c:4 * c + 4, :], AX,
                                      ALU.add).then_inc(s_sum, 1)

                def divide(it):
                    p = it.par
                    seen(dve, s_sum, it, 4)
                    seen(dve, s_o, it, ago=2)
                    dve.reciprocal(recip[p][:, :], total[p][:, :]).then_inc(s_recip, 1)
                    seen(dve, s_recip, it)
                    seen(dve, sm.s_values, it, 4)
                    seen(dve, s_oTp, it, ago=2)
                    dve.tensor_tensor(o_s[p][:, :].rearrange("p (h d) -> p h d", d=D), po[:, :].rearrange("p (h d) -> p h d", d=D),
                                      recip[p][:, :].unsqueeze(2).to_broadcast([P, HEADS, D]), ALU.mult).then_inc(s_o, 1)

                def add(it):
                    y = g.y[:, bass.ts(it.b, P)]
                    dve.tensor_tensor(y, z(it), bias[:, :], ALU.add).then_inc(s_bias, 1)
                    seen(dve, s_bias, it)
                    seen(dve, s_y, it)
                    dve.tensor_tensor(y, po[:, 0:P], y, ALU.add).then_inc(s_out, 1)

                steps = [(hat, 3)]
                if first:
                    steps += [(stats1, 0), (stats2, 1), (stats3, 2)]
                else:
                    steps += [(stats_z, 2)]
                for c in range(4):
                    steps += [(lambda it, c=c: sm.maximum(dve, it, c), 4), (lambda it, c=c: sm.shift(dve, it, c), 4)]
                    if c == 0:
                        steps += [(add, 6)]
                steps += [(lambda it, c=c: row_sum(it, c), 4) for c in range(4)]
                steps += [(divide, 5)]
                skewed(dve, g.B, steps, 8)


def l3_mlp(nc, g, a, name, pre, first):
    F = 4 * P
    FT = F // P
    with Stage(nc, name) as st:
        li2, li3, b3 = st.sb("li2", [P, F]), st.sb("li3", [P, FT, P]), st.sb("b3", [P, P])
        b2, col = st.sb("b2", [P, FT]), st.sb("col", [P, 2])
        ln2_g, ln2_b = st.sb("ln2_g", [P, P]), st.sb("ln2_b", [P, P])
        yh, yT, hT, acc = st.sb2("yh", [P, P]), st.sb2("yT", [P, P]), st.sb2("hT", [P, F]), st.sb2("acc", [P, P])
        ps_t, ps_h, ps_y = [[st.ps(f"{k}{i}") for i in range(2)] for k in ("t", "h", "y")]
        n3 = Norm(st, g, "n3", P, P)
        if first:
            n2 = Norm(st, g, "n2", P, P)
        s_w, s_turn, s_yT, s_h, s_hT, s_y, s_a1, s_a2, s_sum, s_m, s_done = [
            st.sem(k) for k in ("s_w", "s_turn", "s_yT", "s_h", "s_hT", "s_y", "s_a1", "s_a2", "s_sum", "s_m", "s_done")]
        k_ = lambda n: a[f"{pre}_{n}"]
        weights = [(li2[:, :], k_("li2_w")), (li3[:, :, :], k_("li3_w")), (b3[:, :], k_("li3_b").partition_broadcast(P)),
                   (b2[:, :], k_("li2_b")), (col[:, 0:1], k_("ln3_g")), (col[:, 1:2], k_("ln3_b"))]
        if first:
            weights += [(ln2_g[:, :], a["ln2_g"].partition_broadcast(P)), (ln2_b[:, :], a["ln2_b"].partition_broadcast(P))]
        all_weights = 16 * len(weights)

        def y_(it):
            return g.y[:, bass.ts(it.b, P)]

        def z_(it):
            return g.z[:, bass.ts(it.b, P)]

        with nc.Block() as block:
            @block.sync
            def _(sp):
                for dst, src in weights:
                    sp.dma_start(dst, src).then_inc(s_w, 16)

            @block.gpsimd
            def _(pool):
                steps = [(lambda it: n3.inverse_deviation(pool, it), 0)]
                if first:
                    steps.append((lambda it: n2.inverse_deviation(pool, it), 4))
                skewed(pool, g.B, steps, 8)

            @block.tensor
            def _(pe):
                pe.wait_ge(s_w, all_weights)

                def turn(it):
                    seen(pe, n3.s_hat, it)
                    seen(pe, s_yT, it, ago=2)
                    pe.transpose(ps_t[it.par][:, 0:P], yh[it.par][:, :], g.ident[:, :]).then_inc(s_turn, 1)

                def hidden(it):
                    seen(pe, s_yT, it)
                    seen(pe, s_hT, it, FT, ago=2)
                    for t in range(FT):
                        last = pe.matmul(ps_h[it.par][:, t * P:(t + 1) * P], li2[:, t * P:(t + 1) * P], yT[it.par][:, :], start=True, stop=True)
                    last.then_inc(s_h, 1)

                def output(it):
                    seen(pe, s_hT, it, FT)
                    seen(pe, s_sum, it, ago=2)
                    for t in range(FT):
                        last = pe.matmul(ps_y[it.par][:, 0:P], hT[it.par][:, t * P:(t + 1) * P], li3[:, t, :], start=(t == 0), stop=(t == FT - 1))
                    last.then_inc(s_y, 1)

                skewed(pe, g.B, [(turn, 1), (hidden, 2), (output, 3)], 8)

            @block.scalar
            def _(act):
                act.wait_ge(s_w, all_weights)

                def fetch(it):
                    seen(act, s_turn, it)
                    seen(act, s_h, it, ago=2)
                    act.activation(yT[it.par][:, :], ps_t[it.par][:, 0:P], ACT.Identity, bias=col[:, 1:2], scale=col[:, 0:1]).then_inc(s_yT, 1)

                def gelu(it):
                    seen(act, s_h, it)
                    seen(act, s_y, it, ago=2)
                    for t in range(FT):
                        act.activation(hT[it.par][:, t * P:(t + 1) * P], ps_h[it.par][:, t * P:(t + 1) * P], ACT.Gelu,
                                       bias=b2[:, t:t + 1]).then_inc(s_hT, 1)

                skewed(act, g.B, [(fetch, 1), (gelu, 2)], 8)

            @block.vector
            def _(dve):
                dve.wait_ge(s_w, all_weights)

                def hat(it):
                    seen(dve, s_turn, it, ago=2)
                    n3.hat(dve, it, y_(it), yh[it.par][:, :])

                def sums(it):
                    c = acc[it.par][:, :]
                    seen(dve, s_done, it, ago=2)
                    dve.tensor_tensor(c, y_(it), z_(it), ALU.add).then_inc(s_a1, 1)
                    seen(dve, s_a1, it)
                    dve.tensor_tensor(c, c, b3[:, :], ALU.add).then_inc(s_a2, 1)
                    seen(dve, s_a2, it)
                    seen(dve, s_y, it)
                    dve.tensor_tensor(c, ps_y[it.par][:, 0:P], c, ALU.add).then_inc(s_sum, 1)
                    seen(dve, s_sum, it)
                    if first:
                        n2.statistics(dve, it, c)

                def finish(it):
                    c = acc[it.par][:, :]
                    if first:
                        n2.hat(dve, it, c, c)
                        seen(dve, n2.s_hat, it)
                        dve.tensor_tensor(c, c, ln2_g[:, :], ALU.mult).then_inc(s_m, 1)
                        seen(dve, s_m, it)
                        dve.tensor_tensor(z_(it), c, ln2_b[:, :], ALU.add).then_inc(s_done, 1)
                    else:
                        x = g.x[:, bass.ts(it.b, P)]
                        seen(dve, s_sum, it)
                        dve.scalar_tensor_tensor(x, c, g.gates[:, 3:4], x, ALU.mult, ALU.add).then_inc(s_done, 1)

                skewed(dve, g.B, [(hat, 1), (lambda it: n3.statistics(dve, it, y_(it)), 0), (finish, 5), (sums, 4)], 8)


def l3_xattn(nc, g, a):
    with nc.sbuf_tensor("l3_y", [P, g.B * P], F32) as g.y, nc.sbuf_tensor("l3_z", [P, g.B * P], F32) as g.z:
        l3_attention(nc, g, a, "l3a", "a1", True)
        l3_mlp(nc, g, a, "l3b", "a1", True)
        l3_attention(nc, g, a, "l3c", "a2", False)
        l3_mlp(nc, g, a, "l3d", "a2", False)


def l3_ffn(nc, g, a):
    CYC = 3
    Q4 = P // 4
    H2, H3 = P // 2, P // 4
    n = g.B // GROUP
    W = GROUP * P
    with Stage(nc, "l3f") as st:
        w1, w2, w3, w4 = st.sb("w1", [P, P]), st.sb("w2", [P, H2]), st.sb("w3", [H2, H3]), st.sb("w4", [H3, 1])
        v1, v2, v3 = st.sb("v1", [P, H2]), st.sb("v2", [H2, H3]), st.sb("v3", [H3, 1])
        b1, b2, b3 = st.sb("b1", [P, 1]), st.sb("b2", [H2, 1]), st.sb("b3", [H3, 1])
        c1, c2 = st.sb("c1", [H2, 1]), st.sb("c2", [H3, 1])
        rows = st.sb("rows", [P, 3])
        half, r03 = st.sb("half", [P, 2]), st.sb("r03", [P, 2])
        mean_of = st.sb("mean_of", [P, 1])
        mean, gh1, gh2 = st.sb("mean", [P, GROUP]), st.sb("gh1", [H2, GROUP]), st.sb("gh2", [H3, GROUP])
        gth = st.sb("gth", [P, GROUP])
        base = st.sb("base", [P, g.B])
        u = [None] + [st.sb2(f"u{k}_", [P, W]) for k in range(1, CYC)] + [[st.sb("u3", [P, W])] * 2]
        uT = [None] + [st.sb(f"uT{k}", [P, W]) for k in range(1, CYC)]
        h1, h2, h3 = [[st.sb(f"h{m}_{k}", [r, W]) for k in range(CYC)] for m, r in ((1, P), (2, H2), (3, H3))]
        th, cp = [st.sb(f"th{k}", [P, GROUP]) for k in range(CYC)], [st.sb(f"cp{k}", [P, GROUP]) for k in range(CYC)]
        tw = [st.sb(f"tw{k}", [P, W]) for k in range(CYC)]
        ps_xT, ps_g = st.ps("xT"), st.ps("g")
        ps_a, ps_b = [[st.ps(f"cycle_{m}{k}") for k in range(CYC)] for m in "ab"]
        fr = GroupFront(st, g, ps_xT)
        u[0] = fr.xn
        s_w, s_const, s_const2 = st.sem("s_w"), st.sem("s_const"), st.sem("s_const2")
        s_meanp, s_mean, s_g1p, s_g1, s_g2p, s_g2, s_g3p, s_gth, s_base = [
            st.sem(k) for k in ("s_meanp", "s_mean", "s_g1p", "s_g1", "s_g2p", "s_g2", "s_g3p", "s_gth", "s_base")]
        s_uTp, s_uT, s_h1p, s_h1, s_h2p, s_h2, s_h3p, s_h3, s_zp, s_th, s_cpa, s_cp, s_tw, s_u = [
            [st.sem(f"{k}_{i}") for i in range(CYC)] for k in (
                "s_uTp", "s_uT", "s_h1p", "s_h1", "s_h2p", "s_h2", "s_h3p", "s_h3", "s_zp", "s_th", "s_cpa", "s_cp", "s_tw", "s_u")]
        s_x, s_pass = st.sem("s_x"), st.sem("s_pass")
        weights = [(w1[:, :], a["cn_w1"]), (w2[:, :], a["cn_w2"]), (w3[:, :], a["cn_w3"]), (w4[:, :], a["cn_w4"]),
                   (b1[:, :], a["cn_b1"]), (b2[:, :], a["cn_b2"]), (b3[:, :], a["cn_b3"]),
                   (v1[:, :], a["gc_w1"]), (v2[:, :], a["gc_w2"]), (v3[:, :], a["gc_w3"]),
                   (c1[:, :], a["gc_b1"]), (c2[:, :], a["gc_b2"]),
                   (rows[:, 0:1], a["cn_b4"].partition_broadcast(P)), (rows[:, 1:2], a["gc_b3"].partition_broadcast(P)),
                   (rows[:, 2:3], a["adaptive_range"].partition_broadcast(P))]
        all_weights = 16 * len(weights)
        LAG = [2, 3, 4]

        with nc.Block() as block:
            @block.sync
            def _(sp):
                for dst, src in weights:
                    sp.dma_start(dst, src).then_inc(s_w, 16)

            @block.gpsimd
            def _(pool):
                pool.memset(mean_of[:, :], 1.0 / P).then_inc(s_const2, 1)
                skewed(pool, n, [(lambda it: fr.inverse_deviation(pool, it), 0)], 2)

            @block.tensor
            def _(pe):
                pe.wait_ge(s_w, all_weights)
                pe.wait_ge(s_const2, 1)

                def mean_token(it):
                    seen(pe, fr.s_xn, it)
                    seen(pe, s_gth, it, ago=1)
                    for j in range(GROUP):
                        last = pe.matmul(ps_g[:, j:j + 1], fr.xn[it.par][:, j * P:(j + 1) * P], mean_of[:, :], start=True, stop=True)
                    last.then_inc(s_meanp, 1)

                def global1(it):
                    seen(pe, s_mean, it)
                    pe.matmul(ps_g[0:H2, 0:GROUP], v1[:, :], mean[:, :], start=True, stop=True).then_inc(s_g1p, 1)

                def global2(it):
                    seen(pe, s_g1, it)
                    pe.sem_inc(s_pass, 1)
                    pe.matmul(ps_g[0:H3, 0:GROUP], v2[:, :], gh1[:, :], start=True, stop=True).then_inc(s_g2p, 1)

                def global3(it):
                    seen(pe, s_g2, it)
                    pe.matmul(ps_g[:, 0:GROUP], v3[:, :].to_broadcast([H3, P]), gh2[:, :], start=True, stop=True).then_inc(s_g3p, 1)

                def turn(it, k):
                    seen(pe, s_u[k - 1], it)
                    seen(pe, s_th[k], it, ago=1)
                    for j in range(GROUP):
                        last = pe.transpose(ps_a[k][:, j * P:(j + 1) * P], u[k][it.par][:, j * P:(j + 1) * P], g.ident[:, :])
                    last.then_inc(s_uTp[k], 1)

                def layer1(it, k):
                    if k == 0:
                        seen(pe, fr.s_xT, it)
                    else:
                        seen(pe, s_uT[k], it)
                    seen(pe, s_h3[k], it, ago=1)
                    src = fr.xT[it.par] if k == 0 else uT[k]
                    pe.matmul(ps_b[k][:, :], w1[:, :], src[:, :], start=True, stop=True).then_inc(s_h1p[k], 1)

                def layer2(it, k):
                    seen(pe, s_th[k], it, ago=1)
                    seen(pe, s_h1[k], it)
                    pe.matmul(ps_a[k][0:H2, :], w2[:, :], h1[k][:, :], start=True, stop=True).then_inc(s_h2p[k], 1)

                def layer3(it, k):
                    seen(pe, s_h2[k], it)
                    pe.sem_inc(s_pass, 1)
                    pe.matmul(ps_b[k][0:H3, :], w3[:, :], h2[k][:, :], start=True, stop=True).then_inc(s_h3p[k], 1)

                def layer4(it, k):
                    seen(pe, s_h3[k], it)
                    for j in range(GROUP):
                        last = pe.matmul(ps_a[k][:, j:j + 1], h3[k][:, j * P:(j + 1) * P], w4[:, :], start=True, stop=True)
                    last.then_inc(s_zp[k], 1)

                def of(f, k):
                    return (lambda it: f(it, k), LAG[k])

                steps = [of(turn, 2), of(turn, 1), of(layer1, 0), of(layer1, 2), of(layer1, 1), (lambda it: fr.turn(pe, it), 1)]
                steps += [(mean_token, 1), of(layer2, 0), of(layer2, 2), of(layer2, 1), (global1, 1)]
                steps += [of(layer3, 0), of(layer3, 2), of(layer3, 1), (global2, 1)]
                steps += [of(layer4, 0), of(layer4, 2), of(layer4, 1), (global3, 1)]
                skewed(pe, n, steps, 6)

            @block.scalar
            def _(act):
                act.wait_ge(s_w, all_weights)
                act.wait_ge(s_const, 1)

                def fetch(it, k):
                    seen(act, s_uTp[k], it)
                    seen(act, s_h1p[k], it, ago=1)
                    act.copy(uT[k][:, :], ps_a[k][:, :]).then_inc(s_uT[k], 1)

                def gelu1(it, k):
                    seen(act, s_h1p[k], it)
                    seen(act, s_h2p[k], it, ago=1)
                    act.activation(h1[k][:, :], ps_b[k][:, :], ACT.Gelu, bias=b1[:, 0:1]).then_inc(s_h1[k], 1)

                def gelu2(it, k):
                    seen(act, s_h2p[k], it)
                    seen(act, s_h3p[k], it, ago=1)
                    act.activation(h2[k][:, :], ps_a[k][0:H2, :], ACT.Gelu, bias=b2[:, 0:1]).then_inc(s_h2[k], 1)

                def gelu3(it, k):
                    seen(act, s_h3p[k], it)
                    seen(act, s_zp[k], it, ago=1)
                    act.activation(h3[k][:, :], ps_b[k][0:H3, :], ACT.Gelu, bias=b3[:, 0:1]).then_inc(s_h3[k], 1)

                def tanh(it, k):
                    seen(act, s_zp[k], it)
                    seen(act, s_cpa[k], it, ago=1)
                    act.activation(th[k][:, :], ps_a[k][:, 0:GROUP], ACT.Tanh, bias=half[:, 0:1], scale=0.5).then_inc(s_th[k], 1)

                def fetch_mean(it):
                    seen(act, s_meanp, it)
                    act.copy(mean[:, :], ps_g[:, 0:GROUP]).then_inc(s_mean, 1)

                def global1(it):
                    seen(act, s_g1p, it)
                    act.activation(gh1[:, :], ps_g[0:H2, 0:GROUP], ACT.Gelu, bias=c1[:, 0:1]).then_inc(s_g1, 1)

                def global2(it):
                    seen(act, s_g2p, it)
                    act.activation(gh2[:, :], ps_g[0:H3, 0:GROUP], ACT.Gelu, bias=c2[:, 0:1]).then_inc(s_g2, 1)

                def global3(it):
                    seen(act, s_g3p, it)
                    seen(act, s_base, it, ago=1)
                    act.activation(gth[:, :], ps_g[:, 0:GROUP], ACT.Tanh, bias=half[:, 1:2], scale=0.5).then_inc(s_gth, 1)

                def of(f, k):
                    return (lambda it: f(it, k), LAG[k])

                steps = [of(fetch, 2), of(fetch, 1), of(gelu1, 0), of(gelu1, 2), of(gelu1, 1),
                         (lambda it: fr.fetch(act, it, s_h1p[0]), 1), (fetch_mean, 1),
                         of(gelu2, 0), of(gelu2, 2), of(gelu2, 1), (global1, 1),
                         of(gelu3, 0), of(gelu3, 2), of(gelu3, 1), (global2, 1),
                         of(tanh, 0), of(tanh, 2), of(tanh, 1), (global3, 1)]
                skewed(act, n, steps, 6)

            @block.vector
            def _(dve):
                dve.wait_ge(s_w, all_weights)
                dve.tensor_scalar(half[:, :], rows[:, 0:2], 0.5, None, ALU.mult)
                dve.tensor_scalar(r03[:, 0:1], rows[:, 2:3], 0.3, None, ALU.mult)
                dve.tensor_scalar(r03[:, 1:2], rows[:, 2:3], 0.7, None, ALU.mult)
                dve.drain()
                dve.sem_inc(s_const, 1)

                def coupling_base(it):
                    seen(dve, s_gth, it)
                    dve.tensor_scalar(slot(it), gth[:, :], r03[:, 1:2], 0.1, ALU.mult, ALU.add).then_inc(s_base, 1)

                def slot(it):
                    return base[:, bass.ts(it.b, GROUP)]

                def couple(it, k):
                    seen(dve, s_th[k], it)
                    seen(dve, s_base, it)
                    seen(dve, s_tw[k], it, ago=1)
                    dve.scalar_tensor_tensor(cp[k][:, :], th[k][:, :], r03[:, 0:1], slot(it), ALU.mult, ALU.add).then_inc(s_cpa[k], 1)
                    seen(dve, s_cpa[k], it)
                    src = u[k][it.par][:, :].rearrange("p (j d) -> p j d", d=P)
                    t = tw[k][:, :].rearrange("p (j d) -> p j d", d=P)
                    seen(dve, s_u[k], it, ago=1)
                    dve.tensor_tensor(t, src, cp[k][:, :].unsqueeze(2).to_broadcast([P, GROUP, P]), ALU.mult).then_inc(s_tw[k], 1)
                    seen(dve, s_tw[k], it)
                    if k < CYC - 1:
                        seen(dve, s_uTp[k + 1], it, ago=2)
                        seen(dve, s_u[k + 1], it, ago=2)
                    else:
                        seen(dve, s_x, it, ago=1)
                    dst = u[k + 1][it.par][:, :].rearrange("p (j d) -> p j d", d=P)
                    for q, (other, op) in enumerate(((2, ALU.add), (3, ALU.subtract), (0, ALU.subtract), (1, ALU.add))):
                        last = dve.tensor_tensor(dst[:, :, q * Q4:(q + 1) * Q4], src[:, :, q * Q4:(q + 1) * Q4],
                                                 t[:, :, other * Q4:(other + 1) * Q4], op)
                    last.then_inc(s_u[k], 1)

                def add(it):
                    x = g.x[:, bass.ts(it.b, W)]
                    seen(dve, s_u[CYC - 1], it)
                    dve.scalar_tensor_tensor(x, u[CYC][0][:, :], g.gates[:, 7:8], x, ALU.mult, ALU.add).then_inc(s_x, 1)

                def normalize(it):
                    seen(dve, s_u[0], it, ago=2)
                    seen(dve, s_meanp, it, ago=2)
                    fr.normalize(dve, it)

                steps = [(lambda it: couple(it, 0), LAG[0]), (lambda it: couple(it, 2), LAG[2]), (lambda it: couple(it, 1), LAG[1]),
                         (add, LAG[2]), (coupling_base, 1)]
                skewed(dve, n, [(normalize, 1), (lambda it: fr.statistics(dve, it), 0)] + steps, 6)


class Globals:
    pass


def build(nc, a, out, stages):
    g = Globals()
    g.B = a["x"].shape[1]
    g.ctxT_d, g.ctx_d = a["ctxT"], a["ctx"]
    with ExitStack() as ctx:
        def sb(name, shape):
            return ctx.enter_context(nc.sbuf_tensor(name, shape, F32))

        g.x = sb("x_res", [P, g.B * P])
        g.ident, g.head8, g.head32 = sb("ident", [P, P]), sb("head8", [P, HEADS]), sb("head32", [P, 4])
        g.eps, g.minus_half = sb("eps", [P, 4]), sb("minus_half", [P, 4])
        g.gates, gates_in = sb("gates", [P, 8]), sb("gates_in", [P, 8])
        with Stage(nc, "init") as st:
            s_in, s_set, s_ident, s_gates, s_x = st.sem("s_in"), st.sem("s_set"), st.sem("s_ident"), st.sem("s_gates"), st.sem("s_x")
            with nc.Block() as block:
                @block.sync
                def _(sp):
                    sp.dma_start(gates_in[:, 0:4], a["g_xattn"].partition_broadcast(P)).then_inc(s_in, 16)
                    sp.dma_start(gates_in[:, 4:8], a["g_ffn"].partition_broadcast(P)).then_inc(s_in, 16)
                    sp.dma_start(g.x[:, :], a["x"].rearrange("p b d -> p (b d)")).then_inc(s_x, 16)
                    sp.wait_ge(s_x, 16)

                @block.scalar
                def _(act):
                    act.wait_ge(s_in, 32)
                    act.activation(g.gates[:, :], gates_in[:, :], ACT.Tanh).then_inc(s_gates, 1)
                    act.wait_ge(s_gates, 1)

                @block.gpsimd
                def _(pool):
                    pool.memset(g.eps[:, :], LN_EPS).then_inc(s_set, 1)
                    pool.memset(g.minus_half[:, :], -0.5).then_inc(s_set, 1)
                    pool.memset(g.ident[:, :], 0.0).then_inc(s_set, 1)
                    pool.memset(g.head8[:, :], 1.0).then_inc(s_set, 1)
                    pool.memset(g.head32[:, :], 1.0).then_inc(s_set, 1)
                    pool.wait_ge(s_set, 5)
                    pool.affine_select(out=g.ident[:, :], in_=g.ident[:, :], compare_op=ALU.not_equal, fill=1.0,
                                       base=0, pattern=[[-1, P]], channel_multiplier=1).then_inc(s_ident, 1)
                    n = 1
                    for m, w, k in ((g.head8, 8, HEADS), (g.head32, 32, 4)):
                        pool.affine_select(out=m[:, :], in_=m[:, :], compare_op=ALU.is_ge, fill=0.0,
                                           base=0, pattern=[[-w, k]], channel_multiplier=1).then_inc(s_ident, 1)
                        n += 1
                        pool.wait_ge(s_ident, n)
                        pool.affine_select(out=m[:, :], in_=m[:, :], compare_op=ALU.is_ge, fill=0.0,
                                           base=w - 1, pattern=[[w, k]], channel_multiplier=-1).then_inc(s_ident, 1)
                        n += 1
                    pool.wait_ge(s_ident, n)
        for s in stages:
            s(nc, g, a)
        with Stage(nc, "store") as st:
            s_out = st.sem("s_out")
            with nc.Block() as block:
                @block.sync
                def _(sp):
                    sp.dma_start(out.rearrange("p b d -> p (b d)"), g.x[:, :]).then_inc(s_out, 16)
                    sp.wait_ge(s_out, 16)


def l0_xattn(nc, g, a):
    small_head_attention(nc, g, "l0x", a["L0_Wq"], a["L0_Wk"], a["L0_Wv"], a["L0_Wo"], gate=0)


def l2_xattn(nc, g, a):
    small_head_attention(nc, g, "l2x", a["L2_Wq"], a["L2_Wk"], a["L2_Wv"], a["L2_Wo"],
                         a["L2_bq"], a["L2_bk"], a["L2_bv"], a["L2_bo"], gate=2)


def lay_out(i):
    c = np.ascontiguousarray
    o = {"x": c(i["x"].transpose(1, 0, 2)), "ctx": c(i["ctx_512"].transpose(1, 0, 2)),
         "ctxT": c(i["ctx_512"].transpose(2, 0, 1)), "g_xattn": i["g_xattn"], "g_ffn": i["g_ffn"]}
    o["L0_Wq"], o["L0_Wo"] = c(i["L0_xattn_Wq"].T), c(i["L0_xattn_Wo"].T)
    o["L0_Wk"], o["L0_Wv"] = c(i["L0_xattn_Wkv"][:P].T), c(i["L0_xattn_Wkv"][P:].T)
    for n in ("Wq", "Wk", "Wv", "Wo"):
        o["L2_" + n] = i["L2_xattn_" + n]
    o["L2_bq"], o["L2_bk"] = i["L2_xattn_bq"].reshape(P, 1), i["L2_xattn_bk"].reshape(P, 1)
    o["L2_bv"], o["L2_bo"] = i["L2_xattn_bv"].reshape(P, 1), i["L2_xattn_bo"]

    o["L0_Wg"], o["L0_bg"], o["L0_Wi"] = c(i["L0_ffn_Wg"].T), i["L0_ffn_bg"], c(i["L0_ffn_Wi"].T)
    o["L0_A"], o["L0_B"] = c(i["L0_ffn_A"].transpose(1, 0, 2)), c(i["L0_ffn_B"].transpose(2, 0, 1))
    o["L0_Wof"] = c(i["L0_ffn_Wo"].T.reshape(4, P, P).transpose(1, 0, 2))
    o["L1_Wg"], o["L1_W1"], o["L1_W3"] = i["L1_ffn_Wg"], c(i["L1_ffn_W1"].transpose(1, 0, 2)), c(i["L1_ffn_W3"].transpose(1, 0, 2))
    o["L1_W2"] = c(i["L1_ffn_W2"].reshape(8, 4, P, P).transpose(2, 0, 1, 3))
    o["L2_gw"] = c(i["L2_ffn_gate_w"].T)
    o["L2_wg"], o["L2_wu"] = [c(i["L2_ffn_" + n].transpose(1, 0, 2).reshape(P, 1024)) for n in ("w_gate", "w_up")]
    o["L2_wd"] = c(i["L2_ffn_w_down"].reshape(8, P, P).transpose(1, 0, 2))
    o["L2_sg"], o["L2_su"], o["L2_sd"] = i["L2_ffn_ws_gate"], i["L2_ffn_ws_up"], i["L2_ffn_ws_down"]

    o["L1_WqT"] = c(i["L1_xattn_Wq"].reshape(P, 16, 64).transpose(2, 1, 0))
    o["L1_WkT"] = c(i["L1_xattn_Wk"].reshape(64, 16, 64).transpose(2, 1, 0))
    o["L1_WvT"] = c(i["L1_xattn_Wv"].reshape(64, 16, 64).transpose(2, 1, 0))
    o["L1_Woh"] = c(i["L1_xattn_Wo"].reshape(16, 64, P).transpose(1, 0, 2))
    o["L1_bo"] = i["L1_xattn_bo"]
    for n in ("ln1_g", "ln1_b", "ln2_g", "ln2_b"):
        o[n] = i["L3_xattn_" + n]
    for p in ("a1", "a2"):
        s = "L3_xattn_" + p + "_"
        for n in ("wq", "wk", "wv"):
            w = i[s + n]
            o[f"{p}_{n}"] = c(w.transpose(1, 0, 2).reshape(w.shape[1], 512))
        for n in ("li1_w", "li3_w"):
            o[f"{p}_{n}"] = c(i[s + n].reshape(4, P, P).transpose(1, 0, 2))
        o[p + "_li2_w"], o[p + "_li2_b"] = i[s + "li2_w"], c(i[s + "li2_b"].reshape(4, P).T)
        for n in ("li1_b", "li3_b"):
            o[f"{p}_{n}"] = i[s + n]
        for n in ("lnx_g", "lnx_b", "lny_g", "lny_b", "ln3_g", "ln3_b"):
            o[f"{p}_{n}"] = i[s + n].reshape(-1, 1)

    for n in ("cn_w1", "cn_w2", "cn_w3", "cn_w4", "gc_w1", "gc_w2", "gc_w3"):
        o[n] = i["L3_ffn_" + n]
    for n in ("cn_b1", "cn_b2", "cn_b3", "gc_b1", "gc_b2"):
        o[n] = i["L3_ffn_" + n].reshape(-1, 1)
    for n in ("cn_b4", "gc_b3", "adaptive_range"):
        o[n] = i["L3_ffn_" + n]
    return o


STAGES = [l0_xattn, l0_ffn, l1_xattn, l1_ffn, l2_xattn, l2_ffn, l3_xattn, l3_ffn]


def kernel(**inputs):
    import concourse.bacc as bacc
    from concourse.bass_utils import run_bass_kernel_spmd

    laid = lay_out({k: np.asarray(v) for k, v in inputs.items()})
    nc = bacc.Bacc("TRN2", target_bir_lowering=False, num_devices=1)
    arrays, args = {}, {}
    for name, v in laid.items():
        v = np.ascontiguousarray(v)
        arrays[f"in_{name}"] = v
        args[name] = nc.dram_tensor(f"in_{name}", v.shape, mybir.dt.from_np(v.dtype), kind="ExternalInput").ap()
    out = nc.dram_tensor("out_x", laid["x"].shape, F32, kind="ExternalOutput").ap()
    build(nc, args, out, STAGES)
    got = run_bass_kernel_spmd(nc, [arrays], core_ids=[0]).results[0]["out_x"]
    return np.ascontiguousarray(got.transpose(1, 0, 2))
```

```python
from contextlib import ExitStack

import numpy as np
import concourse.bass as bass
from concourse import mybir

F32 = mybir.dt.float32
ALU = mybir.AluOpType
ACT = mybir.ActivationFunctionType
AX = mybir.AxisListType.X

P = 128
HEADS = 16
KEYS = 77
CTX = 64
LN_EPS = 1e-5
BANK = 512
CHUNK = 4


class It:

    def __init__(self, b, half, par):
        self.b, self.half, self.par = b, half, par


def skewed(eng, n, steps, lead):
    lead = min(lead, n)
    last = max(lag for _, lag in steps)
    assert lead % 2 == 0 and n % 2 == 0 and (n == lead or lead >= last + 2)

    def peeled(ts):
        for t in ts:
            for step, lag in steps:
                if 0 <= t - lag < n:
                    step(It(t - lag, (t - lag) // 2, (t - lag) % 2))

    peeled(range(lead))
    if n > lead:
        with eng.Fori(lead // 2, n // 2) as pair:
            for u in range(2):
                for step, lag in steps:
                    step(It(pair * 2 + (u - lag), pair + (u - lag) // 2, (u - lag) % 2))
    peeled(range(n, n + last))


def numbered(name, step, count, lag):
    return {f"{name}{c}": (lambda it, c=c: step(it, c), lag) for c in range(count)}


def in_order(steps, names):
    assert sorted(steps) == sorted(names.split())
    return [steps[name] for name in names.split()]


def nth(it, per=1, c=None, ago=0, back=0):
    value = it.b * per + ((per - 1 if c is None else c) + 1 - back - ago * per)
    return None if isinstance(value, int) and value <= 0 else value


def loads(it, per=1):
    return (it.half + 1) * (16 * per)


class Stage:

    def __init__(self, nc, name):
        self.nc, self.name, self.sems, self.ctx = nc, name, [], ExitStack()

    def __enter__(self):
        return self

    def sb(self, name, shape):
        return self.ctx.enter_context(self.nc.sbuf_tensor(f"{self.name}_{name}", list(shape), F32))

    def sb2(self, name, shape):
        return [self.sb(f"{name}{i}", shape) for i in range(2)]

    def ps(self, name):
        return self.ctx.enter_context(self.nc.psum_tensor(f"{self.name}_{name}", [P, BANK], F32))

    def sem(self, name):
        s = self.ctx.enter_context(self.nc.semaphore(f"{self.name}_{name}"))
        self.sems.append(s)
        return s

    def sem2(self, name):
        return [self.sem(f"{name}{i}") for i in range(2)]

    def __exit__(self, *exc):
        if exc[0] is None:
            with self.nc.Block() as block:
                @block.gpsimd
                def _(pool):
                    for s in self.sems:
                        pool.sem_clear(s)
        self.ctx.__exit__(*exc)
        return False


class LnFront:

    def __init__(self, st, g, ps_xT):
        self.g, self.ps_xT = g, ps_xT
        self.stats, self.mv = st.sb2("stats", [P, 6]), st.sb2("mv", [P, 2])
        self.ve, self.rstd = st.sb2("ve", [P, 1]), st.sb2("rstd", [P, 1])
        self.xn, self.xT = st.sb2("xn", [P, P]), st.sb2("xT", [P, P])
        self.s_mv, self.s_ve = st.sem("s_mv"), st.sem("s_ve")
        self.s_rstd, self.s_xn = st.sem("s_rstd"), st.sem("s_xn")
        self.s_turned, self.s_xT = st.sem("s_turned"), st.sem("s_xT")

    def statistics(self, dve, it):
        p = it.par
        if (due := nth(it, ago=2)) is not None:
            dve.wait_ge(self.s_xn, due)
        if (due := nth(it, ago=2)) is not None:
            dve.wait_ge(self.s_ve, due)
        if (due := nth(it, ago=2)) is not None:
            dve.wait_ge(self.s_mv, due)
        dve.bn_stats(self.stats[p][:, :], self.g.x[:, bass.ts(it.b, P)])
        dve.drain()
        dve.bn_aggr(self.mv[p][:, :], self.stats[p][:, :]).then_inc(self.s_mv, 1)

    def inverse_deviation(self, pool, it):
        p = it.par
        pool.wait_ge(self.s_mv, nth(it))
        if (due := nth(it, ago=2)) is not None:
            pool.wait_ge(self.s_rstd, due)
        pool.tensor_tensor(self.ve[p][:, :], self.mv[p][:, 1:2], self.g.eps[:, 0:1], ALU.add).then_inc(self.s_ve, 1)
        pool.wait_ge(self.s_ve, nth(it))
        if (due := nth(it, ago=2)) is not None:
            pool.wait_ge(self.s_xn, due)
        pool.tensor_tensor(self.rstd[p][:, :], self.ve[p][:, :], self.g.minus_half[:, 0:1],
                           ALU.pow).then_inc(self.s_rstd, 1)

    def normalize(self, dve, it):
        p = it.par
        dve.wait_ge(self.s_mv, nth(it))
        dve.wait_ge(self.s_rstd, nth(it))
        if (due := nth(it, ago=2)) is not None:
            dve.wait_ge(self.s_turned, due)
        dve.tensor_scalar(self.xn[p][:, :], self.g.x[:, bass.ts(it.b, P)], self.mv[p][:, 0:1],
                          self.rstd[p][:, 0:1], ALU.subtract, ALU.mult).then_inc(self.s_xn, 1)

    def turn(self, pe, it):
        pe.wait_ge(self.s_xn, nth(it))
        if (due := nth(it, ago=1)) is not None:
            pe.wait_ge(self.s_xT, due)
        pe.transpose(self.ps_xT, self.xn[it.par][:, :], self.g.ident[:, :]).then_inc(self.s_turned, 1)

    def fetch(self, act, it, used, per=1):
        act.wait_ge(self.s_turned, nth(it))
        if (due := nth(it, per=per, ago=2)) is not None:
            act.wait_ge(used, due)
        act.copy(self.xT[it.par][:, :], self.ps_xT).then_inc(self.s_xT, 1)


class Softmax:

    def __init__(self, st, g, banks, heads_of_bank, keys, scale, ps_turn):
        self.g, self.banks, self.keys, self.scale = g, banks, keys, scale
        self.nb, self.first = len(heads_of_bank), [0]
        for n in heads_of_bank:
            self.first.append(self.first[-1] + n)
        self.ps_turn = ps_turn
        self.mx, self.probs = st.sb2("mx", [P, HEADS]), st.sb2("probs", [P, HEADS, keys])
        self.probsT = st.sb2("probsT", [keys, CHUNK * P])
        self.nc_ = HEADS // CHUNK
        self.s_scores, self.s_max, self.s_shift, self.s_exp = (
            st.sem("s_scores"), st.sem("s_max"), st.sem("s_shift"), st.sem("s_exp"))
        self.s_turn, self.s_fetch, self.s_values = st.sem("s_turnp"), st.sem("s_fetchp"), st.sem("s_values")

    def view(self, c):
        n = self.first[c + 1] - self.first[c]
        return self.banks[c][:, 0:n * self.keys].rearrange("p (h t) -> p h t", t=self.keys)

    def maximum(self, dve, it, c):
        a, b = self.first[c], self.first[c + 1]
        dve.wait_ge(self.s_scores, nth(it, self.nb, c))
        if (due := nth(it, self.nb, ago=2)) is not None:
            dve.wait_ge(self.s_shift, due)
        dve.tensor_reduce(self.mx[it.par][:, a:b], self.view(c), AX, ALU.max).then_inc(self.s_max, 1)

    def shift(self, dve, it, c):
        a, b = self.first[c], self.first[c + 1]
        dve.wait_ge(self.s_max, nth(it, self.nb, c))
        if (due := nth(it, self.nc_, ago=2)) is not None:
            dve.wait_ge(self.s_turn, due)
        dve.tensor_tensor(self.probs[it.par][:, a:b, :], self.view(c),
                          self.mx[it.par][:, a:b].unsqueeze(2).to_broadcast([P, b - a, self.keys]),
                          ALU.subtract).then_inc(self.s_shift, 1)

    def exponential(self, act, it, c):
        a, b = self.first[c], self.first[c + 1]
        act.wait_ge(self.s_shift, nth(it, self.nb, c))
        v = self.probs[it.par][:, a:b, :]
        act.activation(v, v, ACT.Exp, scale=self.scale).then_inc(self.s_exp, 1)

    def turn(self, pe, it, c, ready=None, ready_per=None):
        bank = max(k for k in range(self.nb) if self.first[k] < CHUNK * (c + 1))
        if ready is None:
            pe.wait_ge(self.s_exp, nth(it, self.nb, bank))
        else:
            pe.wait_ge(ready, nth(it, ready_per, c))
        if (due := nth(it, self.nc_, c, back=2)) is not None:
            pe.wait_ge(self.s_fetch, due)
        for k in range(CHUNK):
            last = pe.transpose(self.ps_turn[c % 2][0:self.keys, k * P:(k + 1) * P],
                                self.probs[it.par][:, CHUNK * c + k, :], self.g.ident[:, :])
        last.then_inc(self.s_turn, 1)

    def fetch(self, act, it, c):
        act.wait_ge(self.s_turn, nth(it, self.nc_, c))
        if (due := nth(it, self.nc_, c, back=2)) is not None:
            act.wait_ge(self.s_values, due)
        act.copy(self.probsT[c % 2][:, :], self.ps_turn[c % 2][0:self.keys, :]).then_inc(self.s_fetch, 1)

    def times_values(self, pe, it, c, out_of, values_of):
        pe.wait_ge(self.s_fetch, nth(it, self.nc_, c))
        for k in range(CHUNK):
            h = CHUNK * c + k
            last = pe.matmul(out_of(h), self.probsT[c % 2][:, k * P:(k + 1) * P], values_of(h), start=True, stop=True)
        last.then_inc(self.s_values, 1)


def small_head_attention(nc, g, name, wq, wk, wv, wo, bq=None, bk=None, bv=None, bo=None, gate=0):
    D = P // HEADS
    SPLIT = [6, 6, 4]
    scale = float(D) ** -0.5
    biased = bq is not None
    with Stage(nc, name) as st:
        wq_s, wk_s, wv_s, wo_s = (st.sb("wq", [P, P]), st.sb("wk", [CTX, P]), st.sb("wv", [CTX, P]),
                                  st.sb("wo", [P, P]))
        bqkv_s, bo_s, bvo_s = st.sb("bqkv", [P, 3]), st.sb("bo", [P, P]), st.sb("bvo", [P, P])
        s_bvo, s_bias = st.sem("s_bvo"), st.sem("s_bias")
        ctxT = st.sb2("ctxT", [CTX, KEYS])
        qT, kT = st.sb2("qT", [P, P]), st.sb2("kT", [P, KEYS])
        keys = st.sb2("keys", [P, HEADS, KEYS])
        vals = st.sb2("vals", [KEYS, HEADS, D + 1])
        recip, o_s, oT = st.sb2("recip", [P, HEADS]), st.sb2("o", [P, P]), st.sb2("oT", [P, P])
        scores = [st.ps(f"scores{i}") for i in range(3)]
        turned = [st.ps(f"turned{i}") for i in range(2)]
        pa, po, py = st.ps("pa"), st.ps("po"), st.ps("py")
        q_p, k_p, v_p = pa[:, P:2 * P], pa[:, 2 * P:2 * P + KEYS], pa[0:KEYS, 3 * P:4 * P]
        o_p = po[:, 0:HEADS * (D + 1)].rearrange("p (h e) -> p h e", e=D + 1)
        oT_p, y_p = py[:, 0:P], py[:, P:2 * P]
        ln = LnFront(st, g, pa[:, 0:P])
        sm = Softmax(st, g, scores, SPLIT, KEYS, scale, turned)
        s_w, s_ctx, s_ones = st.sem("s_w"), st.sem2("s_ctx"), st.sem("s_ones")
        s_kv, s_q, s_kT, s_vals, s_qT, s_keys = [st.sem(n) for n in ("s_kv", "s_q", "s_kT", "s_vals", "s_qT", "s_keys")]
        s_recip, s_o, s_oTp, s_oT, s_y, s_x, s_bo = [
            st.sem(n) for n in ("s_recip", "s_o", "s_oTp", "s_oT", "s_y", "s_x", "s_bo")]
        weights = [(wq_s[:, :], wq), (wk_s[:, :], wk), (wv_s[:, :], wv), (wo_s[:, :], wo)]
        if biased:
            weights += [(bqkv_s[:, 0:1], bq), (bqkv_s[:, 1:2], bk), (bqkv_s[:, 2:3], bv),
                        (bo_s[:, :], bo.partition_broadcast(P))]
        all_weights = 16 * len(weights)

        with nc.Block() as block:
            @block.sync
            def _(sp):
                for dst, src in weights:
                    sp.dma_start(dst, src).then_inc(s_w, 16)

                def context(it):
                    if (due := nth(it, ago=2)) is not None:
                        sp.wait_ge(s_kv, due)
                    sp.dma_start(ctxT[it.par][:, :], g.ctxT_d[:, bass.ds(it.b, 1), :].rearrange("c b t -> c (b t)")).then_inc(s_ctx[it.par], 16)

                skewed(sp, g.B, [(context, 0)], 2)

            @block.gpsimd
            def _(pool):
                for i in range(2):
                    pool.memset(vals[i][:, :, D:D + 1], 1.0).then_inc(s_ones, 1)

                def spread(it):
                    pool.wait_ge(s_kT, nth(it))
                    if (due := nth(it, 3, ago=2)) is not None:
                        pool.wait_ge(sm.s_scores, due)
                    pool.tensor_tensor(keys[it.par][:, :, :],
                                       kT[it.par][:, :].unsqueeze(1).to_broadcast([P, HEADS, KEYS]),
                                       g.head8[:, :].unsqueeze(2).to_broadcast([P, HEADS, KEYS]),
                                       ALU.mult).then_inc(s_keys, 1)

                skewed(pool, g.B, [(lambda it: ln.inverse_deviation(pool, it), 0), (spread, 1)], 4)

            @block.tensor
            def _(pe):
                pe.wait_ge(s_w, all_weights)
                if biased:
                    pe.matmul(y_p, bqkv_s[:, 2:3].to_broadcast([P, P]), wo_s[:, :], start=True, stop=True).then_inc(s_bvo, 1)
                    pe.wait_ge(s_bias, 1)

                def keys_values(it):
                    p = it.par
                    pe.wait_ge(s_ctx[it.par], loads(it))
                    if (due := nth(it, ago=1)) is not None:
                        pe.wait_ge(s_qT, due)
                    ln.turn(pe, it)
                    pe.matmul(k_p, wk_s[:, :], ctxT[p][:, :], start=True, stop=True)
                    pe.matmul(v_p, ctxT[p][:, :], wv_s[:, :], start=True, stop=True).then_inc(s_kv, 1)

                def queries(it):
                    p = it.par
                    pe.wait_ge(ln.s_xT, nth(it))
                    pe.wait_ge(s_kT, nth(it))
                    pe.wait_ge(s_vals, nth(it))
                    pe.matmul(q_p, wq_s[:, :], ln.xT[p][:, :], start=True, stop=True).then_inc(s_q, 1)

                def score(it, c):
                    a, b = sm.first[c], sm.first[c + 1]
                    pe.wait_ge(s_qT, nth(it))
                    pe.wait_ge(s_keys, nth(it))
                    if (due := nth(it, 3, c, back=3)) is not None:
                        pe.wait_ge(sm.s_shift, due)
                    pe.matmul(scores[c][:, 0:(b - a) * KEYS], qT[it.par][:, :],
                              keys[it.par][:, a:b, :].rearrange("p h t -> p (h t)"),
                              start=True, stop=True).then_inc(sm.s_scores, 1)

                def weigh(it, c):
                    if c == 0:
                        pe.wait_ge(s_vals, nth(it))
                        if (due := nth(it, ago=1)) is not None:
                            pe.wait_ge(s_o, due)
                        pe.wait_ge(s_ones, 2)
                    sm.times_values(pe, it, c, lambda h: o_p[:, h, :], lambda h: vals[it.par][:, h, :])

                def turn_o(it):
                    pe.wait_ge(s_o, nth(it))
                    if (due := nth(it, ago=1)) is not None:
                        pe.wait_ge(s_x, due)
                    pe.transpose(oT_p, o_s[it.par][:, :], g.ident[:, :]).then_inc(s_oTp, 1)

                def output(it):
                    pe.wait_ge(s_oT, nth(it))
                    pe.matmul(y_p, oT[it.par][:, :], wo_s[:, :], start=True, stop=True).then_inc(s_y, 1)

                steps = {**numbered("turn_p", lambda it, c: sm.turn(pe, it, c), 4, 3), **numbered("score", score, 3, 2),
                         **numbered("weigh", weigh, 4, 3), "keys_values": (keys_values, 1), "queries": (queries, 1),
                         "turn_o": (turn_o, 4), "output": (output, 4)}
                skewed(pe, g.B, in_order(steps, "turn_p0 turn_p1 score0 turn_p2 weigh0 keys_values weigh1 turn_p3 score1 "
                                                "turn_o weigh2 weigh3 score2 output queries"), 6)

            @block.scalar
            def _(act):
                act.wait_ge(s_w, all_weights)

                def project(it):
                    p = it.par
                    act.wait_ge(s_kv, nth(it))
                    ln.fetch(act, it, s_q)
                    if (due := nth(it, ago=2)) is not None:
                        act.wait_ge(s_keys, due)
                    if biased:
                        act.activation(kT[p][:, :], k_p, ACT.Identity, bias=bqkv_s[:, 1:2]).then_inc(s_kT, 1)
                    else:
                        act.copy(kT[p][:, :], k_p).then_inc(s_kT, 1)

                def fetch_values(it):
                    if (due := nth(it, 4, ago=2)) is not None:
                        act.wait_ge(sm.s_values, due)
                    act.copy(vals[it.par][:, :, 0:D], v_p.rearrange("p (h d) -> p h d", d=D)).then_inc(s_vals, 1)

                def fetch_q(it):
                    p = it.par
                    act.wait_ge(s_q, nth(it))
                    if (due := nth(it, 3, ago=2)) is not None:
                        act.wait_ge(sm.s_scores, due)
                    if biased:
                        act.activation(qT[p][:, :], q_p, ACT.Identity, bias=bqkv_s[:, 0:1]).then_inc(s_qT, 1)
                    else:
                        act.copy(qT[p][:, :], q_p).then_inc(s_qT, 1)

                def fetch_o(it):
                    act.wait_ge(s_oTp, nth(it))
                    if (due := nth(it, ago=2)) is not None:
                        act.wait_ge(s_y, due)
                    act.copy(oT[it.par][:, :], oT_p).then_inc(s_oT, 1)

                steps = {**numbered("fetch_p", lambda it, c: sm.fetch(act, it, c), 4, 3),
                         **numbered("exp", lambda it, c: sm.exponential(act, it, c), 3, 2),
                         "fetch_o": (fetch_o, 4), "project": (project, 1), "fetch_values": (fetch_values, 1), "fetch_q": (fetch_q, 1)}
                skewed(act, g.B, in_order(steps, "fetch_p0 fetch_p1 fetch_p2 exp0 fetch_p3 fetch_o project fetch_values "
                                                 "exp1 fetch_q exp2"), 6)

            @block.vector
            def _(dve):
                if biased:
                    dve.wait_ge(s_w, all_weights)
                    dve.wait_ge(s_bvo, 1)
                    dve.tensor_tensor(bvo_s[:, :], y_p, bo_s[:, :], ALU.add).then_inc(s_bias, 1)

                def divide(it):
                    p = it.par
                    dve.wait_ge(sm.s_values, nth(it, 4))
                    if (due := nth(it, ago=2)) is not None:
                        dve.wait_ge(s_o, due)
                    dve.reciprocal(recip[p][:, :], o_p[:, :, D]).then_inc(s_recip, 1)
                    dve.wait_ge(s_recip, nth(it))
                    if (due := nth(it, ago=2)) is not None:
                        dve.wait_ge(s_oTp, due)
                    dve.tensor_tensor(o_s[p][:, :].rearrange("p (h d) -> p h d", d=D), o_p[:, :, 0:D],
                                      recip[p][:, :].unsqueeze(2).to_broadcast([P, HEADS, D]),
                                      ALU.mult).then_inc(s_o, 1)

                def add(it):
                    x = g.x[:, bass.ts(it.b, P)]
                    if biased:
                        dve.wait_ge(s_xnormed, nth(it))
                        dve.scalar_tensor_tensor(x, bvo_s[:, :], g.gates[:, gate:gate + 1], x, ALU.mult, ALU.add).then_inc(s_bo, 1)
                        dve.wait_ge(s_bo, nth(it))
                    dve.wait_ge(s_y, nth(it))
                    dve.wait_ge(ln.s_xn, nth(it))
                    dve.scalar_tensor_tensor(x, y_p, g.gates[:, gate:gate + 1], x, ALU.mult, ALU.add).then_inc(s_x, 1)

                s_xnormed = ln.s_xn
                steps = {**numbered("maximum", lambda it, c: sm.maximum(dve, it, c), 3, 2),
                         **numbered("shift", lambda it, c: sm.shift(dve, it, c), 3, 2),
                         "statistics": (lambda it: ln.statistics(dve, it), 0), "normalize": (lambda it: ln.normalize(dve, it), 1),
                         "divide": (divide, 4), "add": (add, 4)}
                skewed(dve, g.B, in_order(steps, "divide normalize maximum0 statistics shift0 maximum1 shift1 maximum2 shift2 add"), 6)


GROUP = 4


class GroupFront:

    def __init__(self, st, g, ps_xT):
        self.g, self.ps_xT = g, ps_xT
        self.stats, self.mv = st.sb("stats", [P, GROUP, 6]), st.sb2("mv", [P, GROUP, 2])
        self.ve, self.rstd = st.sb2("ve", [P, GROUP]), st.sb2("rstd", [P, GROUP])
        self.xn, self.xT = st.sb2("xn", [P, GROUP * P]), st.sb2("xT", [P, GROUP * P])
        self.s_mv, self.s_ve, self.s_rstd = st.sem("s_mv"), st.sem("s_ve"), st.sem("s_rstd")
        self.s_xn, self.s_turned, self.s_xT = st.sem("s_xn"), st.sem("s_turned"), st.sem("s_xT")

    def statistics(self, dve, it):
        if (due := nth(it, ago=2)) is not None:
            dve.wait_ge(self.s_xn, due)
        if (due := nth(it, ago=2)) is not None:
            dve.wait_ge(self.s_ve, due)
        for j in range(GROUP):
            dve.bn_stats(self.stats[:, j, :], self.g.x[:, bass.ts(it.b * GROUP + j, P)])
        dve.drain()
        for j in range(GROUP):
            last = dve.bn_aggr(self.mv[it.par][:, j, :], self.stats[:, j, :])
        last.then_inc(self.s_mv, 1)
        dve.drain()

    def inverse_deviation(self, pool, it):
        p = it.par
        pool.wait_ge(self.s_mv, nth(it))
        if (due := nth(it, ago=2)) is not None:
            pool.wait_ge(self.s_rstd, due)
        pool.tensor_tensor(self.ve[p][:, :], self.mv[p][:, :, 1], self.g.eps[:, :], ALU.add).then_inc(self.s_ve, 1)
        pool.wait_ge(self.s_ve, nth(it))
        if (due := nth(it, ago=2)) is not None:
            pool.wait_ge(self.s_xn, due)
        pool.tensor_tensor(self.rstd[p][:, :], self.ve[p][:, :], self.g.minus_half[:, :], ALU.pow).then_inc(self.s_rstd, 1)

    def normalize(self, dve, it, used=None):
        p = it.par
        dve.wait_ge(self.s_rstd, nth(it))
        if (due := nth(it, ago=2)) is not None:
            dve.wait_ge(self.s_turned, due)
        for j in range(GROUP):
            last = dve.tensor_scalar(self.xn[p][:, j * P:(j + 1) * P], self.g.x[:, bass.ts(it.b * GROUP + j, P)],
                                     self.mv[p][:, j, 0:1], self.rstd[p][:, j:j + 1], ALU.subtract, ALU.mult)
        last.then_inc(self.s_xn, 1)

    def turn(self, pe, it):
        pe.wait_ge(self.s_xn, nth(it))
        if (due := nth(it, ago=1)) is not None:
            pe.wait_ge(self.s_xT, due)
        for j in range(GROUP):
            last = pe.transpose(self.ps_xT[:, j * P:(j + 1) * P], self.xn[it.par][:, j * P:(j + 1) * P], self.g.ident[:, :])
        last.then_inc(self.s_turned, 1)

    def fetch(self, act, it, used, per=1):
        act.wait_ge(self.s_turned, nth(it))
        if (due := nth(it, per=per, ago=2)) is not None:
            act.wait_ge(used, due)
        act.copy(self.xT[it.par][:, :], self.ps_xT[:, :]).then_inc(self.s_xT, 1)


class Router:

    def __init__(self, st, g, experts, front, ps, wg, bias=None):
        E = self.E = experts
        self.g, self.front, self.ps, self.wg, self.bias = g, front, ps, wg, bias
        self.logits, self.act_in = st.sb("logits", [P, GROUP, E]), st.sb("act_in", [P, GROUP, E])
        self.act_out, self.sel = st.sb("act_out", [P, GROUP, E]), st.sb("sel", [P, GROUP, E])
        self.same, self.above = st.sb("same", [P, GROUP, E, E]), st.sb("above", [P, GROUP, E, E])
        self.before = st.sb("before", [P, E, E])
        self.rank, self.one = st.sb("rank", [P, GROUP, E]), st.sb("one", [P, GROUP])
        self.w = st.sb2("route", [P, GROUP, E])
        self.s_before, self.s_logits, self.s_in, self.s_less, self.s_out, self.s_w = [
            st.sem(n) for n in ("s_before", "s_logits", "s_in", "s_less", "s_out", "s_route")]

    def make_before(self, pool):
        pool.memset(self.before[:, :, :], 1.0).then_inc(self.s_before, 1)
        pool.wait_ge(self.s_before, 1)
        pool.affine_select(out=self.before[:, :, :], in_=self.before[:, :, :], compare_op=ALU.is_ge, fill=0.0,
                           base=-1, pattern=[[1, self.E], [-1, self.E]], channel_multiplier=0).then_inc(self.s_before, 1)

    def score(self, pe, it):
        pe.wait_ge(self.front.s_xT, nth(it))
        if (due := nth(it, ago=1)) is not None:
            pe.wait_ge(self.s_in, due)
        for j in range(GROUP):
            last = pe.matmul(self.ps[:, j * self.E:(j + 1) * self.E], self.front.xT[it.par][:, j * P:(j + 1) * P],
                             self.wg[:, :], start=True, stop=True)
        last.then_inc(self.s_logits, 1)

    def wide(self, v):
        return v[:, :].unsqueeze(2).to_broadcast([P, GROUP, self.E])

    def fetch(self, dve, it):
        E = self.E
        dve.wait_ge(self.s_logits, nth(it))
        if (due := nth(it, ago=1)) is not None:
            dve.wait_ge(self.s_out, due)
        src = self.ps[:, 0:GROUP * E].rearrange("p (j e) -> p j e", e=E)
        if self.bias is None:
            last = dve.tensor_copy(self.logits[:, :, :], src)
        else:
            last = dve.tensor_tensor(self.logits[:, :, :], src,
                                     self.bias[:, :].unsqueeze(1).to_broadcast([P, GROUP, E]), ALU.add)
        last.then_inc(self.s_in, 1)

    def less_maximum(self, dve, it):
        dve.drain()
        dve.tensor_reduce(self.one[:, :], self.logits[:, :, :], AX, ALU.max)
        dve.drain()
        dve.tensor_tensor(self.act_in[:, :, :], self.logits[:, :, :], self.wide(self.one), ALU.subtract).then_inc(self.s_less, 1)

    def function(self, act, it, func):
        less = func == ACT.Exp
        act.wait_ge(self.s_less if less else self.s_in, nth(it))
        if (due := nth(it, ago=1)) is not None:
            act.wait_ge(self.s_w, due)
        act.activation(self.act_out[:, :, :], (self.act_in if less else self.logits)[:, :, :], func).then_inc(self.s_out, 1)

    def reciprocal_of_sum(self, dve, v, eps=None, times=None):
        dve.tensor_reduce(self.one[:, :], v[:, :, :], AX, ALU.add)
        dve.drain()
        if eps is not None:
            dve.tensor_scalar(self.one[:, :], self.one[:, :], eps, None, ALU.add)
            dve.drain()
        dve.reciprocal(self.one[:, :], self.one[:, :])
        dve.drain()
        if times is not None:
            dve.tensor_scalar(self.one[:, :], self.one[:, :], times, None, ALU.mult)
            dve.drain()

    def compare(self, dve, v):
        E = self.E
        other = v[:, :, :].unsqueeze(2).to_broadcast([P, GROUP, E, E])
        own = v[:, :, :].unsqueeze(3).to_broadcast([P, GROUP, E, E])
        dve.tensor_tensor(self.same[:, :, :, :], other, own, ALU.is_equal)
        dve.tensor_tensor(self.above[:, :, :, :], other, own, ALU.is_gt)
        dve.drain()

    def order(self, dve):
        E = self.E
        flat = self.same[:, :, :, :].rearrange("p j a b -> p j (a b)")
        dve.tensor_tensor(flat, flat, self.before[:, :, :].rearrange("p a b -> p (a b)").unsqueeze(1).to_broadcast(
            [P, GROUP, E * E]), ALU.mult)
        dve.drain()
        dve.tensor_tensor(self.same[:, :, :, :], self.same[:, :, :, :], self.above[:, :, :, :], ALU.add)
        dve.drain()

    def select(self, dve):
        dve.tensor_reduce(self.rank[:, :, :], self.same[:, :, :, :], AX, ALU.add)
        dve.drain()
        dve.tensor_scalar(self.sel[:, :, :], self.rank[:, :, :], 1.5, None, ALU.is_lt)
        dve.drain()


def l0_ffn(nc, g, a):
    E, R, F = 4, 4, 512
    FT = F // P
    n = g.B // GROUP
    with Stage(nc, "l0f") as st:
        wg, bg, wi = st.sb("wg", [P, E]), st.sb("bg", [P, E]), st.sb("wi", [P, F])
        la, lb, wo = st.sb("la", [R, E, P]), st.sb("lb", [R, E, F]), st.sb("wo", [P, FT, P])
        we = st.sb("we", [P, E, F])
        relu = [st.sb(f"relu{e}", [P, F]) for e in range(E)]
        hs, hT = st.sb2("hs", [P, F]), st.sb2("hT", [P, F])
        ps_xT, ps_lg, ps_hT, ps_y = st.ps("xT"), st.ps("lg"), st.ps("hT"), st.ps("y")
        ps_h = [st.ps(f"h{e}") for e in range(E)]
        fr = GroupFront(st, g, ps_xT)
        rt = Router(st, g, E, fr, ps_lg, wg, bg)
        s_w, s_low, s_we = st.sem("s_w"), st.sem("s_low"), st.sem("s_we")
        s_h, s_relu, s_pair, s_hs, s_hTp, s_hT, s_y, s_x = [
            st.sem(k) for k in ("s_h", "s_relu", "s_pair", "s_hs", "s_hTp", "s_hT", "s_y", "s_x")]
        weights = [(wg[:, :], a["L0_Wg"]), (bg[:, :], a["L0_bg"].partition_broadcast(P)), (wi[:, :], a["L0_Wi"]),
                   (la[:, :, :], a["L0_A"]), (lb[:, :, :], a["L0_B"]), (wo[:, :, :], a["L0_Wof"])]

        with nc.Block() as block:
            @block.sync
            def _(sp):
                for dst, src in weights:
                    sp.dma_start(dst, src).then_inc(s_w, 16)

            @block.gpsimd
            def _(pool):
                rt.make_before(pool)
                skewed(pool, n, [(lambda it: fr.inverse_deviation(pool, it), 0)], 2)

            @block.tensor
            def _(pe):
                pe.wait_ge(s_w, 16 * len(weights))
                for e in range(E):
                    pe.matmul(ps_h[e][:, :], la[:, e, :], lb[:, e, :], start=True, stop=True).then_inc(s_low, 1)

                def hidden(it, j, e):
                    if j == 0 and e == 0:
                        pe.wait_ge(s_we, E)
                    if (due := nth(it, 4 * GROUP, 4 * j + e, back=4)) is not None:
                        pe.wait_ge(s_relu, due)
                    pe.matmul(ps_h[e][:, :], fr.xT[it.par][:, j * P:(j + 1) * P], we[:, e, :],
                              start=True, stop=True).then_inc(s_h, 1)

                def turn(it, j):
                    pe.wait_ge(s_hs, nth(it, GROUP, j))
                    if (due := nth(it, GROUP, j, back=1)) is not None:
                        pe.wait_ge(s_hT, due)
                    for t in range(FT):
                        last = pe.transpose(ps_hT[:, t * P:(t + 1) * P], hs[j % 2][:, t * P:(t + 1) * P], g.ident[:, :])
                    last.then_inc(s_hTp, 1)

                def down(it, j):
                    pe.wait_ge(s_hT, nth(it, GROUP, j))
                    if (due := nth(it, GROUP, j, back=1)) is not None:
                        pe.wait_ge(s_x, due)
                    for t in range(FT):
                        last = pe.matmul(ps_y[:, 0:P], hT[j % 2][:, t * P:(t + 1) * P], wo[:, t, :],
                                         start=(t == 0), stop=(t == FT - 1))
                    last.then_inc(s_y, 1)

                steps = []
                for j in range(GROUP):
                    j1, j2 = (j - 1) % GROUP, (j - 2) % GROUP
                    l1, l2 = 2 + (j < 1), 2 + (j < 2)
                    hid = [(lambda it, j=j, e=e: hidden(it, j, e), 2) for e in range(E)]
                    steps += [hid[0], hid[1], (lambda it, j=j1: turn(it, j), l1), hid[2], hid[3],
                              (lambda it, j=j2: down(it, j), l2)]
                    if j == 0:
                        steps.append((lambda it: fr.turn(pe, it), 1))
                    if j == 1:
                        steps.append((lambda it: rt.score(pe, it), 1))
                skewed(pe, n, steps, 6)

            @block.scalar
            def _(act):
                def relu_(it, j, e):
                    act.wait_ge(s_h, nth(it, 4 * GROUP, 4 * j + e))
                    if j == 0 and e == 0:
                        act.wait_ge(rt.s_w, nth(it))
                    if (due := nth(it, 3 * GROUP, 3 * j + 2, back=3)) is not None:
                        act.wait_ge(s_pair, due)
                    act.activation(relu[e][:, :], ps_h[e][:, :], ACT.Relu,
                                   scale=rt.w[it.par][:, j, e:e + 1]).then_inc(s_relu, 1)

                def fetch_hT(it, j):
                    act.wait_ge(s_hTp, nth(it, GROUP, j))
                    if (due := nth(it, GROUP, j, back=2)) is not None:
                        act.wait_ge(s_y, due)
                    act.copy(hT[j % 2][:, :], ps_hT[:, :]).then_inc(s_hT, 1)

                steps = []
                for j in range(GROUP):
                    j1, l1 = (j - 1) % GROUP, 2 + (j < 1)
                    rl = [(lambda it, j=j, e=e: relu_(it, j, e), 2) for e in range(E)]
                    steps += [rl[0], rl[1], (lambda it, j=j1: fetch_hT(it, j), l1), rl[2], rl[3]]
                    if j == 0:
                        steps.append((lambda it: fr.fetch(act, it, s_h, 4 * GROUP), 1))
                    if j == 2:
                        steps.append((lambda it: rt.function(act, it, ACT.Exp), 1))
                skewed(act, n, steps, 6)

            @block.vector
            def _(dve):
                dve.wait_ge(s_w, 16 * len(weights))
                for e in range(E):
                    dve.wait_ge(s_low, e + 1)
                    dve.tensor_tensor(we[:, e, :], ps_h[e][:, :], wi[:, :], ALU.add).then_inc(s_we, 1)
                dve.wait_ge(rt.s_before, 2)

                def scores(it):
                    dve.wait_ge(rt.s_out, nth(it))
                    rt.reciprocal_of_sum(dve, rt.act_out)
                    dve.tensor_tensor(rt.act_in[:, :, :], rt.act_out[:, :, :], rt.wide(rt.one), ALU.mult)
                    dve.drain()
                    rt.compare(dve, rt.act_in)

                def choose(it):
                    rt.order(dve)
                    rt.select(dve)
                    if (due := nth(it, 4 * GROUP, ago=2)) is not None:
                        dve.wait_ge(s_relu, due)
                    dve.tensor_tensor(rt.w[it.par][:, :, :], rt.act_in[:, :, :], rt.sel[:, :, :], ALU.mult).then_inc(rt.s_w, 1)

                def add(it, j):
                    x = g.x[:, bass.ts(it.b * GROUP + j, P)]
                    dve.wait_ge(s_y, nth(it, GROUP, j))
                    dve.wait_ge(fr.s_xn, nth(it))
                    dve.scalar_tensor_tensor(x, ps_y[:, 0:P], g.gates[:, 4:5], x, ALU.mult, ALU.add).then_inc(s_x, 1)

                def pair(it, j, i):
                    dve.wait_ge(s_relu, nth(it, 4 * GROUP, 4 * j + 2 * i + 1))
                    r = relu[2 * i]
                    dve.tensor_tensor(r[:, :], r[:, :], relu[2 * i + 1][:, :], ALU.add).then_inc(s_pair, 1)

                def total(it, j):
                    dve.wait_ge(s_pair, nth(it, 3 * GROUP, 3 * j + 1))
                    if (due := nth(it, GROUP, j, back=2)) is not None:
                        dve.wait_ge(s_hTp, due)
                    dve.tensor_tensor(hs[j % 2][:, :], relu[0][:, :], relu[2][:, :], ALU.add).then_inc(s_pair, 1)
                    dve.wait_ge(s_pair, nth(it, 3 * GROUP, 3 * j + 2))
                    dve.sem_inc(s_hs, 1)

                steps = [(lambda it: fr.normalize(dve, it), 1)]
                for j in range(GROUP):
                    j2, l2 = (j - 2) % GROUP, 2 + (j < 2)
                    steps += [(lambda it, j=j: pair(it, j, 0), 2), (lambda it, j=j: pair(it, j, 1), 2),
                              (lambda it, j=j: total(it, j), 2), (lambda it, j=j2: add(it, j), l2)]
                    steps += [[(lambda it: fr.statistics(dve, it), 0)],
                              [(lambda it: rt.fetch(dve, it), 1), (lambda it: rt.less_maximum(dve, it), 1)],
                              [(scores, 1)], [(choose, 1)]][j]
                skewed(dve, n, steps, 6)


def l1_ffn(nc, g, a):
    E, F = 8, 512
    FT = F // P
    T = E * FT
    n = g.B // GROUP
    with Stage(nc, "l1f") as st:
        wg, w1, w3, w2 = st.sb("wg", [P, E]), st.sb("w1", [P, E, F]), st.sb("w3", [P, E, F]), st.sb("w2", [P, E, FT, P])
        silu = st.sb2("silu", [P, GROUP * P])
        gated = [[st.sb(f"gated{i}{t}", [P, GROUP * P]) for t in range(FT)] for i in range(2)]
        acc = st.sb("acc", [P, GROUP * P])
        ps_xT, ps_lg = st.ps("xT"), st.ps("lg")
        ps_1, ps_3, ps_y = [[st.ps(f"{k}{i}") for i in range(2)] for k in ("h1", "h3", "y")]
        fr = GroupFront(st, g, ps_xT)
        rt = Router(st, g, E, fr, ps_lg, wg)
        s_g, s_w13, s_w2 = st.sem("s_g"), [st.sem(f"s_w13{e}") for e in range(E)], st.sem("s_w2")
        s_up, s_silu, s_gated, s_y, s_acc, s_x = [st.sem(k) for k in ("s_up", "s_silu", "s_gated", "s_y", "s_acc", "s_x")]

        with nc.Block() as block:
            @block.sync
            def _(sp):
                sp.dma_start(wg[:, :], a["L1_Wg"]).then_inc(s_g, 16)
                for e in range(E):
                    sp.dma_start(w1[:, e, :], a["L1_W1"][:, e, :]).then_inc(s_w13[e], 16)
                    sp.dma_start(w3[:, e, :], a["L1_W3"][:, e, :]).then_inc(s_w13[e], 16)
                sp.dma_start(w2[:, :, :, :], a["L1_W2"]).then_inc(s_w2, 16)

            @block.gpsimd
            def _(pool):
                rt.make_before(pool)
                skewed(pool, n, [(lambda it: fr.inverse_deviation(pool, it), 0)], 2)

            @block.tensor
            def _(pe):
                pe.wait_ge(s_g, 16)

                def up(it, e, t):
                    c = e * FT + t
                    if t == 0:
                        pe.wait_ge(s_w13[e], 32)
                    if (due := nth(it, T, c, back=2)) is not None:
                        pe.wait_ge(s_silu, due)
                    if (due := nth(it, T, c, back=2)) is not None:
                        pe.wait_ge(s_gated, due)
                    pe.matmul(ps_1[t % 2][:, :], w1[:, e, t * P:(t + 1) * P], fr.xT[it.par][:, :], start=True, stop=True)
                    pe.matmul(ps_3[t % 2][:, :], w3[:, e, t * P:(t + 1) * P], fr.xT[it.par][:, :],
                              start=True, stop=True).then_inc(s_up, 1)

                def down(it, e):
                    pe.wait_ge(s_gated, nth(it, T, e * FT + FT - 1))
                    if (due := nth(it, E, e, back=2)) is not None:
                        pe.wait_ge(s_acc, due)
                    pe.wait_ge(s_w2, 16)
                    for j in range(GROUP):
                        for t in range(FT):
                            last = pe.matmul(ps_y[e % 2][:, j * P:(j + 1) * P], gated[e % 2][t][:, j * P:(j + 1) * P],
                                             w2[:, e, t, :], start=(t == 0), stop=(t == FT - 1))
                    last.then_inc(s_y, 1)

                steps = []
                for e in range(E):
                    us = [(lambda it, e=e, t=t: up(it, e, t), 2) for t in range(FT)]
                    steps += us[0:2] + [(lambda it, e=(e - 1) % E: down(it, e), 2 + (e < 1))] + us[2:4]
                    if e == 1:
                        steps.append((lambda it: fr.turn(pe, it), 1))
                    if e == 3:
                        steps.append((lambda it: rt.score(pe, it), 1))
                skewed(pe, n, steps, 6)

            @block.scalar
            def _(act):
                def silu_(it, c):
                    act.wait_ge(s_up, nth(it, T, c))
                    if (due := nth(it, T, c, back=2)) is not None:
                        act.wait_ge(s_gated, due)
                    act.activation(silu[c % 2][:, :], ps_1[c % 2][:, :], ACT.Silu).then_inc(s_silu, 1)

                steps = []
                for c in range(T):
                    steps.append((lambda it, c=c: silu_(it, c), 2))
                    if c == 2 * FT + 1:
                        steps.append((lambda it: fr.fetch(act, it, s_up, T), 1))
                    if c == 5 * FT + 1:
                        steps.append((lambda it: rt.function(act, it, ACT.Exp), 1))
                skewed(act, n, steps, 6)

            @block.vector
            def _(dve):
                dve.wait_ge(rt.s_before, 2)

                def compare(it):
                    rt.less_maximum(dve, it)
                    rt.compare(dve, rt.logits)

                def choose(it):
                    rt.order(dve)
                    rt.select(dve)

                def weigh(it):
                    dve.wait_ge(rt.s_out, nth(it))
                    dve.tensor_tensor(rt.act_in[:, :, :], rt.act_out[:, :, :], rt.sel[:, :, :], ALU.mult)
                    dve.drain()
                    rt.reciprocal_of_sum(dve, rt.act_in)
                    if (due := nth(it, E, ago=2)) is not None:
                        dve.wait_ge(s_acc, due)
                    dve.tensor_tensor(rt.w[it.par][:, :, :], rt.act_in[:, :, :], rt.wide(rt.one), ALU.mult).then_inc(rt.s_w, 1)

                def gate(it, e, t):
                    c = e * FT + t
                    dve.wait_ge(s_silu, nth(it, T, c))
                    if t == 0:
                        if (due := nth(it, E, e, back=2)) is not None:
                            dve.wait_ge(s_y, due)
                    dve.tensor_tensor(gated[e % 2][t][:, :], ps_3[t % 2][:, :], silu[t % 2][:, :], ALU.mult).then_inc(s_gated, 1)

                def collect(it, e):
                    dve.wait_ge(s_y, nth(it, E, e))
                    if e > 0:
                        if (due := nth(it, E, e, back=1)) is not None:
                            dve.wait_ge(s_acc, due)
                    else:
                        if (due := nth(it, ago=1)) is not None:
                            dve.wait_ge(s_x, due)
                        dve.wait_ge(rt.s_w, nth(it))
                    for j in range(GROUP):
                        y, w, o = ps_y[e % 2][:, j * P:(j + 1) * P], rt.w[it.par][:, j, e:e + 1], acc[:, j * P:(j + 1) * P]
                        if e == 0:
                            last = dve.tensor_scalar(o, y, w, None, ALU.mult)
                        else:
                            last = dve.scalar_tensor_tensor(o, y, w, o, ALU.mult, ALU.add)
                    last.then_inc(s_acc, 1)

                def add(it):
                    x = g.x[:, bass.ts(it.b, GROUP * P)]
                    dve.wait_ge(s_acc, nth(it, E))
                    dve.wait_ge(fr.s_xn, nth(it))
                    dve.scalar_tensor_tensor(x, acc[:, :], g.gates[:, 5:6], x, ALU.mult, ALU.add).then_inc(s_x, 1)

                between = {0: [(add, 3)], 3: [(lambda it: fr.statistics(dve, it), 0)], 4: [(lambda it: rt.fetch(dve, it), 1), (compare, 1)],
                           5: [(choose, 1)], 6: [(weigh, 1)]}
                steps = [(lambda it: fr.normalize(dve, it), 1)]
                for e in range(E):
                    gs = [(lambda it, e=e, t=t: gate(it, e, t), 2) for t in range(FT)]
                    steps += gs[0:2] + [(lambda it, e=(e - 1) % E: collect(it, e), 2 + (e < 1))] + gs[2:4] + between.get(e, [])
                skewed(dve, n, steps, 6)


def l2_ffn(nc, g, a):
    E, M = 16, 64
    SCALE = 2.5
    CH = 3
    n = g.B // GROUP
    K = CH * GROUP
    with Stage(nc, "l2f") as st:
        wg = st.sb("wg", [P, E])
        gate_w, up_w, down_w = st.sb("gate", [P, E * M]), st.sb("up", [P, E * M]), st.sb("down", [P, E * M // P, P])
        sg, su, sd = st.sb("sg", [P, M]), st.sb("su", [P, M]), st.sb("sd", [M, P])
        silu, prod, hid = st.sb2("silu", [P, BANK]), st.sb2("prod", [P, BANK]), st.sb2("hid", [P, BANK])
        hT = st.sb2("hT", [P, BANK])
        ps_xT, ps_lg, ps_hT, ps_y = st.ps("xT"), st.ps("lg"), st.ps("hT"), st.ps("y")
        ps_g, ps_u = [[st.ps(f"{k}{i}") for i in range(2)] for k in "gu"]
        fr = GroupFront(st, g, ps_xT)
        rt = Router(st, g, E, fr, ps_lg, wg)
        s_w, s_pass = st.sem("s_w"), st.sem("s_pass")
        s_up, s_silu, s_prod, s_hid, s_hTp, s_hT, s_down, s_x = [
            st.sem(k) for k in ("s_up", "s_silu", "s_prod", "s_hid", "s_hTp", "s_hT", "s_down", "s_x")]
        weights = [(wg[:, :], a["L2_gw"]), (gate_w[:, :], a["L2_wg"]), (up_w[:, :], a["L2_wu"]),
                   (down_w[:, :, :], a["L2_wd"]), (sg[:, :], a["L2_sg"]), (su[:, :], a["L2_su"]), (sd[:, :], a["L2_sd"])]

        def width(c):
            return M if c == 2 else BANK

        with nc.Block() as block:
            @block.sync
            def _(sp):
                for dst, src in weights:
                    sp.dma_start(dst, src).then_inc(s_w, 16)

            @block.gpsimd
            def _(pool):
                rt.make_before(pool)

                def weigh(it, j, c):
                    k = CH * j + c
                    if k == 0:
                        pool.wait_ge(rt.s_w, nth(it))
                    pool.wait_ge(s_prod, nth(it, K, k))
                    if (due := nth(it, K, k, back=2)) is not None:
                        pool.wait_ge(s_hTp, due)
                    pool.tensor_tensor(hid[k % 2][:, :].rearrange("p (e m) -> p e m", m=M),
                                       prod[k % 2][:, :].rearrange("p (e m) -> p e m", m=M),
                                       rt.w[it.par][:, j, 8 * c:8 * c + 8].unsqueeze(2).to_broadcast([P, 8, M]),
                                       ALU.mult).then_inc(s_hid, 1)

                steps = [(lambda it, j=j, c=c: weigh(it, j, c), 2) for j in range(GROUP) for c in range(2)]
                steps.insert(3, (lambda it: fr.inverse_deviation(pool, it), 0))
                skewed(pool, n, steps, 6)

            @block.tensor
            def _(pe):
                pe.wait_ge(s_w, 16 * len(weights))

                def up(it, k):
                    j, c = k // CH, k % CH
                    x = fr.xT[it.par][:, j * P:(j + 1) * P]
                    wgt = sg[:, :] if c == 2 else gate_w[:, c * BANK:(c + 1) * BANK]
                    wup = su[:, :] if c == 2 else up_w[:, c * BANK:(c + 1) * BANK]
                    if (due := nth(it, K, k, back=2)) is not None:
                        pe.wait_ge(s_silu, due)
                    if (due := nth(it, K, k, back=2)) is not None:
                        pe.wait_ge(s_prod, due)
                    pe.matmul(ps_g[k % 2][:, 0:width(c)], x, wgt, start=True, stop=True)
                    pe.matmul(ps_u[k % 2][:, 0:width(c)], x, wup, start=True, stop=True).then_inc(s_up, 1)

                def turn(it, k):
                    j, c = k // CH, k % CH
                    if c == 2:
                        pe.wait_ge(s_prod, nth(it, K, k))
                    else:
                        pe.wait_ge(s_hid, nth(it, 2 * GROUP, 2 * j + c))
                    if (due := nth(it, K, k, back=1)) is not None:
                        pe.wait_ge(s_hT, due)
                    if c == 2:
                        pe.sem_inc(s_pass, 1)
                        last = pe.transpose(ps_hT[0:M, 0:P], prod[k % 2][:, 0:M], g.ident[:, :])
                    else:
                        for t in range(4):
                            last = pe.transpose(ps_hT[:, t * P:(t + 1) * P], hid[k % 2][:, t * P:(t + 1) * P], g.ident[:, :])
                    last.then_inc(s_hTp, 1)

                def down(it, k):
                    j, c = k // CH, k % CH
                    pe.wait_ge(s_hT, nth(it, K, k))
                    if c == 0:
                        if (due := nth(it, GROUP, j, back=1)) is not None:
                            pe.wait_ge(s_x, due)
                    if c == 2:
                        last = pe.matmul(ps_y[:, 0:P], hT[k % 2][0:M, 0:P], sd[:, :], start=False, stop=True)
                    else:
                        for t in range(4):
                            last = pe.matmul(ps_y[:, 0:P], hT[k % 2][:, t * P:(t + 1) * P], down_w[:, 4 * c + t, :],
                                             start=(c == 0 and t == 0), stop=False)
                    last.then_inc(s_down, 1)

                steps = []
                for k in range(K):
                    k2, k3 = (k - 2) % K, (k - 3) % K
                    steps += [(lambda it, k=k: up(it, k), 2), (lambda it, k=k2: turn(it, k), 2 + (k < 2)),
                              (lambda it, k=k3: down(it, k), 2 + (k < 3))]
                    if k == 1:
                        steps.append((lambda it: fr.turn(pe, it), 1))
                    if k == 3:
                        steps.append((lambda it: rt.score(pe, it), 1))
                skewed(pe, n, steps, 6)

            @block.scalar
            def _(act):
                def silu_(it, k):
                    w = width(k % CH)
                    act.wait_ge(s_up, nth(it, K, k))
                    if (due := nth(it, K, k, back=2)) is not None:
                        act.wait_ge(s_prod, due)
                    act.activation(silu[k % 2][:, 0:w], ps_g[k % 2][:, 0:w], ACT.Silu).then_inc(s_silu, 1)

                def fetch_hT(it, k):
                    act.wait_ge(s_hTp, nth(it, K, k))
                    if (due := nth(it, K, k, back=2)) is not None:
                        act.wait_ge(s_down, due)
                    if k % CH == 2:
                        act.copy(hT[k % 2][0:M, 0:P], ps_hT[0:M, 0:P]).then_inc(s_hT, 1)
                    else:
                        act.copy(hT[k % 2][:, :], ps_hT[:, :]).then_inc(s_hT, 1)

                steps = []
                for k in range(K):
                    steps += [(lambda it, k=k: silu_(it, k), 2), (lambda it, k=(k - 2) % K: fetch_hT(it, k), 2 + (k < 2))]
                    if k == 1:
                        steps.append((lambda it: fr.fetch(act, it, s_up, K), 1))
                    if k == 5:
                        steps.append((lambda it: rt.function(act, it, ACT.Sigmoid), 1))
                skewed(act, n, steps, 6)

            @block.vector
            def _(dve):
                dve.wait_ge(rt.s_before, 2)

                def compare(it):
                    dve.wait_ge(rt.s_out, nth(it))
                    rt.compare(dve, rt.act_out)

                def weigh(it):
                    dve.tensor_tensor(rt.act_in[:, :, :], rt.act_out[:, :, :], rt.sel[:, :, :], ALU.mult)
                    dve.drain()
                    rt.reciprocal_of_sum(dve, rt.act_in, eps=1e-20, times=SCALE)
                    if (due := nth(it, 2 * GROUP, ago=2)) is not None:
                        dve.wait_ge(s_hid, due)
                    dve.tensor_tensor(rt.w[it.par][:, :, :], rt.act_in[:, :, :], rt.wide(rt.one), ALU.mult).then_inc(rt.s_w, 1)

                def add(it, j):
                    x = g.x[:, bass.ts(it.b * GROUP + j, P)]
                    dve.wait_ge(fr.s_xn, nth(it))
                    dve.wait_ge(s_down, nth(it, K, CH * j + 2))
                    dve.scalar_tensor_tensor(x, ps_y[:, 0:P], g.gates[:, 6:7], x, ALU.mult, ALU.add).then_inc(s_x, 1)

                def product(it, k):
                    w = width(k % CH)
                    dve.wait_ge(s_silu, nth(it, K, k))
                    if (due := nth(it, K, k, back=2)) is not None:
                        dve.wait_ge(s_hTp, due)
                    dve.tensor_tensor(prod[k % 2][:, 0:w], ps_u[k % 2][:, 0:w], silu[k % 2][:, 0:w], ALU.mult).then_inc(s_prod, 1)

                between = {0: (lambda it: fr.normalize(dve, it), 1), 2: (lambda it: fr.statistics(dve, it), 0),
                           4: (lambda it: rt.fetch(dve, it), 1), 6: (compare, 1), 8: (lambda it: rt.order(dve), 1),
                           10: (lambda it: rt.select(dve), 1), 11: (weigh, 1)}
                steps = []
                for k in range(K):
                    if (k - 4) % CH == 2:
                        steps.append((lambda it, j=(k - 4) % K // CH: add(it, j), 2 + (k < 4)))
                    steps.append((lambda it, k=k: product(it, k), 2))
                    if k in between:
                        steps.append(between[k])
                skewed(dve, n, steps, 6)


def l1_xattn(nc, g, a):
    D = 64
    PAIRS = HEADS // 2
    SPLIT = [6, 6, 4]
    W = CTX + 1
    scale = float(D) ** -0.5
    with Stage(nc, "l1x") as st:
        wqT, wkT = st.sb("wqT", [D, HEADS, P]), st.sb("wkT", [D, HEADS, CTX])
        wvT, wo = st.sb("wvT", [D, HEADS, CTX]), st.sb("wo", [D, HEADS, P])
        qk, vo, bo = st.sb("qk", [P, HEADS * CTX]), st.sb("vo", [P, PAIRS, P]), st.sb("bo", [P, P])
        pair_ctx, ctx1 = st.sb2("pair_ctx", [P, 2 * KEYS]), st.sb2("ctx1", [KEYS, W])
        qT = st.sb2("qT", [P, PAIRS, P])
        recip, o_s, oT = st.sb2("recip", [P, HEADS]), st.sb2("o", [P, HEADS, CTX]), st.sb2("oT", [P, PAIRS, P])
        scores = [st.ps(f"scores{i}") for i in range(3)]
        turned = [st.ps(f"turned{i}") for i in range(2)]
        pa, po, py = st.ps("pa"), st.ps("po"), st.ps("py")
        o_p = po[:, 0:CHUNK * W].rearrange("p (h e) -> p h e", e=W)
        y_p = py[:, 0:P]
        ln = LnFront(st, g, pa[:, 0:P])
        sm = Softmax(st, g, scores, SPLIT, KEYS, scale, turned)
        s_w, s_ctx, s_set = st.sem("s_w"), st.sem2("s_ctx"), st.sem("s_set")
        s_pre, s_fused = st.sem("s_pre"), st.sem("s_fused")
        s_q, s_qT, s_recip, s_o, s_oTp, s_oT, s_y, s_x, s_bo = [
            st.sem(n) for n in ("s_q", "s_qT", "s_recip", "s_o", "s_oTp", "s_oT", "s_y", "s_x", "s_bo")]
        weights = [(wqT[:, :, :], a["L1_WqT"]), (wkT[:, :, :], a["L1_WkT"]), (wvT[:, :, :], a["L1_WvT"]),
                   (wo[:, :, :], a["L1_Woh"]), (bo[:, :], a["L1_bo"].partition_broadcast(P))]

        with nc.Block() as block:
            @block.sync
            def _(sp):
                for dst, src in weights:
                    sp.dma_start(dst, src).then_inc(s_w, 16)
                sp.wait_ge(s_set, 4)

                def context(it):
                    p = it.par
                    if (due := nth(it, 3, ago=2)) is not None:
                        sp.wait_ge(sm.s_scores, due)
                    if (due := nth(it, 4, ago=2)) is not None:
                        sp.wait_ge(sm.s_values, due)
                    one = g.ctxT_d[:, bass.ds(it.b, 1), :].rearrange("c b t -> c (b t)")
                    sp.dma_start(pair_ctx[p][0:CTX, 0:KEYS], one).then_inc(s_ctx[p], 16)
                    sp.dma_start(pair_ctx[p][CTX:P, KEYS:2 * KEYS], one).then_inc(s_ctx[p], 16)
                    sp.dma_start(ctx1[p][:, 0:CTX], g.ctx_d[:, bass.ds(it.b, 1), :].rearrange("t b c -> t (b c)")).then_inc(s_ctx[p], 16)

                skewed(sp, g.B, [(context, 0)], 2)

            @block.gpsimd
            def _(pool):
                for i in range(2):
                    pool.memset(pair_ctx[i][:, :], 0.0).then_inc(s_set, 1)
                    pool.memset(ctx1[i][:, CTX:W], 1.0).then_inc(s_set, 1)
                skewed(pool, g.B, [(lambda it: ln.inverse_deviation(pool, it), 0)], 4)

            @block.tensor
            def _(pe):
                pe.wait_ge(s_w, 16 * len(weights))
                banks = [scores[0], scores[1], turned[0], turned[1]]
                for h in range(HEADS):
                    last = pe.matmul(banks[h // 8][:, (h % 8) * CTX:(h % 8 + 1) * CTX], wqT[:, h, :], wkT[:, h, :],
                                     start=True, stop=True)
                    if h % 8 == 7:
                        last.then_inc(s_pre, 1)
                for h in range(HEADS):
                    r, i = CTX * (h % 2), h // 2
                    last = pe.matmul(banks[2 + i // 4][r:r + CTX, (i % 4) * P:(i % 4 + 1) * P], wvT[:, h, :], wo[:, h, :],
                                     start=True, stop=True)
                    if h % 8 == 7:
                        last.then_inc(s_pre, 1)
                pe.wait_ge(s_fused, 4)

                def turn(it):
                    if (due := nth(it, 2, ago=1)) is not None:
                        pe.wait_ge(s_qT, due)
                    ln.turn(pe, it)

                def queries(it, c):
                    if c == 0:
                        pe.wait_ge(ln.s_xT, nth(it))
                    else:
                        pe.wait_ge(s_qT, nth(it, 2, 0))
                    for k in range(4):
                        last = pe.matmul(pa[:, k * P:(k + 1) * P], qk[:, (4 * c + k) * P:(4 * c + k + 1) * P],
                                         ln.xT[it.par][:, :], start=True, stop=True)
                    last.then_inc(s_q, 1)

                def score(it, c):
                    pe.wait_ge(s_ctx[it.par], loads(it, 3))
                    pe.wait_ge(s_qT, nth(it, 2))
                    if (due := nth(it, 3, c, back=3)) is not None:
                        pe.wait_ge(sm.s_shift, due)
                    for h in range(sm.first[c], sm.first[c + 1], 2):
                        r = (h - sm.first[c]) * KEYS
                        last = pe.matmul(scores[c][:, r:r + 2 * KEYS], qT[it.par][:, h // 2, :], pair_ctx[it.par][:, :],
                                         start=True, stop=True)
                    last.then_inc(sm.s_scores, 1)

                def weigh(it, c):
                    if (due := nth(it, 4, c, back=1)) is not None:
                        pe.wait_ge(s_o, due)
                    sm.times_values(pe, it, c, lambda h: o_p[:, h % CHUNK, :], lambda h: ctx1[it.par][:, :])

                def turn_o(it, c):
                    pe.wait_ge(s_o, nth(it, 4))
                    if c == 0:
                        if (due := nth(it, ago=1)) is not None:
                            pe.wait_ge(s_x, due)
                    else:
                        pe.wait_ge(s_oT, nth(it, 2, 0))
                    for k in range(4):
                        i = 4 * c + k
                        last = pe.transpose(py[:, k * P:(k + 1) * P],
                                            o_s[it.par][:, 2 * i:2 * i + 2, :].rearrange("p h e -> p (h e)"), g.ident[:, :])
                    last.then_inc(s_oTp, 1)

                def output(it):
                    pe.wait_ge(s_oT, nth(it, 2))
                    for i in range(PAIRS):
                        last = pe.matmul(y_p, oT[it.par][:, i, :], vo[:, i, :], start=(i == 0), stop=(i == PAIRS - 1))
                    last.then_inc(s_y, 1)

                steps = {**numbered("turn_p", lambda it, c: sm.turn(pe, it, c), 4, 3), **numbered("score", score, 3, 2),
                         **numbered("weigh", weigh, 4, 3), "turn": (turn, 1), **numbered("queries", queries, 2, 1),
                         **numbered("turn_o", turn_o, 2, 4), "output": (output, 4)}
                skewed(pe, g.B, in_order(steps, "turn_p0 turn_o0 turn_p1 weigh0 turn_p2 score0 turn_p3 score1 turn score2 "
                                                "turn_o1 weigh1 queries0 weigh2 output weigh3 queries1"), 6)

            @block.scalar
            def _(act):
                for i, (bank, dst) in enumerate([(scores[0], qk[:, 0:BANK]), (scores[1], qk[:, BANK:2 * BANK]),
                                                 (turned[0], vo[:, 0:4, :].rearrange("p i d -> p (i d)")),
                                                 (turned[1], vo[:, 4:8, :].rearrange("p i d -> p (i d)"))]):
                    act.wait_ge(s_pre, i + 1)
                    act.copy(dst, bank[:, :]).then_inc(s_fused, 1)

                def fetch_q(it, c):
                    act.wait_ge(s_q, nth(it, 2, c))
                    if (due := nth(it, 3, ago=2)) is not None:
                        act.wait_ge(sm.s_scores, due)
                    act.copy(qT[it.par][:, 4 * c:4 * c + 4, :].rearrange("p i t -> p (i t)"), pa[:, :]).then_inc(s_qT, 1)

                def fetch_o(it, c):
                    act.wait_ge(s_oTp, nth(it, 2, c))
                    if (due := nth(it, ago=2)) is not None:
                        act.wait_ge(s_y, due)
                    act.copy(oT[it.par][:, 4 * c:4 * c + 4, :].rearrange("p i t -> p (i t)"), py[:, :]).then_inc(s_oT, 1)

                steps = {**numbered("fetch_p", lambda it, c: sm.fetch(act, it, c), 4, 3),
                         **numbered("exp", lambda it, c: sm.exponential(act, it, c), 3, 2),
                         **numbered("fetch_o", fetch_o, 2, 4), "fetch_x": (lambda it: ln.fetch(act, it, s_q, 2), 1),
                         **numbered("fetch_q", fetch_q, 2, 1)}
                steps["fetch_p0"] = (steps["fetch_p0"][0], 2)
                skewed(act, g.B, in_order(steps, "fetch_o0 fetch_p1 exp0 fetch_p2 fetch_x fetch_o1 fetch_p3 fetch_q0 exp1 "
                                                 "fetch_q1 exp2 fetch_p0"), 6)

            @block.vector
            def _(dve):
                dve.wait_ge(s_w, 16 * len(weights))

                def divide(it, c):
                    p = it.par
                    dve.wait_ge(sm.s_values, nth(it, 4, c))
                    if (due := nth(it, 4, c, back=8)) is not None:
                        dve.wait_ge(s_o, due)
                    dve.reciprocal(recip[p][:, 4 * c:4 * c + 4], o_p[:, :, CTX]).then_inc(s_recip, 1)
                    dve.wait_ge(s_recip, nth(it, 4, c))
                    if (due := nth(it, 2, ago=2)) is not None:
                        dve.wait_ge(s_oTp, due)
                    dve.tensor_tensor(o_s[p][:, 4 * c:4 * c + 4, :], o_p[:, :, 0:CTX],
                                      recip[p][:, 4 * c:4 * c + 4].unsqueeze(2).to_broadcast([P, CHUNK, CTX]),
                                      ALU.mult).then_inc(s_o, 1)

                def add(it):
                    x = g.x[:, bass.ts(it.b, P)]
                    dve.wait_ge(ln.s_xn, nth(it))
                    dve.scalar_tensor_tensor(x, bo[:, :], g.gates[:, 1:2], x, ALU.mult, ALU.add).then_inc(s_bo, 1)
                    dve.wait_ge(s_bo, nth(it))
                    dve.wait_ge(s_y, nth(it))
                    dve.scalar_tensor_tensor(x, y_p, g.gates[:, 1:2], x, ALU.mult, ALU.add).then_inc(s_x, 1)

                steps = {**numbered("maximum", lambda it, c: sm.maximum(dve, it, c), 3, 2),
                         **numbered("shift", lambda it, c: sm.shift(dve, it, c), 3, 2), **numbered("divide", divide, 4, 3),
                         "statistics": (lambda it: ln.statistics(dve, it), 0), "normalize": (lambda it: ln.normalize(dve, it), 1),
                         "add": (add, 4)}
                steps["divide3"] = (steps["divide3"][0], 4)
                skewed(dve, g.B, in_order(steps, "divide3 statistics normalize maximum0 shift0 divide0 divide1 maximum1 "
                                                 "divide2 shift1 maximum2 add shift2"), 6)


class Norm:

    def __init__(self, st, g, name, rows, width):
        self.g, self.rows, self.width = g, rows, width
        self.stats, self.mv = st.sb(f"{name}_st", [rows, 6]), st.sb2(f"{name}_mv", [rows, 2])
        self.ve, self.rstd = st.sb2(f"{name}_ve", [rows, 1]), st.sb2(f"{name}_rs", [rows, 1])
        self.s_mv, self.s_ve, self.s_rstd, self.s_hat, self.s_pass = [
            st.sem(f"{name}_{k}") for k in ("s_mv", "s_ve", "s_rstd", "s_hat", "s_pass")]

    def statistics(self, dve, it, src):
        if (due := nth(it, ago=2)) is not None:
            dve.wait_ge(self.s_hat, due)
        if (due := nth(it, ago=2)) is not None:
            dve.wait_ge(self.s_ve, due)
        dve.sem_inc(self.s_pass, 1)
        dve.bn_stats(self.stats[:, :], src)
        dve.drain()
        dve.bn_aggr(self.mv[it.par][:, :], self.stats[:, :]).then_inc(self.s_mv, 1)
        dve.drain()

    def inverse_deviation(self, pool, it):
        p, r = it.par, self.rows
        pool.wait_ge(self.s_mv, nth(it))
        if (due := nth(it, ago=2)) is not None:
            pool.wait_ge(self.s_rstd, due)
        pool.tensor_tensor(self.ve[p][:, :], self.mv[p][:, 1:2], self.g.eps[0:r, 0:1], ALU.add).then_inc(self.s_ve, 1)
        pool.wait_ge(self.s_ve, nth(it))
        if (due := nth(it, ago=2)) is not None:
            pool.wait_ge(self.s_hat, due)
        pool.tensor_tensor(self.rstd[p][:, :], self.ve[p][:, :], self.g.minus_half[0:r, 0:1], ALU.pow).then_inc(self.s_rstd, 1)

    def hat(self, dve, it, src, dst):
        p = it.par
        dve.wait_ge(self.s_rstd, nth(it))
        dve.tensor_scalar(dst, src, self.mv[p][:, 0:1], self.rstd[p][:, 0:1], ALU.subtract, ALU.mult).then_inc(self.s_hat, 1)


def l3_attention(nc, g, a, name, pre, first):
    D = 32
    G4 = P // D
    J = HEADS // G4
    T = P if first else KEYS
    C = P if first else CTX
    scale = float(D) ** -0.5
    with Stage(nc, name) as st:
        wq, wk, wv = st.sb("wq", [P, HEADS * D]), st.sb("wk", [C, HEADS * D]), st.sb("wv", [C, HEADS * D])
        li1, bias, col = st.sb("li1", [P, J, P]), st.sb("bias", [P, P]), st.sb("col", [P, 4])
        ln1_g, ln1_b = st.sb("ln1_g", [P, P]), st.sb("ln1_b", [P, P])
        xa, xh = st.sb2("xa", [P, P]), st.sb2("xh", [P, P])
        ctx_in, yh = st.sb2("ctx_in", [KEYS, CTX]), st.sb2("yh", [KEYS, CTX])
        xT, yT = st.sb2("xT", [P, P]), st.sb2("yT", [C, T])
        qT, kT, vals = st.sb2("qT", [P, J, P]), st.sb2("kT", [P, J, T]), st.sb2("vals", [T, HEADS * D])
        keys = st.sb2("keys", [P, J, G4, T])
        total, recip = st.sb2("total", [P, HEADS]), st.sb2("recip", [P, HEADS])
        o_s, oT = st.sb2("o", [P, HEADS * D]), st.sb2("oT", [P, J, P])
        later = st.sb("later", [P, T])
        scores = [st.ps(f"scores{i}") for i in range(4)]
        turned = [st.ps(f"turned{i}") for i in range(2)]
        pa, po = st.ps("pa"), st.ps("po")
        sm = Softmax(st, g, scores, [4] * 4, T, scale, turned)
        n3 = Norm(st, g, "n3", P, P)
        if first:
            n1, n2 = Norm(st, g, "n1", P, P), Norm(st, g, "n2", P, P)
            s_aff = st.sem("s_aff")
        else:
            ny = Norm(st, g, "ny", KEYS, CTX)
        s_w, s_ctx, s_mask, s_x1 = st.sem("s_w"), st.sem2("s_ctx"), st.sem("s_later"), st.sem("s_x1")
        s_turn, s_xT, s_q, s_qT, s_k, s_kT, s_v, s_vals, s_keys = [
            st.sem(n) for n in ("s_turn", "s_xT", "s_q", "s_qT", "s_k", "s_kT", "s_v", "s_vals", "s_keys")]
        s_sum, s_masked, s_recip, s_o, s_oTp, s_oT, s_y, s_out, s_bias = [
            st.sem(n) for n in ("s_sum", "s_masked", "s_recip", "s_o", "s_oTp", "s_oT", "s_y", "s_out", "s_bias")]
        k_ = lambda n: a[f"{pre}_{n}"]
        weights = [(wq[:, :], k_("wq")), (wk[:, :], k_("wk")), (wv[:, :], k_("wv")), (li1[:, :, :], k_("li1_w")),
                   (bias[:, :], k_("li1_b").partition_broadcast(P)), (col[:, 0:1], k_("lnx_g")), (col[:, 1:2], k_("lnx_b")),
                   (col[0:C, 2:3], k_("lny_g")), (col[0:C, 3:4], k_("lny_b"))]
        if first:
            weights += [(ln1_g[:, :], a["ln1_g"].partition_broadcast(P)), (ln1_b[:, :], a["ln1_b"].partition_broadcast(P))]
        all_weights = 16 * len(weights)

        def z(it):
            return g.z[:, bass.ts(it.b, P)]

        with nc.Block() as block:
            @block.sync
            def _(sp):
                for dst, src in weights:
                    sp.dma_start(dst, src).then_inc(s_w, 16)
                if not first:
                    def context(it):
                        if (due := nth(it, ago=2)) is not None:
                            sp.wait_ge(ny.s_hat, due)
                        sp.dma_start(ctx_in[it.par][:, :], g.ctx_d[:, bass.ds(it.b, 1), :].rearrange("t b c -> t (b c)")).then_inc(s_ctx[it.par], 16)

                    skewed(sp, g.B, [(context, 0)], 2)

            @block.gpsimd
            def _(pool):
                if first:
                    pool.memset(later[:, :], 1.0).then_inc(s_mask, 1)
                    pool.wait_ge(s_mask, 1)
                    pool.affine_select(out=later[:, :], in_=later[:, :], compare_op=ALU.is_gt, fill=0.0,
                                       base=0, pattern=[[1, T]], channel_multiplier=-1).then_inc(s_mask, 1)
                    pool.wait_ge(s_mask, 2)

                def spread(it):
                    pool.wait_ge(s_kT, nth(it))
                    if (due := nth(it, 4, ago=2)) is not None:
                        pool.wait_ge(sm.s_scores, due)
                    pool.tensor_tensor(keys[it.par][:, :, :, :],
                                       kT[it.par][:, :, :].unsqueeze(2).to_broadcast([P, J, G4, T]),
                                       g.head32[:, :].unsqueeze(1).unsqueeze(3).to_broadcast([P, J, G4, T]),
                                       ALU.mult).then_inc(s_keys, 1)

                def drop_earlier(it, c):
                    v = sm.probs[it.par][:, 4 * c:4 * c + 4, :]
                    pool.wait_ge(s_sum, nth(it, 4, c))
                    pool.tensor_tensor(v, v, later[:, :].unsqueeze(1).to_broadcast([P, 4, T]), ALU.mult).then_inc(s_masked, 1)

                steps = {"spread": (spread, 3), "deviation3": (lambda it: n3.inverse_deviation(pool, it), 2 if first else 1)}
                if first:
                    steps.update(deviation1=(lambda it: n1.inverse_deviation(pool, it), 0),
                                 deviation2=(lambda it: n2.inverse_deviation(pool, it), 1), **numbered("drop", drop_earlier, 4, 4))
                    names = "deviation3 drop0 spread deviation2 deviation1 drop1 drop2 drop3"
                else:
                    steps["deviation_y"] = (lambda it: ny.inverse_deviation(pool, it), 2)
                    names = "deviation_y spread deviation3"
                skewed(pool, g.B, in_order(steps, names), 8)

            @block.tensor
            def _(pe):
                pe.wait_ge(s_w, all_weights)

                def turn(it):
                    pe.wait_ge(n3.s_hat, nth(it))
                    if (due := nth(it, ago=1)) is not None:
                        pe.wait_ge(s_vals, due)
                    if not first:
                        pe.wait_ge(ny.s_hat, nth(it))
                    last = pe.transpose(pa[:, 0:P], xh[it.par][:, :], g.ident[:, :])
                    if not first:
                        last = pe.transpose(pa[0:CTX, P:P + KEYS], yh[it.par][:, :], g.ident[0:KEYS, 0:KEYS])
                    last.then_inc(s_turn, 1)

                def queries(it):
                    pe.wait_ge(s_xT, nth(it))
                    for j in range(J):
                        last = pe.matmul(pa[:, j * P:(j + 1) * P], wq[:, j * P:(j + 1) * P], xT[it.par][:, :], start=True, stop=True)
                    last.then_inc(s_q, 1)

                def keys_of(it):
                    pe.wait_ge(s_qT, nth(it))
                    for j in range(J):
                        last = pe.matmul(pa[:, j * T:(j + 1) * T], wk[:, j * P:(j + 1) * P], yT[it.par][:, :], start=True, stop=True)
                    last.then_inc(s_k, 1)

                def values(it):
                    pe.wait_ge(s_kT, nth(it))
                    pe.matmul(pa[0:T, :], yT[it.par][:, :], wv[:, :], start=True, stop=True).then_inc(s_v, 1)

                def score(it, c):
                    pe.wait_ge(s_keys, nth(it))
                    pe.wait_ge(s_qT, nth(it))
                    if (due := nth(it, 4, c, back=4)) is not None:
                        pe.wait_ge(sm.s_shift, due)
                    pe.matmul(scores[c][:, 0:G4 * T], qT[it.par][:, c, :], keys[it.par][:, c, :, :].rearrange("p h t -> p (h t)"),
                              start=True, stop=True).then_inc(sm.s_scores, 1)

                def turn_p(it, c):
                    sm.turn(pe, it, c, s_masked if first else None, 4)

                def weigh(it, c):
                    if c == 0:
                        pe.wait_ge(s_vals, nth(it))
                        if (due := nth(it, ago=1)) is not None:
                            pe.wait_ge(s_out, due)
                    sm.times_values(pe, it, c, lambda h: po[:, h * D:(h + 1) * D], lambda h: vals[it.par][:, h * D:(h + 1) * D])

                def turn_o(it):
                    pe.wait_ge(s_o, nth(it))
                    for j in range(J):
                        last = pe.transpose(po[:, j * P:(j + 1) * P], o_s[it.par][:, j * P:(j + 1) * P], g.ident[:, :])
                    last.then_inc(s_oTp, 1)

                def output(it):
                    pe.wait_ge(s_oT, nth(it))
                    for j in range(J):
                        last = pe.matmul(po[:, 0:P], oT[it.par][:, j, :], li1[:, j, :], start=(j == 0), stop=(j == J - 1))
                    last.then_inc(s_y, 1)

                steps = {**numbered("turn_p", turn_p, 4, 5), **numbered("score", score, 4, 4), **numbered("weigh", weigh, 4, 5),
                         "turn": (turn, 3), "queries": (queries, 3), "keys": (keys_of, 3), "values": (values, 3),
                         "turn_o": (turn_o, 6), "output": (output, 6)}
                if first:
                    names = ("turn_o score0 turn score1 output score2 queries score3 turn_p0 turn_p1 keys weigh0 turn_p2 weigh1 "
                             "turn_p3 weigh2 weigh3 values")
                else:
                    names = ("score0 turn_p0 turn_p1 turn turn_o score1 turn_p2 output queries turn_p3 weigh0 score2 weigh1 "
                             "keys score3 values weigh2 weigh3")
                skewed(pe, g.B, in_order(steps, names), 8)

            @block.scalar
            def _(act):
                act.wait_ge(s_w, all_weights)

                def fetch_x(it):
                    p = it.par
                    act.wait_ge(s_turn, nth(it))
                    if (due := nth(it, ago=2)) is not None:
                        act.wait_ge(s_q, due)
                    act.activation(xT[p][:, :], pa[:, 0:P], ACT.Identity, bias=col[:, 1:2], scale=col[:, 0:1])
                    if (due := nth(it, ago=2)) is not None:
                        act.wait_ge(s_v, due)
                    src = pa[:, 0:P] if first else pa[0:CTX, P:P + KEYS]
                    act.activation(yT[p][:, :], src, ACT.Identity, bias=col[0:C, 3:4], scale=col[0:C, 2:3]).then_inc(s_xT, 1)

                def fetch_q(it):
                    act.wait_ge(s_q, nth(it))
                    if (due := nth(it, 4, ago=2)) is not None:
                        act.wait_ge(sm.s_scores, due)
                    act.copy(qT[it.par][:, :, :].rearrange("p j t -> p (j t)"), pa[:, :]).then_inc(s_qT, 1)

                def fetch_k(it):
                    act.wait_ge(s_k, nth(it))
                    if (due := nth(it, ago=2)) is not None:
                        act.wait_ge(s_keys, due)
                    act.copy(kT[it.par][:, :, :].rearrange("p j t -> p (j t)"), pa[:, 0:J * T]).then_inc(s_kT, 1)

                def fetch_v(it):
                    act.wait_ge(s_v, nth(it))
                    if (due := nth(it, 4, ago=2)) is not None:
                        act.wait_ge(sm.s_values, due)
                    act.copy(vals[it.par][:, :], pa[0:T, :]).then_inc(s_vals, 1)

                def fetch_o(it):
                    act.wait_ge(s_oTp, nth(it))
                    if (due := nth(it, ago=2)) is not None:
                        act.wait_ge(s_y, due)
                    act.copy(oT[it.par][:, :, :].rearrange("p j t -> p (j t)"), po[:, :]).then_inc(s_oT, 1)

                steps = {**numbered("fetch_p", lambda it, c: sm.fetch(act, it, c), 4, 5),
                         **numbered("exp", lambda it, c: sm.exponential(act, it, c), 4, 4), "fetch_x": (fetch_x, 3),
                         "fetch_q": (fetch_q, 3), "fetch_k": (fetch_k, 3), "fetch_v": (fetch_v, 3), "fetch_o": (fetch_o, 6)}
                if first:
                    names = "fetch_o fetch_x exp0 fetch_q exp1 fetch_p0 fetch_p1 fetch_k exp2 fetch_p2 exp3 fetch_p3 fetch_v"
                else:
                    names = "fetch_p0 fetch_o fetch_x exp0 fetch_p1 fetch_q exp1 fetch_k fetch_p2 fetch_p3 exp2 exp3 fetch_v"
                skewed(act, g.B, in_order(steps, names), 8)

            @block.vector
            def _(dve):
                dve.wait_ge(s_w, all_weights)

                def stats1(it):
                    n1.statistics(dve, it, g.x[:, bass.ts(it.b, P)])

                def stats2(it):
                    if (due := nth(it, ago=2)) is not None:
                        dve.wait_ge(s_x1, due)
                    n1.hat(dve, it, g.x[:, bass.ts(it.b, P)], xa[it.par][:, :])
                    dve.wait_ge(n1.s_hat, nth(it))
                    n2.statistics(dve, it, xa[it.par][:, :])

                def stats3(it):
                    v = xa[it.par][:, :]
                    n2.hat(dve, it, v, v)
                    dve.wait_ge(n2.s_hat, nth(it))
                    dve.tensor_tensor(v, v, ln1_g[:, :], ALU.mult).then_inc(s_aff, 1)
                    dve.wait_ge(s_aff, nth(it))
                    dve.tensor_tensor(z(it), v, ln1_b[:, :], ALU.add).then_inc(s_x1, 1)
                    dve.wait_ge(s_x1, nth(it))
                    n3.statistics(dve, it, z(it))

                def stats_z(it):
                    n3.statistics(dve, it, z(it))
                    dve.wait_ge(s_ctx[it.par], loads(it))
                    ny.statistics(dve, it, ctx_in[it.par][:, :])

                def hat(it):
                    if (due := nth(it, ago=2)) is not None:
                        dve.wait_ge(s_turn, due)
                    n3.hat(dve, it, z(it), xh[it.par][:, :])
                    if not first:
                        ny.hat(dve, it, ctx_in[it.par][:, :], yh[it.par][:, :])

                def row_sum(it, c):
                    dve.wait_ge(sm.s_exp, nth(it, 4, c))
                    if (due := nth(it, ago=2)) is not None:
                        dve.wait_ge(s_recip, due)
                    dve.tensor_reduce(total[it.par][:, 4 * c:4 * c + 4], sm.probs[it.par][:, 4 * c:4 * c + 4, :], AX,
                                      ALU.add).then_inc(s_sum, 1)

                def divide(it):
                    p = it.par
                    dve.wait_ge(s_sum, nth(it, 4))
                    if (due := nth(it, ago=2)) is not None:
                        dve.wait_ge(s_o, due)
                    dve.reciprocal(recip[p][:, :], total[p][:, :]).then_inc(s_recip, 1)
                    dve.wait_ge(s_recip, nth(it))
                    dve.wait_ge(sm.s_values, nth(it, 4))
                    if (due := nth(it, ago=2)) is not None:
                        dve.wait_ge(s_oTp, due)
                    dve.tensor_tensor(o_s[p][:, :].rearrange("p (h d) -> p h d", d=D), po[:, :].rearrange("p (h d) -> p h d", d=D),
                                      recip[p][:, :].unsqueeze(2).to_broadcast([P, HEADS, D]), ALU.mult).then_inc(s_o, 1)

                def add(it):
                    y = g.y[:, bass.ts(it.b, P)]
                    dve.tensor_tensor(y, z(it), bias[:, :], ALU.add).then_inc(s_bias, 1)
                    dve.wait_ge(s_bias, nth(it))
                    dve.wait_ge(s_y, nth(it))
                    dve.tensor_tensor(y, po[:, 0:P], y, ALU.add).then_inc(s_out, 1)

                steps = {**numbered("maximum", lambda it, c: sm.maximum(dve, it, c), 4, 4),
                         **numbered("shift", lambda it, c: sm.shift(dve, it, c), 4, 4), **numbered("sum", row_sum, 4, 4),
                         "hat": (hat, 3), "divide": (divide, 5 if first else 6), "add": (add, 6)}
                if first:
                    steps.update(stats1=(stats1, 0), stats2=(stats2, 1), stats3=(stats3, 2))
                    names = ("hat stats1 stats3 maximum0 stats2 shift0 maximum1 add shift1 maximum2 sum0 maximum3 shift2 shift3 "
                             "sum1 sum2 sum3 divide")
                else:
                    steps["stats_z"] = (stats_z, 2)
                    names = ("hat divide maximum0 shift0 stats_z add maximum1 shift1 sum0 maximum2 shift2 maximum3 sum1 shift3 "
                             "sum2 sum3")
                skewed(dve, g.B, in_order(steps, names), 8)


def l3_mlp(nc, g, a, name, pre, first):
    F = 4 * P
    FT = F // P
    with Stage(nc, name) as st:
        li2, li3, b3 = st.sb("li2", [P, F]), st.sb("li3", [P, FT, P]), st.sb("b3", [P, P])
        b2, col = st.sb("b2", [P, FT]), st.sb("col", [P, 2])
        ln2_g, ln2_b = st.sb("ln2_g", [P, P]), st.sb("ln2_b", [P, P])
        yh, yT, hT, acc = st.sb2("yh", [P, P]), st.sb2("yT", [P, P]), st.sb2("hT", [P, F]), st.sb2("acc", [P, P])
        ps_t, ps_h, ps_y = [[st.ps(f"{k}{i}") for i in range(2)] for k in ("t", "h", "y")]
        n3 = Norm(st, g, "n3", P, P)
        if first:
            n2 = Norm(st, g, "n2", P, P)
        s_w, s_turn, s_yT, s_h, s_hT, s_y, s_a1, s_a2, s_sum, s_m, s_done = [
            st.sem(k) for k in ("s_w", "s_turn", "s_yT", "s_h", "s_hT", "s_y", "s_a1", "s_a2", "s_sum", "s_m", "s_done")]
        k_ = lambda n: a[f"{pre}_{n}"]
        weights = [(li2[:, :], k_("li2_w")), (li3[:, :, :], k_("li3_w")), (b3[:, :], k_("li3_b").partition_broadcast(P)),
                   (b2[:, :], k_("li2_b")), (col[:, 0:1], k_("ln3_g")), (col[:, 1:2], k_("ln3_b"))]
        if first:
            weights += [(ln2_g[:, :], a["ln2_g"].partition_broadcast(P)), (ln2_b[:, :], a["ln2_b"].partition_broadcast(P))]
        all_weights = 16 * len(weights)

        def y_(it):
            return g.y[:, bass.ts(it.b, P)]

        def z_(it):
            return g.z[:, bass.ts(it.b, P)]

        with nc.Block() as block:
            @block.sync
            def _(sp):
                for dst, src in weights:
                    sp.dma_start(dst, src).then_inc(s_w, 16)

            @block.gpsimd
            def _(pool):
                steps = [(lambda it: n3.inverse_deviation(pool, it), 0)]
                if first:
                    steps.append((lambda it: n2.inverse_deviation(pool, it), 4))
                skewed(pool, g.B, steps, 8)

            @block.tensor
            def _(pe):
                pe.wait_ge(s_w, all_weights)

                def turn(it):
                    pe.wait_ge(n3.s_hat, nth(it))
                    if (due := nth(it, ago=2)) is not None:
                        pe.wait_ge(s_yT, due)
                    pe.transpose(ps_t[it.par][:, 0:P], yh[it.par][:, :], g.ident[:, :]).then_inc(s_turn, 1)

                def hidden(it):
                    pe.wait_ge(s_yT, nth(it))
                    if (due := nth(it, FT, ago=2)) is not None:
                        pe.wait_ge(s_hT, due)
                    for t in range(FT):
                        last = pe.matmul(ps_h[it.par][:, t * P:(t + 1) * P], li2[:, t * P:(t + 1) * P], yT[it.par][:, :], start=True, stop=True)
                    last.then_inc(s_h, 1)

                def output(it):
                    pe.wait_ge(s_hT, nth(it, FT))
                    if (due := nth(it, ago=2)) is not None:
                        pe.wait_ge(s_sum, due)
                    for t in range(FT):
                        last = pe.matmul(ps_y[it.par][:, 0:P], hT[it.par][:, t * P:(t + 1) * P], li3[:, t, :], start=(t == 0), stop=(t == FT - 1))
                    last.then_inc(s_y, 1)

                skewed(pe, g.B, [(turn, 1), (hidden, 2), (output, 3)], 8)

            @block.scalar
            def _(act):
                act.wait_ge(s_w, all_weights)

                def fetch(it):
                    act.wait_ge(s_turn, nth(it))
                    if (due := nth(it, ago=2)) is not None:
                        act.wait_ge(s_h, due)
                    act.activation(yT[it.par][:, :], ps_t[it.par][:, 0:P], ACT.Identity, bias=col[:, 1:2], scale=col[:, 0:1]).then_inc(s_yT, 1)

                def gelu(it):
                    act.wait_ge(s_h, nth(it))
                    if (due := nth(it, ago=2)) is not None:
                        act.wait_ge(s_y, due)
                    for t in range(FT):
                        act.activation(hT[it.par][:, t * P:(t + 1) * P], ps_h[it.par][:, t * P:(t + 1) * P], ACT.Gelu,
                                       bias=b2[:, t:t + 1]).then_inc(s_hT, 1)

                skewed(act, g.B, [(fetch, 1), (gelu, 2)], 8)

            @block.vector
            def _(dve):
                dve.wait_ge(s_w, all_weights)

                def hat(it):
                    if (due := nth(it, ago=2)) is not None:
                        dve.wait_ge(s_turn, due)
                    n3.hat(dve, it, y_(it), yh[it.par][:, :])

                def sums(it):
                    c = acc[it.par][:, :]
                    if (due := nth(it, ago=2)) is not None:
                        dve.wait_ge(s_done, due)
                    dve.tensor_tensor(c, y_(it), z_(it), ALU.add).then_inc(s_a1, 1)
                    dve.wait_ge(s_a1, nth(it))
                    dve.tensor_tensor(c, c, b3[:, :], ALU.add).then_inc(s_a2, 1)
                    dve.wait_ge(s_a2, nth(it))
                    dve.wait_ge(s_y, nth(it))
                    dve.tensor_tensor(c, ps_y[it.par][:, 0:P], c, ALU.add).then_inc(s_sum, 1)
                    dve.wait_ge(s_sum, nth(it))
                    if first:
                        n2.statistics(dve, it, c)

                def finish(it):
                    c = acc[it.par][:, :]
                    if first:
                        n2.hat(dve, it, c, c)
                        dve.wait_ge(n2.s_hat, nth(it))
                        dve.tensor_tensor(c, c, ln2_g[:, :], ALU.mult).then_inc(s_m, 1)
                        dve.wait_ge(s_m, nth(it))
                        dve.tensor_tensor(z_(it), c, ln2_b[:, :], ALU.add).then_inc(s_done, 1)
                    else:
                        x = g.x[:, bass.ts(it.b, P)]
                        dve.wait_ge(s_sum, nth(it))
                        dve.scalar_tensor_tensor(x, c, g.gates[:, 3:4], x, ALU.mult, ALU.add).then_inc(s_done, 1)

                skewed(dve, g.B, [(hat, 1), (lambda it: n3.statistics(dve, it, y_(it)), 0), (finish, 5), (sums, 4)], 8)


def l3_xattn(nc, g, a):
    with nc.sbuf_tensor("l3_y", [P, g.B * P], F32) as g.y, nc.sbuf_tensor("l3_z", [P, g.B * P], F32) as g.z:
        l3_attention(nc, g, a, "l3a", "a1", True)
        l3_mlp(nc, g, a, "l3b", "a1", True)
        l3_attention(nc, g, a, "l3c", "a2", False)
        l3_mlp(nc, g, a, "l3d", "a2", False)


def l3_ffn(nc, g, a):
    CYC = 3
    Q4 = P // 4
    H2, H3 = P // 2, P // 4
    n = g.B // GROUP
    W = GROUP * P
    with Stage(nc, "l3f") as st:
        w1, w2, w3, w4 = st.sb("w1", [P, P]), st.sb("w2", [P, H2]), st.sb("w3", [H2, H3]), st.sb("w4", [H3, 1])
        v1, v2, v3 = st.sb("v1", [P, H2]), st.sb("v2", [H2, H3]), st.sb("v3", [H3, 1])
        b1, b2, b3 = st.sb("b1", [P, 1]), st.sb("b2", [H2, 1]), st.sb("b3", [H3, 1])
        c1, c2 = st.sb("c1", [H2, 1]), st.sb("c2", [H3, 1])
        rows = st.sb("rows", [P, 3])
        half, r03 = st.sb("half", [P, 2]), st.sb("r03", [P, 2])
        mean_of = st.sb("mean_of", [P, 1])
        mean, gh1, gh2 = st.sb("mean", [P, GROUP]), st.sb("gh1", [H2, GROUP]), st.sb("gh2", [H3, GROUP])
        gth = st.sb("gth", [P, GROUP])
        base = st.sb("base", [P, g.B])
        u = [None] + [st.sb2(f"u{k}_", [P, W]) for k in range(1, CYC)] + [[st.sb("u3", [P, W])] * 2]
        uT = [None] + [st.sb(f"uT{k}", [P, W]) for k in range(1, CYC)]
        h1, h2, h3 = [[st.sb(f"h{m}_{k}", [r, W]) for k in range(CYC)] for m, r in ((1, P), (2, H2), (3, H3))]
        th, cp = [st.sb(f"th{k}", [P, GROUP]) for k in range(CYC)], [st.sb(f"cp{k}", [P, GROUP]) for k in range(CYC)]
        tw = [st.sb(f"tw{k}", [P, W]) for k in range(CYC)]
        ps_xT, ps_g = st.ps("xT"), st.ps("g")
        ps_a, ps_b = [[st.ps(f"cycle_{m}{k}") for k in range(CYC)] for m in "ab"]
        fr = GroupFront(st, g, ps_xT)
        u[0] = fr.xn
        s_w, s_const, s_const2 = st.sem("s_w"), st.sem("s_const"), st.sem("s_const2")
        s_meanp, s_mean, s_g1p, s_g1, s_g2p, s_g2, s_g3p, s_gth, s_base = [
            st.sem(k) for k in ("s_meanp", "s_mean", "s_g1p", "s_g1", "s_g2p", "s_g2", "s_g3p", "s_gth", "s_base")]
        s_uTp, s_uT, s_h1p, s_h1, s_h2p, s_h2, s_h3p, s_h3, s_zp, s_th, s_cpa, s_cp, s_tw, s_u = [
            [st.sem(f"{k}_{i}") for i in range(CYC)] for k in (
                "s_uTp", "s_uT", "s_h1p", "s_h1", "s_h2p", "s_h2", "s_h3p", "s_h3", "s_zp", "s_th", "s_cpa", "s_cp", "s_tw", "s_u")]
        s_x, s_pass = st.sem("s_x"), st.sem("s_pass")
        weights = [(w1[:, :], a["cn_w1"]), (w2[:, :], a["cn_w2"]), (w3[:, :], a["cn_w3"]), (w4[:, :], a["cn_w4"]),
                   (b1[:, :], a["cn_b1"]), (b2[:, :], a["cn_b2"]), (b3[:, :], a["cn_b3"]),
                   (v1[:, :], a["gc_w1"]), (v2[:, :], a["gc_w2"]), (v3[:, :], a["gc_w3"]),
                   (c1[:, :], a["gc_b1"]), (c2[:, :], a["gc_b2"]),
                   (rows[:, 0:1], a["cn_b4"].partition_broadcast(P)), (rows[:, 1:2], a["gc_b3"].partition_broadcast(P)),
                   (rows[:, 2:3], a["adaptive_range"].partition_broadcast(P))]
        all_weights = 16 * len(weights)
        LAG = [2, 3, 4]

        with nc.Block() as block:
            @block.sync
            def _(sp):
                for dst, src in weights:
                    sp.dma_start(dst, src).then_inc(s_w, 16)

            @block.gpsimd
            def _(pool):
                pool.memset(mean_of[:, :], 1.0 / P).then_inc(s_const2, 1)
                skewed(pool, n, [(lambda it: fr.inverse_deviation(pool, it), 0)], 2)

            @block.tensor
            def _(pe):
                pe.wait_ge(s_w, all_weights)
                pe.wait_ge(s_const2, 1)

                def mean_token(it):
                    pe.wait_ge(fr.s_xn, nth(it))
                    if (due := nth(it, ago=1)) is not None:
                        pe.wait_ge(s_gth, due)
                    for j in range(GROUP):
                        last = pe.matmul(ps_g[:, j:j + 1], fr.xn[it.par][:, j * P:(j + 1) * P], mean_of[:, :], start=True, stop=True)
                    last.then_inc(s_meanp, 1)

                def global1(it):
                    pe.wait_ge(s_mean, nth(it))
                    pe.matmul(ps_g[0:H2, 0:GROUP], v1[:, :], mean[:, :], start=True, stop=True).then_inc(s_g1p, 1)

                def global2(it):
                    pe.wait_ge(s_g1, nth(it))
                    pe.sem_inc(s_pass, 1)
                    pe.matmul(ps_g[0:H3, 0:GROUP], v2[:, :], gh1[:, :], start=True, stop=True).then_inc(s_g2p, 1)

                def global3(it):
                    pe.wait_ge(s_g2, nth(it))
                    pe.matmul(ps_g[:, 0:GROUP], v3[:, :].to_broadcast([H3, P]), gh2[:, :], start=True, stop=True).then_inc(s_g3p, 1)

                def turn(it, k):
                    pe.wait_ge(s_u[k - 1], nth(it))
                    if (due := nth(it, ago=1)) is not None:
                        pe.wait_ge(s_th[k], due)
                    for j in range(GROUP):
                        last = pe.transpose(ps_a[k][:, j * P:(j + 1) * P], u[k][it.par][:, j * P:(j + 1) * P], g.ident[:, :])
                    last.then_inc(s_uTp[k], 1)

                def layer1(it, k):
                    if k == 0:
                        pe.wait_ge(fr.s_xT, nth(it))
                    else:
                        pe.wait_ge(s_uT[k], nth(it))
                    if (due := nth(it, ago=1)) is not None:
                        pe.wait_ge(s_h3[k], due)
                    src = fr.xT[it.par] if k == 0 else uT[k]
                    pe.matmul(ps_b[k][:, :], w1[:, :], src[:, :], start=True, stop=True).then_inc(s_h1p[k], 1)

                def layer2(it, k):
                    if (due := nth(it, ago=1)) is not None:
                        pe.wait_ge(s_th[k], due)
                    pe.wait_ge(s_h1[k], nth(it))
                    pe.matmul(ps_a[k][0:H2, :], w2[:, :], h1[k][:, :], start=True, stop=True).then_inc(s_h2p[k], 1)

                def layer3(it, k):
                    pe.wait_ge(s_h2[k], nth(it))
                    pe.sem_inc(s_pass, 1)
                    pe.matmul(ps_b[k][0:H3, :], w3[:, :], h2[k][:, :], start=True, stop=True).then_inc(s_h3p[k], 1)

                def layer4(it, k):
                    pe.wait_ge(s_h3[k], nth(it))
                    for j in range(GROUP):
                        last = pe.matmul(ps_a[k][:, j:j + 1], h3[k][:, j * P:(j + 1) * P], w4[:, :], start=True, stop=True)
                    last.then_inc(s_zp[k], 1)

                def of(f, k):
                    return (lambda it: f(it, k), LAG[k])

                steps = [of(turn, 2), of(turn, 1), of(layer1, 0), of(layer1, 2), of(layer1, 1), (lambda it: fr.turn(pe, it), 1)]
                steps += [(mean_token, 1), of(layer2, 0), of(layer2, 2), of(layer2, 1), (global1, 1)]
                steps += [of(layer3, 0), of(layer3, 2), of(layer3, 1), (global2, 1)]
                steps += [of(layer4, 0), of(layer4, 2), of(layer4, 1), (global3, 1)]
                skewed(pe, n, steps, 6)

            @block.scalar
            def _(act):
                act.wait_ge(s_w, all_weights)
                act.wait_ge(s_const, 1)

                def fetch(it, k):
                    act.wait_ge(s_uTp[k], nth(it))
                    if (due := nth(it, ago=1)) is not None:
                        act.wait_ge(s_h1p[k], due)
                    act.copy(uT[k][:, :], ps_a[k][:, :]).then_inc(s_uT[k], 1)

                def gelu1(it, k):
                    act.wait_ge(s_h1p[k], nth(it))
                    if (due := nth(it, ago=1)) is not None:
                        act.wait_ge(s_h2p[k], due)
                    act.activation(h1[k][:, :], ps_b[k][:, :], ACT.Gelu, bias=b1[:, 0:1]).then_inc(s_h1[k], 1)

                def gelu2(it, k):
                    act.wait_ge(s_h2p[k], nth(it))
                    if (due := nth(it, ago=1)) is not None:
                        act.wait_ge(s_h3p[k], due)
                    act.activation(h2[k][:, :], ps_a[k][0:H2, :], ACT.Gelu, bias=b2[:, 0:1]).then_inc(s_h2[k], 1)

                def gelu3(it, k):
                    act.wait_ge(s_h3p[k], nth(it))
                    if (due := nth(it, ago=1)) is not None:
                        act.wait_ge(s_zp[k], due)
                    act.activation(h3[k][:, :], ps_b[k][0:H3, :], ACT.Gelu, bias=b3[:, 0:1]).then_inc(s_h3[k], 1)

                def tanh(it, k):
                    act.wait_ge(s_zp[k], nth(it))
                    if (due := nth(it, ago=1)) is not None:
                        act.wait_ge(s_cpa[k], due)
                    act.activation(th[k][:, :], ps_a[k][:, 0:GROUP], ACT.Tanh, bias=half[:, 0:1], scale=0.5).then_inc(s_th[k], 1)

                def fetch_mean(it):
                    act.wait_ge(s_meanp, nth(it))
                    act.copy(mean[:, :], ps_g[:, 0:GROUP]).then_inc(s_mean, 1)

                def global1(it):
                    act.wait_ge(s_g1p, nth(it))
                    act.activation(gh1[:, :], ps_g[0:H2, 0:GROUP], ACT.Gelu, bias=c1[:, 0:1]).then_inc(s_g1, 1)

                def global2(it):
                    act.wait_ge(s_g2p, nth(it))
                    act.activation(gh2[:, :], ps_g[0:H3, 0:GROUP], ACT.Gelu, bias=c2[:, 0:1]).then_inc(s_g2, 1)

                def global3(it):
                    act.wait_ge(s_g3p, nth(it))
                    if (due := nth(it, ago=1)) is not None:
                        act.wait_ge(s_base, due)
                    act.activation(gth[:, :], ps_g[:, 0:GROUP], ACT.Tanh, bias=half[:, 1:2], scale=0.5).then_inc(s_gth, 1)

                def of(f, k):
                    return (lambda it: f(it, k), LAG[k])

                steps = [of(fetch, 2), of(fetch, 1), of(gelu1, 0), of(gelu1, 2), of(gelu1, 1),
                         (lambda it: fr.fetch(act, it, s_h1p[0]), 1), (fetch_mean, 1),
                         of(gelu2, 0), of(gelu2, 2), of(gelu2, 1), (global1, 1),
                         of(gelu3, 0), of(gelu3, 2), of(gelu3, 1), (global2, 1),
                         of(tanh, 0), of(tanh, 2), of(tanh, 1), (global3, 1)]
                skewed(act, n, steps, 6)

            @block.vector
            def _(dve):
                dve.wait_ge(s_w, all_weights)
                dve.tensor_scalar(half[:, :], rows[:, 0:2], 0.5, None, ALU.mult)
                dve.tensor_scalar(r03[:, 0:1], rows[:, 2:3], 0.3, None, ALU.mult)
                dve.tensor_scalar(r03[:, 1:2], rows[:, 2:3], 0.7, None, ALU.mult)
                dve.drain()
                dve.sem_inc(s_const, 1)

                def coupling_base(it):
                    dve.wait_ge(s_gth, nth(it))
                    dve.tensor_scalar(slot(it), gth[:, :], r03[:, 1:2], 0.1, ALU.mult, ALU.add).then_inc(s_base, 1)

                def slot(it):
                    return base[:, bass.ts(it.b, GROUP)]

                def couple(it, k):
                    dve.wait_ge(s_th[k], nth(it))
                    dve.wait_ge(s_base, nth(it))
                    if (due := nth(it, ago=1)) is not None:
                        dve.wait_ge(s_tw[k], due)
                    dve.scalar_tensor_tensor(cp[k][:, :], th[k][:, :], r03[:, 0:1], slot(it), ALU.mult, ALU.add).then_inc(s_cpa[k], 1)
                    dve.wait_ge(s_cpa[k], nth(it))
                    src = u[k][it.par][:, :].rearrange("p (j d) -> p j d", d=P)
                    t = tw[k][:, :].rearrange("p (j d) -> p j d", d=P)
                    if (due := nth(it, ago=1)) is not None:
                        dve.wait_ge(s_u[k], due)
                    dve.tensor_tensor(t, src, cp[k][:, :].unsqueeze(2).to_broadcast([P, GROUP, P]), ALU.mult).then_inc(s_tw[k], 1)
                    dve.wait_ge(s_tw[k], nth(it))
                    if k < CYC - 1:
                        if (due := nth(it, ago=2)) is not None:
                            dve.wait_ge(s_uTp[k + 1], due)
                        if (due := nth(it, ago=2)) is not None:
                            dve.wait_ge(s_u[k + 1], due)
                    else:
                        if (due := nth(it, ago=1)) is not None:
                            dve.wait_ge(s_x, due)
                    dst = u[k + 1][it.par][:, :].rearrange("p (j d) -> p j d", d=P)
                    for q, (other, op) in enumerate(((2, ALU.add), (3, ALU.subtract), (0, ALU.subtract), (1, ALU.add))):
                        last = dve.tensor_tensor(dst[:, :, q * Q4:(q + 1) * Q4], src[:, :, q * Q4:(q + 1) * Q4],
                                                 t[:, :, other * Q4:(other + 1) * Q4], op)
                    last.then_inc(s_u[k], 1)

                def add(it):
                    x = g.x[:, bass.ts(it.b, W)]
                    dve.wait_ge(s_u[CYC - 1], nth(it))
                    dve.scalar_tensor_tensor(x, u[CYC][0][:, :], g.gates[:, 7:8], x, ALU.mult, ALU.add).then_inc(s_x, 1)

                def normalize(it):
                    if (due := nth(it, ago=2)) is not None:
                        dve.wait_ge(s_u[0], due)
                    if (due := nth(it, ago=2)) is not None:
                        dve.wait_ge(s_meanp, due)
                    fr.normalize(dve, it)

                steps = [(lambda it: couple(it, 0), LAG[0]), (lambda it: couple(it, 2), LAG[2]), (lambda it: couple(it, 1), LAG[1]),
                         (add, LAG[2]), (coupling_base, 1)]
                skewed(dve, n, [(normalize, 1), (lambda it: fr.statistics(dve, it), 0)] + steps, 6)


class Globals:
    pass


def build(nc, a, out, stages):
    g = Globals()
    g.B = a["x"].shape[1]
    g.ctxT_d, g.ctx_d = a["ctxT"], a["ctx"]
    with ExitStack() as ctx:
        def sb(name, shape):
            return ctx.enter_context(nc.sbuf_tensor(name, shape, F32))

        g.x = sb("x_res", [P, g.B * P])
        g.ident, g.head8, g.head32 = sb("ident", [P, P]), sb("head8", [P, HEADS]), sb("head32", [P, 4])
        g.eps, g.minus_half = sb("eps", [P, 4]), sb("minus_half", [P, 4])
        g.gates, gates_in = sb("gates", [P, 8]), sb("gates_in", [P, 8])
        with Stage(nc, "init") as st:
            s_in, s_set, s_ident, s_gates, s_x = st.sem("s_in"), st.sem("s_set"), st.sem("s_ident"), st.sem("s_gates"), st.sem("s_x")
            with nc.Block() as block:
                @block.sync
                def _(sp):
                    sp.dma_start(gates_in[:, 0:4], a["g_xattn"].partition_broadcast(P)).then_inc(s_in, 16)
                    sp.dma_start(gates_in[:, 4:8], a["g_ffn"].partition_broadcast(P)).then_inc(s_in, 16)
                    sp.dma_start(g.x[:, :], a["x"].rearrange("p b d -> p (b d)")).then_inc(s_x, 16)
                    sp.wait_ge(s_x, 16)

                @block.scalar
                def _(act):
                    act.wait_ge(s_in, 32)
                    act.activation(g.gates[:, :], gates_in[:, :], ACT.Tanh).then_inc(s_gates, 1)
                    act.wait_ge(s_gates, 1)

                @block.gpsimd
                def _(pool):
                    pool.memset(g.eps[:, :], LN_EPS).then_inc(s_set, 1)
                    pool.memset(g.minus_half[:, :], -0.5).then_inc(s_set, 1)
                    pool.memset(g.ident[:, :], 0.0).then_inc(s_set, 1)
                    pool.memset(g.head8[:, :], 1.0).then_inc(s_set, 1)
                    pool.memset(g.head32[:, :], 1.0).then_inc(s_set, 1)
                    pool.wait_ge(s_set, 5)
                    pool.affine_select(out=g.ident[:, :], in_=g.ident[:, :], compare_op=ALU.not_equal, fill=1.0,
                                       base=0, pattern=[[-1, P]], channel_multiplier=1).then_inc(s_ident, 1)
                    n = 1
                    for m, w, k in ((g.head8, 8, HEADS), (g.head32, 32, 4)):
                        pool.affine_select(out=m[:, :], in_=m[:, :], compare_op=ALU.is_ge, fill=0.0,
                                           base=0, pattern=[[-w, k]], channel_multiplier=1).then_inc(s_ident, 1)
                        n += 1
                        pool.wait_ge(s_ident, n)
                        pool.affine_select(out=m[:, :], in_=m[:, :], compare_op=ALU.is_ge, fill=0.0,
                                           base=w - 1, pattern=[[w, k]], channel_multiplier=-1).then_inc(s_ident, 1)
                        n += 1
                    pool.wait_ge(s_ident, n)
        for s in stages:
            s(nc, g, a)
        with Stage(nc, "store") as st:
            s_out = st.sem("s_out")
            with nc.Block() as block:
                @block.sync
                def _(sp):
                    sp.dma_start(out.rearrange("p b d -> p (b d)"), g.x[:, :]).then_inc(s_out, 16)
                    sp.wait_ge(s_out, 16)


def l0_xattn(nc, g, a):
    small_head_attention(nc, g, "l0x", a["L0_Wq"], a["L0_Wk"], a["L0_Wv"], a["L0_Wo"], gate=0)


def l2_xattn(nc, g, a):
    small_head_attention(nc, g, "l2x", a["L2_Wq"], a["L2_Wk"], a["L2_Wv"], a["L2_Wo"],
                         a["L2_bq"], a["L2_bk"], a["L2_bv"], a["L2_bo"], gate=2)


def lay_out(i):
    c = np.ascontiguousarray
    o = {"x": c(i["x"].transpose(1, 0, 2)), "ctx": c(i["ctx_512"].transpose(1, 0, 2)),
         "ctxT": c(i["ctx_512"].transpose(2, 0, 1)), "g_xattn": i["g_xattn"], "g_ffn": i["g_ffn"]}
    o["L0_Wq"], o["L0_Wo"] = c(i["L0_xattn_Wq"].T), c(i["L0_xattn_Wo"].T)
    o["L0_Wk"], o["L0_Wv"] = c(i["L0_xattn_Wkv"][:P].T), c(i["L0_xattn_Wkv"][P:].T)
    for n in ("Wq", "Wk", "Wv", "Wo"):
        o["L2_" + n] = i["L2_xattn_" + n]
    o["L2_bq"], o["L2_bk"] = i["L2_xattn_bq"].reshape(P, 1), i["L2_xattn_bk"].reshape(P, 1)
    o["L2_bv"], o["L2_bo"] = i["L2_xattn_bv"].reshape(P, 1), i["L2_xattn_bo"]

    o["L0_Wg"], o["L0_bg"], o["L0_Wi"] = c(i["L0_ffn_Wg"].T), i["L0_ffn_bg"], c(i["L0_ffn_Wi"].T)
    o["L0_A"], o["L0_B"] = c(i["L0_ffn_A"].transpose(1, 0, 2)), c(i["L0_ffn_B"].transpose(2, 0, 1))
    o["L0_Wof"] = c(i["L0_ffn_Wo"].T.reshape(4, P, P).transpose(1, 0, 2))
    o["L1_Wg"], o["L1_W1"], o["L1_W3"] = i["L1_ffn_Wg"], c(i["L1_ffn_W1"].transpose(1, 0, 2)), c(i["L1_ffn_W3"].transpose(1, 0, 2))
    o["L1_W2"] = c(i["L1_ffn_W2"].reshape(8, 4, P, P).transpose(2, 0, 1, 3))
    o["L2_gw"] = c(i["L2_ffn_gate_w"].T)
    o["L2_wg"], o["L2_wu"] = [c(i["L2_ffn_" + n].transpose(1, 0, 2).reshape(P, 1024)) for n in ("w_gate", "w_up")]
    o["L2_wd"] = c(i["L2_ffn_w_down"].reshape(8, P, P).transpose(1, 0, 2))
    o["L2_sg"], o["L2_su"], o["L2_sd"] = i["L2_ffn_ws_gate"], i["L2_ffn_ws_up"], i["L2_ffn_ws_down"]

    o["L1_WqT"] = c(i["L1_xattn_Wq"].reshape(P, 16, 64).transpose(2, 1, 0))
    o["L1_WkT"] = c(i["L1_xattn_Wk"].reshape(64, 16, 64).transpose(2, 1, 0))
    o["L1_WvT"] = c(i["L1_xattn_Wv"].reshape(64, 16, 64).transpose(2, 1, 0))
    o["L1_Woh"] = c(i["L1_xattn_Wo"].reshape(16, 64, P).transpose(1, 0, 2))
    o["L1_bo"] = i["L1_xattn_bo"]
    for n in ("ln1_g", "ln1_b", "ln2_g", "ln2_b"):
        o[n] = i["L3_xattn_" + n]
    for p in ("a1", "a2"):
        s = "L3_xattn_" + p + "_"
        for n in ("wq", "wk", "wv"):
            w = i[s + n]
            o[f"{p}_{n}"] = c(w.transpose(1, 0, 2).reshape(w.shape[1], 512))
        for n in ("li1_w", "li3_w"):
            o[f"{p}_{n}"] = c(i[s + n].reshape(4, P, P).transpose(1, 0, 2))
        o[p + "_li2_w"], o[p + "_li2_b"] = i[s + "li2_w"], c(i[s + "li2_b"].reshape(4, P).T)
        for n in ("li1_b", "li3_b"):
            o[f"{p}_{n}"] = i[s + n]
        for n in ("lnx_g", "lnx_b", "lny_g", "lny_b", "ln3_g", "ln3_b"):
            o[f"{p}_{n}"] = i[s + n].reshape(-1, 1)

    for n in ("cn_w1", "cn_w2", "cn_w3", "cn_w4", "gc_w1", "gc_w2", "gc_w3"):
        o[n] = i["L3_ffn_" + n]
    for n in ("cn_b1", "cn_b2", "cn_b3", "gc_b1", "gc_b2"):
        o[n] = i["L3_ffn_" + n].reshape(-1, 1)
    for n in ("cn_b4", "gc_b3", "adaptive_range"):
        o[n] = i["L3_ffn_" + n]
    return o


STAGES = [l0_xattn, l0_ffn, l1_xattn, l1_ffn, l2_xattn, l2_ffn, l3_xattn, l3_ffn]


def kernel(**inputs):
    import concourse.bacc as bacc
    from concourse.bass_utils import run_bass_kernel_spmd

    laid = lay_out({k: np.asarray(v) for k, v in inputs.items()})
    nc = bacc.Bacc("TRN2", target_bir_lowering=False, num_devices=1)
    arrays, args = {}, {}
    for name, v in laid.items():
        v = np.ascontiguousarray(v)
        arrays[f"in_{name}"] = v
        args[name] = nc.dram_tensor(f"in_{name}", v.shape, mybir.dt.from_np(v.dtype), kind="ExternalInput").ap()
    out = nc.dram_tensor("out_x", laid["x"].shape, F32, kind="ExternalOutput").ap()
    build(nc, args, out, STAGES)
    got = run_bass_kernel_spmd(nc, [arrays], core_ids=[0]).results[0]["out_x"]
    return np.ascontiguousarray(got.transpose(1, 0, 2))
```

```python
from contextlib import ExitStack

import numpy as np
import concourse.bass as bass
from concourse import mybir

F32 = mybir.dt.float32
F16 = mybir.dt.float16
ALU = mybir.AluOpType
ACT = mybir.ActivationFunctionType
AX = mybir.AxisListType.X

P = 128
HEADS = 16
KEYS = 77
CTX = 64
LN_EPS = 1e-5
BANK = 512
SPLIT = 64.0
SPLIT_EXP = 1024.0
AHEAD = 4
CHUNK = 4


class It:

    def __init__(self, b, half, par):
        self.b, self.half, self.par = b, half, par


def skewed(eng, n, steps, lead):
    lead = min(lead, n)
    last = max(lag for _, lag in steps)
    assert lead % 2 == 0 and n % 2 == 0 and (n == lead or lead >= last + 2)

    def peeled(ts):
        for t in ts:
            for step, lag in steps:
                if 0 <= t - lag < n:
                    step(It(t - lag, (t - lag) // 2, (t - lag) % 2))

    peeled(range(lead))
    if n > lead:
        with eng.Fori(lead // 2, n // 2) as pair:
            for u in range(2):
                for step, lag in steps:
                    step(It(pair * 2 + (u - lag), pair + (u - lag) // 2, (u - lag) % 2))
    peeled(range(n, n + last))


def first_of(it):
    return isinstance(it.b, int) and it.b == 0


def numbered(name, step, count, lag):
    return {f"{name}{c}": (lambda it, c=c: step(it, c), lag) for c in range(count)}


def later(steps, names):
    for name in names.split():
        steps[name] = (steps[name][0], steps[name][1] + 1)


def in_order(steps, names):
    assert sorted(steps) == sorted(names.split())
    return [steps[name] for name in names.split()]


def nth(it, per=1, c=None, ago=0, back=0):
    value = it.b * per + ((per - 1 if c is None else c) + 1 - back - ago * per)
    return None if isinstance(value, int) and value <= 0 else value


def loads(it, per=1):
    return (it.half + 1) * (16 * per)


class Stage:

    def __init__(self, nc, name):
        self.nc, self.name, self.sems, self.ctx = nc, name, [], ExitStack()

    def __enter__(self):
        return self

    def sb(self, name, shape, dtype=F32):
        return self.ctx.enter_context(self.nc.sbuf_tensor(f"{self.name}_{name}", list(shape), dtype))

    def sb2(self, name, shape, dtype=F32):
        return [self.sb(f"{name}{i}", shape, dtype) for i in range(2)]

    def ps(self, name):
        return self.ctx.enter_context(self.nc.psum_tensor(f"{self.name}_{name}", [P, BANK], F32))

    def sem(self, name):
        s = self.ctx.enter_context(self.nc.semaphore(f"{self.name}_{name}"))
        self.sems.append(s)
        return s

    def sem2(self, name):
        return [self.sem(f"{name}{i}") for i in range(2)]

    def __exit__(self, *exc):
        if exc[0] is None:
            with self.nc.Block() as block:
                @block.gpsimd
                def _(pool):
                    for s in self.sems:
                        pool.sem_clear(s)
        self.ctx.__exit__(*exc)
        return False


class LnFront:

    def __init__(self, st, g, ps_xT):
        self.g, self.ps_xT = g, ps_xT
        self.stats, self.mv = st.sb2("stats", [P, 6]), st.sb2("mv", [P, 2])
        self.ve, self.rstd = st.sb2("ve", [P, 1]), st.sb2("rstd", [P, 1])
        self.xn, self.xT = st.sb2("xn", [P, P]), st.sb2("xT", [P, P])
        self.s_mv, self.s_ve = st.sem("s_mv"), st.sem("s_ve")
        self.s_rstd, self.s_xn = st.sem("s_rstd"), st.sem("s_xn")
        self.s_turned, self.s_xT = st.sem("s_turned"), st.sem("s_xT")

    def statistics(self, dve, it):
        p = it.par
        if (due := nth(it, ago=2)) is not None:
            dve.wait_ge(self.s_xn, due)
        if (due := nth(it, ago=2)) is not None:
            dve.wait_ge(self.s_ve, due)
        if (due := nth(it, ago=2)) is not None:
            dve.wait_ge(self.s_mv, due)
        dve.bn_stats(self.stats[p][:, :], self.g.x[:, bass.ts(it.b, P)])
        dve.drain()
        dve.bn_aggr(self.mv[p][:, :], self.stats[p][:, :]).then_inc(self.s_mv, 1)

    def inverse_deviation(self, pool, it):
        p = it.par
        pool.wait_ge(self.s_mv, nth(it))
        if (due := nth(it, ago=2)) is not None:
            pool.wait_ge(self.s_rstd, due)
        pool.tensor_tensor(self.ve[p][:, :], self.mv[p][:, 1:2], self.g.eps[:, 0:1], ALU.add).then_inc(self.s_ve, 1)
        pool.wait_ge(self.s_ve, nth(it))
        if (due := nth(it, ago=2)) is not None:
            pool.wait_ge(self.s_xn, due)
        pool.tensor_tensor(self.rstd[p][:, :], self.ve[p][:, :], self.g.minus_half[:, 0:1],
                           ALU.pow).then_inc(self.s_rstd, 1)

    def normalize(self, dve, it):
        p = it.par
        dve.wait_ge(self.s_mv, nth(it))
        dve.wait_ge(self.s_rstd, nth(it))
        if (due := nth(it, ago=2)) is not None:
            dve.wait_ge(self.s_turned, due)
        dve.tensor_scalar(self.xn[p][:, :], self.g.x[:, bass.ts(it.b, P)], self.mv[p][:, 0:1],
                          self.rstd[p][:, 0:1], ALU.subtract, ALU.mult).then_inc(self.s_xn, 1)

    def turn(self, pe, it):
        pe.wait_ge(self.s_xn, nth(it))
        if (due := nth(it, ago=1)) is not None:
            pe.wait_ge(self.s_xT, due)
        pe.transpose(self.ps_xT, self.xn[it.par][:, :], self.g.ident[:, :]).then_inc(self.s_turned, 1)

    def fetch(self, act, it, used, per=1):
        act.wait_ge(self.s_turned, nth(it))
        if (due := nth(it, per=per, ago=2)) is not None:
            act.wait_ge(used, due)
        act.copy(self.xT[it.par][:, :], self.ps_xT).then_inc(self.s_xT, 1)


class Softmax:

    def __init__(self, st, g, banks, heads_of_bank, keys, scale, ps_turn, split=False):
        self.g, self.banks, self.keys, self.scale = g, banks, keys, scale
        self.nb, self.first = len(heads_of_bank), [0]
        for n in heads_of_bank:
            self.first.append(self.first[-1] + n)
        self.ps_turn = ps_turn
        self.mx, self.probs = st.sb2("mx", [P, HEADS]), st.sb2("probs", [P, HEADS, keys])
        self.split = split
        if split:
            self.hiT, self.loT = st.sb2("hiT", [keys, CHUNK * P], F16), st.sb2("loT", [keys, CHUNK * P], F16)
            self.s_rest = st.sem("s_rest")
        else:
            self.probsT = st.sb2("probsT", [keys, CHUNK * P])
        self.nc_ = HEADS // CHUNK
        self.s_scores, self.s_max, self.s_shift, self.s_exp = (
            st.sem("s_scores"), st.sem("s_max"), st.sem("s_shift"), st.sem("s_exp"))
        self.s_turn, self.s_fetch, self.s_values = st.sem("s_turnp"), st.sem("s_fetchp"), st.sem("s_values")

    def view(self, c):
        n = self.first[c + 1] - self.first[c]
        return self.banks[c][:, 0:n * self.keys].rearrange("p (h t) -> p h t", t=self.keys)

    def maximum(self, dve, it, c):
        a, b = self.first[c], self.first[c + 1]
        dve.wait_ge(self.s_scores, nth(it, self.nb, c))
        if (due := nth(it, self.nb, ago=2)) is not None:
            dve.wait_ge(self.s_shift, due)
        dve.tensor_reduce(self.mx[it.par][:, a:b], self.view(c), AX, ALU.max).then_inc(self.s_max, 1)

    def shift(self, dve, it, c):
        a, b = self.first[c], self.first[c + 1]
        dve.wait_ge(self.s_max, nth(it, self.nb, c))
        if (due := nth(it, self.nc_, ago=2)) is not None:
            dve.wait_ge(self.s_turn, due)
        dve.tensor_tensor(self.probs[it.par][:, a:b, :], self.view(c),
                          self.mx[it.par][:, a:b].unsqueeze(2).to_broadcast([P, b - a, self.keys]),
                          ALU.subtract).then_inc(self.s_shift, 1)

    def exponential(self, act, it, c):
        a, b = self.first[c], self.first[c + 1]
        act.wait_ge(self.s_shift, nth(it, self.nb, c))
        v = self.probs[it.par][:, a:b, :]
        act.activation(v, v, ACT.Exp, scale=self.scale).then_inc(self.s_exp, 1)

    def turn(self, pe, it, c, ready=None, ready_per=None):
        bank = max(k for k in range(self.nb) if self.first[k] < CHUNK * (c + 1))
        if ready is None:
            pe.wait_ge(self.s_exp, nth(it, self.nb, bank))
        else:
            pe.wait_ge(ready, nth(it, ready_per, c))
        if (due := nth(it, self.nc_, c, back=2)) is not None:
            pe.wait_ge(self.s_rest if self.split else self.s_fetch, due)
        for k in range(CHUNK):
            last = pe.transpose(self.ps_turn[c % 2][0:self.keys, k * P:(k + 1) * P],
                                self.probs[it.par][:, CHUNK * c + k, :], self.g.ident[:, :])
        last.then_inc(self.s_turn, 1)

    def fetch(self, act, it, c):
        act.wait_ge(self.s_turn, nth(it, self.nc_, c))
        if (due := nth(it, self.nc_, c, back=2)) is not None:
            act.wait_ge(self.s_values, due)
        src = self.ps_turn[c % 2][0:self.keys, :]
        if self.split:
            act.activation(self.hiT[c % 2][:, :], src, ACT.Copy, scale=SPLIT_EXP).then_inc(self.s_fetch, 1)
        else:
            act.copy(self.probsT[c % 2][:, :], src).then_inc(self.s_fetch, 1)

    def remainder(self, dve, it, c):
        dve.wait_ge(self.s_fetch, nth(it, self.nc_, c))
        dve.scalar_tensor_tensor(self.loT[c % 2][:, :], self.ps_turn[c % 2][0:self.keys, :], SPLIT_EXP,
                                 self.hiT[c % 2][:, :], ALU.mult, ALU.subtract).then_inc(self.s_rest, 1)

    def times_values(self, pe, it, c, out_of, values_of):
        pe.wait_ge(self.s_rest if self.split else self.s_fetch, nth(it, self.nc_, c))
        for k in range(CHUNK):
            h, cols = CHUNK * c + k, slice(k * P, (k + 1) * P)
            if self.split:
                vhi, vlo = values_of(h)
                products = ((self.hiT, vhi), (self.hiT, vlo), (self.loT, vhi))
            else:
                products = ((self.probsT, values_of(h)),)
            for i, (p, v) in enumerate(products):
                last = pe.matmul(out_of(h), p[c % 2][:, cols], v, start=(i == 0), stop=(i == len(products) - 1))
        last.then_inc(self.s_values, 1)


def small_head_attention(nc, g, name, wq, wk, wv, wo, bq=None, bk=None, bv=None, bo=None, gate=0):
    D = P // HEADS
    HELD = [6, 6, 4]
    scale = float(D) ** -0.5
    biased = bq is not None
    with Stage(nc, name) as st:
        wq_s, wk_s, wv_s, wo_s = (st.sb("wq", [P, P]), st.sb("wk", [CTX, P]), st.sb("wv", [CTX, P]),
                                  st.sb("wo", [P, P]))
        bqkv_s, bo_s, bvo_s = st.sb("bqkv", [P, 3]), st.sb("bo", [P, P]), st.sb("bvo", [P, P])
        s_bvo, s_bias = st.sem("s_bvo"), st.sem("s_bias")
        ctxT = st.sb2("ctxT", [CTX, KEYS])
        qT, kT = st.sb2("qT", [P, P]), st.sb2("kT", [P, KEYS])
        keys = st.sb2("keys", [P, HEADS, KEYS])
        vhi, vlo = st.sb2("vhi", [KEYS, HEADS, D + 1], F16), st.sb2("vlo", [KEYS, HEADS, D + 1], F16)
        recip, o_s, oT = st.sb2("recip", [P, HEADS]), st.sb2("o", [P, P]), st.sb2("oT", [P, P])
        scores = [st.ps(f"scores{i}") for i in range(3)]
        turned = [st.ps(f"turned{i}") for i in range(2)]
        pa, po, py = st.ps("pa"), st.ps("po"), st.ps("py")
        q_p, k_p, v_p = pa[:, P:2 * P], pa[:, 2 * P:2 * P + KEYS], pa[0:KEYS, 3 * P:4 * P]
        v_heads = v_p.rearrange("p (h d) -> p h d", d=D)
        o_p = po[:, 0:HEADS * (D + 1)].rearrange("p (h e) -> p h e", e=D + 1)
        oT_p, y_p = py[:, 0:P], py[:, P:2 * P]
        ln = LnFront(st, g, pa[:, 0:P])
        sm = Softmax(st, g, scores, HELD, KEYS, scale, turned, split=True)
        s_w, s_ctx, s_ones = st.sem("s_w"), st.sem2("s_ctx"), st.sem("s_ones")
        s_kv, s_q, s_kT, s_vhi, s_vlo, s_qT, s_keys = [st.sem(n) for n in ("s_kv", "s_q", "s_kT", "s_vhi", "s_vlo", "s_qT", "s_keys")]
        s_recip, s_o, s_oTp, s_oT, s_y, s_x, s_bo = [
            st.sem(n) for n in ("s_recip", "s_o", "s_oTp", "s_oT", "s_y", "s_x", "s_bo")]
        weights = [(wq_s[:, :], wq), (wk_s[:, :], wk), (wv_s[:, :], wv), (wo_s[:, :], wo)]
        if biased:
            weights += [(bqkv_s[:, 0:1], bq), (bqkv_s[:, 1:2], bk), (bqkv_s[:, 2:3], bv),
                        (bo_s[:, :], bo.partition_broadcast(P))]
        all_weights = 16 * len(weights)

        with nc.Block() as block:
            @block.sync
            def _(sp):
                for dst, src in weights:
                    sp.dma_start(dst, src).then_inc(s_w, 16)

                def context(it):
                    if (due := nth(it, ago=2)) is not None:
                        sp.wait_ge(s_kv, due)
                    sp.dma_start(ctxT[it.par][:, :], g.ctxT_d[:, bass.ds(it.b, 1), :].rearrange("c b t -> c (b t)")).then_inc(s_ctx[it.par], 16)

                skewed(sp, g.B, [(context, 0)], 2)

            @block.gpsimd
            def _(pool):
                for i in range(2):
                    pool.memset(vhi[i][:, :, D:D + 1], SPLIT).then_inc(s_ones, 1)
                    pool.memset(vlo[i][:, :, D:D + 1], 0.0).then_inc(s_ones, 1)

                def spread(it):
                    pool.wait_ge(s_kT, nth(it))
                    if (due := nth(it, 3, ago=2)) is not None:
                        pool.wait_ge(sm.s_scores, due)
                    pool.tensor_tensor(keys[it.par][:, :, :],
                                       kT[it.par][:, :].unsqueeze(1).to_broadcast([P, HEADS, KEYS]),
                                       g.head8[:, :].unsqueeze(2).to_broadcast([P, HEADS, KEYS]),
                                       ALU.mult).then_inc(s_keys, 1)

                def add_bias(it):
                    x = g.x[:, bass.ts(it.b, P)]
                    pool.wait_ge(ln.s_xn, nth(it))
                    pool.tensor_tensor(x, x, bvo_s[:, :], ALU.add).then_inc(s_bo, 1)

                steps = [(spread, 1), (lambda it: ln.inverse_deviation(pool, it), 0)]
                if biased:
                    steps.insert(0, (add_bias, 3))
                    pool.wait_ge(s_bias, 2)
                skewed(pool, g.B, steps, 6)

            @block.tensor
            def _(pe):
                pe.wait_ge(s_w, all_weights)
                if biased:
                    pe.matmul(y_p, bqkv_s[:, 2:3].to_broadcast([P, P]), wo_s[:, :], start=True, stop=True).then_inc(s_bvo, 1)
                    pe.wait_ge(s_bias, 1)

                def keys_values(it):
                    p = it.par
                    pe.wait_ge(s_ctx[it.par], loads(it))
                    if (due := nth(it, ago=1)) is not None:
                        pe.wait_ge(s_qT, due)
                    ln.turn(pe, it)
                    pe.matmul(k_p, wk_s[:, :], ctxT[p][:, :], start=True, stop=True)
                    pe.matmul(v_p, ctxT[p][:, :], wv_s[:, :], start=True, stop=True).then_inc(s_kv, 1)

                def queries(it):
                    p = it.par
                    pe.wait_ge(ln.s_xT, nth(it))
                    pe.wait_ge(s_kT, nth(it))
                    pe.wait_ge(s_vlo, nth(it))
                    pe.matmul(q_p, wq_s[:, :], ln.xT[p][:, :], start=True, stop=True).then_inc(s_q, 1)

                def score(it, c):
                    a, b = sm.first[c], sm.first[c + 1]
                    pe.wait_ge(s_qT, nth(it))
                    pe.wait_ge(s_keys, nth(it))
                    if (due := nth(it, 3, c, back=3)) is not None:
                        pe.wait_ge(sm.s_shift, due)
                    pe.matmul(scores[c][:, 0:(b - a) * KEYS], qT[it.par][:, :],
                              keys[it.par][:, a:b, :].rearrange("p h t -> p (h t)"),
                              start=True, stop=True).then_inc(sm.s_scores, 1)

                def weigh(it, c):
                    if c == 0:
                        pe.wait_ge(s_vlo, nth(it))
                        if (due := nth(it, ago=1)) is not None:
                            pe.wait_ge(s_o, due)
                        pe.wait_ge(s_ones, 4)
                    sm.times_values(pe, it, c, lambda h: o_p[:, h, :], lambda h: (vhi[it.par][:, h, :], vlo[it.par][:, h, :]))

                def turn_o(it):
                    pe.wait_ge(s_o, nth(it))
                    if (due := nth(it, ago=1)) is not None:
                        pe.wait_ge(s_x, due)
                    pe.transpose(oT_p, o_s[it.par][:, :], g.ident[:, :]).then_inc(s_oTp, 1)

                def output(it):
                    pe.wait_ge(s_oT, nth(it))
                    pe.matmul(y_p, oT[it.par][:, :], wo_s[:, :], start=True, stop=True).then_inc(s_y, 1)

                steps = {**numbered("turn_p", lambda it, c: sm.turn(pe, it, c), 4, 3), **numbered("score", score, 3, 2),
                         **numbered("weigh", weigh, 4, 3), "keys_values": (keys_values, 1), "queries": (queries, 1),
                         "turn_o": (turn_o, 4), "output": (output, 4)}
                skewed(pe, g.B, in_order(steps, "turn_p0 turn_p1 score0 turn_p2 score1 weigh0 turn_p3 weigh1 turn_o keys_values "
                                                "score2 output weigh2 weigh3 queries"), 6)

            @block.scalar
            def _(act):
                act.wait_ge(s_w, all_weights)

                def project(it):
                    p = it.par
                    act.wait_ge(s_kv, nth(it))
                    ln.fetch(act, it, s_q)
                    if (due := nth(it, ago=2)) is not None:
                        act.wait_ge(s_keys, due)
                    if biased:
                        act.activation(kT[p][:, :], k_p, ACT.Identity, bias=bqkv_s[:, 1:2]).then_inc(s_kT, 1)
                    else:
                        act.copy(kT[p][:, :], k_p).then_inc(s_kT, 1)

                def fetch_values(it):
                    if (due := nth(it, 4, ago=2)) is not None:
                        act.wait_ge(sm.s_values, due)
                    act.activation(vhi[it.par][:, :, 0:D], v_heads, ACT.Copy, scale=SPLIT).then_inc(s_vhi, 1)

                def fetch_q(it):
                    p = it.par
                    act.wait_ge(s_q, nth(it))
                    if (due := nth(it, 3, ago=2)) is not None:
                        act.wait_ge(sm.s_scores, due)
                    if biased:
                        act.activation(qT[p][:, :], q_p, ACT.Identity, bias=bqkv_s[:, 0:1]).then_inc(s_qT, 1)
                    else:
                        act.copy(qT[p][:, :], q_p).then_inc(s_qT, 1)

                def fetch_o(it):
                    act.wait_ge(s_oTp, nth(it))
                    if (due := nth(it, ago=2)) is not None:
                        act.wait_ge(s_y, due)
                    act.copy(oT[it.par][:, :], oT_p).then_inc(s_oT, 1)

                steps = {**numbered("fetch_p", lambda it, c: sm.fetch(act, it, c), 4, 3),
                         **numbered("exp", lambda it, c: sm.exponential(act, it, c), 3, 2),
                         "fetch_o": (fetch_o, 4), "project": (project, 1), "fetch_values": (fetch_values, 1), "fetch_q": (fetch_q, 1)}
                later(steps, "exp2")
                skewed(act, g.B, in_order(steps, "fetch_p0 fetch_p1 exp2 fetch_p2 fetch_p3 fetch_o exp0 project fetch_values "
                                                 "exp1 fetch_q"), 6)

            @block.vector
            def _(dve):
                if biased:
                    dve.wait_ge(s_w, all_weights)
                    dve.wait_ge(s_bvo, 1)
                    dve.tensor_tensor(bvo_s[:, :], y_p, bo_s[:, :], ALU.add).then_inc(s_bias, 1)
                    dve.wait_ge(s_bias, 1)
                    dve.tensor_scalar(bvo_s[:, :], bvo_s[:, :], g.gates[:, gate:gate + 1], None, ALU.mult).then_inc(s_bias, 1)

                def divide(it):
                    p = it.par
                    dve.wait_ge(sm.s_values, nth(it, 4))
                    if (due := nth(it, ago=2)) is not None:
                        dve.wait_ge(s_o, due)
                    dve.reciprocal(recip[p][:, :], o_p[:, :, D]).then_inc(s_recip, 1)
                    dve.wait_ge(s_recip, nth(it))
                    if (due := nth(it, ago=2)) is not None:
                        dve.wait_ge(s_oTp, due)
                    dve.tensor_tensor(o_s[p][:, :].rearrange("p (h d) -> p h d", d=D), o_p[:, :, 0:D],
                                      recip[p][:, :].unsqueeze(2).to_broadcast([P, HEADS, D]),
                                      ALU.mult).then_inc(s_o, 1)

                def statistics(it):
                    if isinstance(it.b, int) and it.b == AHEAD:
                        dve.wait_ge(g.s_x_rest, 16)
                    ln.statistics(dve, it)

                def value_remainder(it):
                    dve.wait_ge(s_vhi, nth(it))
                    dve.scalar_tensor_tensor(vlo[it.par][:, :, 0:D], v_heads, SPLIT, vhi[it.par][:, :, 0:D],
                                             ALU.mult, ALU.subtract).then_inc(s_vlo, 1)

                def add(it):
                    x = g.x[:, bass.ts(it.b, P)]
                    if biased:
                        dve.wait_ge(s_bo, nth(it))
                    dve.wait_ge(s_y, nth(it))
                    dve.wait_ge(ln.s_xn, nth(it))
                    dve.scalar_tensor_tensor(x, y_p, g.gates[:, gate:gate + 1], x, ALU.mult, ALU.add).then_inc(s_x, 1)

                steps = {**numbered("maximum", lambda it, c: sm.maximum(dve, it, c), 3, 2),
                         **numbered("shift", lambda it, c: sm.shift(dve, it, c), 3, 2),
                         "statistics": (statistics, 0), "normalize": (lambda it: ln.normalize(dve, it), 1),
                         **numbered("remainder", lambda it, c: sm.remainder(dve, it, c), 4, 3),
                         "values": (value_remainder, 1), "divide": (divide, 4), "add": (add, 4)}
                skewed(dve, g.B, in_order(steps, "divide remainder0 remainder1 maximum0 normalize maximum1 shift0 remainder2 remainder3 "
                                                 "shift1 statistics values maximum2 add shift2"), 6)


GROUP = 4


class GroupFront:

    def __init__(self, st, g, ps_xT, split=True):
        self.g, self.ps_xT, self.split = g, ps_xT, split
        self.stats, self.mv = st.sb("stats", [P, GROUP, 6]), st.sb2("mv", [P, GROUP, 2])
        self.ve, self.rstd = st.sb2("ve", [P, GROUP]), st.sb2("rstd", [P, GROUP])
        self.xn, self.xT = st.sb2("xn", [P, GROUP * P]), st.sb2("xT", [P, GROUP * P])
        self.s_mv, self.s_ve, self.s_rstd = st.sem("s_mv"), st.sem("s_ve"), st.sem("s_rstd")
        self.s_xn, self.s_turned, self.s_xT = st.sem("s_xn"), st.sem("s_turned"), st.sem("s_xT")
        if split:
            self.xhi, self.xlo = st.sb2("xhi", [P, GROUP * P], F16), st.sb2("xlo", [P, GROUP * P], F16)
            self.s_hi, self.s_lo = st.sem("s_hi"), st.sem("s_lo")

    def statistics(self, dve, it):
        if (due := nth(it, ago=2)) is not None:
            dve.wait_ge(self.s_xn, due)
        if (due := nth(it, ago=2)) is not None:
            dve.wait_ge(self.s_ve, due)
        for j in range(GROUP):
            dve.bn_stats(self.stats[:, j, :], self.g.x[:, bass.ts(it.b * GROUP + j, P)])
        dve.drain()
        for j in range(GROUP):
            last = dve.bn_aggr(self.mv[it.par][:, j, :], self.stats[:, j, :])
        last.then_inc(self.s_mv, 1)
        dve.drain()

    def inverse_deviation(self, pool, it):
        p = it.par
        pool.wait_ge(self.s_mv, nth(it))
        if (due := nth(it, ago=2)) is not None:
            pool.wait_ge(self.s_rstd, due)
        pool.tensor_tensor(self.ve[p][:, :], self.mv[p][:, :, 1], self.g.eps[:, :], ALU.add).then_inc(self.s_ve, 1)
        pool.wait_ge(self.s_ve, nth(it))
        if (due := nth(it, ago=2)) is not None:
            pool.wait_ge(self.s_xn, due)
        pool.tensor_tensor(self.rstd[p][:, :], self.ve[p][:, :], self.g.minus_half[:, :], ALU.pow).then_inc(self.s_rstd, 1)

    def normalize(self, dve, it):
        p = it.par
        dve.wait_ge(self.s_rstd, nth(it))
        if (due := nth(it, ago=2)) is not None:
            dve.wait_ge(self.s_turned, due)
        for j in range(GROUP):
            last = dve.tensor_scalar(self.xn[p][:, j * P:(j + 1) * P], self.g.x[:, bass.ts(it.b * GROUP + j, P)],
                                     self.mv[p][:, j, 0:1], self.rstd[p][:, j:j + 1], ALU.subtract, ALU.mult)
        last.then_inc(self.s_xn, 1)

    def turn(self, pe, it):
        pe.wait_ge(self.s_xn, nth(it))
        if (due := nth(it, ago=1)) is not None:
            pe.wait_ge(self.s_xT, due)
        for j in range(GROUP):
            last = pe.transpose(self.ps_xT[:, j * P:(j + 1) * P], self.xn[it.par][:, j * P:(j + 1) * P], self.g.ident[:, :])
        last.then_inc(self.s_turned, 1)

    def fetch(self, act, it, used, per=1):
        act.wait_ge(self.s_turned, nth(it))
        if (due := nth(it, per=per, ago=2)) is not None:
            act.wait_ge(used, due)
        act.copy(self.xT[it.par][:, :], self.ps_xT[:, :]).then_inc(self.s_xT, 1)
        if self.split:
            act.wait_ge(self.s_xT, nth(it))
            act.activation(self.xhi[it.par][:, :], self.xT[it.par][:, :], ACT.Copy, scale=SPLIT).then_inc(self.s_hi, 1)

    def remainder(self, dve, it):
        dve.wait_ge(self.s_hi, nth(it))
        dve.scalar_tensor_tensor(self.xlo[it.par][:, :], self.xT[it.par][:, :], SPLIT, self.xhi[it.par][:, :],
                                 ALU.mult, ALU.subtract).then_inc(self.s_lo, 1)


class Router:

    def __init__(self, st, g, experts, front, ps, wg, bias=None):
        E = self.E = experts
        self.g, self.front, self.ps, self.wg, self.bias = g, front, ps, wg, bias
        self.logits, self.act_in = st.sb("logits", [P, GROUP, E]), st.sb("act_in", [P, GROUP, E])
        self.act_out, self.sel = st.sb("act_out", [P, GROUP, E]), st.sb("sel", [P, GROUP, E])
        self.same, self.above = st.sb("same", [P, GROUP, E, E]), st.sb("above", [P, GROUP, E, E])
        self.before = st.sb("before", [P, E, E])
        self.rank, self.one = st.sb("rank", [P, GROUP, E]), st.sb("one", [P, GROUP])
        self.w = st.sb2("route", [P, GROUP, E])
        self.s_before, self.s_logits, self.s_in, self.s_less, self.s_out, self.s_w = [
            st.sem(n) for n in ("s_before", "s_logits", "s_in", "s_less", "s_out", "s_route")]

    def make_before(self, pool):
        pool.memset(self.before[:, :, :], 1.0).then_inc(self.s_before, 1)
        pool.wait_ge(self.s_before, 1)
        pool.affine_select(out=self.before[:, :, :], in_=self.before[:, :, :], compare_op=ALU.is_ge, fill=0.0,
                           base=-1, pattern=[[1, self.E], [-1, self.E]], channel_multiplier=0).then_inc(self.s_before, 1)

    def score(self, pe, it):
        pe.wait_ge(self.front.s_xT, nth(it))
        if (due := nth(it, ago=1)) is not None:
            pe.wait_ge(self.s_in, due)
        for j in range(GROUP):
            last = pe.matmul(self.ps[:, j * self.E:(j + 1) * self.E], self.front.xT[it.par][:, j * P:(j + 1) * P],
                             self.wg[:, :], start=True, stop=True)
        last.then_inc(self.s_logits, 1)

    def wide(self, v):
        return v[:, :].unsqueeze(2).to_broadcast([P, GROUP, self.E])

    def fetch(self, dve, it):
        E = self.E
        dve.wait_ge(self.s_logits, nth(it))
        if (due := nth(it, ago=1)) is not None:
            dve.wait_ge(self.s_out, due)
        src = self.ps[:, 0:GROUP * E].rearrange("p (j e) -> p j e", e=E)
        if self.bias is None:
            last = dve.tensor_copy(self.logits[:, :, :], src)
        else:
            last = dve.tensor_tensor(self.logits[:, :, :], src,
                                     self.bias[:, :].unsqueeze(1).to_broadcast([P, GROUP, E]), ALU.add)
        last.then_inc(self.s_in, 1)

    def less_maximum(self, dve, it):
        dve.drain()
        dve.tensor_reduce(self.one[:, :], self.logits[:, :, :], AX, ALU.max)
        dve.drain()
        dve.tensor_tensor(self.act_in[:, :, :], self.logits[:, :, :], self.wide(self.one), ALU.subtract).then_inc(self.s_less, 1)

    def function(self, act, it, func):
        less = func == ACT.Exp
        act.wait_ge(self.s_less if less else self.s_in, nth(it))
        if (due := nth(it, ago=1)) is not None:
            act.wait_ge(self.s_w, due)
        act.activation(self.act_out[:, :, :], (self.act_in if less else self.logits)[:, :, :], func).then_inc(self.s_out, 1)

    def reciprocal_of_sum(self, dve, v, eps=None, times=None):
        dve.tensor_reduce(self.one[:, :], v[:, :, :], AX, ALU.add)
        dve.drain()
        if eps is not None:
            dve.tensor_scalar(self.one[:, :], self.one[:, :], eps, None, ALU.add)
            dve.drain()
        dve.reciprocal(self.one[:, :], self.one[:, :])
        dve.drain()
        if times is not None:
            dve.tensor_scalar(self.one[:, :], self.one[:, :], times, None, ALU.mult)
            dve.drain()

    def compare(self, dve, v):
        E = self.E
        other = v[:, :, :].unsqueeze(2).to_broadcast([P, GROUP, E, E])
        own = v[:, :, :].unsqueeze(3).to_broadcast([P, GROUP, E, E])
        dve.tensor_tensor(self.same[:, :, :, :], other, own, ALU.is_equal)
        dve.tensor_tensor(self.above[:, :, :, :], other, own, ALU.is_gt)
        dve.drain()

    def order(self, dve):
        E = self.E
        flat = self.same[:, :, :, :].rearrange("p j a b -> p j (a b)")
        dve.tensor_tensor(flat, flat, self.before[:, :, :].rearrange("p a b -> p (a b)").unsqueeze(1).to_broadcast(
            [P, GROUP, E * E]), ALU.mult)
        dve.drain()
        dve.tensor_tensor(self.same[:, :, :, :], self.same[:, :, :, :], self.above[:, :, :, :], ALU.add)
        dve.drain()

    def select(self, dve):
        dve.tensor_reduce(self.rank[:, :, :], self.same[:, :, :, :], AX, ALU.add)
        dve.drain()
        dve.tensor_scalar(self.sel[:, :, :], self.rank[:, :, :], 1.5, None, ALU.is_lt)
        dve.drain()


def l0_ffn(nc, g, a):
    E, R, F = 4, 4, 512
    FT = F // P
    n = g.B // GROUP
    with Stage(nc, "l0f") as st:
        wg, bg, wi = st.sb("wg", [P, E]), st.sb("bg", [P, E]), st.sb("wi", [P, F])
        la, lb, wo = st.sb("la", [R, E, P]), st.sb("lb", [R, E, F]), st.sb("wo", [P, FT, P])
        we = st.sb("we", [P, E, F])
        hi, lo = st.sb("hi", [P, E, F], F16), st.sb("lo", [P, E, F], F16)
        s_whi, s_wlo = st.sem("s_whi"), st.sem("s_wlo")
        relu = [st.sb(f"relu{e}", [P, F]) for e in range(E)]
        hs, hT = st.sb2("hs", [P, F]), st.sb2("hT", [P, F])
        ps_xT, ps_lg, ps_hT, ps_y = st.ps("xT"), st.ps("lg"), st.ps("hT"), st.ps("y")
        ps_h = [st.ps(f"h{e}") for e in range(E)]
        fr = GroupFront(st, g, ps_xT)
        rt = Router(st, g, E, fr, ps_lg, wg, bg)
        s_w, s_low, s_we = st.sem("s_w"), st.sem("s_low"), st.sem("s_we")
        s_h, s_relu, s_pair, s_hs, s_hTp, s_hT, s_y, s_x = [
            st.sem(k) for k in ("s_h", "s_relu", "s_pair", "s_hs", "s_hTp", "s_hT", "s_y", "s_x")]
        weights = [(wg[:, :], a["L0_Wg"]), (bg[:, :], a["L0_bg"].partition_broadcast(P)), (wi[:, :], a["L0_Wi"]),
                   (la[:, :, :], a["L0_A"]), (lb[:, :, :], a["L0_B"]), (wo[:, :, :], a["L0_Wof"])]

        with nc.Block() as block:
            @block.sync
            def _(sp):
                for dst, src in weights:
                    sp.dma_start(dst, src).then_inc(s_w, 16)

            @block.gpsimd
            def _(pool):
                rt.make_before(pool)
                skewed(pool, n, [(lambda it: fr.inverse_deviation(pool, it), 0)], 2)

            @block.tensor
            def _(pe):
                pe.wait_ge(s_w, 16 * len(weights))
                for e in range(E):
                    pe.matmul(ps_h[e][:, :], la[:, e, :], lb[:, e, :], start=True, stop=True).then_inc(s_low, 1)

                def hidden(it, j, e):
                    if j == 0 and e == 0:
                        pe.wait_ge(s_wlo, E)
                        pe.wait_ge(fr.s_lo, nth(it))
                    if (due := nth(it, 4 * GROUP, 4 * j + e, back=4)) is not None:
                        pe.wait_ge(s_relu, due)
                    for k, (x, w) in enumerate(((fr.xhi, hi), (fr.xhi, lo), (fr.xlo, hi))):
                        last = pe.matmul(ps_h[e][:, :], x[it.par][:, j * P:(j + 1) * P], w[:, e, :], start=(k == 0), stop=(k == 2))
                    last.then_inc(s_h, 1)

                def turn(it, j):
                    pe.wait_ge(s_hs, nth(it, GROUP, j))
                    if (due := nth(it, GROUP, j, back=1)) is not None:
                        pe.wait_ge(s_hT, due)
                    for t in range(FT):
                        last = pe.transpose(ps_hT[:, t * P:(t + 1) * P], hs[j % 2][:, t * P:(t + 1) * P], g.ident[:, :])
                    last.then_inc(s_hTp, 1)

                def down(it, j):
                    pe.wait_ge(s_hT, nth(it, GROUP, j))
                    if (due := nth(it, GROUP, j, back=1)) is not None:
                        pe.wait_ge(s_x, due)
                    for t in range(FT):
                        last = pe.matmul(ps_y[:, 0:P], hT[j % 2][:, t * P:(t + 1) * P], wo[:, t, :],
                                         start=(t == 0), stop=(t == FT - 1))
                    last.then_inc(s_y, 1)

                steps = {**numbered("hidden", lambda it, c: hidden(it, c // E, c % E), GROUP * E, 2),
                         **numbered("turn", turn, GROUP, 2), **numbered("down", down, GROUP, 2),
                         "turn_x": (lambda it: fr.turn(pe, it), 1), "score": (lambda it: rt.score(pe, it), 1)}
                later(steps, "turn3 down2 down3")
                skewed(pe, n, in_order(steps, "hidden0 hidden1 hidden2 turn3 hidden3 down2 turn_x hidden4 hidden5 score turn0 "
                                              "hidden6 hidden7 down3 hidden8 hidden9 hidden10 turn1 hidden11 down0 hidden12 "
                                              "hidden13 hidden14 hidden15 turn2 down1"), 6)

            @block.scalar
            def _(act):
                for e in range(E):
                    act.wait_ge(s_we, e + 1)
                    act.activation(hi[:, e, :], we[:, e, :], ACT.Copy, scale=SPLIT).then_inc(s_whi, 1)

                def relu_(it, j, e):
                    act.wait_ge(s_h, nth(it, 4 * GROUP, 4 * j + e))
                    if j == 0 and e == 0:
                        act.wait_ge(rt.s_w, nth(it))
                    if (due := nth(it, 3 * GROUP, 3 * j + 2, back=3)) is not None:
                        act.wait_ge(s_pair, due)
                    act.activation(relu[e][:, :], ps_h[e][:, :], ACT.Relu,
                                   scale=rt.w[it.par][:, j, e:e + 1]).then_inc(s_relu, 1)

                def fetch_hT(it, j):
                    act.wait_ge(s_hTp, nth(it, GROUP, j))
                    if (due := nth(it, GROUP, j, back=2)) is not None:
                        act.wait_ge(s_y, due)
                    act.copy(hT[j % 2][:, :], ps_hT[:, :]).then_inc(s_hT, 1)

                steps = {**numbered("relu", lambda it, c: relu_(it, c // E, c % E), GROUP * E, 2),
                         **numbered("fetch", fetch_hT, GROUP, 2), "fetch_x": (lambda it: fr.fetch(act, it, s_h, 4 * GROUP), 1),
                         "exp": (lambda it: rt.function(act, it, ACT.Exp), 1)}
                later(steps, "fetch3")
                skewed(act, n, in_order(steps, "relu0 relu1 relu2 relu3 fetch3 fetch_x relu4 relu5 relu6 relu7 fetch0 relu8 relu9 "
                                               "relu10 relu11 fetch1 exp relu12 relu13 relu14 relu15 fetch2"), 6)

            @block.vector
            def _(dve):
                dve.wait_ge(s_w, 16 * len(weights))
                for e in range(E):
                    dve.wait_ge(s_low, e + 1)
                    dve.tensor_tensor(we[:, e, :], ps_h[e][:, :], wi[:, :], ALU.add).then_inc(s_we, 1)
                for e in range(E):
                    dve.wait_ge(s_whi, e + 1)
                    dve.scalar_tensor_tensor(lo[:, e, :], we[:, e, :], SPLIT, hi[:, e, :], ALU.mult, ALU.subtract).then_inc(s_wlo, 1)
                dve.wait_ge(rt.s_before, 2)

                def scores(it):
                    dve.wait_ge(rt.s_out, nth(it))
                    rt.reciprocal_of_sum(dve, rt.act_out, times=SPLIT ** -2)
                    dve.tensor_tensor(rt.act_in[:, :, :], rt.act_out[:, :, :], rt.wide(rt.one), ALU.mult)
                    dve.drain()
                    rt.compare(dve, rt.act_in)

                def choose(it):
                    rt.order(dve)
                    rt.select(dve)
                    if (due := nth(it, 4 * GROUP, ago=2)) is not None:
                        dve.wait_ge(s_relu, due)
                    dve.tensor_tensor(rt.w[it.par][:, :, :], rt.act_in[:, :, :], rt.sel[:, :, :], ALU.mult).then_inc(rt.s_w, 1)

                def add(it, j):
                    x = g.x[:, bass.ts(it.b * GROUP + j, P)]
                    dve.wait_ge(s_y, nth(it, GROUP, j))
                    dve.wait_ge(fr.s_xn, nth(it))
                    dve.scalar_tensor_tensor(x, ps_y[:, 0:P], g.gates[:, 4:5], x, ALU.mult, ALU.add).then_inc(s_x, 1)

                def pair(it, j, i):
                    dve.wait_ge(s_relu, nth(it, 4 * GROUP, 4 * j + 2 * i + 1))
                    r = relu[2 * i]
                    dve.tensor_tensor(r[:, :], r[:, :], relu[2 * i + 1][:, :], ALU.add).then_inc(s_pair, 1)

                def total(it, j):
                    dve.wait_ge(s_pair, nth(it, 3 * GROUP, 3 * j + 1))
                    if (due := nth(it, GROUP, j, back=2)) is not None:
                        dve.wait_ge(s_hTp, due)
                    dve.tensor_tensor(hs[j % 2][:, :], relu[0][:, :], relu[2][:, :], ALU.add).then_inc(s_pair, 1)
                    dve.wait_ge(s_pair, nth(it, 3 * GROUP, 3 * j + 2))
                    dve.sem_inc(s_hs, 1)

                steps = {**numbered("pair", lambda it, c: pair(it, c // 2, c % 2), 2 * GROUP, 2), **numbered("total", total, GROUP, 2),
                         **numbered("add", add, GROUP, 2), "normalize": (lambda it: fr.normalize(dve, it), 1),
                         "statistics": (lambda it: fr.statistics(dve, it), 0), "remainder": (lambda it: fr.remainder(dve, it), 1),
                         "logits": (lambda it: rt.fetch(dve, it), 1), "less_maximum": (lambda it: rt.less_maximum(dve, it), 1),
                         "scores": (scores, 1), "choose": (choose, 1)}
                later(steps, "add2 add3")
                steps = in_order(steps, "normalize pair0 pair1 total0 add2 statistics pair2 pair3 total1 remainder add3 logits "
                                        "pair4 less_maximum pair5 total2 scores add0 pair6 pair7 total3 choose add1")
                skewed(dve, n, steps, 6)


def l1_ffn(nc, g, a):
    E, F = 8, 512
    FT = F // P
    T = E * FT
    n = g.B // GROUP
    with Stage(nc, "l1f") as st:
        wg, w2, w13 = st.sb("wg", [P, E]), st.sb("w2", [P, E, FT, P]), st.sb2("w13", [P, 2, F])
        hi, lo = st.sb("hi", [P, E, 2, F], F16), st.sb("lo", [P, E, 2, F], F16)
        silu = st.sb2("silu", [P, GROUP * P])
        gated = [[st.sb(f"gated{i}{t}", [P, GROUP * P]) for t in range(FT)] for i in range(2)]
        acc = st.sb("acc", [P, GROUP * P])
        ps_xT, ps_lg = st.ps("xT"), st.ps("lg")
        ps_1, ps_3, ps_y = [[st.ps(f"{k}{i}") for i in range(2)] for k in ("h1", "h3", "y")]
        fr = GroupFront(st, g, ps_xT)
        rt = Router(st, g, E, fr, ps_lg, wg)
        s_g, s_w13, s_w2 = st.sem("s_g"), [st.sem(f"s_w13{e}") for e in range(E)], st.sem("s_w2")
        s_whi, s_wlo = st.sem("s_whi"), st.sem("s_wlo")
        s_up, s_silu, s_gated, s_y, s_acc, s_x = [st.sem(k) for k in ("s_up", "s_silu", "s_gated", "s_y", "s_acc", "s_x")]

        with nc.Block() as block:
            @block.sync
            def _(sp):
                sp.dma_start(wg[:, :], a["L1_Wg"]).then_inc(s_g, 16)
                for e in range(E):
                    if e == 2:
                        sp.dma_start(w2[:, :, :, :], a["L1_W2"]).then_inc(s_w2, 16)
                    if e >= 2:
                        sp.wait_ge(s_wlo, e - 1)
                    sp.dma_start(w13[e % 2][:, 0, :], a["L1_W1"][:, e, :]).then_inc(s_w13[e], 16)
                    sp.dma_start(w13[e % 2][:, 1, :], a["L1_W3"][:, e, :]).then_inc(s_w13[e], 16)

            @block.gpsimd
            def _(pool):
                rt.make_before(pool)
                skewed(pool, n, [(lambda it: fr.inverse_deviation(pool, it), 0)], 2)

            @block.tensor
            def _(pe):
                pe.wait_ge(s_g, 16)

                def up(it, e, t):
                    c = e * FT + t
                    if t == 0:
                        pe.wait_ge(fr.s_lo, nth(it))
                        pe.wait_ge(s_wlo, e + 1)
                    if (due := nth(it, T, c, back=2)) is not None:
                        pe.wait_ge(s_silu, due)
                    if (due := nth(it, T, c, back=2)) is not None:
                        pe.wait_ge(s_gated, due)
                    f = slice(t * P, (t + 1) * P)
                    for bank, i in ((ps_1[t % 2], 0), (ps_3[t % 2], 1)):
                        for k, (w, x) in enumerate(((hi, fr.xhi), (hi, fr.xlo), (lo, fr.xhi))):
                            last = pe.matmul(bank[:, :], w[:, e, i, f], x[it.par][:, :], start=(k == 0), stop=(k == 2))
                    last.then_inc(s_up, 1)

                def down(it, e):
                    pe.wait_ge(s_gated, nth(it, T, e * FT + FT - 1))
                    if (due := nth(it, E, e, back=2)) is not None:
                        pe.wait_ge(s_acc, due)
                    pe.wait_ge(s_w2, 16)
                    for j in range(GROUP):
                        for t in range(FT):
                            last = pe.matmul(ps_y[e % 2][:, j * P:(j + 1) * P], gated[e % 2][t][:, j * P:(j + 1) * P],
                                             w2[:, e, t, :], start=(t == 0), stop=(t == FT - 1))
                    last.then_inc(s_y, 1)

                steps = []
                for e in range(E):
                    us = [(lambda it, e=e, t=t: up(it, e, t), 2) for t in range(FT)]
                    steps += us[0:2] + [(lambda it, e=(e - 1) % E: down(it, e), 2 + (e < 1))] + us[2:4]
                    if e == 1:
                        steps.append((lambda it: fr.turn(pe, it), 1))
                    if e == 3:
                        steps.append((lambda it: rt.score(pe, it), 1))
                skewed(pe, n, steps, 6)

            @block.scalar
            def _(act):
                def round_weights(e):
                    act.wait_ge(s_w13[e], 32)
                    act.activation(hi[:, e, :, :], w13[e % 2][:, :, :], ACT.Copy, scale=SPLIT).then_inc(s_whi, 1)

                def silu_(it, c):
                    if first_of(it) and c % FT == 0:
                        for e in range(c // FT + (c > 0), min(c // FT + 2, E)):
                            round_weights(e)
                    act.wait_ge(s_up, nth(it, T, c))
                    if (due := nth(it, T, c, back=2)) is not None:
                        act.wait_ge(s_gated, due)
                    act.activation(silu[c % 2][:, :], ps_1[c % 2][:, :], ACT.Silu,
                                   scale=SPLIT ** -2).then_inc(s_silu, 1)

                steps = []
                for c in range(T):
                    steps.append((lambda it, c=c: silu_(it, c), 2))
                    if c == 2 * FT + 1:
                        steps.append((lambda it: fr.fetch(act, it, s_up, T), 1))
                    if c == 5 * FT + 1:
                        steps.append((lambda it: rt.function(act, it, ACT.Exp), 1))
                skewed(act, n, steps, 6)

            @block.vector
            def _(dve):
                dve.wait_ge(rt.s_before, 2)

                def split_weights(e):
                    dve.wait_ge(s_whi, e + 1)
                    dve.scalar_tensor_tensor(lo[:, e, :, :], w13[e % 2][:, :, :], SPLIT, hi[:, e, :, :],
                                             ALU.mult, ALU.subtract).then_inc(s_wlo, 1)


                def compare(it):
                    rt.less_maximum(dve, it)
                    rt.compare(dve, rt.logits)

                def choose(it):
                    rt.order(dve)
                    rt.select(dve)

                def weigh(it):
                    dve.wait_ge(rt.s_out, nth(it))
                    dve.tensor_tensor(rt.act_in[:, :, :], rt.act_out[:, :, :], rt.sel[:, :, :], ALU.mult)
                    dve.drain()
                    rt.reciprocal_of_sum(dve, rt.act_in, times=SPLIT ** -2)
                    if (due := nth(it, E, ago=2)) is not None:
                        dve.wait_ge(s_acc, due)
                    dve.tensor_tensor(rt.w[it.par][:, :, :], rt.act_in[:, :, :], rt.wide(rt.one), ALU.mult).then_inc(rt.s_w, 1)

                def gate(it, e, t):
                    if first_of(it) and t == 0:
                        for k in range(e + (e > 0), min(e + 2, E)):
                            split_weights(k)
                    c = e * FT + t
                    dve.wait_ge(s_silu, nth(it, T, c))
                    if t == 0:
                        if (due := nth(it, E, e, back=2)) is not None:
                            dve.wait_ge(s_y, due)
                    dve.tensor_tensor(gated[e % 2][t][:, :], ps_3[t % 2][:, :], silu[t % 2][:, :], ALU.mult).then_inc(s_gated, 1)

                def collect(it, e):
                    dve.wait_ge(s_y, nth(it, E, e))
                    if e > 0:
                        if (due := nth(it, E, e, back=1)) is not None:
                            dve.wait_ge(s_acc, due)
                    else:
                        if (due := nth(it, ago=1)) is not None:
                            dve.wait_ge(s_x, due)
                        dve.wait_ge(rt.s_w, nth(it))
                    for j in range(GROUP):
                        y, w, o = ps_y[e % 2][:, j * P:(j + 1) * P], rt.w[it.par][:, j, e:e + 1], acc[:, j * P:(j + 1) * P]
                        if e == 0:
                            last = dve.tensor_scalar(o, y, w, None, ALU.mult)
                        else:
                            last = dve.scalar_tensor_tensor(o, y, w, o, ALU.mult, ALU.add)
                    last.then_inc(s_acc, 1)

                def add(it):
                    x = g.x[:, bass.ts(it.b, GROUP * P)]
                    dve.wait_ge(s_acc, nth(it, E))
                    dve.wait_ge(fr.s_xn, nth(it))
                    dve.scalar_tensor_tensor(x, acc[:, :], g.gates[:, 5:6], x, ALU.mult, ALU.add).then_inc(s_x, 1)

                between = {0: [(add, 3)], 3: [(lambda it: fr.statistics(dve, it), 0)], 4: [(lambda it: fr.remainder(dve, it), 1), (lambda it: rt.fetch(dve, it), 1), (compare, 1)],
                           5: [(choose, 1)], 6: [(weigh, 1)]}
                steps = [(lambda it: fr.normalize(dve, it), 1)]
                for e in range(E):
                    gs = [(lambda it, e=e, t=t: gate(it, e, t), 2) for t in range(FT)]
                    steps += gs[0:2] + [(lambda it, e=(e - 1) % E: collect(it, e), 2 + (e < 1))] + gs[2:4] + between.get(e, [])
                skewed(dve, n, steps, 6)


def l2_ffn(nc, g, a):
    E, M = 16, 64
    SCALE = 2.5
    CH = 3
    n = g.B // GROUP
    K = CH * GROUP
    with Stage(nc, "l2f") as st:
        wg = st.sb("wg", [P, E])
        gate_w, up_w, down_w = st.sb("gate", [P, E * M]), st.sb("up", [P, E * M]), st.sb("down", [P, E * M // P, P])
        sg, su, sd = st.sb("sg", [P, M]), st.sb("su", [P, M]), st.sb("sd", [M, P])
        parts = [[st.sb(f"{k}{i}", [P, E * M + M], F16) for i in ("hi", "lo")] for k in ("gate", "up")]
        s_whi, s_wlo = st.sem("s_whi"), st.sem("s_wlo")
        silu, prod, hid = st.sb2("silu", [P, BANK]), st.sb2("prod", [P, BANK]), st.sb2("hid", [P, BANK])
        hT = st.sb2("hT", [P, BANK])
        ps_xT, ps_lg, ps_hT, ps_y = st.ps("xT"), st.ps("lg"), st.ps("hT"), st.ps("y")
        ps_g, ps_u = [[st.ps(f"{k}{i}") for i in range(2)] for k in "gu"]
        fr = GroupFront(st, g, ps_xT)
        rt = Router(st, g, E, fr, ps_lg, wg)
        s_w, s_pass = st.sem("s_w"), st.sem("s_pass")
        s_up, s_silu, s_prod, s_hid, s_hTp, s_hT, s_down, s_x = [
            st.sem(k) for k in ("s_up", "s_silu", "s_prod", "s_hid", "s_hTp", "s_hT", "s_down", "s_x")]
        weights = [(wg[:, :], a["L2_gw"]), (gate_w[:, :], a["L2_wg"]), (up_w[:, :], a["L2_wu"]),
                   (down_w[:, :, :], a["L2_wd"]), (sg[:, :], a["L2_sg"]), (su[:, :], a["L2_su"]), (sd[:, :], a["L2_sd"])]

        def width(c):
            return M if c == 2 else BANK

        with nc.Block() as block:
            @block.sync
            def _(sp):
                for dst, src in weights:
                    sp.dma_start(dst, src).then_inc(s_w, 16)

            @block.gpsimd
            def _(pool):
                rt.make_before(pool)

                def weigh(it, j, c):
                    k = CH * j + c
                    if k == 0:
                        pool.wait_ge(rt.s_w, nth(it))
                    pool.wait_ge(s_prod, nth(it, K, k))
                    if (due := nth(it, K, k, back=2)) is not None:
                        pool.wait_ge(s_hTp, due)
                    pool.tensor_tensor(hid[k % 2][:, :].rearrange("p (e m) -> p e m", m=M),
                                       prod[k % 2][:, :].rearrange("p (e m) -> p e m", m=M),
                                       rt.w[it.par][:, j, 8 * c:8 * c + 8].unsqueeze(2).to_broadcast([P, 8, M]),
                                       ALU.mult).then_inc(s_hid, 1)

                steps = {**numbered("weigh", lambda it, c: weigh(it, c // 2, c % 2), 2 * GROUP, 2),
                         "deviation": (lambda it: fr.inverse_deviation(pool, it), 0)}
                skewed(pool, n, in_order(steps, "weigh0 weigh1 deviation weigh2 weigh3 weigh4 weigh5 weigh6 weigh7"), 6)

            @block.tensor
            def _(pe):
                def score(it):
                    if first_of(it):
                        pe.wait_ge(s_w, 16 * len(weights))
                    rt.score(pe, it)

                def up(it, k):
                    j, c = k // CH, k % CH
                    if k == 0:
                        pe.wait_ge(s_wlo, 4)
                        pe.wait_ge(fr.s_lo, nth(it))
                    if (due := nth(it, K, k, back=2)) is not None:
                        pe.wait_ge(s_silu, due)
                    if (due := nth(it, K, k, back=2)) is not None:
                        pe.wait_ge(s_prod, due)
                    for bank, (hi, lo) in ((ps_g[k % 2], parts[0]), (ps_u[k % 2], parts[1])):
                        for i, (x, w) in enumerate(((fr.xhi, hi), (fr.xhi, lo), (fr.xlo, hi))):
                            last = pe.matmul(bank[:, 0:width(c)], x[it.par][:, j * P:(j + 1) * P],
                                             w[:, c * BANK:c * BANK + width(c)], start=(i == 0), stop=(i == 2))
                    last.then_inc(s_up, 1)

                def turn(it, k):
                    j, c = k // CH, k % CH
                    if c == 2:
                        pe.wait_ge(s_prod, nth(it, K, k))
                    else:
                        pe.wait_ge(s_hid, nth(it, 2 * GROUP, 2 * j + c))
                    if (due := nth(it, K, k, back=1)) is not None:
                        pe.wait_ge(s_hT, due)
                    if c == 2:
                        pe.sem_inc(s_pass, 1)
                        last = pe.transpose(ps_hT[0:M, 0:P], prod[k % 2][:, 0:M], g.ident[:, :])
                    else:
                        for t in range(4):
                            last = pe.transpose(ps_hT[:, t * P:(t + 1) * P], hid[k % 2][:, t * P:(t + 1) * P], g.ident[:, :])
                    last.then_inc(s_hTp, 1)

                def down(it, k):
                    j, c = k // CH, k % CH
                    pe.wait_ge(s_hT, nth(it, K, k))
                    if c == 0:
                        if (due := nth(it, GROUP, j, back=1)) is not None:
                            pe.wait_ge(s_x, due)
                    if c == 2:
                        last = pe.matmul(ps_y[:, 0:P], hT[k % 2][0:M, 0:P], sd[:, :], start=False, stop=True)
                    else:
                        for t in range(4):
                            last = pe.matmul(ps_y[:, 0:P], hT[k % 2][:, t * P:(t + 1) * P], down_w[:, 4 * c + t, :],
                                             start=(c == 0 and t == 0), stop=False)
                    last.then_inc(s_down, 1)

                steps = {**numbered("up", up, K, 2), **numbered("turn", turn, K, 2), **numbered("down", down, K, 2),
                         "turn_x": (lambda it: fr.turn(pe, it), 1), "score": (score, 1)}
                later(steps, "turn10 turn11 down9 down10 down11")
                skewed(pe, n, in_order(steps, "up0 turn10 up1 down9 up2 turn11 down10 turn_x down11 turn0 up3 turn1 score up4 down0 "
                                              "up5 turn2 down1 down2 turn3 up6 turn4 down3 up7 turn5 down4 up8 turn6 down5 up9 "
                                              "turn7 up10 down6 turn8 down7 turn9 down8 up11"), 6)

            @block.scalar
            def _(act):
                def fetch_x(it):
                    fr.fetch(act, it, s_up, K)
                    if first_of(it):
                        act.wait_ge(s_w, 16 * len(weights))
                        for (hi, lo), routed, shared in ((parts[0], gate_w, sg), (parts[1], up_w, su)):
                            act.activation(hi[:, 0:E * M], routed[:, :], ACT.Copy, scale=SPLIT).then_inc(s_whi, 1)
                            act.activation(hi[:, E * M:], shared[:, :], ACT.Copy, scale=SPLIT).then_inc(s_whi, 1)

                def silu_(it, k):
                    w = width(k % CH)
                    act.wait_ge(s_up, nth(it, K, k))
                    if (due := nth(it, K, k, back=2)) is not None:
                        act.wait_ge(s_prod, due)
                    act.activation(silu[k % 2][:, 0:w], ps_g[k % 2][:, 0:w], ACT.Silu,
                                   scale=SPLIT ** -2).then_inc(s_silu, 1)

                def fetch_hT(it, k):
                    act.wait_ge(s_hTp, nth(it, K, k))
                    if (due := nth(it, K, k, back=2)) is not None:
                        act.wait_ge(s_down, due)
                    if k % CH == 2:
                        act.copy(hT[k % 2][0:M, 0:P], ps_hT[0:M, 0:P]).then_inc(s_hT, 1)
                    else:
                        act.copy(hT[k % 2][:, :], ps_hT[:, :]).then_inc(s_hT, 1)

                steps = {**numbered("silu", silu_, K, 2), **numbered("fetch", fetch_hT, K, 2),
                         "fetch_x": (fetch_x, 1),
                         "sigmoid": (lambda it: rt.function(act, it, ACT.Sigmoid), 1)}
                later(steps, "fetch10 fetch11")
                skewed(act, n, in_order(steps, "silu0 fetch10 silu1 fetch11 silu2 fetch0 fetch_x fetch1 silu3 silu4 fetch2 silu5 "
                                               "sigmoid fetch3 silu6 fetch4 silu7 fetch5 fetch6 silu8 silu9 fetch7 silu10 fetch8 "
                                               "fetch9 silu11"), 6)

            @block.vector
            def _(dve):
                def remainder(it):
                    if first_of(it):
                        n_parts = 0
                        for (hi, lo), routed, shared in ((parts[0], gate_w, sg), (parts[1], up_w, su)):
                            for cols, w in ((slice(0, E * M), routed), (slice(E * M, E * M + M), shared)):
                                n_parts += 1
                                dve.wait_ge(s_whi, n_parts)
                                dve.scalar_tensor_tensor(lo[:, cols], w[:, :], SPLIT, hi[:, cols],
                                                         ALU.mult, ALU.subtract).then_inc(s_wlo, 1)
                    fr.remainder(dve, it)

                dve.wait_ge(rt.s_before, 2)

                def compare(it):
                    dve.wait_ge(rt.s_out, nth(it))
                    rt.compare(dve, rt.act_out)

                def weigh(it):
                    dve.tensor_tensor(rt.act_in[:, :, :], rt.act_out[:, :, :], rt.sel[:, :, :], ALU.mult)
                    dve.drain()
                    rt.reciprocal_of_sum(dve, rt.act_in, eps=1e-20, times=SCALE * SPLIT ** -2)
                    if (due := nth(it, 2 * GROUP, ago=2)) is not None:
                        dve.wait_ge(s_hid, due)
                    dve.tensor_tensor(rt.w[it.par][:, :, :], rt.act_in[:, :, :], rt.wide(rt.one), ALU.mult).then_inc(rt.s_w, 1)

                def add(it, j):
                    x = g.x[:, bass.ts(it.b * GROUP + j, P)]
                    dve.wait_ge(fr.s_xn, nth(it))
                    dve.wait_ge(s_down, nth(it, K, CH * j + 2))
                    dve.scalar_tensor_tensor(x, ps_y[:, 0:P], g.gates[:, 6:7], x, ALU.mult, ALU.add).then_inc(s_x, 1)

                def product(it, k):
                    w = width(k % CH)
                    dve.wait_ge(s_silu, nth(it, K, k))
                    if (due := nth(it, K, k, back=2)) is not None:
                        dve.wait_ge(s_hTp, due)
                    if k % CH == 2:
                        dve.scalar_tensor_tensor(prod[k % 2][:, 0:w], ps_u[k % 2][:, 0:w], SPLIT ** -2, silu[k % 2][:, 0:w],
                                                 ALU.mult, ALU.mult).then_inc(s_prod, 1)
                    else:
                        dve.tensor_tensor(prod[k % 2][:, 0:w], ps_u[k % 2][:, 0:w], silu[k % 2][:, 0:w], ALU.mult).then_inc(s_prod, 1)

                steps = {**numbered("product", product, K, 2), **numbered("add", add, GROUP, 2),
                         "normalize": (lambda it: fr.normalize(dve, it), 1), "statistics": (lambda it: fr.statistics(dve, it), 0),
                         "remainder": (remainder, 1), "logits": (lambda it: rt.fetch(dve, it), 1),
                         "compare": (compare, 1), "order": (lambda it: rt.order(dve), 1), "select": (lambda it: rt.select(dve), 1),
                         "weigh": (weigh, 1)}
                later(steps, "add2 add3")
                skewed(dve, n, in_order(steps, "add2 product0 normalize product1 product2 add3 statistics product3 remainder "
                                               "product4 logits add0 product5 product6 compare product7 add1 product8 order "
                                               "product9 product10 select product11 weigh"), 6)


def l1_xattn(nc, g, a):
    D = 64
    PAIRS = HEADS // 2
    HELD = [6, 6, 4]
    W = CTX + 1
    scale = float(D) ** -0.5
    with Stage(nc, "l1x") as st:
        wqT, wkT = st.sb("wqT", [D, HEADS, P]), st.sb("wkT", [D, HEADS, CTX])
        wvT, wo = st.sb("wvT", [D, HEADS, CTX]), st.sb("wo", [D, HEADS, P])
        qk, vo, bo = st.sb("qk", [P, HEADS * CTX]), st.sb("vo", [P, PAIRS, P]), st.sb("bo", [P, P])
        pair_ctx, ctx1 = st.sb2("pair_ctx", [P, 2 * KEYS]), st.sb2("ctx1", [KEYS, W])
        ctx_hi, ctx_lo = st.sb2("ctx_hi", [KEYS, W], F16), st.sb2("ctx_lo", [KEYS, W], F16)
        s_gated_bo = st.sem("s_gated_bo")
        s_chi, s_clo = st.sem("s_chi"), st.sem("s_clo")
        qT = st.sb2("qT", [P, PAIRS, P])
        recip, o_s, oT = st.sb2("recip", [P, HEADS]), st.sb2("o", [P, HEADS, CTX]), st.sb2("oT", [P, PAIRS, P])
        scores = [st.ps(f"scores{i}") for i in range(3)]
        turned = [st.ps(f"turned{i}") for i in range(2)]
        pa, po, py = st.ps("pa"), st.ps("po"), st.ps("py")
        o_p = po[:, 0:CHUNK * W].rearrange("p (h e) -> p h e", e=W)
        y_p = py[:, 0:P]
        ln = LnFront(st, g, pa[:, 0:P])
        sm = Softmax(st, g, scores, HELD, KEYS, scale, turned, split=True)
        s_w, s_ctx, s_set = st.sem("s_w"), st.sem2("s_ctx"), st.sem("s_set")
        s_pre, s_fused = st.sem("s_pre"), st.sem("s_fused")
        s_q, s_qT, s_recip, s_o, s_oTp, s_oT, s_y, s_x, s_bo = [
            st.sem(n) for n in ("s_q", "s_qT", "s_recip", "s_o", "s_oTp", "s_oT", "s_y", "s_x", "s_bo")]
        weights = [(wqT[:, :, :], a["L1_WqT"]), (wkT[:, :, :], a["L1_WkT"]), (wvT[:, :, :], a["L1_WvT"]),
                   (wo[:, :, :], a["L1_Woh"]), (bo[:, :], a["L1_bo"].partition_broadcast(P))]

        with nc.Block() as block:
            @block.sync
            def _(sp):
                for dst, src in weights:
                    sp.dma_start(dst, src).then_inc(s_w, 16)
                sp.wait_ge(s_set, 4)

                def context(it):
                    p = it.par
                    if (due := nth(it, 3, ago=2)) is not None:
                        sp.wait_ge(sm.s_scores, due)
                    if (due := nth(it, 4, ago=2)) is not None:
                        sp.wait_ge(sm.s_values, due)
                    one = g.ctxT_d[:, bass.ds(it.b, 1), :].rearrange("c b t -> c (b t)")
                    sp.dma_start(pair_ctx[p][0:CTX, 0:KEYS], one).then_inc(s_ctx[p], 16)
                    sp.dma_start(pair_ctx[p][CTX:P, KEYS:2 * KEYS], one).then_inc(s_ctx[p], 16)
                    sp.dma_start(ctx1[p][:, 0:CTX], g.ctx_d[:, bass.ds(it.b, 1), :].rearrange("t b c -> t (b c)")).then_inc(s_ctx[p], 16)

                skewed(sp, g.B, [(context, 0)], 2)

            @block.gpsimd
            def _(pool):
                for i in range(2):
                    pool.memset(pair_ctx[i][:, :], 0.0).then_inc(s_set, 1)
                    pool.memset(ctx1[i][:, CTX:W], 1.0).then_inc(s_set, 1)

                def add_bias(it):
                    x = g.x[:, bass.ts(it.b, P)]
                    pool.wait_ge(ln.s_xn, nth(it))
                    pool.tensor_tensor(x, x, bo[:, :], ALU.add).then_inc(s_bo, 1)

                pool.wait_ge(s_gated_bo, 1)
                skewed(pool, g.B, [(add_bias, 2), (lambda it: ln.inverse_deviation(pool, it), 0)], 4)

            @block.tensor
            def _(pe):
                pe.wait_ge(s_w, 16 * len(weights))
                banks = [scores[0], scores[1], turned[0], turned[1]]
                for h in range(HEADS):
                    last = pe.matmul(banks[h // 8][:, (h % 8) * CTX:(h % 8 + 1) * CTX], wqT[:, h, :], wkT[:, h, :],
                                     start=True, stop=True)
                    if h % 8 == 7:
                        last.then_inc(s_pre, 1)
                for h in range(HEADS):
                    r, i = CTX * (h % 2), h // 2
                    last = pe.matmul(banks[2 + i // 4][r:r + CTX, (i % 4) * P:(i % 4 + 1) * P], wvT[:, h, :], wo[:, h, :],
                                     start=True, stop=True)
                    if h % 8 == 7:
                        last.then_inc(s_pre, 1)
                pe.wait_ge(s_fused, 4)

                def turn(it):
                    if (due := nth(it, 2, ago=1)) is not None:
                        pe.wait_ge(s_qT, due)
                    ln.turn(pe, it)

                def queries(it, c):
                    if c == 0:
                        pe.wait_ge(ln.s_xT, nth(it))
                    else:
                        pe.wait_ge(s_qT, nth(it, 2, 0))
                    for k in range(4):
                        last = pe.matmul(pa[:, k * P:(k + 1) * P], qk[:, (4 * c + k) * P:(4 * c + k + 1) * P],
                                         ln.xT[it.par][:, :], start=True, stop=True)
                    last.then_inc(s_q, 1)

                def score(it, c):
                    pe.wait_ge(s_ctx[it.par], loads(it, 3))
                    pe.wait_ge(s_qT, nth(it, 2))
                    if (due := nth(it, 3, c, back=3)) is not None:
                        pe.wait_ge(sm.s_shift, due)
                    for h in range(sm.first[c], sm.first[c + 1], 2):
                        r = (h - sm.first[c]) * KEYS
                        last = pe.matmul(scores[c][:, r:r + 2 * KEYS], qT[it.par][:, h // 2, :], pair_ctx[it.par][:, :],
                                         start=True, stop=True)
                    last.then_inc(sm.s_scores, 1)

                def weigh(it, c):
                    if c == 0:
                        pe.wait_ge(s_clo, nth(it))
                    if (due := nth(it, 4, c, back=1)) is not None:
                        pe.wait_ge(s_o, due)
                    sm.times_values(pe, it, c, lambda h: o_p[:, h % CHUNK, :], lambda h: (ctx_hi[it.par][:, :], ctx_lo[it.par][:, :]))

                def turn_o(it, c):
                    pe.wait_ge(s_o, nth(it, 4))
                    if c == 0:
                        if (due := nth(it, ago=1)) is not None:
                            pe.wait_ge(s_x, due)
                    else:
                        pe.wait_ge(s_oT, nth(it, 2, 0))
                    for k in range(4):
                        i = 4 * c + k
                        last = pe.transpose(py[:, k * P:(k + 1) * P],
                                            o_s[it.par][:, 2 * i:2 * i + 2, :].rearrange("p h e -> p (h e)"), g.ident[:, :])
                    last.then_inc(s_oTp, 1)

                def output(it):
                    pe.wait_ge(s_oT, nth(it, 2))
                    for i in range(PAIRS):
                        last = pe.matmul(y_p, oT[it.par][:, i, :], vo[:, i, :], start=(i == 0), stop=(i == PAIRS - 1))
                    last.then_inc(s_y, 1)

                steps = {**numbered("turn_p", lambda it, c: sm.turn(pe, it, c), 4, 3), **numbered("score", score, 3, 2),
                         **numbered("weigh", weigh, 4, 3), "turn": (turn, 1), **numbered("queries", queries, 2, 1),
                         **numbered("turn_o", turn_o, 2, 4), "output": (output, 4)}
                steps["turn_p0"] = (steps["turn_p0"][0], 2)
                skewed(pe, g.B, in_order(steps, "turn_p1 turn_o0 score0 turn_p2 weigh0 turn_p3 turn score1 turn_o1 weigh1 queries0 "
                                                "score2 weigh2 turn_p0 weigh3 output queries1"), 6)

            @block.scalar
            def _(act):
                for i, (bank, dst) in enumerate([(scores[0], qk[:, 0:BANK]), (scores[1], qk[:, BANK:2 * BANK]),
                                                 (turned[0], vo[:, 0:4, :].rearrange("p i d -> p (i d)")),
                                                 (turned[1], vo[:, 4:8, :].rearrange("p i d -> p (i d)"))]):
                    act.wait_ge(s_pre, i + 1)
                    act.copy(dst, bank[:, :]).then_inc(s_fused, 1)

                def round_context(it):
                    act.wait_ge(s_ctx[it.par], loads(it, 3))
                    if (due := nth(it, 4, ago=2)) is not None:
                        act.wait_ge(sm.s_values, due)
                    act.activation(ctx_hi[it.par][:, :], ctx1[it.par][:, :], ACT.Copy, scale=SPLIT).then_inc(s_chi, 1)

                def fetch_q(it, c):
                    act.wait_ge(s_q, nth(it, 2, c))
                    if (due := nth(it, 3, ago=2)) is not None:
                        act.wait_ge(sm.s_scores, due)
                    act.copy(qT[it.par][:, 4 * c:4 * c + 4, :].rearrange("p i t -> p (i t)"), pa[:, :]).then_inc(s_qT, 1)

                def fetch_o(it, c):
                    act.wait_ge(s_oTp, nth(it, 2, c))
                    if (due := nth(it, ago=2)) is not None:
                        act.wait_ge(s_y, due)
                    act.copy(oT[it.par][:, 4 * c:4 * c + 4, :].rearrange("p i t -> p (i t)"), py[:, :]).then_inc(s_oT, 1)

                steps = {**numbered("fetch_p", lambda it, c: sm.fetch(act, it, c), 4, 3),
                         **numbered("exp", lambda it, c: sm.exponential(act, it, c), 3, 2),
                         **numbered("fetch_o", fetch_o, 2, 4), "context": (round_context, 1), "fetch_x": (lambda it: ln.fetch(act, it, s_q, 2), 1),
                         **numbered("fetch_q", fetch_q, 2, 1)}
                skewed(act, g.B, in_order(steps, "fetch_p0 fetch_p1 fetch_o0 fetch_p2 fetch_x exp0 fetch_p3 fetch_o1 fetch_q0 exp1 "
                                                 "exp2 fetch_q1 context"), 6)

            @block.vector
            def _(dve):
                dve.wait_ge(s_w, 16 * len(weights))
                dve.tensor_scalar(bo[:, :], bo[:, :], g.gates[:, 1:2], None, ALU.mult).then_inc(s_gated_bo, 1)

                def divide(it, c):
                    p = it.par
                    dve.wait_ge(sm.s_values, nth(it, 4, c))
                    if (due := nth(it, 4, c, back=8)) is not None:
                        dve.wait_ge(s_o, due)
                    dve.reciprocal(recip[p][:, 4 * c:4 * c + 4], o_p[:, :, CTX]).then_inc(s_recip, 1)
                    dve.wait_ge(s_recip, nth(it, 4, c))
                    if (due := nth(it, 2, ago=2)) is not None:
                        dve.wait_ge(s_oTp, due)
                    dve.tensor_tensor(o_s[p][:, 4 * c:4 * c + 4, :], o_p[:, :, 0:CTX],
                                      recip[p][:, 4 * c:4 * c + 4].unsqueeze(2).to_broadcast([P, CHUNK, CTX]),
                                      ALU.mult).then_inc(s_o, 1)

                def context_remainder(it):
                    dve.wait_ge(s_chi, nth(it))
                    dve.scalar_tensor_tensor(ctx_lo[it.par][:, :], ctx1[it.par][:, :], SPLIT, ctx_hi[it.par][:, :],
                                             ALU.mult, ALU.subtract).then_inc(s_clo, 1)

                def add(it):
                    x = g.x[:, bass.ts(it.b, P)]
                    dve.wait_ge(ln.s_xn, nth(it))
                    dve.wait_ge(s_bo, nth(it))
                    dve.wait_ge(s_y, nth(it))
                    dve.scalar_tensor_tensor(x, y_p, g.gates[:, 1:2], x, ALU.mult, ALU.add).then_inc(s_x, 1)

                steps = {**numbered("maximum", lambda it, c: sm.maximum(dve, it, c), 3, 2),
                         **numbered("shift", lambda it, c: sm.shift(dve, it, c), 3, 2), **numbered("divide", divide, 4, 3),
                         "statistics": (lambda it: ln.statistics(dve, it), 0), "normalize": (lambda it: ln.normalize(dve, it), 1),
                         **numbered("remainder", lambda it, c: sm.remainder(dve, it, c), 4, 3),
                         "context": (context_remainder, 2), "add": (add, 4)}
                later(steps, "divide3")
                skewed(dve, g.B, in_order(steps, "normalize divide3 remainder0 remainder1 maximum0 divide0 shift0 remainder2 maximum1 context divide1 "
                                                 "remainder3 divide2 maximum2 statistics shift1 shift2 add"), 6)


class Norm:

    def __init__(self, st, g, name, rows, width):
        self.g, self.rows, self.width = g, rows, width
        self.stats, self.mv = st.sb(f"{name}_st", [rows, 6]), st.sb2(f"{name}_mv", [rows, 2])
        self.ve, self.rstd = st.sb2(f"{name}_ve", [rows, 1]), st.sb2(f"{name}_rs", [rows, 1])
        self.s_mv, self.s_ve, self.s_rstd, self.s_hat, self.s_pass = [
            st.sem(f"{name}_{k}") for k in ("s_mv", "s_ve", "s_rstd", "s_hat", "s_pass")]

    def statistics(self, dve, it, src):
        if (due := nth(it, ago=2)) is not None:
            dve.wait_ge(self.s_hat, due)
        if (due := nth(it, ago=2)) is not None:
            dve.wait_ge(self.s_ve, due)
        dve.sem_inc(self.s_pass, 1)
        dve.bn_stats(self.stats[:, :], src)
        dve.drain()
        dve.bn_aggr(self.mv[it.par][:, :], self.stats[:, :]).then_inc(self.s_mv, 1)
        dve.drain()

    def inverse_deviation(self, pool, it):
        p, r = it.par, self.rows
        pool.wait_ge(self.s_mv, nth(it))
        if (due := nth(it, ago=2)) is not None:
            pool.wait_ge(self.s_rstd, due)
        pool.tensor_tensor(self.ve[p][:, :], self.mv[p][:, 1:2], self.g.eps[0:r, 0:1], ALU.add).then_inc(self.s_ve, 1)
        pool.wait_ge(self.s_ve, nth(it))
        if (due := nth(it, ago=2)) is not None:
            pool.wait_ge(self.s_hat, due)
        pool.tensor_tensor(self.rstd[p][:, :], self.ve[p][:, :], self.g.minus_half[0:r, 0:1], ALU.pow).then_inc(self.s_rstd, 1)

    def hat(self, dve, it, src, dst):
        p = it.par
        dve.wait_ge(self.s_rstd, nth(it))
        dve.tensor_scalar(dst, src, self.mv[p][:, 0:1], self.rstd[p][:, 0:1], ALU.subtract, ALU.mult).then_inc(self.s_hat, 1)


def l3_attention(nc, g, a, name, pre, first):
    D = 32
    G4 = P // D
    J = HEADS // G4
    T = P if first else KEYS
    C = P if first else CTX
    scale = float(D) ** -0.5
    with Stage(nc, name) as st:
        wq, wk, wv = st.sb("wq", [P, HEADS * D]), st.sb("wk", [C, HEADS * D]), st.sb("wv", [C, HEADS * D])
        li1, bias, col = st.sb("li1", [P, J, P]), st.sb("bias", [P, P]), st.sb("col", [P, 4])
        ln1_g, ln1_b = st.sb("ln1_g", [P, P]), st.sb("ln1_b", [P, P])
        xa, xh = st.sb2("xa", [P, P]), st.sb2("xh", [P, P])
        ctx_in, yh = st.sb2("ctx_in", [KEYS, CTX]), st.sb2("yh", [KEYS, CTX])
        xT, yT = st.sb2("xT", [P, P]), st.sb2("yT", [C, T])
        qT, kT, vals = st.sb2("qT", [P, J, P]), st.sb2("kT", [P, J, T]), st.sb2("vals", [T, HEADS * D])
        keys = st.sb2("keys", [P, J, G4, T])
        if not first:
            vhi, vlo = st.sb2("vhi", [T, HEADS * D], F16), st.sb2("vlo", [T, HEADS * D], F16)
            s_vhi, s_vlo = st.sem("s_vhi"), st.sem("s_vlo")
        total, recip = st.sb2("total", [P, HEADS]), st.sb2("recip", [P, HEADS])
        o_s, oT = st.sb2("o", [P, HEADS * D]), st.sb2("oT", [P, J, P])
        later = st.sb("later", [P, T])
        scores = [st.ps(f"scores{i}") for i in range(4)]
        turned = [st.ps(f"turned{i}") for i in range(2)]
        pa, po = st.ps("pa"), st.ps("po")
        sm = Softmax(st, g, scores, [4] * 4, T, scale, turned, split=not first)
        n3 = Norm(st, g, "n3", P, P)
        if first:
            n1, n2 = Norm(st, g, "n1", P, P), Norm(st, g, "n2", P, P)
            s_aff = st.sem("s_aff")
        else:
            ny = Norm(st, g, "ny", KEYS, CTX)
        s_w, s_ctx, s_mask, s_x1 = st.sem("s_w"), st.sem2("s_ctx"), st.sem("s_later"), st.sem("s_x1")
        s_turn, s_xT, s_q, s_qT, s_k, s_kT, s_v, s_vals, s_keys = [
            st.sem(n) for n in ("s_turn", "s_xT", "s_q", "s_qT", "s_k", "s_kT", "s_v", "s_vals", "s_keys")]
        s_sum, s_masked, s_recip, s_o, s_oTp, s_oT, s_y, s_out, s_bias = [
            st.sem(n) for n in ("s_sum", "s_masked", "s_recip", "s_o", "s_oTp", "s_oT", "s_y", "s_out", "s_bias")]
        k_ = lambda n: a[f"{pre}_{n}"]
        weights = [(wq[:, :], k_("wq")), (wk[:, :], k_("wk")), (wv[:, :], k_("wv")), (li1[:, :, :], k_("li1_w")),
                   (bias[:, :], k_("li1_b").partition_broadcast(P)), (col[:, 0:1], k_("lnx_g")), (col[:, 1:2], k_("lnx_b")),
                   (col[0:C, 2:3], k_("lny_g")), (col[0:C, 3:4], k_("lny_b"))]
        if first:
            weights += [(ln1_g[:, :], a["ln1_g"].partition_broadcast(P)), (ln1_b[:, :], a["ln1_b"].partition_broadcast(P))]
        all_weights = 16 * len(weights)

        def z(it):
            return g.z[:, bass.ts(it.b, P)]

        with nc.Block() as block:
            @block.sync
            def _(sp):
                for dst, src in weights:
                    sp.dma_start(dst, src).then_inc(s_w, 16)
                if not first:
                    def context(it):
                        if (due := nth(it, ago=2)) is not None:
                            sp.wait_ge(ny.s_hat, due)
                        sp.dma_start(ctx_in[it.par][:, :], g.ctx_d[:, bass.ds(it.b, 1), :].rearrange("t b c -> t (b c)")).then_inc(s_ctx[it.par], 16)

                    skewed(sp, g.B, [(context, 0)], 2)

            @block.gpsimd
            def _(pool):
                if first:
                    pool.memset(later[:, :], 1.0).then_inc(s_mask, 1)
                    pool.wait_ge(s_mask, 1)
                    pool.affine_select(out=later[:, :], in_=later[:, :], compare_op=ALU.is_gt, fill=0.0,
                                       base=0, pattern=[[1, T]], channel_multiplier=-1).then_inc(s_mask, 1)
                    pool.wait_ge(s_mask, 2)

                def spread(it):
                    pool.wait_ge(s_kT, nth(it))
                    if (due := nth(it, 4, ago=2)) is not None:
                        pool.wait_ge(sm.s_scores, due)
                    pool.tensor_tensor(keys[it.par][:, :, :, :],
                                       kT[it.par][:, :, :].unsqueeze(2).to_broadcast([P, J, G4, T]),
                                       g.head32[:, :].unsqueeze(1).unsqueeze(3).to_broadcast([P, J, G4, T]),
                                       ALU.mult).then_inc(s_keys, 1)

                def begin_y(it):
                    if first_of(it):
                        pool.wait_ge(s_w, all_weights)
                    pool.tensor_tensor(g.y[:, bass.ts(it.b, P)], z(it), bias[:, :], ALU.add).then_inc(s_bias, 1)

                def drop_earlier(it, c):
                    v = sm.probs[it.par][:, 4 * c:4 * c + 4, :]
                    pool.wait_ge(s_sum, nth(it, 4, c))
                    pool.tensor_tensor(v, v, later[:, :].unsqueeze(1).to_broadcast([P, 4, T]), ALU.mult).then_inc(s_masked, 1)

                steps = {"spread": (spread, 3), "deviation3": (lambda it: n3.inverse_deviation(pool, it), 2 if first else 1)}
                if first:
                    steps.update(deviation1=(lambda it: n1.inverse_deviation(pool, it), 0),
                                 deviation2=(lambda it: n2.inverse_deviation(pool, it), 1), **numbered("drop", drop_earlier, 4, 4))
                    names = "spread deviation3 deviation2 deviation1 drop0 drop1 drop2 drop3"
                else:
                    steps.update(deviation_y=(lambda it: ny.inverse_deviation(pool, it), 2), begin_y=(begin_y, 4))
                    names = "deviation_y spread deviation3 begin_y"
                skewed(pool, g.B, in_order(steps, names), 8)

            @block.tensor
            def _(pe):
                def turn(it):
                    pe.wait_ge(n3.s_hat, nth(it))
                    if (due := nth(it, ago=1)) is not None:
                        pe.wait_ge(s_vals if first else s_vlo, due)
                    if not first:
                        pe.wait_ge(ny.s_hat, nth(it))
                    last = pe.transpose(pa[:, 0:P], xh[it.par][:, :], g.ident[:, :])
                    if not first:
                        last = pe.transpose(pa[0:CTX, P:P + KEYS], yh[it.par][:, :], g.ident[0:KEYS, 0:KEYS])
                    last.then_inc(s_turn, 1)

                def queries(it):
                    if first_of(it):
                        pe.wait_ge(s_w, all_weights)
                    pe.wait_ge(s_xT, nth(it))
                    for j in range(J):
                        last = pe.matmul(pa[:, j * P:(j + 1) * P], wq[:, j * P:(j + 1) * P], xT[it.par][:, :], start=True, stop=True)
                    last.then_inc(s_q, 1)

                def keys_of(it):
                    pe.wait_ge(s_qT, nth(it))
                    for j in range(J):
                        last = pe.matmul(pa[:, j * T:(j + 1) * T], wk[:, j * P:(j + 1) * P], yT[it.par][:, :], start=True, stop=True)
                    last.then_inc(s_k, 1)

                def values(it):
                    pe.wait_ge(s_kT, nth(it))
                    pe.matmul(pa[0:T, :], yT[it.par][:, :], wv[:, :], start=True, stop=True).then_inc(s_v, 1)

                def score(it, c):
                    pe.wait_ge(s_keys, nth(it))
                    pe.wait_ge(s_qT, nth(it))
                    if (due := nth(it, 4, c, back=4)) is not None:
                        pe.wait_ge(sm.s_shift, due)
                    pe.matmul(scores[c][:, 0:G4 * T], qT[it.par][:, c, :], keys[it.par][:, c, :, :].rearrange("p h t -> p (h t)"),
                              start=True, stop=True).then_inc(sm.s_scores, 1)

                def turn_p(it, c):
                    sm.turn(pe, it, c, s_masked if first else None, 4)

                def weigh(it, c):
                    if c == 0:
                        pe.wait_ge(s_vals if first else s_vlo, nth(it))
                        if (due := nth(it, ago=1)) is not None:
                            pe.wait_ge(s_out, due)
                    def values_of(h):
                        cols = slice(h * D, (h + 1) * D)
                        return vals[it.par][:, cols] if first else (vhi[it.par][:, cols], vlo[it.par][:, cols])

                    sm.times_values(pe, it, c, lambda h: po[:, h * D:(h + 1) * D], values_of)

                def turn_o(it):
                    pe.wait_ge(s_o, nth(it))
                    for j in range(J):
                        last = pe.transpose(po[:, j * P:(j + 1) * P], o_s[it.par][:, j * P:(j + 1) * P], g.ident[:, :])
                    last.then_inc(s_oTp, 1)

                def output(it):
                    pe.wait_ge(s_oT, nth(it))
                    for j in range(J):
                        last = pe.matmul(po[:, 0:P], oT[it.par][:, j, :], li1[:, j, :], start=(j == 0), stop=(j == J - 1))
                    last.then_inc(s_y, 1)

                steps = {**numbered("turn_p", turn_p, 4, 5), **numbered("score", score, 4, 4), **numbered("weigh", weigh, 4, 5),
                         "turn": (turn, 3), "queries": (queries, 3), "keys": (keys_of, 3), "values": (values, 3),
                         "turn_o": (turn_o, 6), "output": (output, 6)}
                if first:
                    names = ("score0 turn_o turn score1 score2 turn_p0 output queries score3 keys turn_p1 weigh0 turn_p2 weigh1 "
                             "turn_p3 weigh2 weigh3 values")
                else:
                    names = ("turn_p0 score0 turn_p1 turn score1 turn_o queries output turn_p2 score2 weigh0 turn_p3 keys "
                             "weigh1 score3 weigh2 values weigh3")
                skewed(pe, g.B, in_order(steps, names), 8)

            @block.scalar
            def _(act):
                act.wait_ge(s_w, all_weights)

                def fetch_x(it):
                    p = it.par
                    act.wait_ge(s_turn, nth(it))
                    if (due := nth(it, ago=2)) is not None:
                        act.wait_ge(s_q, due)
                    act.activation(xT[p][:, :], pa[:, 0:P], ACT.Identity, bias=col[:, 1:2], scale=col[:, 0:1])
                    if (due := nth(it, ago=2)) is not None:
                        act.wait_ge(s_v, due)
                    src = pa[:, 0:P] if first else pa[0:CTX, P:P + KEYS]
                    act.activation(yT[p][:, :], src, ACT.Identity, bias=col[0:C, 3:4], scale=col[0:C, 2:3]).then_inc(s_xT, 1)

                def fetch_q(it):
                    act.wait_ge(s_q, nth(it))
                    if (due := nth(it, 4, ago=2)) is not None:
                        act.wait_ge(sm.s_scores, due)
                    act.copy(qT[it.par][:, :, :].rearrange("p j t -> p (j t)"), pa[:, :]).then_inc(s_qT, 1)

                def fetch_k(it):
                    act.wait_ge(s_k, nth(it))
                    if (due := nth(it, ago=2)) is not None:
                        act.wait_ge(s_keys, due)
                    act.copy(kT[it.par][:, :, :].rearrange("p j t -> p (j t)"), pa[:, 0:J * T]).then_inc(s_kT, 1)

                def fetch_v(it):
                    act.wait_ge(s_v, nth(it))
                    if (due := nth(it, 4, ago=2)) is not None:
                        act.wait_ge(sm.s_values, due)
                    if first:
                        act.copy(vals[it.par][:, :], pa[0:T, :]).then_inc(s_vals, 1)
                    else:
                        act.activation(vhi[it.par][:, :], pa[0:T, :], ACT.Copy, scale=SPLIT).then_inc(s_vhi, 1)

                def fetch_o(it):
                    act.wait_ge(s_oTp, nth(it))
                    if (due := nth(it, ago=2)) is not None:
                        act.wait_ge(s_y, due)
                    act.activation(oT[it.par][:, :, :].rearrange("p j t -> p (j t)"), po[:, :], ACT.Copy,
                                   scale=1.0 if first else 1.0 / (SPLIT * SPLIT_EXP)).then_inc(s_oT, 1)

                steps = {**numbered("fetch_p", lambda it, c: sm.fetch(act, it, c), 4, 5),
                         **numbered("exp", lambda it, c: sm.exponential(act, it, c), 4, 4), "fetch_x": (fetch_x, 3),
                         "fetch_q": (fetch_q, 3), "fetch_k": (fetch_k, 3), "fetch_v": (fetch_v, 3), "fetch_o": (fetch_o, 6)}
                if first:
                    names = "fetch_o fetch_x fetch_p0 exp0 fetch_q exp1 fetch_k fetch_p1 exp2 fetch_p2 exp3 fetch_p3 fetch_v"
                else:
                    names = "fetch_p0 fetch_x fetch_o fetch_p1 fetch_q fetch_p2 exp0 exp1 fetch_k fetch_p3 exp2 exp3 fetch_v"
                skewed(act, g.B, in_order(steps, names), 8)

            @block.vector
            def _(dve):
                def stats1(it):
                    n1.statistics(dve, it, g.x[:, bass.ts(it.b, P)])

                def stats2(it):
                    if (due := nth(it, ago=2)) is not None:
                        dve.wait_ge(s_x1, due)
                    n1.hat(dve, it, g.x[:, bass.ts(it.b, P)], xa[it.par][:, :])
                    dve.wait_ge(n1.s_hat, nth(it))
                    n2.statistics(dve, it, xa[it.par][:, :])

                def stats3(it):
                    if first_of(it):
                        dve.wait_ge(s_w, all_weights)
                    v = xa[it.par][:, :]
                    n2.hat(dve, it, v, v)
                    dve.wait_ge(n2.s_hat, nth(it))
                    dve.tensor_tensor(v, v, ln1_g[:, :], ALU.mult).then_inc(s_aff, 1)
                    dve.wait_ge(s_aff, nth(it))
                    dve.tensor_tensor(z(it), v, ln1_b[:, :], ALU.add).then_inc(s_x1, 1)
                    dve.wait_ge(s_x1, nth(it))
                    n3.statistics(dve, it, z(it))

                def stats_z(it):
                    n3.statistics(dve, it, z(it))
                    dve.wait_ge(s_ctx[it.par], loads(it))
                    ny.statistics(dve, it, ctx_in[it.par][:, :])

                def hat(it):
                    if (due := nth(it, ago=2)) is not None:
                        dve.wait_ge(s_turn, due)
                    n3.hat(dve, it, z(it), xh[it.par][:, :])
                    if not first:
                        ny.hat(dve, it, ctx_in[it.par][:, :], yh[it.par][:, :])

                def value_remainder(it):
                    dve.wait_ge(s_vhi, nth(it))
                    dve.scalar_tensor_tensor(vlo[it.par][:, :], pa[0:T, :], SPLIT, vhi[it.par][:, :],
                                             ALU.mult, ALU.subtract).then_inc(s_vlo, 1)

                def row_sum(it, c):
                    dve.wait_ge(sm.s_exp, nth(it, 4, c))
                    if (due := nth(it, ago=2)) is not None:
                        dve.wait_ge(s_recip, due)
                    dve.tensor_reduce(total[it.par][:, 4 * c:4 * c + 4], sm.probs[it.par][:, 4 * c:4 * c + 4, :], AX,
                                      ALU.add).then_inc(s_sum, 1)

                def divide(it):
                    p = it.par
                    dve.wait_ge(s_sum, nth(it, 4))
                    if (due := nth(it, ago=2)) is not None:
                        dve.wait_ge(s_o, due)
                    dve.reciprocal(recip[p][:, :], total[p][:, :]).then_inc(s_recip, 1)
                    dve.wait_ge(s_recip, nth(it))
                    dve.wait_ge(sm.s_values, nth(it, 4))
                    if (due := nth(it, ago=2)) is not None:
                        dve.wait_ge(s_oTp, due)
                    dve.tensor_tensor(o_s[p][:, :].rearrange("p (h d) -> p h d", d=D), po[:, :].rearrange("p (h d) -> p h d", d=D),
                                      recip[p][:, :].unsqueeze(2).to_broadcast([P, HEADS, D]), ALU.mult).then_inc(s_o, 1)

                def add(it):
                    y = g.y[:, bass.ts(it.b, P)]
                    if first:
                        dve.tensor_tensor(y, z(it), bias[:, :], ALU.add).then_inc(s_bias, 1)
                    dve.wait_ge(s_bias, nth(it))
                    dve.wait_ge(s_y, nth(it))
                    dve.tensor_tensor(y, po[:, 0:P], y, ALU.add).then_inc(s_out, 1)

                steps = {**numbered("maximum", lambda it, c: sm.maximum(dve, it, c), 4, 4),
                         **numbered("shift", lambda it, c: sm.shift(dve, it, c), 4, 4), **numbered("sum", row_sum, 4, 4),
                         "hat": (hat, 3 if first else 2), "divide": (divide, 5 if first else 6), "add": (add, 6)}
                if first:
                    steps.update(stats1=(stats1, 0), stats2=(stats2, 1), stats3=(stats3, 2))
                    names = ("hat stats3 maximum0 stats2 shift0 maximum1 add shift1 maximum2 maximum3 shift2 shift3 sum0 "
                             "sum1 stats1 sum2 sum3 divide")
                else:
                    steps.update(stats_z=(stats_z, 2), values=(value_remainder, 3),
                                 **numbered("remainder", lambda it, c: sm.remainder(dve, it, c), 4, 5))
                    names = ("divide maximum0 remainder0 shift0 stats_z add remainder1 maximum1 shift1 maximum2 remainder2 "
                             "sum0 shift2 remainder3 maximum3 sum2 shift3 sum1 hat sum3 values")
                skewed(dve, g.B, in_order(steps, names), 8)


class GroupNorm:

    def __init__(self, st, g, name):
        self.g, self.stats, self.mv = g, st.sb(f"{name}_st", [P, GROUP, 6]), st.sb2(f"{name}_mv", [P, GROUP, 2])
        self.ve, self.rstd = st.sb2(f"{name}_ve", [P, GROUP]), st.sb2(f"{name}_rs", [P, GROUP])
        self.s_mv, self.s_ve, self.s_rstd, self.s_hat, self.s_pass = [
            st.sem(f"{name}_{k}") for k in ("s_mv", "s_ve", "s_rstd", "s_hat", "s_pass")]

    def statistics(self, dve, it, src):
        if (due := nth(it, ago=2)) is not None:
            dve.wait_ge(self.s_hat, due)
            dve.wait_ge(self.s_ve, due)
        dve.sem_inc(self.s_pass, 1)
        for j in range(GROUP):
            dve.bn_stats(self.stats[:, j, :], src(j))
        dve.drain()
        for j in range(GROUP):
            last = dve.bn_aggr(self.mv[it.par][:, j, :], self.stats[:, j, :])
        last.then_inc(self.s_mv, 1)
        dve.drain()

    def inverse_deviation(self, pool, it):
        p = it.par
        pool.wait_ge(self.s_mv, nth(it))
        if (due := nth(it, ago=2)) is not None:
            pool.wait_ge(self.s_rstd, due)
        pool.tensor_tensor(self.ve[p][:, :], self.mv[p][:, :, 1], self.g.eps[:, :], ALU.add).then_inc(self.s_ve, 1)
        pool.wait_ge(self.s_ve, nth(it))
        if (due := nth(it, ago=2)) is not None:
            pool.wait_ge(self.s_hat, due)
        pool.tensor_tensor(self.rstd[p][:, :], self.ve[p][:, :], self.g.minus_half[:, :], ALU.pow).then_inc(self.s_rstd, 1)

    def hat(self, dve, it, src, dst):
        p = it.par
        dve.wait_ge(self.s_rstd, nth(it))
        for j in range(GROUP):
            last = dve.tensor_scalar(dst(j), src(j), self.mv[p][:, j, 0:1], self.rstd[p][:, j:j + 1], ALU.subtract, ALU.mult)
        last.then_inc(self.s_hat, 1)


def l3_mlp(nc, g, a, name, pre, first):
    F = 4 * P
    FT = F // P
    W = GROUP * P
    n = g.B // GROUP
    with Stage(nc, name) as st:
        li2, li3, b3 = st.sb("li2", [P, F]), st.sb("li3", [P, FT, P]), st.sb("b3", [P, P])
        b2, col = st.sb("b2", [P, FT]), st.sb("col", [P, 2])
        ln2_g, ln2_b = st.sb("ln2_g", [P, P]), st.sb("ln2_b", [P, P])
        yh, yT, acc = st.sb2("yh", [P, W]), st.sb2("yT", [P, W]), st.sb2("acc", [P, W])
        hT = st.sb2("hT", [P, FT, W])
        ps_t, ps_h, ps_y = st.ps("t"), [st.ps(f"h{t}") for t in range(FT)], [st.ps(f"y{i}") for i in range(2)]
        n3 = GroupNorm(st, g, "n3")
        if first:
            n2 = GroupNorm(st, g, "n2")
        s_w, s_turn, s_yT, s_h, s_hT, s_y, s_a1, s_a2, s_sum, s_m, s_done = [
            st.sem(k) for k in ("s_w", "s_turn", "s_yT", "s_h", "s_hT", "s_y", "s_a1", "s_a2", "s_sum", "s_m", "s_done")]
        k_ = lambda n: a[f"{pre}_{n}"]
        weights = [(li2[:, :], k_("li2_w")), (li3[:, :, :], k_("li3_w")), (b3[:, :], k_("li3_b").partition_broadcast(P)),
                   (b2[:, :], k_("li2_b")), (col[:, 0:1], k_("ln3_g")), (col[:, 1:2], k_("ln3_b"))]
        if first:
            weights += [(ln2_g[:, :], a["ln2_g"].partition_broadcast(P)), (ln2_b[:, :], a["ln2_b"].partition_broadcast(P))]
        all_weights = 16 * len(weights)

        def group(v, it):
            return v[:, bass.ts(it.b, W)]

        def rows(v):
            return v[:, :].unsqueeze(1).to_broadcast([P, GROUP, P])

        def wide(v):
            return v.rearrange("p (j d) -> p j d", d=P)

        with nc.Block() as block:
            @block.sync
            def _(sp):
                for dst, src in weights:
                    sp.dma_start(dst, src).then_inc(s_w, 16)

            @block.gpsimd
            def _(pool):
                def begin_sum(it):
                    if first_of(it):
                        pool.wait_ge(s_w, all_weights)
                    c = acc[it.par][:, :]
                    if (due := nth(it, ago=2)) is not None:
                        pool.wait_ge(s_done, due)
                    pool.tensor_tensor(c, group(g.y, it), group(g.z, it), ALU.add).then_inc(s_a1, 1)
                    pool.wait_ge(s_a1, nth(it))
                    pool.tensor_tensor(wide(c), wide(c), rows(b3), ALU.add).then_inc(s_a2, 1)

                def affine(it):
                    c = acc[it.par][:, :]
                    pool.wait_ge(n2.s_hat, nth(it))
                    pool.tensor_tensor(wide(c), wide(c), rows(ln2_g), ALU.mult).then_inc(s_m, 1)
                    pool.wait_ge(s_m, nth(it))
                    pool.tensor_tensor(wide(group(g.z, it)), wide(c), rows(ln2_b), ALU.add).then_inc(s_done, 1)

                steps = {"deviation3": (lambda it: n3.inverse_deviation(pool, it), 0), "begin": (begin_sum, 2)}
                names = "begin deviation3"
                if first:
                    steps.update(deviation2=(lambda it: n2.inverse_deviation(pool, it), 3), affine=(affine, 4))
                    names = "deviation3 affine deviation2 begin"
                skewed(pool, n, in_order(steps, names), 6)

            @block.tensor
            def _(pe):
                def turn(it):
                    pe.wait_ge(n3.s_hat, nth(it))
                    if (due := nth(it, ago=1)) is not None:
                        pe.wait_ge(s_yT, due)
                    for j in range(GROUP):
                        last = pe.transpose(ps_t[:, j * P:(j + 1) * P], yh[it.par][:, j * P:(j + 1) * P], g.ident[:, :])
                    last.then_inc(s_turn, 1)

                def hidden(it, t):
                    if first_of(it):
                        pe.wait_ge(s_w, all_weights)
                    pe.wait_ge(s_yT, nth(it))
                    if (due := nth(it, FT, t, back=FT)) is not None:
                        pe.wait_ge(s_hT, due)
                    pe.matmul(ps_h[t][:, :], li2[:, t * P:(t + 1) * P], yT[it.par][:, :], start=True, stop=True).then_inc(s_h, 1)

                def output(it, j):
                    pe.wait_ge(s_hT, nth(it, FT))
                    if (due := nth(it, ago=2)) is not None:
                        pe.wait_ge(s_sum, due)
                    for t in range(FT):
                        last = pe.matmul(ps_y[it.par][:, j * P:(j + 1) * P], hT[it.par][:, t, j * P:(j + 1) * P], li3[:, t, :],
                                         start=(t == 0), stop=(t == FT - 1))
                    last.then_inc(s_y, 1)

                steps = {"turn": (turn, 1), **numbered("hidden", hidden, FT, 2), **numbered("output", output, GROUP, 3)}
                skewed(pe, n, in_order(steps, "output0 hidden0 hidden1 hidden2 hidden3 output2 output1 turn output3" if first else
                                            "hidden0 output0 hidden1 output1 turn hidden2 output2 hidden3 output3"), 6)

            @block.scalar
            def _(act):
                act.wait_ge(s_w, all_weights)

                def fetch(it):
                    act.wait_ge(s_turn, nth(it))
                    if (due := nth(it, FT, ago=2)) is not None:
                        act.wait_ge(s_h, due)
                    act.activation(yT[it.par][:, :], ps_t[:, :], ACT.Identity, bias=col[:, 1:2], scale=col[:, 0:1]).then_inc(s_yT, 1)

                def gelu(it, t):
                    act.wait_ge(s_h, nth(it, FT, t))
                    if (due := nth(it, GROUP, ago=2)) is not None:
                        act.wait_ge(s_y, due)
                    act.activation(hT[it.par][:, t, :], ps_h[t][:, :], ACT.Gelu, bias=b2[:, t:t + 1]).then_inc(s_hT, 1)

                steps = {"fetch": (fetch, 1), **numbered("gelu", gelu, FT, 2)}
                skewed(act, n, in_order(steps, "gelu0 gelu1 gelu2 gelu3 fetch" if first else "gelu1 gelu0 fetch gelu2 gelu3"), 6)

            @block.vector
            def _(dve):
                def batch(v, it, j):
                    return v[:, bass.ts(it.b * GROUP + j, P)]

                def part(v, it, j):
                    return v[it.par][:, j * P:(j + 1) * P]

                def hat(it):
                    if (due := nth(it, ago=2)) is not None:
                        dve.wait_ge(s_turn, due)
                    n3.hat(dve, it, lambda j: batch(g.y, it, j), lambda j: part(yh, it, j))

                def end_sum(it):
                    c = acc[it.par][:, :]
                    dve.wait_ge(s_a2, nth(it))
                    dve.wait_ge(s_y, nth(it, GROUP))
                    dve.tensor_tensor(c, ps_y[it.par][:, :], c, ALU.add).then_inc(s_sum, 1)
                    dve.wait_ge(s_sum, nth(it))
                    if first:
                        n2.statistics(dve, it, lambda j: part(acc, it, j))
                    else:
                        x = group(g.x, it)
                        dve.scalar_tensor_tensor(x, c, g.gates[:, 3:4], x, ALU.mult, ALU.add).then_inc(s_done, 1)

                steps = {"hat": (hat, 1), "stats": (lambda it: n3.statistics(dve, it, lambda j: batch(g.y, it, j)), 0),
                         "sum": (end_sum, 3)}
                names = "hat stats sum"
                if first:
                    steps["hat2"] = (lambda it: n2.hat(dve, it, lambda j: part(acc, it, j), lambda j: part(acc, it, j)), 4)
                    names = "stats hat hat2 sum"
                skewed(dve, n, in_order(steps, names), 6)


def l3_xattn(nc, g, a):
    with nc.sbuf_tensor("l3_y", [P, g.B * P], F32) as g.y, nc.sbuf_tensor("l3_z", [P, g.B * P], F32) as g.z:
        l3_attention(nc, g, a, "l3a", "a1", True)
        l3_mlp(nc, g, a, "l3b", "a1", True)
        l3_attention(nc, g, a, "l3c", "a2", False)
        l3_mlp(nc, g, a, "l3d", "a2", False)


def l3_ffn(nc, g, a):
    CYC = 3
    Q4 = P // 4
    H2, H3 = P // 2, P // 4
    n = g.B // GROUP
    W = GROUP * P
    with Stage(nc, "l3f") as st:
        w1, w2, w3, w4 = st.sb("w1", [P, P]), st.sb("w2", [P, H2]), st.sb("w3", [H2, H3]), st.sb("w4", [H3, 1])
        v1, v2, v3 = st.sb("v1", [P, H2]), st.sb("v2", [H2, H3]), st.sb("v3", [H3, 1])
        b1, b2, b3 = st.sb("b1", [P, 1]), st.sb("b2", [H2, 1]), st.sb("b3", [H3, 1])
        c1, c2 = st.sb("c1", [H2, 1]), st.sb("c2", [H3, 1])
        rows = st.sb("rows", [P, 3])
        half, r03 = st.sb("half", [P, 2]), st.sb("r03", [P, 2])
        mean_of = st.sb("mean_of", [P, 1])
        mean, gh1, gh2 = st.sb("mean", [P, GROUP]), st.sb("gh1", [H2, GROUP]), st.sb("gh2", [H3, GROUP])
        gth = st.sb("gth", [P, GROUP])
        base = st.sb("base", [P, g.B])
        u = [None] + [st.sb2(f"u{k}_", [P, W]) for k in range(1, CYC)] + [[st.sb("u3", [P, W])] * 2]
        uT = [None] + [st.sb(f"uT{k}", [P, W]) for k in range(1, CYC)]
        h1, h2, h3 = [[st.sb(f"h{m}_{k}", [r, W]) for k in range(CYC)] for m, r in ((1, P), (2, H2), (3, H3))]
        th, cp = [st.sb(f"th{k}", [P, GROUP]) for k in range(CYC)], [st.sb(f"cp{k}", [P, GROUP]) for k in range(CYC)]
        tw = [st.sb(f"tw{k}", [P, W]) for k in range(CYC)]
        ps_xT, ps_g = st.ps("xT"), st.ps("g")
        ps_a, ps_b = [[st.ps(f"cycle_{m}{k}") for k in range(CYC)] for m in "ab"]
        fr = GroupFront(st, g, ps_xT, split=False)
        u[0] = fr.xn
        s_w, s_const, s_const2 = st.sem("s_w"), st.sem("s_const"), st.sem("s_const2")
        s_meanp, s_mean, s_g1p, s_g1, s_g2p, s_g2, s_g3p, s_gth, s_base = [
            st.sem(k) for k in ("s_meanp", "s_mean", "s_g1p", "s_g1", "s_g2p", "s_g2", "s_g3p", "s_gth", "s_base")]
        s_uTp, s_uT, s_h1p, s_h1, s_h2p, s_h2, s_h3p, s_h3, s_zp, s_th, s_cpa, s_cp, s_tw, s_u = [
            [st.sem(f"{k}_{i}") for i in range(CYC)] for k in (
                "s_uTp", "s_uT", "s_h1p", "s_h1", "s_h2p", "s_h2", "s_h3p", "s_h3", "s_zp", "s_th", "s_cpa", "s_cp", "s_tw", "s_u")]
        s_x, s_pass, s_out = st.sem("s_x"), st.sem("s_pass"), st.sem("s_out")
        weights = [(w1[:, :], a["cn_w1"]), (w2[:, :], a["cn_w2"]), (w3[:, :], a["cn_w3"]), (w4[:, :], a["cn_w4"]),
                   (b1[:, :], a["cn_b1"]), (b2[:, :], a["cn_b2"]), (b3[:, :], a["cn_b3"]),
                   (v1[:, :], a["gc_w1"]), (v2[:, :], a["gc_w2"]), (v3[:, :], a["gc_w3"]),
                   (c1[:, :], a["gc_b1"]), (c2[:, :], a["gc_b2"]),
                   (rows[:, 0:1], a["cn_b4"].partition_broadcast(P)), (rows[:, 1:2], a["gc_b3"].partition_broadcast(P)),
                   (rows[:, 2:3], a["adaptive_range"].partition_broadcast(P))]
        all_weights = 16 * len(weights)
        LAG = [2, 3, 4]

        with nc.Block() as block:
            @block.sync
            def _(sp):
                for dst, src in weights:
                    sp.dma_start(dst, src).then_inc(s_w, 16)

                def store(it):
                    sp.wait_ge(s_x, nth(it))
                    sp.dma_start(g.out[:, bass.ds(it.b * GROUP, GROUP), :].rearrange("p b d -> p (b d)"),
                                 g.x[:, bass.ts(it.b, W)]).then_inc(s_out, 16)

                skewed(sp, n, [(store, 0)], 2)
                sp.wait_ge(s_out, 16 * n)

            @block.gpsimd
            def _(pool):
                pool.memset(mean_of[:, :], 1.0 / P).then_inc(s_const2, 1)
                skewed(pool, n, [(lambda it: fr.inverse_deviation(pool, it), 0)], 2)

            @block.tensor
            def _(pe):
                pe.wait_ge(s_const2, 1)

                def mean_token(it):
                    pe.wait_ge(fr.s_xn, nth(it))
                    if (due := nth(it, ago=1)) is not None:
                        pe.wait_ge(s_gth, due)
                    for j in range(GROUP):
                        last = pe.matmul(ps_g[:, j:j + 1], fr.xn[it.par][:, j * P:(j + 1) * P], mean_of[:, :], start=True, stop=True)
                    last.then_inc(s_meanp, 1)

                def global1(it):
                    if first_of(it):
                        pe.wait_ge(s_w, all_weights)
                    pe.wait_ge(s_mean, nth(it))
                    pe.matmul(ps_g[0:H2, 0:GROUP], v1[:, :], mean[:, :], start=True, stop=True).then_inc(s_g1p, 1)

                def global2(it):
                    pe.wait_ge(s_g1, nth(it))
                    pe.sem_inc(s_pass, 1)
                    pe.matmul(ps_g[0:H3, 0:GROUP], v2[:, :], gh1[:, :], start=True, stop=True).then_inc(s_g2p, 1)

                def global3(it):
                    pe.wait_ge(s_g2, nth(it))
                    pe.matmul(ps_g[:, 0:GROUP], v3[:, :].to_broadcast([H3, P]), gh2[:, :], start=True, stop=True).then_inc(s_g3p, 1)

                def turn(it, k):
                    pe.wait_ge(s_u[k - 1], nth(it))
                    if (due := nth(it, ago=1)) is not None:
                        pe.wait_ge(s_th[k], due)
                    for j in range(GROUP):
                        last = pe.transpose(ps_a[k][:, j * P:(j + 1) * P], u[k][it.par][:, j * P:(j + 1) * P], g.ident[:, :])
                    last.then_inc(s_uTp[k], 1)

                def layer1(it, k):
                    if k == 0:
                        pe.wait_ge(fr.s_xT, nth(it))
                    else:
                        pe.wait_ge(s_uT[k], nth(it))
                    if (due := nth(it, ago=1)) is not None:
                        pe.wait_ge(s_h3[k], due)
                    src = fr.xT[it.par] if k == 0 else uT[k]
                    pe.matmul(ps_b[k][:, :], w1[:, :], src[:, :], start=True, stop=True).then_inc(s_h1p[k], 1)

                def layer2(it, k):
                    if (due := nth(it, ago=1)) is not None:
                        pe.wait_ge(s_th[k], due)
                    pe.wait_ge(s_h1[k], nth(it))
                    pe.matmul(ps_a[k][0:H2, :], w2[:, :], h1[k][:, :], start=True, stop=True).then_inc(s_h2p[k], 1)

                def layer3(it, k):
                    pe.wait_ge(s_h2[k], nth(it))
                    pe.sem_inc(s_pass, 1)
                    pe.matmul(ps_b[k][0:H3, :], w3[:, :], h2[k][:, :], start=True, stop=True).then_inc(s_h3p[k], 1)

                def layer4(it, k):
                    pe.wait_ge(s_h3[k], nth(it))
                    for j in range(GROUP):
                        last = pe.matmul(ps_a[k][:, j:j + 1], h3[k][:, j * P:(j + 1) * P], w4[:, :], start=True, stop=True)
                    last.then_inc(s_zp[k], 1)

                steps = {"turn_x": (lambda it: fr.turn(pe, it), 1), "mean": (mean_token, 1), "global1": (global1, 1),
                         "global2": (global2, 1), "global3": (global3, 1)}
                for k in range(CYC):
                    for name, f in (("layer1", layer1), ("layer2", layer2), ("layer3", layer3), ("layer4", layer4)):
                        steps[f"{name}_{k}"] = (lambda it, k=k, f=f: f(it, k), LAG[k])
                    if k:
                        steps[f"turn{k}"] = (lambda it, k=k: turn(it, k), LAG[k])
                skewed(pe, n, in_order(steps, "turn1 layer1_0 turn2 layer1_2 layer1_1 mean turn_x layer2_0 layer2_2 layer2_1 "
                                              "layer3_0 layer3_2 global1 layer3_1 global2 layer4_0 layer4_2 layer4_1 global3"), 6)

            @block.scalar
            def _(act):
                def fetch(it, k):
                    act.wait_ge(s_uTp[k], nth(it))
                    if (due := nth(it, ago=1)) is not None:
                        act.wait_ge(s_h1p[k], due)
                    act.copy(uT[k][:, :], ps_a[k][:, :]).then_inc(s_uT[k], 1)

                def gelu1(it, k):
                    act.wait_ge(s_h1p[k], nth(it))
                    if (due := nth(it, ago=1)) is not None:
                        act.wait_ge(s_h2p[k], due)
                    act.activation(h1[k][:, :], ps_b[k][:, :], ACT.Gelu, bias=b1[:, 0:1]).then_inc(s_h1[k], 1)

                def gelu2(it, k):
                    act.wait_ge(s_h2p[k], nth(it))
                    if (due := nth(it, ago=1)) is not None:
                        act.wait_ge(s_h3p[k], due)
                    act.activation(h2[k][:, :], ps_a[k][0:H2, :], ACT.Gelu, bias=b2[:, 0:1]).then_inc(s_h2[k], 1)

                def gelu3(it, k):
                    act.wait_ge(s_h3p[k], nth(it))
                    if (due := nth(it, ago=1)) is not None:
                        act.wait_ge(s_zp[k], due)
                    act.activation(h3[k][:, :], ps_b[k][0:H3, :], ACT.Gelu, bias=b3[:, 0:1]).then_inc(s_h3[k], 1)

                def tanh(it, k):
                    act.wait_ge(s_zp[k], nth(it))
                    if (due := nth(it, ago=1)) is not None:
                        act.wait_ge(s_cpa[k], due)
                    act.activation(th[k][:, :], ps_a[k][:, 0:GROUP], ACT.Tanh, bias=half[:, 0:1], scale=0.5).then_inc(s_th[k], 1)

                def fetch_mean(it):
                    act.wait_ge(s_meanp, nth(it))
                    act.copy(mean[:, :], ps_g[:, 0:GROUP]).then_inc(s_mean, 1)
                    if first_of(it):
                        act.wait_ge(s_w, all_weights)
                        act.wait_ge(s_const, 1)

                def global1(it):
                    act.wait_ge(s_g1p, nth(it))
                    act.activation(gh1[:, :], ps_g[0:H2, 0:GROUP], ACT.Gelu, bias=c1[:, 0:1]).then_inc(s_g1, 1)

                def global2(it):
                    act.wait_ge(s_g2p, nth(it))
                    act.activation(gh2[:, :], ps_g[0:H3, 0:GROUP], ACT.Gelu, bias=c2[:, 0:1]).then_inc(s_g2, 1)

                def global3(it):
                    act.wait_ge(s_g3p, nth(it))
                    if (due := nth(it, ago=1)) is not None:
                        act.wait_ge(s_base, due)
                    act.activation(gth[:, :], ps_g[:, 0:GROUP], ACT.Tanh, bias=half[:, 1:2], scale=0.5).then_inc(s_gth, 1)

                steps = {"fetch_x": (lambda it: fr.fetch(act, it, s_h1p[0]), 1), "fetch_mean": (fetch_mean, 1),
                         "global1": (global1, 1), "global2": (global2, 1), "global3": (global3, 1)}
                for k in range(CYC):
                    for name, f in (("gelu1", gelu1), ("gelu2", gelu2), ("gelu3", gelu3), ("tanh", tanh)):
                        steps[f"{name}_{k}"] = (lambda it, k=k, f=f: f(it, k), LAG[k])
                    if k:
                        steps[f"fetch{k}"] = (lambda it, k=k: fetch(it, k), LAG[k])
                skewed(act, n, in_order(steps, "fetch1 fetch2 gelu1_0 fetch_x gelu1_2 gelu1_1 gelu2_0 fetch_mean gelu2_2 gelu2_1 "
                                               "gelu3_0 global1 gelu3_2 global2 gelu3_1 tanh_0 tanh_1 global3 tanh_2"), 6)

            @block.vector
            def _(dve):
                def constants():
                    dve.wait_ge(s_w, all_weights)
                    dve.tensor_scalar(half[:, :], rows[:, 0:2], 0.5, None, ALU.mult)
                    dve.tensor_scalar(r03[:, 0:1], rows[:, 2:3], 0.3, None, ALU.mult)
                    dve.tensor_scalar(r03[:, 1:2], rows[:, 2:3], 0.7, None, ALU.mult)
                    dve.drain()
                    dve.sem_inc(s_const, 1)

                def coupling_base(it):
                    dve.wait_ge(s_gth, nth(it))
                    dve.tensor_scalar(slot(it), gth[:, :], r03[:, 1:2], 0.1, ALU.mult, ALU.add).then_inc(s_base, 1)

                def slot(it):
                    return base[:, bass.ts(it.b, GROUP)]

                def couple(it, k):
                    dve.wait_ge(s_th[k], nth(it))
                    dve.wait_ge(s_base, nth(it))
                    if (due := nth(it, ago=1)) is not None:
                        dve.wait_ge(s_tw[k], due)
                    dve.scalar_tensor_tensor(cp[k][:, :], th[k][:, :], r03[:, 0:1], slot(it), ALU.mult, ALU.add).then_inc(s_cpa[k], 1)
                    dve.wait_ge(s_cpa[k], nth(it))
                    src = u[k][it.par][:, :].rearrange("p (j d) -> p j d", d=P)
                    t = tw[k][:, :].rearrange("p (j d) -> p j d", d=P)
                    if (due := nth(it, ago=1)) is not None:
                        dve.wait_ge(s_u[k], due)
                    dve.tensor_tensor(t, src, cp[k][:, :].unsqueeze(2).to_broadcast([P, GROUP, P]), ALU.mult).then_inc(s_tw[k], 1)
                    dve.wait_ge(s_tw[k], nth(it))
                    if k < CYC - 1:
                        if (due := nth(it, ago=2)) is not None:
                            dve.wait_ge(s_uTp[k + 1], due)
                        if (due := nth(it, ago=2)) is not None:
                            dve.wait_ge(s_u[k + 1], due)
                    else:
                        if (due := nth(it, ago=1)) is not None:
                            dve.wait_ge(s_x, due)
                    dst = u[k + 1][it.par][:, :].rearrange("p (j d) -> p j d", d=P)
                    for q, (other, op) in enumerate(((2, ALU.add), (3, ALU.subtract), (0, ALU.subtract), (1, ALU.add))):
                        last = dve.tensor_tensor(dst[:, :, q * Q4:(q + 1) * Q4], src[:, :, q * Q4:(q + 1) * Q4],
                                                 t[:, :, other * Q4:(other + 1) * Q4], op)
                    last.then_inc(s_u[k], 1)

                def add(it):
                    x = g.x[:, bass.ts(it.b, W)]
                    dve.wait_ge(s_u[CYC - 1], nth(it))
                    dve.scalar_tensor_tensor(x, u[CYC][0][:, :], g.gates[:, 7:8], x, ALU.mult, ALU.add).then_inc(s_x, 1)

                def normalize(it):
                    if (due := nth(it, ago=2)) is not None:
                        dve.wait_ge(s_u[0], due)
                    if (due := nth(it, ago=2)) is not None:
                        dve.wait_ge(s_meanp, due)
                    fr.normalize(dve, it)
                    if first_of(it):
                        constants()

                steps = {**{f"couple{k}": (lambda it, k=k: couple(it, k), LAG[k]) for k in range(CYC)}, "add": (add, LAG[2]),
                         "base": (coupling_base, 1), "normalize": (normalize, 1), "statistics": (lambda it: fr.statistics(dve, it), 0)}
                skewed(dve, n, in_order(steps, "normalize statistics couple0 couple1 couple2 base add"), 6)


class Globals:
    pass


def build(nc, a, out, stages):
    g = Globals()
    g.B = a["x"].shape[1]
    g.ctxT_d, g.ctx_d = a["ctxT"], a["ctx"]
    with ExitStack() as ctx:
        def sb(name, shape):
            return ctx.enter_context(nc.sbuf_tensor(name, shape, F32))

        g.x = sb("x_res", [P, g.B * P])
        g.ident, g.head8, g.head32 = sb("ident", [P, P]), sb("head8", [P, HEADS]), sb("head32", [P, 4])
        g.eps, g.minus_half = sb("eps", [P, 4]), sb("minus_half", [P, 4])
        g.gates, gates_in = sb("gates", [P, 8]), sb("gates_in", [P, 8])
        g.out = out
        g.s_x_rest = ctx.enter_context(nc.semaphore("s_x_rest"))
        with Stage(nc, "init") as st:
            s_in, s_set, s_ident, s_gates, s_x = st.sem("s_in"), st.sem("s_set"), st.sem("s_ident"), st.sem("s_gates"), st.sem("s_x")
            with nc.Block() as block:
                @block.sync
                def _(sp):
                    sp.dma_start(gates_in[:, 0:4], a["g_xattn"].partition_broadcast(P)).then_inc(s_in, 16)
                    sp.dma_start(gates_in[:, 4:8], a["g_ffn"].partition_broadcast(P)).then_inc(s_in, 16)
                    sp.dma_start(g.x[:, 0:AHEAD * P], a["x"][:, 0:AHEAD, :].rearrange("p b d -> p (b d)")).then_inc(s_x, 16)
                    sp.dma_start(g.x[:, AHEAD * P:], a["x"][:, AHEAD:, :].rearrange("p b d -> p (b d)")).then_inc(g.s_x_rest, 16)
                    sp.wait_ge(s_x, 16)

                @block.scalar
                def _(act):
                    act.wait_ge(s_in, 32)
                    act.activation(g.gates[:, :], gates_in[:, :], ACT.Tanh).then_inc(s_gates, 1)
                    act.wait_ge(s_gates, 1)

                @block.gpsimd
                def _(pool):
                    pool.memset(g.eps[:, :], LN_EPS).then_inc(s_set, 1)
                    pool.memset(g.minus_half[:, :], -0.5).then_inc(s_set, 1)
                    pool.memset(g.ident[:, :], 0.0).then_inc(s_set, 1)
                    pool.memset(g.head8[:, :], 1.0).then_inc(s_set, 1)
                    pool.memset(g.head32[:, :], 1.0).then_inc(s_set, 1)
                    pool.wait_ge(s_set, 5)
                    pool.affine_select(out=g.ident[:, :], in_=g.ident[:, :], compare_op=ALU.not_equal, fill=1.0,
                                       base=0, pattern=[[-1, P]], channel_multiplier=1).then_inc(s_ident, 1)
                    n = 1
                    for m, w, k in ((g.head8, 8, HEADS), (g.head32, 32, 4)):
                        pool.affine_select(out=m[:, :], in_=m[:, :], compare_op=ALU.is_ge, fill=0.0,
                                           base=0, pattern=[[-w, k]], channel_multiplier=1).then_inc(s_ident, 1)
                        n += 1
                        pool.wait_ge(s_ident, n)
                        pool.affine_select(out=m[:, :], in_=m[:, :], compare_op=ALU.is_ge, fill=0.0,
                                           base=w - 1, pattern=[[w, k]], channel_multiplier=-1).then_inc(s_ident, 1)
                        n += 1
                    pool.wait_ge(s_ident, n)
        for s in stages:
            s(nc, g, a)


def l0_xattn(nc, g, a):
    small_head_attention(nc, g, "l0x", a["L0_Wq"], a["L0_Wk"], a["L0_Wv"], a["L0_Wo"], gate=0)


def l2_xattn(nc, g, a):
    small_head_attention(nc, g, "l2x", a["L2_Wq"], a["L2_Wk"], a["L2_Wv"], a["L2_Wo"],
                         a["L2_bq"], a["L2_bk"], a["L2_bv"], a["L2_bo"], gate=2)


def lay_out(i):
    c = np.ascontiguousarray
    o = {"x": c(i["x"].transpose(1, 0, 2)), "ctx": c(i["ctx_512"].transpose(1, 0, 2)),
         "ctxT": c(i["ctx_512"].transpose(2, 0, 1)), "g_xattn": i["g_xattn"], "g_ffn": i["g_ffn"]}
    o["L0_Wq"], o["L0_Wo"] = c(i["L0_xattn_Wq"].T), c(i["L0_xattn_Wo"].T)
    o["L0_Wk"], o["L0_Wv"] = c(i["L0_xattn_Wkv"][:P].T), c(i["L0_xattn_Wkv"][P:].T)
    for n in ("Wq", "Wk", "Wv", "Wo"):
        o["L2_" + n] = i["L2_xattn_" + n]
    o["L2_bq"], o["L2_bk"] = i["L2_xattn_bq"].reshape(P, 1), i["L2_xattn_bk"].reshape(P, 1)
    o["L2_bv"], o["L2_bo"] = i["L2_xattn_bv"].reshape(P, 1), i["L2_xattn_bo"]

    o["L0_Wg"], o["L0_bg"], o["L0_Wi"] = c(i["L0_ffn_Wg"].T), i["L0_ffn_bg"], c(i["L0_ffn_Wi"].T)
    o["L0_A"], o["L0_B"] = c(i["L0_ffn_A"].transpose(1, 0, 2)), c(i["L0_ffn_B"].transpose(2, 0, 1))
    o["L0_Wof"] = c(i["L0_ffn_Wo"].T.reshape(4, P, P).transpose(1, 0, 2))
    o["L1_Wg"], o["L1_W1"], o["L1_W3"] = i["L1_ffn_Wg"], c(i["L1_ffn_W1"].transpose(1, 0, 2)), c(i["L1_ffn_W3"].transpose(1, 0, 2))
    o["L1_W2"] = c(i["L1_ffn_W2"].reshape(8, 4, P, P).transpose(2, 0, 1, 3))
    o["L2_gw"] = c(i["L2_ffn_gate_w"].T)
    o["L2_wg"], o["L2_wu"] = [c(i["L2_ffn_" + n].transpose(1, 0, 2).reshape(P, 1024)) for n in ("w_gate", "w_up")]
    o["L2_wd"] = c(i["L2_ffn_w_down"].reshape(8, P, P).transpose(1, 0, 2))
    o["L2_sg"], o["L2_su"], o["L2_sd"] = i["L2_ffn_ws_gate"], i["L2_ffn_ws_up"], i["L2_ffn_ws_down"]

    o["L1_WqT"] = c(i["L1_xattn_Wq"].reshape(P, 16, 64).transpose(2, 1, 0))
    o["L1_WkT"] = c(i["L1_xattn_Wk"].reshape(64, 16, 64).transpose(2, 1, 0))
    o["L1_WvT"] = c(i["L1_xattn_Wv"].reshape(64, 16, 64).transpose(2, 1, 0))
    o["L1_Woh"] = c(i["L1_xattn_Wo"].reshape(16, 64, P).transpose(1, 0, 2))
    o["L1_bo"] = i["L1_xattn_bo"]
    for n in ("ln1_g", "ln1_b", "ln2_g", "ln2_b"):
        o[n] = i["L3_xattn_" + n]
    for p in ("a1", "a2"):
        s = "L3_xattn_" + p + "_"
        for n in ("wq", "wk", "wv"):
            w = i[s + n]
            o[f"{p}_{n}"] = c(w.transpose(1, 0, 2).reshape(w.shape[1], 512))
        for n in ("li1_w", "li3_w"):
            o[f"{p}_{n}"] = c(i[s + n].reshape(4, P, P).transpose(1, 0, 2))
        o[p + "_li2_w"], o[p + "_li2_b"] = i[s + "li2_w"], c(i[s + "li2_b"].reshape(4, P).T)
        for n in ("li1_b", "li3_b"):
            o[f"{p}_{n}"] = i[s + n]
        for n in ("lnx_g", "lnx_b", "lny_g", "lny_b", "ln3_g", "ln3_b"):
            o[f"{p}_{n}"] = i[s + n].reshape(-1, 1)

    for n in ("cn_w1", "cn_w2", "cn_w3", "cn_w4", "gc_w1", "gc_w2", "gc_w3"):
        o[n] = i["L3_ffn_" + n]
    for n in ("cn_b1", "cn_b2", "cn_b3", "gc_b1", "gc_b2"):
        o[n] = i["L3_ffn_" + n].reshape(-1, 1)
    for n in ("cn_b4", "gc_b3", "adaptive_range"):
        o[n] = i["L3_ffn_" + n]
    return o


STAGES = [l0_xattn, l0_ffn, l1_xattn, l1_ffn, l2_xattn, l2_ffn, l3_xattn, l3_ffn]


def kernel(**inputs):
    import concourse.bacc as bacc
    from concourse.bass_utils import run_bass_kernel_spmd

    laid = lay_out({k: np.asarray(v) for k, v in inputs.items()})
    nc = bacc.Bacc("TRN2", target_bir_lowering=False, num_devices=1)
    arrays, args = {}, {}
    for name, v in laid.items():
        v = np.ascontiguousarray(v)
        arrays[f"in_{name}"] = v
        args[name] = nc.dram_tensor(f"in_{name}", v.shape, mybir.dt.from_np(v.dtype), kind="ExternalInput").ap()
    out = nc.dram_tensor("out_x", laid["x"].shape, F32, kind="ExternalOutput").ap()
    build(nc, args, out, STAGES)
    got = run_bass_kernel_spmd(nc, [arrays], core_ids=[0]).results[0]["out_x"]
    return np.ascontiguousarray(got.transpose(1, 0, 2))
```
